# Optimizing a Trainium2 kernel written in Bass

```python
import numpy as np
import jax
import jax.numpy as jnp

def _softmax(x, axis=-1):
    return jax.nn.softmax(x, axis=axis)

def _gelu(x):
    return jax.nn.gelu(x, approximate=True)

def _silu(x):
    return jax.nn.silu(x)

def _sigmoid(x):
    return jax.nn.sigmoid(x)

def _layernorm(x, axis=-1, eps=1e-05):
    m = jnp.mean(x, axis=axis, keepdims=True)
    v = jnp.var(x, axis=axis, keepdims=True)
    return (x - m) / jnp.sqrt(v + eps)

def _scatter_add(tgt, idx, src, axis=0):
    return tgt.at[idx].add(src)

def _segment_sum(src, seg, n):
    return jax.ops.segment_sum(src, seg, n)
kernel_name = 'mk_recurrent_d4_jaxref_r8_358218'

def setup_inputs(seed: int=0):
    np.random.seed(seed)
    _w = jnp.asarray

    def _L0_attn_setup():
        import jax, jax.numpy as jnp
        import numpy as np
        NHEAD = 16

        def _forward(x, time_maa_x, time_maa, time_maa_w1, time_maa_w2, time_decay, time_decay_w1, time_decay_w2, time_aaaaa, time_aaa_w1, time_aaa_w2, time_kkk_w1, time_kkk_w2, gate_w1, gate_w2, time_misc_a, ma_w1, ma_w2, time_misc_k, mk_w1, mk_w2, receptance, key_w, value, output, ln_w, ln_b, time_faaaa):
            B, T, C = x.shape
            H, N = (NHEAD, C // NHEAD)
            xprev = jnp.pad(x, ((0, 0), (1, 0), (0, 0)))[:, :T]
            xx = xprev - x
            xxx = x + xx * time_maa_x
            mix = jnp.tanh(xxx @ time_maa_w1.T).reshape(B, T, 4, -1)
            deltas = jnp.einsum('btfd,fcd->fbtc', mix, time_maa_w2)
            xrg, xwa, xk, xv = x[None] + xx[None] * (time_maa + deltas)
            r = xrg @ receptance.T
            g = jnp.tanh(xrg @ gate_w1.T) @ gate_w2.T
            k = xk @ key_w.T
            kk1 = jnp.tanh(xk @ time_kkk_w1.T)
            mk1 = xk @ mk_w1.T
            v = xv @ value.T
            w1 = jnp.tanh(xwa @ time_decay_w1.T)
            a1 = xwa @ time_aaa_w1.T
            ma1 = xwa @ ma_w1.T
            w = -jax.nn.softplus(-(time_decay + w1 @ time_decay_w2.T)) - 0.5
            kk = k + kk1 @ time_kkk_w2.T
            kk = kk.reshape(B, T, H, N)
            kk = kk / jnp.maximum(jnp.linalg.norm(kk, axis=-1, keepdims=True), 1e-12)
            kk = kk.reshape(B, T, C)
            a = jax.nn.sigmoid(time_aaaaa + a1 @ time_aaa_w2.T)
            ma = jax.nn.sigmoid(time_misc_a + ma1 @ ma_w2.T)
            k = k * ma + k * a * (1 - ma)
            mk = jax.nn.sigmoid(time_misc_k + mk1 @ mk_w2.T)
            k = k * jnp.exp(w * mk)
            b = -kk * a

            def heads(z):
                return z.reshape(B, T, H, N).transpose(1, 0, 2, 3)
            rh, wh, kh, vh, kkh, bh = map(heads, (r, w, k, v, kk, b))

            def step(S, inp):
                r_, w_, k_, v_, kk_, b_ = inp
                sab = jnp.einsum('bhvk,bhk->bhv', S, kk_)
                S = S * jnp.exp(w_)[:, :, None, :] + sab[..., None] * b_[:, :, None, :] + v_[..., None] * k_[:, :, None, :]
                y = jnp.einsum('bhvk,bhk->bhv', S, r_)
                return (S, y)
            S0 = jnp.zeros((B, H, N, N), x.dtype)
            _, y = jax.lax.scan(step, S0, (rh, wh, kh, vh, kkh, bh))
            y = y.transpose(1, 0, 2, 3)
            mu = y.mean(-1, keepdims=True)
            var = ((y - mu) ** 2).mean(-1, keepdims=True)
            yn = (y - mu) / jnp.sqrt(var + 0.00064) * ln_w.reshape(H, N) + ln_b.reshape(H, N)
            r4 = r.reshape(B, T, H, N)
            k4 = k.reshape(B, T, H, N)
            v4 = v.reshape(B, T, H, N)
            bonus = (r4 * k4 * time_faaaa.reshape(H, N)).sum(-1, keepdims=True) * v4
            out = (yn + bonus).reshape(B, T, C) * g
            return out @ output.T
        key = jax.random.key(seed)
        ks = iter(jax.random.split(key, 40))
        B, T, C = (2, 128, 128)

        def n(shape, s=1.0):
            return jax.random.normal(next(ks), shape, jnp.float32) * s

        def u(shape, lo, hi):
            return jax.random.uniform(next(ks), shape, jnp.float32, lo, hi)
        d = {}
        d['x'] = n((B, T, C))
        d['time_maa_x'] = u((1, 1, C), 0.0, 1.0)
        d['time_maa'] = u((4, 1, 1, C), 0.0, 1.0)
        d['time_maa_w1'] = n((128, C), 0.02)
        d['time_maa_w2'] = n((4, C, 32), 0.05)
        d['time_decay'] = u((1, 1, C), -6.5, -1.5)
        d['time_decay_w1'] = n((64, C), 0.02)
        d['time_decay_w2'] = n((C, 64), 0.05)
        d['time_aaaaa'] = n((1, 1, C), 0.1)
        d['time_aaa_w1'] = n((16, C), 0.02)
        d['time_aaa_w2'] = n((C, 16), 0.05)
        d['time_kkk_w1'] = n((16, C), 0.02)
        d['time_kkk_w2'] = n((C, 16), 0.05)
        d['gate_w1'] = n((128, C), 0.05)
        d['gate_w2'] = n((C, 128), 0.05)
        d['time_misc_a'] = n((1, 1, C), 0.1)
        d['ma_w1'] = n((16, C), 0.02)
        d['ma_w2'] = n((C, 16), 0.05)
        d['time_misc_k'] = n((1, 1, C), 0.1)
        d['mk_w1'] = n((16, C), 0.02)
        d['mk_w2'] = n((C, 16), 0.05)
        s = 0.5 / C ** 0.5
        d['receptance'] = u((C, C), -s, s)
        d['key_w'] = u((C, C), -0.1 * s, 0.1 * s)
        d['value'] = u((C, C), -s, s)
        d['output'] = n((C, C), 0.02)
        d['ln_w'] = jnp.ones((C,), jnp.float32)
        d['ln_b'] = jnp.zeros((C,), jnp.float32)
        d['time_faaaa'] = n((C,), 0.1)
        return d
    _L0_attn_in = _L0_attn_setup()

    def _L0_ffn_setup():
        import jax, jax.numpy as jnp
        import numpy as np
        CAP_FACTOR = 1.5
        key = jax.random.key(seed)
        ks = jax.random.split(key, 6)
        E, S, D, M = (48, 4, 128, 128)
        K = D // S
        x = jax.random.normal(ks[0], (4, 512, D), dtype=jnp.float32)
        Wr = jax.random.normal(ks[1], (E, D), dtype=jnp.float32) * 0.02
        W1 = jax.random.normal(ks[2], (E, S, D, M), dtype=jnp.float32) * (1.0 / np.sqrt(D))
        b1 = jnp.zeros((E, S, M), dtype=jnp.float32)
        W2 = jax.random.normal(ks[3], (E, S, M, K), dtype=jnp.float32) * (1.0 / np.sqrt(M))
        b2 = jnp.zeros((E, S, K), dtype=jnp.float32)
        return {'x': x, 'Wr': Wr, 'W1': W1, 'b1': b1, 'W2': W2, 'b2': b2}
    _L0_ffn_in = _L0_ffn_setup()

    def _L1_attn_setup():
        import jax, jax.numpy as jnp
        import numpy as np
        import math
        FEATURE_DIM = 16
        NUM_HEADS = 16
        HIDDEN = 128
        HEAD_DIM = HIDDEN // NUM_HEADS
        EPS = 1e-12
        IU, JU = np.triu_indices(FEATURE_DIM, 1)
        RD = math.sqrt(FEATURE_DIM)
        RRD = math.sqrt(RD)
        R2 = math.sqrt(2.0)

        def taylor_feature_map(x):
            x2 = x[..., :, None] * x[..., None, :]
            off = x2[..., IU, JU]
            diag = jnp.square(x)
            ones = jnp.ones_like(x[..., :1])
            return jnp.concatenate([ones, x / RRD, diag / (RD * R2), off / RD], axis=-1)
        key = jax.random.key(seed)
        k0, k1, k2, k3, k4 = jax.random.split(key, 5)
        b, t = (2, 64)
        s = 1.0 / math.sqrt(HIDDEN)
        return {'hidden_states': jax.random.normal(k0, (b, t, HIDDEN), jnp.float32), 'Wq': jax.random.normal(k1, (NUM_HEADS * FEATURE_DIM, HIDDEN), jnp.float32) * s, 'Wk': jax.random.normal(k2, (NUM_HEADS * FEATURE_DIM, HIDDEN), jnp.float32) * s, 'Wv': jax.random.normal(k3, (HIDDEN, HIDDEN), jnp.float32) * s, 'Wo': jax.random.normal(k4, (HIDDEN, HIDDEN), jnp.float32) * s}
    _L1_attn_in = _L1_attn_setup()

    def _L1_ffn_setup():
        import jax, jax.numpy as jnp
        import numpy as np
        B, L, H, E, FF, C = (4, 256, 128, 8, 512, 2)
        key = jax.random.key(seed)
        ks = jax.random.split(key, 6)
        s = 0.02
        return {'x': jax.random.normal(ks[0], (B, L, H), dtype=jnp.float32), 'Wg': jax.random.normal(ks[1], (H, E), dtype=jnp.float32) * s, 'W1': jax.random.normal(ks[2], (E, H, FF), dtype=jnp.float32) * s, 'b1': jnp.zeros((E, FF), dtype=jnp.float32), 'W2': jax.random.normal(ks[3], (E, FF, H), dtype=jnp.float32) * s, 'b2': jnp.zeros((E, H), dtype=jnp.float32)}
    _L1_ffn_in = _L1_ffn_setup()

    def _L2_attn_setup():
        import jax, jax.numpy as jnp
        import numpy as np
        B, S, D, H = (2, 256, 128, 16)
        HD = D // H
        FF = 512
        NUM_ITERS = 8
        DT = 0.1
        LN_EPS = 1e-05

        def _ln(x, g, b):
            m = jnp.mean(x, axis=-1, keepdims=True)
            v = jnp.var(x, axis=-1, keepdims=True)
            return (x - m) * jax.lax.rsqrt(v + LN_EPS) * g + b

        def _forward(x, qkv_w, qkv_b, out_w, out_b, g_attn, b_attn, g1, b1, g2, b2, w_ctx, w_x, b_inl, ff_w1, ff_b1, ff_w2, ff_b2):
            b, s, d = x.shape
            xn = _ln(x, g_attn, b_attn)
            qkv = (xn @ qkv_w + qkv_b).reshape(b, s, 3, H, HD)
            qkv = jnp.transpose(qkv, (2, 0, 3, 1, 4))
            q, k, v = (qkv[0], qkv[1], qkv[2])
            scores = jnp.einsum('bhqd,bhkd->bhqk', q, k) / np.sqrt(HD).astype(np.float32)
            causal = jnp.triu(jnp.ones((s, s), dtype=bool), 1)
            scores = jnp.where(causal[None, None], -jnp.inf, scores)
            attn_w = jax.nn.softmax(scores, axis=-1)
            attn = jnp.einsum('bhqk,bhkd->bhqd', attn_w, v)
            attn = jnp.transpose(attn, (0, 2, 1, 3)).reshape(b, s, d)
            attn = attn @ out_w + out_b
            x = x + attn
            ctx = attn.reshape(b * s, d)
            xs = _ln(x, g1, b1).reshape(b * s, d)
            vs = jnp.zeros_like(xs)

            def step(carry, _):
                xs, vs = carry
                u = jnp.tanh(ctx @ w_ctx + xs @ w_x + b_inl)
                vn = vs + DT * (u - xs - vs)
                xn_ = xs + DT * vn
                return ((xn_, vn), None)
            (xs, vs), _ = jax.lax.scan(step, (xs, vs), None, length=NUM_ITERS)
            x = x + xs.reshape(b, s, d)
            h = _ln(x, g2, b2)
            h = jax.nn.gelu(h @ ff_w1 + ff_b1, approximate=False)
            x = x + (h @ ff_w2 + ff_b2)
            return x
        key = jax.random.key(seed)
        ks = jax.random.split(key, 16)

        def xav(k, shape):
            lim = np.sqrt(6.0 / (shape[0] + shape[1]))
            return jax.random.uniform(k, shape, minval=-lim, maxval=lim, dtype=jnp.float32)
        return {'x': jax.random.normal(ks[0], (B, S, D), dtype=jnp.float32), 'qkv_w': xav(ks[1], (D, 3 * D)), 'qkv_b': jnp.zeros((3 * D,), jnp.float32), 'out_w': xav(ks[2], (D, D)), 'out_b': jnp.zeros((D,), jnp.float32), 'g_attn': jnp.ones((D,), jnp.float32), 'b_attn': jnp.zeros((D,), jnp.float32), 'g1': jnp.ones((D,), jnp.float32), 'b1': jnp.zeros((D,), jnp.float32), 'g2': jnp.ones((D,), jnp.float32), 'b2': jnp.zeros((D,), jnp.float32), 'w_ctx': xav(ks[3], (D, D)), 'w_x': xav(ks[4], (D, D)), 'b_inl': jnp.zeros((D,), jnp.float32), 'ff_w1': xav(ks[5], (D, FF)), 'ff_b1': jnp.zeros((FF,), jnp.float32), 'ff_w2': xav(ks[6], (FF, D)), 'ff_b2': jnp.zeros((D,), jnp.float32)}
    _L2_attn_in = _L2_attn_setup()

    def _L2_ffn_setup():
        import jax, jax.numpy as jnp
        import numpy as np
        D_IN, D_HID = (128, 512)

        def _ternary(key, shape):
            return jax.random.randint(key, shape, -1, 2).astype(jnp.float32)

        def _tlin(x, w, s):
            return jnp.einsum('bsi,oi->bso', x, w) * s
        key = jax.random.key(seed)
        ks = jax.random.split(key, 12)
        inv = lambda fan: 1.0 / np.sqrt(fan).astype(np.float32)
        return {'x': jax.random.normal(ks[0], (4, 256, D_IN), dtype=jnp.float32), 'w1_w': _ternary(ks[1], (D_HID, D_IN)), 'w1_s': jax.random.uniform(ks[2], (D_HID,), dtype=jnp.float32) * inv(D_IN), 'w2_w': _ternary(ks[3], (D_HID, D_IN)), 'w2_s': jax.random.uniform(ks[4], (D_HID,), dtype=jnp.float32) * inv(D_IN), 'h1_w': _ternary(ks[5], (D_HID, D_HID)), 'h1_s': jax.random.uniform(ks[6], (D_HID,), dtype=jnp.float32) * inv(D_HID), 'h2_w': _ternary(ks[7], (D_HID, D_HID)), 'h2_s': jax.random.uniform(ks[8], (D_HID,), dtype=jnp.float32) * inv(D_HID), 'w3_w': _ternary(ks[9], (D_IN, D_HID)), 'w3_s': jax.random.uniform(ks[10], (D_IN,), dtype=jnp.float32) * inv(D_HID)}
    _L2_ffn_in = _L2_ffn_setup()

    def _L3_attn_setup():
        import jax, jax.numpy as jnp
        import numpy as np
        D_MODEL = 128
        D_STATE = 128
        EXPAND = 2
        HEADDIM = 64
        NGROUPS = 1
        D_INNER = EXPAND * D_MODEL
        NHEADS = D_INNER // HEADDIM
        N_ANGLES = D_STATE // 2 // 2
        CHUNK = 64
        DT_MIN, DT_MAX, DT_FLOOR, A_FLOOR = (0.001, 0.1, 0.0001, 0.0001)
        EPS = 1e-05
        BATCH, SEQLEN = (2, 256)

        def _rope(t, theta):
            na = theta.shape[-1]
            x1, x2, rest = (t[..., :na], t[..., na:2 * na], t[..., 2 * na:])
            c, s = (jnp.cos(theta), jnp.sin(theta))
            return jnp.concatenate([x1 * c - x2 * s, x1 * s + x2 * c, rest], axis=-1)

        def _rmsnorm(t, w):
            var = jnp.mean(t * t, axis=-1, keepdims=True)
            return t * jax.lax.rsqrt(var + EPS) * w

        def _forward(u, W_in, W_out, dt_bias, B_bias, C_bias, B_norm_w, C_norm_w, D):
            b, L, _ = u.shape
            proj = u @ W_in
            sizes = [D_INNER, D_INNER, D_STATE * NGROUPS, D_STATE * NGROUPS, NHEADS, NHEADS, NHEADS, N_ANGLES]
            z, x, Bg, Cg, dd_dt, dd_A, trap, angles = jnp.split(proj, np.cumsum(sizes)[:-1], axis=-1)
            z = z.reshape(b, L, NHEADS, HEADDIM)
            x = x.reshape(b, L, NHEADS, HEADDIM)
            a = jnp.minimum(-jax.nn.softplus(dd_A), -A_FLOOR)
            dt = jax.nn.softplus(dd_dt + dt_bias)
            adt = a * dt
            theta = jnp.cumsum(angles[:, :, None, :] * dt[..., None], axis=1)
            Bn = _rmsnorm(Bg, B_norm_w)
            Cn = _rmsnorm(Cg, C_norm_w)
            K = _rope(Bn[:, :, None, :] + B_bias, theta)
            Q = _rope(Cn[:, :, None, :] + C_bias, theta)
            beta = jax.nn.sigmoid(trap)
            g1 = beta * dt
            dt_prev = jnp.pad(dt[:, :-1], ((0, 0), (1, 0), (0, 0)))
            g2 = (1.0 - beta) * jnp.exp(adt) * dt_prev
            Kp = jnp.pad(K[:, :-1], ((0, 0), (1, 0), (0, 0), (0, 0)))
            xp = jnp.pad(x[:, :-1], ((0, 0), (1, 0), (0, 0), (0, 0)))
            nc = L // CHUNK
            ch = lambda t: t.reshape(b, nc, CHUNK, *t.shape[2:])
            Qc, Kc, Kpc, xc, xpc = (ch(Q), ch(K), ch(Kp), ch(x), ch(xp))
            g1c, g2c, adtc = (ch(g1), ch(g2), ch(adt))
            ell = jnp.cumsum(adtc, axis=2)
            decay = jnp.exp(ell[:, :, :, None, :] - ell[:, :, None, :, :])
            mask = jnp.tril(jnp.ones((CHUNK, CHUNK), bool))
            decay = jnp.where(mask[None, None, :, :, None], decay, 0.0)
            S1 = jnp.einsum('bcihn,bcjhn->bcijh', Qc, Kc) * g1c[:, :, None, :, :] * decay
            S2 = jnp.einsum('bcihn,bcjhn->bcijh', Qc, Kpc) * g2c[:, :, None, :, :] * decay
            y_intra = jnp.einsum('bcijh,bcjhp->bcihp', S1, xc) + jnp.einsum('bcijh,bcjhp->bcihp', S2, xpc)
            dec_end = jnp.exp(ell[:, :, -1:, :] - ell)
            Wsum = jnp.einsum('bcjh,bcjhp,bcjhn->bchpn', g1c * dec_end, xc, Kc) + jnp.einsum('bcjh,bcjhp,bcjhn->bchpn', g2c * dec_end, xpc, Kpc)
            chunk_decay = jnp.exp(ell[:, :, -1, :])

            def step(Hprev, inp):
                wc, cd = inp
                return (cd[:, :, None, None] * Hprev + wc, Hprev)
            H0 = jnp.zeros((b, NHEADS, HEADDIM, D_STATE), u.dtype)
            _, Hprevs = jax.lax.scan(step, H0, (jnp.moveaxis(Wsum, 1, 0), jnp.moveaxis(chunk_decay, 1, 0)))
            Hprevs = jnp.moveaxis(Hprevs, 0, 1)
            y_inter = jnp.einsum('bcihn,bcih,bchpn->bcihp', Qc, jnp.exp(ell), Hprevs)
            y = (y_intra + y_inter).reshape(b, L, NHEADS, HEADDIM)
            y = y + D[None, None, :, None] * x
            y = y * jax.nn.silu(z)
            return y.reshape(b, L, D_INNER) @ W_out
        key = jax.random.key(seed)
        ks = jax.random.split(key, 4)
        d_in_proj = 2 * D_INNER + 2 * D_STATE * NGROUPS + 3 * NHEADS + N_ANGLES
        u = jax.random.normal(ks[0], (BATCH, SEQLEN, D_MODEL), jnp.float32)
        W_in = jax.random.normal(ks[1], (D_MODEL, d_in_proj), jnp.float32) * 0.02
        W_out = jax.random.normal(ks[2], (D_INNER, D_MODEL), jnp.float32) * 0.02
        _dt = jnp.exp(jax.random.uniform(ks[3], (NHEADS,), jnp.float32) * (np.log(DT_MAX) - np.log(DT_MIN)) + np.log(DT_MIN))
        _dt = jnp.maximum(_dt, DT_FLOOR)
        dt_bias = _dt + jnp.log(-jnp.expm1(-_dt))
        return dict(u=u, W_in=W_in, W_out=W_out, dt_bias=dt_bias, B_bias=jnp.ones((NHEADS, D_STATE), jnp.float32), C_bias=jnp.ones((NHEADS, D_STATE), jnp.float32), B_norm_w=jnp.ones((D_STATE,), jnp.float32), C_norm_w=jnp.ones((D_STATE,), jnp.float32), D=jnp.ones((NHEADS,), jnp.float32))
    _L3_attn_in = _L3_attn_setup()

    def _L3_ffn_setup():
        import jax, jax.numpy as jnp
        import numpy as np
        from functools import partial
        HEADS = 16
        EPS = 1e-12

        def _l2_normalize(z):
            n = jnp.linalg.norm(z, axis=-1, keepdims=True)
            return z / jnp.maximum(n, EPS)
        key = jax.random.key(seed)
        kx, kq, kk, kv, ko, kf = jax.random.split(key, 6)
        B, S, D, L = (2, 256, 128, 128)
        scale = 0.02
        return {'x': jax.random.normal(kx, (B, S, D), dtype=jnp.float32), 'Wq': jax.random.normal(kq, (D, L), dtype=jnp.float32) * scale, 'Wk': jax.random.normal(kk, (D, L), dtype=jnp.float32) * scale, 'Wv': jax.random.normal(kv, (D, L), dtype=jnp.float32) * scale, 'Wo': jax.random.normal(ko, (L, D), dtype=jnp.float32) * scale, 'Wff': jax.random.normal(kf, (D, D), dtype=jnp.float32) * scale}
    _L3_ffn_in = _L3_ffn_setup()
    _d = {'L0_attn_x': _L0_attn_in['x'], 'L0_attn_time_maa_x': _L0_attn_in['time_maa_x'], 'L0_attn_time_maa': _L0_attn_in['time_maa'], 'L0_attn_time_maa_w1': _L0_attn_in['time_maa_w1'], 'L0_attn_time_maa_w2': _L0_attn_in['time_maa_w2'], 'L0_attn_time_decay': _L0_attn_in['time_decay'], 'L0_attn_time_decay_w1': _L0_attn_in['time_decay_w1'], 'L0_attn_time_decay_w2': _L0_attn_in['time_decay_w2'], 'L0_attn_time_aaaaa': _L0_attn_in['time_aaaaa'], 'L0_attn_time_aaa_w1': _L0_attn_in['time_aaa_w1'], 'L0_attn_time_aaa_w2': _L0_attn_in['time_aaa_w2'], 'L0_attn_time_kkk_w1': _L0_attn_in['time_kkk_w1'], 'L0_attn_time_kkk_w2': _L0_attn_in['time_kkk_w2'], 'L0_attn_gate_w1': _L0_attn_in['gate_w1'], 'L0_attn_gate_w2': _L0_attn_in['gate_w2'], 'L0_attn_time_misc_a': _L0_attn_in['time_misc_a'], 'L0_attn_ma_w1': _L0_attn_in['ma_w1'], 'L0_attn_ma_w2': _L0_attn_in['ma_w2'], 'L0_attn_time_misc_k': _L0_attn_in['time_misc_k'], 'L0_attn_mk_w1': _L0_attn_in['mk_w1'], 'L0_attn_mk_w2': _L0_attn_in['mk_w2'], 'L0_attn_receptance': _L0_attn_in['receptance'], 'L0_attn_key_w': _L0_attn_in['key_w'], 'L0_attn_value': _L0_attn_in['value'], 'L0_attn_output': _L0_attn_in['output'], 'L0_attn_ln_w': _L0_attn_in['ln_w'], 'L0_attn_ln_b': _L0_attn_in['ln_b'], 'L0_attn_time_faaaa': _L0_attn_in['time_faaaa'], 'L0_ffn_Wr': _L0_ffn_in['Wr'], 'L0_ffn_W1': _L0_ffn_in['W1'], 'L0_ffn_b1': _L0_ffn_in['b1'], 'L0_ffn_W2': _L0_ffn_in['W2'], 'L0_ffn_b2': _L0_ffn_in['b2'], 'L1_attn_Wq': _L1_attn_in['Wq'], 'L1_attn_Wk': _L1_attn_in['Wk'], 'L1_attn_Wv': _L1_attn_in['Wv'], 'L1_attn_Wo': _L1_attn_in['Wo'], 'L1_ffn_Wg': _L1_ffn_in['Wg'], 'L1_ffn_W1': _L1_ffn_in['W1'], 'L1_ffn_b1': _L1_ffn_in['b1'], 'L1_ffn_W2': _L1_ffn_in['W2'], 'L1_ffn_b2': _L1_ffn_in['b2'], 'L2_attn_qkv_w': _L2_attn_in['qkv_w'], 'L2_attn_qkv_b': _L2_attn_in['qkv_b'], 'L2_attn_out_w': _L2_attn_in['out_w'], 'L2_attn_out_b': _L2_attn_in['out_b'], 'L2_attn_g_attn': _L2_attn_in['g_attn'], 'L2_attn_b_attn': _L2_attn_in['b_attn'], 'L2_attn_g1': _L2_attn_in['g1'], 'L2_attn_b1': _L2_attn_in['b1'], 'L2_attn_g2': _L2_attn_in['g2'], 'L2_attn_b2': _L2_attn_in['b2'], 'L2_attn_w_ctx': _L2_attn_in['w_ctx'], 'L2_attn_w_x': _L2_attn_in['w_x'], 'L2_attn_b_inl': _L2_attn_in['b_inl'], 'L2_attn_ff_w1': _L2_attn_in['ff_w1'], 'L2_attn_ff_b1': _L2_attn_in['ff_b1'], 'L2_attn_ff_w2': _L2_attn_in['ff_w2'], 'L2_attn_ff_b2': _L2_attn_in['ff_b2'], 'L2_ffn_w1_w': _L2_ffn_in['w1_w'], 'L2_ffn_w1_s': _L2_ffn_in['w1_s'], 'L2_ffn_w2_w': _L2_ffn_in['w2_w'], 'L2_ffn_w2_s': _L2_ffn_in['w2_s'], 'L2_ffn_h1_w': _L2_ffn_in['h1_w'], 'L2_ffn_h1_s': _L2_ffn_in['h1_s'], 'L2_ffn_h2_w': _L2_ffn_in['h2_w'], 'L2_ffn_h2_s': _L2_ffn_in['h2_s'], 'L2_ffn_w3_w': _L2_ffn_in['w3_w'], 'L2_ffn_w3_s': _L2_ffn_in['w3_s'], 'L3_attn_W_in': _L3_attn_in['W_in'], 'L3_attn_W_out': _L3_attn_in['W_out'], 'L3_attn_dt_bias': _L3_attn_in['dt_bias'], 'L3_attn_B_bias': _L3_attn_in['B_bias'], 'L3_attn_C_bias': _L3_attn_in['C_bias'], 'L3_attn_B_norm_w': _L3_attn_in['B_norm_w'], 'L3_attn_C_norm_w': _L3_attn_in['C_norm_w'], 'L3_attn_D': _L3_attn_in['D'], 'L3_ffn_Wq': _L3_ffn_in['Wq'], 'L3_ffn_Wk': _L3_ffn_in['Wk'], 'L3_ffn_Wv': _L3_ffn_in['Wv'], 'L3_ffn_Wo': _L3_ffn_in['Wo'], 'L3_ffn_Wff': _L3_ffn_in['Wff']}
    _x0 = _d['L0_attn_x']
    _d['L0_attn_x'] = jax.random.normal(jax.random.fold_in(jax.random.key(seed), 1), (8, 512, 128), dtype=_x0.dtype)
    del _x0
    return _d

def reference(L0_attn_x, L0_attn_time_maa_x, L0_attn_time_maa, L0_attn_time_maa_w1, L0_attn_time_maa_w2, L0_attn_time_decay, L0_attn_time_decay_w1, L0_attn_time_decay_w2, L0_attn_time_aaaaa, L0_attn_time_aaa_w1, L0_attn_time_aaa_w2, L0_attn_time_kkk_w1, L0_attn_time_kkk_w2, L0_attn_gate_w1, L0_attn_gate_w2, L0_attn_time_misc_a, L0_attn_ma_w1, L0_attn_ma_w2, L0_attn_time_misc_k, L0_attn_mk_w1, L0_attn_mk_w2, L0_attn_receptance, L0_attn_key_w, L0_attn_value, L0_attn_output, L0_attn_ln_w, L0_attn_ln_b, L0_attn_time_faaaa, L0_ffn_Wr, L0_ffn_W1, L0_ffn_b1, L0_ffn_W2, L0_ffn_b2, L1_attn_Wq, L1_attn_Wk, L1_attn_Wv, L1_attn_Wo, L1_ffn_Wg, L1_ffn_W1, L1_ffn_b1, L1_ffn_W2, L1_ffn_b2, L2_attn_qkv_w, L2_attn_qkv_b, L2_attn_out_w, L2_attn_out_b, L2_attn_g_attn, L2_attn_b_attn, L2_attn_g1, L2_attn_b1, L2_attn_g2, L2_attn_b2, L2_attn_w_ctx, L2_attn_w_x, L2_attn_b_inl, L2_attn_ff_w1, L2_attn_ff_b1, L2_attn_ff_w2, L2_attn_ff_b2, L2_ffn_w1_w, L2_ffn_w1_s, L2_ffn_w2_w, L2_ffn_w2_s, L2_ffn_h1_w, L2_ffn_h1_s, L2_ffn_h2_w, L2_ffn_h2_s, L2_ffn_w3_w, L2_ffn_w3_s, L3_attn_W_in, L3_attn_W_out, L3_attn_dt_bias, L3_attn_B_bias, L3_attn_C_bias, L3_attn_B_norm_w, L3_attn_C_norm_w, L3_attn_D, L3_ffn_Wq, L3_ffn_Wk, L3_ffn_Wv, L3_ffn_Wo, L3_ffn_Wff):

    def _L0_attn_ref(x, time_maa_x, time_maa, time_maa_w1, time_maa_w2, time_decay, time_decay_w1, time_decay_w2, time_aaaaa, time_aaa_w1, time_aaa_w2, time_kkk_w1, time_kkk_w2, gate_w1, gate_w2, time_misc_a, ma_w1, ma_w2, time_misc_k, mk_w1, mk_w2, receptance, key_w, value, output, ln_w, ln_b, time_faaaa):
        import jax, jax.numpy as jnp
        import numpy as np
        NHEAD = 16

        def _forward(x, time_maa_x, time_maa, time_maa_w1, time_maa_w2, time_decay, time_decay_w1, time_decay_w2, time_aaaaa, time_aaa_w1, time_aaa_w2, time_kkk_w1, time_kkk_w2, gate_w1, gate_w2, time_misc_a, ma_w1, ma_w2, time_misc_k, mk_w1, mk_w2, receptance, key_w, value, output, ln_w, ln_b, time_faaaa):
            B, T, C = x.shape
            H, N = (NHEAD, C // NHEAD)
            xprev = jnp.pad(x, ((0, 0), (1, 0), (0, 0)))[:, :T]
            xx = xprev - x
            xxx = x + xx * time_maa_x
            mix = jnp.tanh(xxx @ time_maa_w1.T).reshape(B, T, 4, -1)
            deltas = jnp.einsum('btfd,fcd->fbtc', mix, time_maa_w2)
            xrg, xwa, xk, xv = x[None] + xx[None] * (time_maa + deltas)
            r = xrg @ receptance.T
            g = jnp.tanh(xrg @ gate_w1.T) @ gate_w2.T
            k = xk @ key_w.T
            kk1 = jnp.tanh(xk @ time_kkk_w1.T)
            mk1 = xk @ mk_w1.T
            v = xv @ value.T
            w1 = jnp.tanh(xwa @ time_decay_w1.T)
            a1 = xwa @ time_aaa_w1.T
            ma1 = xwa @ ma_w1.T
            w = -jax.nn.softplus(-(time_decay + w1 @ time_decay_w2.T)) - 0.5
            kk = k + kk1 @ time_kkk_w2.T
            kk = kk.reshape(B, T, H, N)
            kk = kk / jnp.maximum(jnp.linalg.norm(kk, axis=-1, keepdims=True), 1e-12)
            kk = kk.reshape(B, T, C)
            a = jax.nn.sigmoid(time_aaaaa + a1 @ time_aaa_w2.T)
            ma = jax.nn.sigmoid(time_misc_a + ma1 @ ma_w2.T)
            k = k * ma + k * a * (1 - ma)
            mk = jax.nn.sigmoid(time_misc_k + mk1 @ mk_w2.T)
            k = k * jnp.exp(w * mk)
            b = -kk * a

            def heads(z):
                return z.reshape(B, T, H, N).transpose(1, 0, 2, 3)
            rh, wh, kh, vh, kkh, bh = map(heads, (r, w, k, v, kk, b))

            def step(S, inp):
                r_, w_, k_, v_, kk_, b_ = inp
                sab = jnp.einsum('bhvk,bhk->bhv', S, kk_)
                S = S * jnp.exp(w_)[:, :, None, :] + sab[..., None] * b_[:, :, None, :] + v_[..., None] * k_[:, :, None, :]
                y = jnp.einsum('bhvk,bhk->bhv', S, r_)
                return (S, y)
            S0 = jnp.zeros((B, H, N, N), x.dtype)
            _, y = jax.lax.scan(step, S0, (rh, wh, kh, vh, kkh, bh))
            y = y.transpose(1, 0, 2, 3)
            mu = y.mean(-1, keepdims=True)
            var = ((y - mu) ** 2).mean(-1, keepdims=True)
            yn = (y - mu) / jnp.sqrt(var + 0.00064) * ln_w.reshape(H, N) + ln_b.reshape(H, N)
            r4 = r.reshape(B, T, H, N)
            k4 = k.reshape(B, T, H, N)
            v4 = v.reshape(B, T, H, N)
            bonus = (r4 * k4 * time_faaaa.reshape(H, N)).sum(-1, keepdims=True) * v4
            out = (yn + bonus).reshape(B, T, C) * g
            return out @ output.T
        return _forward(x, time_maa_x, time_maa, time_maa_w1, time_maa_w2, time_decay, time_decay_w1, time_decay_w2, time_aaaaa, time_aaa_w1, time_aaa_w2, time_kkk_w1, time_kkk_w2, gate_w1, gate_w2, time_misc_a, ma_w1, ma_w2, time_misc_k, mk_w1, mk_w2, receptance, key_w, value, output, ln_w, ln_b, time_faaaa)

    def _L0_ffn_ref(x, Wr, W1, b1, W2, b2):
        import jax, jax.numpy as jnp
        import numpy as np
        CAP_FACTOR = 1.5
        orig_shape = x.shape
        D = x.shape[-1]
        E = Wr.shape[0]
        xf = x.reshape(-1, D)
        T = xf.shape[0]
        cap = int(CAP_FACTOR * T / E)
        logits = xf @ Wr.T
        vals, idx = jax.lax.top_k(logits.T, cap)
        w = jax.nn.softmax(vals, axis=-1)
        xg = xf[idx]
        h = jax.nn.gelu(jnp.einsum('ecd,esdm->ecsm', xg, W1) + b1[:, None], approximate=False)
        y = jnp.einsum('ecsm,esmk->ecsk', h, W2) + b2[:, None]
        y = y.reshape(E, cap, D) * w[..., None]
        out = jnp.zeros_like(xf).at[idx.reshape(-1)].add(y.reshape(-1, D))
        return out.reshape(orig_shape)

    def _L1_attn_ref(hidden_states, Wq, Wk, Wv, Wo):
        import jax, jax.numpy as jnp
        import numpy as np
        import math
        FEATURE_DIM = 16
        NUM_HEADS = 16
        HIDDEN = 128
        HEAD_DIM = HIDDEN // NUM_HEADS
        EPS = 1e-12
        IU, JU = np.triu_indices(FEATURE_DIM, 1)
        RD = math.sqrt(FEATURE_DIM)
        RRD = math.sqrt(RD)
        R2 = math.sqrt(2.0)

        def taylor_feature_map(x):
            x2 = x[..., :, None] * x[..., None, :]
            off = x2[..., IU, JU]
            diag = jnp.square(x)
            ones = jnp.ones_like(x[..., :1])
            return jnp.concatenate([ones, x / RRD, diag / (RD * R2), off / RD], axis=-1)
        b, t, _ = hidden_states.shape
        q = (hidden_states @ Wq.T).reshape(b, t, NUM_HEADS, FEATURE_DIM).transpose(0, 2, 1, 3)
        k = (hidden_states @ Wk.T).reshape(b, t, NUM_HEADS, FEATURE_DIM).transpose(0, 2, 1, 3)
        v = (hidden_states @ Wv.T).reshape(b, t, NUM_HEADS, HEAD_DIM).transpose(0, 2, 1, 3)
        q = taylor_feature_map(q)
        k = taylor_feature_map(k)
        kv = jnp.cumsum(k[..., None, :] * v[..., :, None], axis=2)
        y = jnp.einsum('bhtD,bhtdD->bhtd', q, kv)
        z = jnp.cumsum(k, axis=2)
        denom = jnp.sum(q * z, axis=-1, keepdims=True) + EPS
        y = y / denom
        y = y.transpose(0, 2, 1, 3).reshape(b, t, NUM_HEADS * HEAD_DIM)
        return y @ Wo.T

    def _L1_ffn_ref(x, Wg, W1, b1, W2, b2):
        import jax, jax.numpy as jnp
        import numpy as np
        B, L, H, E, FF, C = (4, 256, 128, 8, 512, 2)
        b, l, h = x.shape
        e = Wg.shape[1]
        n = b * l
        k = min(max(int(n * C / e), 1), n)
        xt = x.reshape(n, h)
        S = jax.nn.sigmoid(xt @ Wg).T
        G, I = jax.lax.top_k(S, k)
        ex = xt[I]
        hid = jax.nn.gelu(jnp.einsum('ekh,ehf->ekf', ex, W1) + b1[:, None, :], approximate=False)
        out = (jnp.einsum('ekf,efh->ekh', hid, W2) + b2[:, None, :]) * G[..., None]
        new_x = jnp.zeros_like(xt).at[I.reshape(-1)].add(out.reshape(-1, h))
        return new_x.reshape(b, l, h)

    def _L2_attn_ref(x, qkv_w, qkv_b, out_w, out_b, g_attn, b_attn, g1, b1, g2, b2, w_ctx, w_x, b_inl, ff_w1, ff_b1, ff_w2, ff_b2):
        import jax, jax.numpy as jnp
        import numpy as np
        B, S, D, H = (2, 256, 128, 16)
        HD = D // H
        FF = 512
        NUM_ITERS = 8
        DT = 0.1
        LN_EPS = 1e-05

        def _ln(x, g, b):
            m = jnp.mean(x, axis=-1, keepdims=True)
            v = jnp.var(x, axis=-1, keepdims=True)
            return (x - m) * jax.lax.rsqrt(v + LN_EPS) * g + b

        def _forward(x, qkv_w, qkv_b, out_w, out_b, g_attn, b_attn, g1, b1, g2, b2, w_ctx, w_x, b_inl, ff_w1, ff_b1, ff_w2, ff_b2):
            b, s, d = x.shape
            xn = _ln(x, g_attn, b_attn)
            qkv = (xn @ qkv_w + qkv_b).reshape(b, s, 3, H, HD)
            qkv = jnp.transpose(qkv, (2, 0, 3, 1, 4))
            q, k, v = (qkv[0], qkv[1], qkv[2])
            scores = jnp.einsum('bhqd,bhkd->bhqk', q, k) / np.sqrt(HD).astype(np.float32)
            causal = jnp.triu(jnp.ones((s, s), dtype=bool), 1)
            scores = jnp.where(causal[None, None], -jnp.inf, scores)
            attn_w = jax.nn.softmax(scores, axis=-1)
            attn = jnp.einsum('bhqk,bhkd->bhqd', attn_w, v)
            attn = jnp.transpose(attn, (0, 2, 1, 3)).reshape(b, s, d)
            attn = attn @ out_w + out_b
            x = x + attn
            ctx = attn.reshape(b * s, d)
            xs = _ln(x, g1, b1).reshape(b * s, d)
            vs = jnp.zeros_like(xs)

            def step(carry, _):
                xs, vs = carry
                u = jnp.tanh(ctx @ w_ctx + xs @ w_x + b_inl)
                vn = vs + DT * (u - xs - vs)
                xn_ = xs + DT * vn
                return ((xn_, vn), None)
            (xs, vs), _ = jax.lax.scan(step, (xs, vs), None, length=NUM_ITERS)
            x = x + xs.reshape(b, s, d)
            h = _ln(x, g2, b2)
            h = jax.nn.gelu(h @ ff_w1 + ff_b1, approximate=False)
            x = x + (h @ ff_w2 + ff_b2)
            return x
        return _forward(x, qkv_w, qkv_b, out_w, out_b, g_attn, b_attn, g1, b1, g2, b2, w_ctx, w_x, b_inl, ff_w1, ff_b1, ff_w2, ff_b2)

    def _L2_ffn_ref(x, w1_w, w1_s, w2_w, w2_s, h1_w, h1_s, h2_w, h2_s, w3_w, w3_s):
        import jax, jax.numpy as jnp
        import numpy as np
        D_IN, D_HID = (128, 512)

        def _ternary(key, shape):
            return jax.random.randint(key, shape, -1, 2).astype(jnp.float32)

        def _tlin(x, w, s):
            return jnp.einsum('bsi,oi->bso', x, w) * s
        h = jax.nn.silu(_tlin(x, w1_w, w1_s)) * _tlin(x, w2_w, w2_s)
        h = jax.nn.gelu(_tlin(h, h1_w, h1_s), approximate=False)
        h = jax.nn.gelu(_tlin(h, h2_w, h2_s), approximate=False)
        return _tlin(h, w3_w, w3_s)

    def _L3_attn_ref(u, W_in, W_out, dt_bias, B_bias, C_bias, B_norm_w, C_norm_w, D):
        import jax, jax.numpy as jnp
        import numpy as np
        D_MODEL = 128
        D_STATE = 128
        EXPAND = 2
        HEADDIM = 64
        NGROUPS = 1
        D_INNER = EXPAND * D_MODEL
        NHEADS = D_INNER // HEADDIM
        N_ANGLES = D_STATE // 2 // 2
        CHUNK = 64
        DT_MIN, DT_MAX, DT_FLOOR, A_FLOOR = (0.001, 0.1, 0.0001, 0.0001)
        EPS = 1e-05
        BATCH, SEQLEN = (2, 256)

        def _rope(t, theta):
            na = theta.shape[-1]
            x1, x2, rest = (t[..., :na], t[..., na:2 * na], t[..., 2 * na:])
            c, s = (jnp.cos(theta), jnp.sin(theta))
            return jnp.concatenate([x1 * c - x2 * s, x1 * s + x2 * c, rest], axis=-1)

        def _rmsnorm(t, w):
            var = jnp.mean(t * t, axis=-1, keepdims=True)
            return t * jax.lax.rsqrt(var + EPS) * w

        def _forward(u, W_in, W_out, dt_bias, B_bias, C_bias, B_norm_w, C_norm_w, D):
            b, L, _ = u.shape
            proj = u @ W_in
            sizes = [D_INNER, D_INNER, D_STATE * NGROUPS, D_STATE * NGROUPS, NHEADS, NHEADS, NHEADS, N_ANGLES]
            z, x, Bg, Cg, dd_dt, dd_A, trap, angles = jnp.split(proj, np.cumsum(sizes)[:-1], axis=-1)
            z = z.reshape(b, L, NHEADS, HEADDIM)
            x = x.reshape(b, L, NHEADS, HEADDIM)
            a = jnp.minimum(-jax.nn.softplus(dd_A), -A_FLOOR)
            dt = jax.nn.softplus(dd_dt + dt_bias)
            adt = a * dt
            theta = jnp.cumsum(angles[:, :, None, :] * dt[..., None], axis=1)
            Bn = _rmsnorm(Bg, B_norm_w)
            Cn = _rmsnorm(Cg, C_norm_w)
            K = _rope(Bn[:, :, None, :] + B_bias, theta)
            Q = _rope(Cn[:, :, None, :] + C_bias, theta)
            beta = jax.nn.sigmoid(trap)
            g1 = beta * dt
            dt_prev = jnp.pad(dt[:, :-1], ((0, 0), (1, 0), (0, 0)))
            g2 = (1.0 - beta) * jnp.exp(adt) * dt_prev
            Kp = jnp.pad(K[:, :-1], ((0, 0), (1, 0), (0, 0), (0, 0)))
            xp = jnp.pad(x[:, :-1], ((0, 0), (1, 0), (0, 0), (0, 0)))
            nc = L // CHUNK
            ch = lambda t: t.reshape(b, nc, CHUNK, *t.shape[2:])
            Qc, Kc, Kpc, xc, xpc = (ch(Q), ch(K), ch(Kp), ch(x), ch(xp))
            g1c, g2c, adtc = (ch(g1), ch(g2), ch(adt))
            ell = jnp.cumsum(adtc, axis=2)
            decay = jnp.exp(ell[:, :, :, None, :] - ell[:, :, None, :, :])
            mask = jnp.tril(jnp.ones((CHUNK, CHUNK), bool))
            decay = jnp.where(mask[None, None, :, :, None], decay, 0.0)
            S1 = jnp.einsum('bcihn,bcjhn->bcijh', Qc, Kc) * g1c[:, :, None, :, :] * decay
            S2 = jnp.einsum('bcihn,bcjhn->bcijh', Qc, Kpc) * g2c[:, :, None, :, :] * decay
            y_intra = jnp.einsum('bcijh,bcjhp->bcihp', S1, xc) + jnp.einsum('bcijh,bcjhp->bcihp', S2, xpc)
            dec_end = jnp.exp(ell[:, :, -1:, :] - ell)
            Wsum = jnp.einsum('bcjh,bcjhp,bcjhn->bchpn', g1c * dec_end, xc, Kc) + jnp.einsum('bcjh,bcjhp,bcjhn->bchpn', g2c * dec_end, xpc, Kpc)
            chunk_decay = jnp.exp(ell[:, :, -1, :])

            def step(Hprev, inp):
                wc, cd = inp
                return (cd[:, :, None, None] * Hprev + wc, Hprev)
            H0 = jnp.zeros((b, NHEADS, HEADDIM, D_STATE), u.dtype)
            _, Hprevs = jax.lax.scan(step, H0, (jnp.moveaxis(Wsum, 1, 0), jnp.moveaxis(chunk_decay, 1, 0)))
            Hprevs = jnp.moveaxis(Hprevs, 0, 1)
            y_inter = jnp.einsum('bcihn,bcih,bchpn->bcihp', Qc, jnp.exp(ell), Hprevs)
            y = (y_intra + y_inter).reshape(b, L, NHEADS, HEADDIM)
            y = y + D[None, None, :, None] * x
            y = y * jax.nn.silu(z)
            return y.reshape(b, L, D_INNER) @ W_out
        return _forward(u, W_in, W_out, dt_bias, B_bias, C_bias, B_norm_w, C_norm_w, D)

    def _L3_ffn_ref(x, Wq, Wk, Wv, Wo, Wff):
        import jax, jax.numpy as jnp
        import numpy as np
        from functools import partial
        HEADS = 16
        EPS = 1e-12

        def _l2_normalize(z):
            n = jnp.linalg.norm(z, axis=-1, keepdims=True)
            return z / jnp.maximum(n, EPS)
        B, S, D = x.shape
        H = HEADS
        L = Wq.shape[1]
        dh = L // H

        def split_heads(t):
            return t.reshape(B, S, H, dh).transpose(0, 2, 1, 3).reshape(B * H, S, dh)
        q = split_heads(x @ Wq)
        k = split_heads(x @ Wk)
        v = split_heads(x @ Wv)
        scores = jnp.einsum('bqd,bkd->bkq', q, k) / jnp.sqrt(jnp.asarray(D, x.dtype))
        attn = jax.nn.softmax(scores, axis=-1)
        out = jnp.einsum('bkq,bkv->bqv', attn, v)
        z = out.reshape(B, H, S, dh).transpose(0, 2, 1, 3).reshape(B, S, L)
        z = z @ Wo
        z = _l2_normalize(z)
        z = z @ Wff
        z = _l2_normalize(z)
        z = jax.nn.gelu(z, approximate=False)
        return z
    x = L0_attn_x
    xn = _layernorm(x, axis=-1)
    s = _L0_attn_ref(xn, L0_attn_time_maa_x, L0_attn_time_maa, L0_attn_time_maa_w1, L0_attn_time_maa_w2, L0_attn_time_decay, L0_attn_time_decay_w1, L0_attn_time_decay_w2, L0_attn_time_aaaaa, L0_attn_time_aaa_w1, L0_attn_time_aaa_w2, L0_attn_time_kkk_w1, L0_attn_time_kkk_w2, L0_attn_gate_w1, L0_attn_gate_w2, L0_attn_time_misc_a, L0_attn_ma_w1, L0_attn_ma_w2, L0_attn_time_misc_k, L0_attn_mk_w1, L0_attn_mk_w2, L0_attn_receptance, L0_attn_key_w, L0_attn_value, L0_attn_output, L0_attn_ln_w, L0_attn_ln_b, L0_attn_time_faaaa)
    g = _silu(_L0_ffn_ref(xn, L0_ffn_Wr, L0_ffn_W1, L0_ffn_b1, L0_ffn_W2, L0_ffn_b2))
    x = x + s * g
    xn = _layernorm(x, axis=-1)
    s = _L1_attn_ref(xn, L1_attn_Wq, L1_attn_Wk, L1_attn_Wv, L1_attn_Wo)
    g = _silu(_L1_ffn_ref(xn, L1_ffn_Wg, L1_ffn_W1, L1_ffn_b1, L1_ffn_W2, L1_ffn_b2))
    x = x + s * g
    xn = _layernorm(x, axis=-1)
    s = _L2_attn_ref(xn, L2_attn_qkv_w, L2_attn_qkv_b, L2_attn_out_w, L2_attn_out_b, L2_attn_g_attn, L2_attn_b_attn, L2_attn_g1, L2_attn_b1, L2_attn_g2, L2_attn_b2, L2_attn_w_ctx, L2_attn_w_x, L2_attn_b_inl, L2_attn_ff_w1, L2_attn_ff_b1, L2_attn_ff_w2, L2_attn_ff_b2)
    g = _silu(_L2_ffn_ref(xn, L2_ffn_w1_w, L2_ffn_w1_s, L2_ffn_w2_w, L2_ffn_w2_s, L2_ffn_h1_w, L2_ffn_h1_s, L2_ffn_h2_w, L2_ffn_h2_s, L2_ffn_w3_w, L2_ffn_w3_s))
    x = x + s * g
    xn = _layernorm(x, axis=-1)
    s = _L3_attn_ref(xn, L3_attn_W_in, L3_attn_W_out, L3_attn_dt_bias, L3_attn_B_bias, L3_attn_C_bias, L3_attn_B_norm_w, L3_attn_C_norm_w, L3_attn_D)
    g = _silu(_L3_ffn_ref(xn, L3_ffn_Wq, L3_ffn_Wk, L3_ffn_Wv, L3_ffn_Wo, L3_ffn_Wff))
    x = x + s * g
    return x

_drawn_inputs = setup_inputs


def setup_inputs(seed=0):
    import zlib

    import numpy as np

    out = dict(_drawn_inputs(seed))
    spreads = {'L0_attn_ln_w': (1.0, 0.2),
     'L0_attn_ln_b': (0.0, 0.1),
     'L0_ffn_b1': (0.0, 0.1),
     'L0_ffn_b2': (0.0, 0.1),
     'L1_ffn_b1': (0.0, 0.1),
     'L1_ffn_b2': (0.0, 0.1),
     'L2_attn_qkv_b': (0.0, 0.1),
     'L2_attn_out_b': (0.0, 0.1),
     'L2_attn_g_attn': (1.0, 0.2),
     'L2_attn_b_attn': (0.0, 0.1),
     'L2_attn_g1': (1.0, 0.2),
     'L2_attn_b1': (0.0, 0.1),
     'L2_attn_g2': (1.0, 0.2),
     'L2_attn_b2': (0.0, 0.1),
     'L2_attn_b_inl': (0.0, 0.1),
     'L2_attn_ff_b1': (0.0, 0.1),
     'L2_attn_ff_b2': (0.0, 0.1),
     'L3_attn_B_bias': (1.0, 0.2),
     'L3_attn_C_bias': (1.0, 0.2),
     'L3_attn_B_norm_w': (1.0, 0.2),
     'L3_attn_C_norm_w': (1.0, 0.2),
     'L3_attn_D': (1.0, 0.2)}
    factors = {}
    for name, (base, spread) in spreads.items():
        noise = np.random.default_rng([zlib.crc32(name.encode()), seed]).standard_normal(out[name].shape)
        drawn = base * np.exp(spread * noise) if base else spread * noise
        out[name] = jnp.asarray(drawn.astype(out[name].dtype))
    for name, factor in factors.items():
        out[name] = (out[name] * factor).astype(out[name].dtype)
    return out
```

```python
from contextlib import ExitStack

import numpy as np

import concourse.bass as bass
from concourse import mybir

F32 = mybir.dt.float32
BF16 = mybir.dt.bfloat16
U32 = mybir.dt.uint32
I32 = mybir.dt.int32
ALU = mybir.AluOpType
ACT = mybir.ActivationFunctionType
AX = mybir.AxisListType

B, T, C = 8, 512, 128
NT = B * T
NB = T // 128
E, CAP, S4 = 48, 128, 4
E1, CAP1, BITS = 8, 1024, 30
LANES = 2


def sems(nc, ctx, tag, names, lanes=1):
    made = {n: [nc.alloc_semaphore(f"{tag}_{n}{a}") for a in range(lanes)] for n in names.split()}
    ctx.callback(clear, nc, [s for lane in made.values() for s in lane])
    return made if lanes > 1 else {n: s[0] for n, s in made.items()}


def clear(nc, used):
    nc.clear_and_free_semaphores(used)
    nc.all_engine_barrier()


def norm_phase(nc, K, layer, src="X", dst="XN", gain=None, shift=None):
    X, XN, cst = K[src], K[dst], K["cst"]
    with ExitStack() as ctx:
        S = sems(nc, ctx, f"n{layer}", "mean cent sq var std rstd gained xn", LANES)
        ps = ctx.enter_context(nc.psum_tensor(f"n{layer}_ps", [128, 4, T], F32))
        xc = ctx.enter_context(nc.sbuf_tensor(f"n{layer}_xc", [128, LANES, T], F32))
        sq = ctx.enter_context(nc.sbuf_tensor(f"n{layer}_sq", [128, LANES, T], F32))
        block = ctx.enter_context(nc.Block())

        @block.tensor
        def _(pe):
            with pe.Fori(0, B // LANES) as i:
                n = i * LANES
                for a in range(LANES):
                    pe.wait_ge(S["cent"][a], i)
                    pe.matmul(ps[:, a, :], cst("mean"), X[:, bass.ds((n + a) * T, T)],
                              start=True, stop=True).then_inc(S["mean"][a], 1)
                for a in range(LANES):
                    pe.wait_ge(S["sq"][a], i + 1)
                    pe.wait_ge(S["std"][a], i)
                    pe.matmul(ps[:, 2 + a, :], cst("mean"), sq[:, a, :],
                              start=True, stop=True).then_inc(S["var"][a], 1)

        @block.vector
        def _(v):
            with v.Fori(0, B // LANES) as i:
                n = i * LANES
                for a in range(LANES):
                    v.wait_ge(S["mean"][a], i + 1)
                    v.wait_ge(S["xn"][a], i)
                    v.tensor_tensor(xc[:, a, :], X[:, bass.ds((n + a) * T, T)], ps[:, a, :],
                                    ALU.subtract).then_inc(S["cent"][a], 1)
                for a in range(LANES):
                    v.wait_ge(S["std"][a], i + 1)
                    v.reciprocal(sq[:, a, :], sq[:, a, :]).then_inc(S["rstd"][a], 1)
                for a in range(LANES):
                    v.wait_ge(S["rstd"][a], i + 1)
                    if gain is None:
                        v.tensor_tensor(XN[:, bass.ds((n + a) * T, T)], xc[:, a, :], sq[:, a, :],
                                        ALU.mult).then_inc(S["xn"][a], 1)
                        continue
                    v.scalar_tensor_tensor(out=xc[:, a, :], in0=xc[:, a, :], scalar=gain, in1=sq[:, a, :],
                                           op0=ALU.mult, op1=ALU.mult).then_inc(S["gained"][a], 1)
                    v.wait_ge(S["gained"][a], i + 1)
                    v.tensor_scalar(XN[:, bass.ds((n + a) * T, T)], xc[:, a, :], shift, None,
                                    ALU.add).then_inc(S["xn"][a], 1)

        @block.scalar
        def _(act):
            with act.Fori(0, B // LANES) as i:
                n = i * LANES
                for a in range(LANES):
                    act.wait_ge(S["cent"][a], i + 1)
                    act.wait_ge(S["xn"][a], i)
                    act.activation(sq[:, a, :], xc[:, a, :], ACT.Square).then_inc(S["sq"][a], 1)
                for a in range(LANES):
                    act.wait_ge(S["var"][a], i + 1)
                    act.activation(sq[:, a, :], ps[:, 2 + a, :], ACT.Sqrt,
                                   bias=cst("eps")).then_inc(S["std"][a], 1)


def rwkv_pre_phase(nc, K):
    XN, cst, W, Qd = K["XN"], K["cst"], K["w0"], K["Qd"]
    KK, EW, BB, KV, VV, RR, BON, GG = range(8)
    with ExitStack() as ctx:
        S = sems(nc, ctx, "rp", "diff xxx mixps mix delta xf lowps lowr low hips hev kksq z "
                 "lateps a ma mk nrm az ez lz w ew wm km f1 f2 k2 kn rn kkn b vps v k3 rk bonps q stored", LANES)
        ps = ctx.enter_context(nc.psum_tensor("rp_ps", [128, LANES, 4, T], F32))
        sb = lambda name, n: ctx.enter_context(nc.sbuf_tensor("rp_" + name, [128, LANES, n, T], F32))
        xp = ctx.enter_context(nc.sbuf_tensor("rp_xp", [128, LANES, T], F32))
        xf = sb("xf", 4)
        t = sb("t", 6)
        q = sb("q", 8)
        block = ctx.enter_context(nc.Block())
        IT = B // LANES

        def row(i, a):
            return bass.ds((i * LANES + a) * T, T)

        @block.vector
        def _(v):
            with v.Fori(0, IT) as i:
                for a in range(LANES):
                    x = XN[:, row(i, a)]
                    v.wait_ge(S["rk"][a], i)
                    v.wait_ge(S["xf"][a], i)
                    v.tensor_tensor(xp[:, a, 1:T], XN[:, bass.ds((i * LANES + a) * T, T - 1)],
                                    XN[:, bass.ds((i * LANES + a) * T + 1, T - 1)], ALU.subtract)
                    v.tensor_scalar(xp[:, a, 0:1], XN[:, bass.ds((i * LANES + a) * T, 1)], -1.0, None,
                                    ALU.mult).then_inc(S["diff"][a], 1)
                    v.wait_ge(S["diff"][a], i + 1)
                    v.wait_ge(S["mixps"][a], i)
                    v.wait_ge(S["stored"][a], 16 * i)
                    v.scalar_tensor_tensor(out=t[:, a, 0, :], in0=xp[:, a, :], scalar=W("maa_x"), in1=x,
                                           op0=ALU.mult, op1=ALU.add).then_inc(S["xxx"][a], 1)
                for a in range(LANES):
                    x = XN[:, row(i, a)]
                    v.wait_ge(S["delta"][a], i + 1)
                    for f in range(4):
                        last = v.scalar_tensor_tensor(out=t[:, a, 1 + f, :], in0=ps[:, a, f, :],
                                                      scalar=W("maa")[:, f:f + 1], in1=xp[:, a, :],
                                                      op0=ALU.add, op1=ALU.mult)
                    last.then_inc(S["f1"][a], 1)
                    v.wait_ge(S["f1"][a], 2 * i + 1)
                    for f in range(4):
                        last = v.tensor_tensor(xf[:, a, f, :], t[:, a, 1 + f, :], x, ALU.add)
                    last.then_inc(S["xf"][a], 1)
                for a in range(LANES):
                    v.wait_ge(S["lowps"][a], i + 1)
                    v.tensor_copy(q[:, a, RR, :], ps[:, a, 0, :]).then_inc(S["lowr"][a], 1)
                for a in range(LANES):
                    v.wait_ge(S["hips"][a], i + 1)
                    v.tensor_copy(q[:, a, GG, :], ps[:, a, 0, :])
                    v.tensor_copy(q[:, a, KV, :], ps[:, a, 1, :])
                    v.tensor_scalar(t[:, a, 0, :], ps[:, a, 3, :], W("decay"), None,
                                    ALU.add).then_inc(S["z"][a], 1)
                    v.tensor_copy(q[:, a, KK, :], ps[:, a, 2, :]).then_inc(S["hev"][a], 1)
                for a in range(LANES):
                    v.wait_ge(S["lz"][a], i + 1)
                    v.scalar_tensor_tensor(out=t[:, a, 0, :], in0=t[:, a, 0, :], scalar=0.0, in1=t[:, a, 1, :],
                                           op0=ALU.min, op1=ALU.subtract).then_inc(S["w"][a], 1)
                    v.wait_ge(S["mk"][a], i + 1)
                    v.wait_ge(S["w"][a], i + 1)
                    v.scalar_tensor_tensor(out=t[:, a, 2, :], in0=t[:, a, 0, :], scalar=-0.5, in1=t[:, a, 5, :],
                                           op0=ALU.add, op1=ALU.mult).then_inc(S["wm"][a], 1)
                    v.scalar_tensor_tensor(out=t[:, a, 1, :], in0=t[:, a, 4, :], scalar=-1.0, in1=t[:, a, 3, :],
                                           op0=ALU.add, op1=ALU.mult).then_inc(S["f1"][a], 1)
                    v.wait_ge(S["f1"][a], 2 * i + 2)
                    v.tensor_tensor(t[:, a, 1, :], t[:, a, 4, :], t[:, a, 1, :],
                                    ALU.subtract).then_inc(S["f2"][a], 1)
                    v.wait_ge(S["f2"][a], i + 1)
                    v.tensor_tensor(q[:, a, KV, :], q[:, a, KV, :], t[:, a, 1, :],
                                    ALU.mult).then_inc(S["k2"][a], 1)
                    v.wait_ge(S["km"][a], i + 1)
                    v.wait_ge(S["k2"][a], i + 1)
                    v.tensor_tensor(q[:, a, KV, :], q[:, a, KV, :], t[:, a, 2, :],
                                    ALU.mult).then_inc(S["k3"][a], 1)
                    v.wait_ge(S["k3"][a], i + 1)
                    v.scalar_tensor_tensor(out=t[:, a, 1, :], in0=q[:, a, RR, :], scalar=W("faaaa"),
                                           in1=q[:, a, KV, :], op0=ALU.mult, op1=ALU.mult).then_inc(S["rk"][a], 1)
                    v.wait_ge(S["nrm"][a], i + 1)
                    v.reciprocal(t[:, a, 2, :], xf[:, a, 1, :]).then_inc(S["rn"][a], 1)
                    v.wait_ge(S["rn"][a], i + 1)
                    v.tensor_tensor(q[:, a, KK, :], q[:, a, KK, :], t[:, a, 2, :],
                                    ALU.mult).then_inc(S["kkn"][a], 1)
                    v.wait_ge(S["kkn"][a], i + 1)
                    v.scalar_tensor_tensor(out=q[:, a, BB, :], in0=q[:, a, KK, :], scalar=-1.0, in1=t[:, a, 3, :],
                                           op0=ALU.mult, op1=ALU.mult)
                    v.wait_ge(S["vps"][a], i + 1)
                    v.tensor_copy(q[:, a, VV, :], ps[:, a, 0, :]).then_inc(S["v"][a], 1)
                    v.wait_ge(S["v"][a], i + 1)
                    v.wait_ge(S["bonps"][a], i + 1)
                    v.tensor_tensor(q[:, a, BON, :], ps[:, a, 1, :], q[:, a, VV, :],
                                    ALU.mult).then_inc(S["q"][a], 1)

        @block.tensor
        def _(pe):
            with pe.Fori(0, IT) as i:
                for a in range(LANES):
                    pe.wait_ge(S["xxx"][a], i + 1)
                    pe.wait_ge(S["q"][a], i)
                    pe.matmul(ps[:, a, 0, :], W("maa_w1"), t[:, a, 0, :],
                              start=True, stop=True).then_inc(S["mixps"][a], 1)
                for a in range(LANES):
                    pe.wait_ge(S["mix"][a], i + 1)
                    for f in range(4):
                        r = slice(32 * f, 32 * f + 32)
                        last = pe.matmul(ps[:, a, f, :], W("maa_w2")[r, :], xf[r, a, 0, :], start=True, stop=True)
                    last.then_inc(S["delta"][a], 1)
                for a in range(LANES):
                    pe.wait_ge(S["xf"][a], i + 1)
                    pe.matmul(ps[:, a, 0, :], W("receptance"), xf[:, a, 0, :], start=True, stop=True)
                    pe.matmul(ps[:, a, 1, :], W("gate_w1"), xf[:, a, 0, :], start=True, stop=True)
                    pe.matmul(ps[0:64, a, 2, :], W("kkk_mk_w1"), xf[:, a, 2, :], start=True, stop=True)
                    pe.matmul(ps[:, a, 3, :], W("decay_aaa_ma_w1"), xf[:, a, 1, :],
                              start=True, stop=True).then_inc(S["lowps"][a], 1)
                for a in range(LANES):
                    pe.wait_ge(S["low"][a], i + 1)
                    pe.wait_ge(S["lowr"][a], i + 1)
                    pe.matmul(ps[:, a, 0, :], W("gate_w2"), t[:, a, 1, :], start=True, stop=True)
                    pe.matmul(ps[:, a, 1, :], W("key_w"), xf[:, a, 2, :], start=True, stop=True)
                    pe.matmul(ps[:, a, 2, :], W("key_w"), xf[:, a, 2, :], start=True, stop=False)
                    pe.matmul(ps[:, a, 2, :], W("kkk_w2"), t[0:32, a, 2, :], start=False, stop=True)
                    pe.matmul(ps[:, a, 3, :], W("decay_w2"), t[0:64, a, 3, :],
                              start=True, stop=True).then_inc(S["hips"][a], 1)
                for a in range(LANES):
                    pe.wait_ge(S["hev"][a], i + 1)
                    pe.wait_ge(S["kksq"][a], i + 1)
                    pe.matmul(ps[:, a, 0, :], W("aaa_w2")[64:96, :], t[64:96, a, 3, :], start=True, stop=True)
                    pe.matmul(ps[:, a, 1, :], W("ma_w2")[96:128, :], t[96:128, a, 3, :], start=True, stop=True)
                    pe.matmul(ps[:, a, 3, :], W("mk_w2")[32:64, :], t[32:64, a, 2, :], start=True, stop=True)
                    pe.matmul(ps[:, a, 2, :], cst("headsum"), xf[:, a, 0, :],
                              start=True, stop=True).then_inc(S["lateps"][a], 1)
                for a in range(LANES):
                    pe.wait_ge(S["a"][a], i + 1)
                    pe.matmul(ps[:, a, 0, :], W("value"), xf[:, a, 3, :],
                              start=True, stop=True).then_inc(S["vps"][a], 1)
                    pe.wait_ge(S["rk"][a], i + 1)
                    pe.matmul(ps[:, a, 1, :], cst("headsum"), t[:, a, 1, :],
                              start=True, stop=True).then_inc(S["bonps"][a], 1)

        @block.scalar
        def _(act):
            with act.Fori(0, IT) as i:
                for a in range(LANES):
                    act.wait_ge(S["mixps"][a], i + 1)
                    act.wait_ge(S["vps"][a], i)
                    act.activation(xf[:, a, 0, :], ps[:, a, 0, :], ACT.Tanh).then_inc(S["mix"][a], 1)
                for a in range(LANES):
                    act.wait_ge(S["lowps"][a], i + 1)
                    act.activation(t[:, a, 1, :], ps[:, a, 1, :], ACT.Tanh)
                    act.activation(t[0:32, a, 2, :], ps[0:32, a, 2, :], ACT.Tanh)
                    act.activation(t[32:64, a, 2, :], ps[32:64, a, 2, :], ACT.Copy)
                    act.activation(t[0:64, a, 3, :], ps[0:64, a, 3, :], ACT.Tanh)
                    act.activation(t[64:128, a, 3, :], ps[64:128, a, 3, :], ACT.Copy).then_inc(S["low"][a], 1)
                for a in range(LANES):
                    act.wait_ge(S["hev"][a], i + 1)
                    act.activation(xf[:, a, 0, :], q[:, a, KK, :], ACT.Square).then_inc(S["kksq"][a], 1)
                for a in range(LANES):
                    act.wait_ge(S["lateps"][a], i + 1)
                    act.activation(t[:, a, 3, :], ps[:, a, 0, :], ACT.Sigmoid, bias=W("aaaaa")).then_inc(S["a"][a], 1)
                    act.activation(t[:, a, 4, :], ps[:, a, 1, :], ACT.Sigmoid, bias=W("misc_a"))
                    act.activation(t[:, a, 5, :], ps[:, a, 3, :], ACT.Sigmoid, bias=W("misc_k")).then_inc(S["mk"][a], 1)
                for a in range(LANES):
                    act.activation(xf[:, a, 1, :], ps[:, a, 2, :], ACT.Sqrt, bias=cst("tiny")).then_inc(S["nrm"][a], 1)
                for a in range(LANES):
                    act.wait_ge(S["z"][a], i + 1)
                    act.activation(t[:, a, 1, :], t[:, a, 0, :], ACT.Abs).then_inc(S["az"][a], 1)
                    act.wait_ge(S["az"][a], i + 1)
                    act.activation(t[:, a, 1, :], t[:, a, 1, :], ACT.Exp, scale=-1.0).then_inc(S["ez"][a], 1)
                    act.wait_ge(S["ez"][a], i + 1)
                    act.activation(t[:, a, 1, :], t[:, a, 1, :], ACT.Ln, bias=1.0).then_inc(S["lz"][a], 1)
                for a in range(LANES):
                    act.wait_ge(S["w"][a], i + 1)
                    act.activation(q[:, a, EW, :], t[:, a, 0, :], ACT.Exp, bias=cst("mhalf")).then_inc(S["ew"][a], 1)
                    act.wait_ge(S["wm"][a], i + 1)
                    act.activation(t[:, a, 2, :], t[:, a, 2, :], ACT.Exp).then_inc(S["km"][a], 1)

        @block.sync
        def _(sp):
            with sp.Fori(0, IT) as i:
                for a in range(LANES):
                    sp.wait_ge(S["q"][a], i + 1)
                    sp.wait_ge(S["ew"][a], i + 1)
                    sp.dma_start(Qd[:, i * LANES + a].rearrange("q c t -> c q t"), q[:, a]).then_inc(S["stored"][a], 16)
            for a in range(LANES):
                sp.wait_ge(S["stored"][a], 16 * IT)


def rwkv_scan_phase(nc, K):
    Qd, Yd = K["Qd"], K["Yd"]
    H, N = 16, 8
    Qh = Qd.rearrange("q b (h n) t -> q (b h) n t", n=N)
    CH = 32
    IT = T // CH // LANES
    KK, EW, BB, KV, VV, RR = range(6)
    with ExitStack() as ctx:
        S = sems(nc, ctx, "rs", "loaded vk steps yprod y stored", LANES)
        zeroed, chain = sems(nc, ctx, "rs", "zeroed chain").values()
        land = ctx.enter_context(nc.sbuf_tensor("rs_land", [128, LANES, 6, N, CH], F32))
        vk = ctx.enter_context(nc.sbuf_tensor("rs_vk", [128, LANES, CH, N, N], F32))
        hist = ctx.enter_context(nc.sbuf_tensor("rs_hist", [128, LANES, CH, N, N], F32))
        yp = ctx.enter_context(nc.sbuf_tensor("rs_yp", [128, LANES, CH, N, N], F32))
        y = ctx.enter_context(nc.sbuf_tensor("rs_y", [128, LANES, N, CH], F32))
        prod = ctx.enter_context(nc.sbuf_tensor("rs_prod", [128, 2, N, N], F32))
        sab = ctx.enter_context(nc.sbuf_tensor("rs_sab", [128, N], F32))
        outer = ctx.enter_context(nc.sbuf_tensor("rs_outer", [128, N, N], F32))
        block = ctx.enter_context(nc.Block())

        def load(sp, i, a):
            for q in range(6):
                sp.dma_start(land[:, a, q], Qh[q, :, :, bass.ds((i * LANES + a) * CH, CH)]).then_inc(S["loaded"][a], 16)

        @block.sync
        def _(sp):
            with sp.Fori(0, IT) as i:
                for a in range(LANES):
                    sp.wait_ge(S["steps"][a], i)
                    sp.wait_ge(S["yprod"][a], i)
                    load(sp, i, a)

        @block.gpsimd
        def _(g):
            with g.Fori(0, IT) as i:
                for a in range(LANES):
                    g.wait_ge(S["loaded"][a], 96 * (i + 1))
                    g.wait_ge(S["steps"][a], i)
                    kt = land[:, a, KV].rearrange("p n t -> p t n")
                    vt = land[:, a, VV].rearrange("p n t -> p t n")
                    for n in range(N):
                        last = g.tensor_tensor(vk[:, a, :, n, :], kt, vt[:, :, n:n + 1].to_broadcast([128, CH, N]),
                                               ALU.mult)
                    last.then_inc(S["vk"][a], 1)
                    g.wait_ge(S["steps"][a], i + 1)
                    g.wait_ge(S["y"][a], i)
                    rt = land[:, a, RR].rearrange("p n t -> p t n")
                    for n in range(N):
                        last = g.tensor_tensor(yp[:, a, :, n, :], hist[:, a, :, n, :], rt, ALU.mult)
                    last.then_inc(S["yprod"][a], 1)

        @block.vector
        def _(v):
            v.memset(hist[:, LANES - 1, CH - 1], 0.0).then_inc(zeroed, 1)
            v.wait_ge(zeroed, 1)
            v.sem_clear(chain)
            with v.Fori(0, IT) as i:
                for a in range(LANES):
                    v.wait_ge(S["vk"][a], i + 1)
                    v.wait_ge(S["loaded"][a], 96 * (i + 1))
                    v.wait_ge(S["yprod"][a], i)
                    c = 0
                    for t in range(CH):
                        prev = hist[:, a, t - 1] if t else hist[:, (a - 1) % LANES, CH - 1]
                        new = hist[:, a, t]
                        v.tensor_tensor(prod[:], prev.unsqueeze(1).to_broadcast([128, 2, N, N]),
                                        land[:, a, 0:2, :, t].unsqueeze(2).to_broadcast([128, 2, N, N]),
                                        ALU.mult).then_inc(chain, 1)
                        v.wait_ge(chain, c + 1)
                        v.tensor_reduce(sab[:], prod[:, 0], AX.X, ALU.add).then_inc(chain, 1)
                        v.wait_ge(chain, c + 2)
                        v.tensor_tensor(outer[:], sab[:].unsqueeze(2).to_broadcast([128, N, N]),
                                        land[:, a, BB, :, t].unsqueeze(1).to_broadcast([128, N, N]),
                                        ALU.mult)
                        v.tensor_tensor(new, prod[:, 1], vk[:, a, t], ALU.add).then_inc(chain, 1)
                        v.wait_ge(chain, c + 3)
                        last = v.tensor_tensor(new, new, outer[:], ALU.add).then_inc(chain, 1)
                        v.wait_ge(chain, c + 4)
                        c += 4
                    v.sem_clear(chain)
                    v.nop().then_inc(S["steps"][a], 1)
                    v.wait_ge(S["yprod"][a], i + 1)
                    v.wait_ge(S["stored"][a], 16 * i)
                    v.tensor_reduce(y[:, a].rearrange("p n t -> p t n"), yp[:, a], AX.X,
                                    ALU.add).then_inc(S["y"][a], 1)

        @block.scalar
        def _(act):
            with act.Fori(0, IT) as i:
                for a in range(LANES):
                    act.wait_ge(S["y"][a], i + 1)
                    act.dma_start(Yd[:, :, bass.ds((i * LANES + a) * CH, CH)], y[:, a]).then_inc(S["stored"][a], 16)
            for a in range(LANES):
                act.wait_ge(S["stored"][a], 16 * IT)


def rwkv_out_phase(nc, K):
    SX, cst, W, Qd, Yd = K["SX"], K["cst"], K["w0"], K["Qd"], K["Yd"]
    Yv = Yd.rearrange("(b h) v t -> b (h v) t", b=B)
    IT = B // LANES
    with ExitStack() as ctx:
        S = sems(nc, ctx, "ro", "loaded mean cent sq var std rstd yn ynb yb o sps s", LANES)
        ps = ctx.enter_context(nc.psum_tensor("ro_ps", [128, LANES, 3, T], F32))
        y = ctx.enter_context(nc.sbuf_tensor("ro_y", [128, LANES, 3, T], F32))
        sq = ctx.enter_context(nc.sbuf_tensor("ro_sq", [128, LANES, T], F32))
        block = ctx.enter_context(nc.Block())

        @block.sync
        def _(sp):
            with sp.Fori(0, IT) as i:
                for a in range(LANES):
                    sp.wait_ge(S["sps"][a], i)
                    sp.dma_start(y[:, a, 0, :], Yv[i * LANES + a]).then_inc(S["loaded"][a], 16)
                    sp.dma_start(y[:, a, 1:3, :], Qd[6:8, i * LANES + a].rearrange("q c t -> c q t")).then_inc(S["loaded"][a], 16)

        @block.tensor
        def _(pe):
            with pe.Fori(0, IT) as i:
                for a in range(LANES):
                    pe.wait_ge(S["loaded"][a], 32 * (i + 1))
                    pe.wait_ge(S["cent"][a], i)
                    pe.matmul(ps[:, a, 0, :], cst("headmean"), y[:, a, 0, :],
                              start=True, stop=True).then_inc(S["mean"][a], 1)
                for a in range(LANES):
                    pe.wait_ge(S["sq"][a], i + 1)
                    pe.wait_ge(S["std"][a], i)
                    pe.matmul(ps[:, a, 1, :], cst("headmean"), sq[:, a, :],
                              start=True, stop=True).then_inc(S["var"][a], 1)
                for a in range(LANES):
                    pe.wait_ge(S["o"][a], i + 1)
                    pe.wait_ge(S["s"][a], i)
                    pe.matmul(ps[:, a, 2, :], W("output"), y[:, a, 0, :],
                              start=True, stop=True).then_inc(S["sps"][a], 1)

        @block.scalar
        def _(act):
            with act.Fori(0, IT) as i:
                for a in range(LANES):
                    act.wait_ge(S["cent"][a], i + 1)
                    act.wait_ge(S["yn"][a], i)
                    act.activation(sq[:, a, :], y[:, a, 0, :], ACT.Square).then_inc(S["sq"][a], 1)
                for a in range(LANES):
                    act.wait_ge(S["var"][a], i + 1)
                    act.activation(sq[:, a, :], ps[:, a, 1, :], ACT.Sqrt, bias=cst("gn_eps")).then_inc(S["std"][a], 1)
                for a in range(LANES):
                    act.wait_ge(S["sps"][a], i + 1)
                    act.activation(SX[:, bass.ds((i * LANES + a) * T, T)], ps[:, a, 2, :], ACT.Copy).then_inc(S["s"][a], 1)

        @block.vector
        def _(v):
            with v.Fori(0, IT) as i:
                for a in range(LANES):
                    v.wait_ge(S["mean"][a], i + 1)
                    v.tensor_tensor(y[:, a, 0, :], y[:, a, 0, :], ps[:, a, 0, :], ALU.subtract).then_inc(S["cent"][a], 1)
                for a in range(LANES):
                    v.wait_ge(S["std"][a], i + 1)
                    v.reciprocal(sq[:, a, :], sq[:, a, :]).then_inc(S["rstd"][a], 1)
                    v.wait_ge(S["rstd"][a], i + 1)
                    v.tensor_tensor(y[:, a, 0, :], y[:, a, 0, :], sq[:, a, :], ALU.mult).then_inc(S["yn"][a], 1)
                    v.wait_ge(S["yn"][a], i + 1)
                    v.tensor_scalar(y[:, a, 0, :], y[:, a, 0, :], W("ln_w"), W("ln_b"), ALU.mult, ALU.add).then_inc(S["ynb"][a], 1)
                    v.wait_ge(S["ynb"][a], i + 1)
                    v.tensor_tensor(y[:, a, 0, :], y[:, a, 0, :], y[:, a, 1, :], ALU.add).then_inc(S["yb"][a], 1)
                    v.wait_ge(S["yb"][a], i + 1)
                    v.tensor_tensor(y[:, a, 0, :], y[:, a, 0, :], y[:, a, 2, :], ALU.mult).then_inc(S["o"][a], 1)


def route_phase(nc, K):
    XN, cst, W, Xt, Acc = K["XN"], K["cst"], K["w0"], K["Xt"], K["Acc"]
    IDX, WGT = K["IDX"], K["WGT"]
    IT = B // LANES
    Xv = Xt.rearrange("(b j p) c -> b p j c", p=128, j=NB)
    with ExitStack() as ctx:
        S = sems(nc, ctx, "rt", "xs logps logit tps tok stored", LANES)
        P = sems(nc, ctx, "rtp", "best at taken neg e rsum w atf colps cols zero zeroed")
        lps = ctx.enter_context(nc.psum_tensor("rt_lps", [128, LANES, T], F32))
        tps = ctx.enter_context(nc.psum_tensor("rt_tps", [128, LANES, NB, C], F32))
        cps = ctx.enter_context(nc.psum_tensor("rt_cps", [128, 2, E], F32))
        xs = ctx.enter_context(nc.sbuf_tensor("rt_xs", [128, LANES, T], F32))
        logits = ctx.enter_context(nc.sbuf_tensor("rt_logits", [E, NT], F32))
        tok = ctx.enter_context(nc.sbuf_tensor("rt_tok", [128, LANES, NB, C], F32))
        best = ctx.enter_context(nc.sbuf_tensor("rt_best", [E, CAP], F32))
        wrow = ctx.enter_context(nc.sbuf_tensor("rt_wrow", [E, CAP], F32))
        at = ctx.enter_context(nc.sbuf_tensor("rt_at", [E, CAP], U32))
        atf = ctx.enter_context(nc.sbuf_tensor("rt_atf", [E, CAP], F32))
        small = ctx.enter_context(nc.sbuf_tensor("rt_small", [E, 4], F32))
        zero = ctx.enter_context(nc.sbuf_tensor("rt_zero", [128, NT // 128 * C], F32))
        block = ctx.enter_context(nc.Block())

        @block.tensor
        def _(pe):
            with pe.Fori(0, IT) as i:
                for a in range(LANES):
                    pe.wait_ge(S["xs"][a], i + 1)
                    pe.wait_ge(S["logit"][a], i)
                    pe.wait_ge(S["tok"][a], i)
                    pe.matmul(lps[0:E, a, :], W("router"), xs[:, a, :],
                              start=True, stop=True).then_inc(S["logps"][a], 1)
                    for j in range(NB):
                        last = pe.transpose(tps[:, a, j, :], xs[:, a, j * 128:(j + 1) * 128], cst("ident"))
                    last.then_inc(S["tps"][a], 1)
            pe.wait_ge(P["w"], 1)
            pe.transpose(cps[:, 0, :], wrow[:], cst("ident")[0:E, 0:E])
            pe.wait_ge(P["atf"], 1)
            pe.transpose(cps[:, 1, :], atf[:], cst("ident")[0:E, 0:E]).then_inc(P["colps"], 1)

        @block.scalar
        def _(act):
            with act.Fori(0, IT) as i:
                for a in range(LANES):
                    act.wait_ge(S["tps"][a], i)
                    act.activation(xs[:, a, :], XN[:, bass.ds((i * LANES + a) * T, T)],
                                   ACT.Copy).then_inc(S["xs"][a], 1)
                for a in range(LANES):
                    act.wait_ge(S["logps"][a], i + 1)
                    act.activation(logits[:, bass.ds((i * LANES + a) * T, T)], lps[0:E, a, :],
                                   ACT.Copy).then_inc(S["logit"][a], 1)
            act.wait_ge(P["neg"], 1)
            act.activation(wrow[:], best[:], ACT.Exp, bias=small[:, 0:1], accum_out=small[:, 1:2]).then_inc(P["e"], 1)

        @block.vector
        def _(v):
            v.memset(zero[:], 0.0).then_inc(P["zero"], 1)
            with v.Fori(0, IT) as i:
                for a in range(LANES):
                    v.wait_ge(S["tps"][a], i + 1)
                    v.wait_ge(S["stored"][a], 16 * i)
                    v.tensor_copy(tok[:, a], tps[:, a]).then_inc(S["tok"][a], 1)
            for a in range(LANES):
                v.wait_ge(S["logit"][a], IT)
            for r in range(CAP // 8):
                eight = slice(8 * r, 8 * r + 8)
                v.wait_ge(P["taken"], r)
                v.max(best[:, eight], logits[:]).then_inc(P["best"], 1)
                v.wait_ge(P["best"], r + 1)
                v.max_index(at[:, eight], best[:, eight], logits[:]).then_inc(P["at"], 1)
                v.wait_ge(P["at"], r + 1)
                v.match_replace(logits[:], best[:, eight], logits[:], -3.0e38).then_inc(P["taken"], 1)
            v.tensor_scalar(small[:, 0:1], best[:, 0:1], -1.0, None, ALU.mult).then_inc(P["neg"], 1)
            v.tensor_copy(atf[:], at[:]).then_inc(P["atf"], 1)
            v.wait_ge(P["e"], 1)
            v.reciprocal(small[:, 2:3], small[:, 1:2]).then_inc(P["rsum"], 1)
            v.wait_ge(P["rsum"], 1)
            v.tensor_scalar(wrow[:], wrow[:], small[:, 2:3], None, ALU.mult).then_inc(P["w"], 1)
            v.wait_ge(P["colps"], 1)
            v.tensor_copy(WGT[:], cps[:, 0, :])
            v.tensor_copy(IDX[:], cps[:, 1, :]).then_inc(P["cols"], 1)
            v.wait_ge(P["cols"], 1)

        @block.sync
        def _(sp):
            sp.wait_ge(P["zero"], 1)
            sp.dma_start(Acc.rearrange("(p r) c -> p (r c)", p=128), zero[:]).then_inc(P["zeroed"], 16)
            with sp.Fori(0, IT) as i:
                for a in range(LANES):
                    sp.wait_ge(S["tok"][a], i + 1)
                    sp.dma_start(Xv[i * LANES + a], tok[:, a]).then_inc(S["stored"][a], 16)
            sp.wait_ge(P["zeroed"], 16)
            for a in range(LANES):
                sp.wait_ge(S["stored"][a], 16 * IT)


def experts_phase(nc, K):
    cst, Xt, Acc, IDX, WGT = K["cst"], K["Xt"], K["Acc"], K["IDX"], K["WGT"]
    w1d, w2d, b1d, b2d = K["A"]["e_w1"], K["A"]["e_w2"], K["A"]["e_b1"], K["A"]["e_b2"]
    EL = 4
    IT = E // EL
    with ExitStack() as ctx:
        S = sems(nc, ctx, "ex", "w xg idx fetched tps xgt hps h yps y added", EL)
        biases = sems(nc, ctx, "exb", "biases")["biases"]
        tps = ctx.enter_context(nc.psum_tensor("ex_tps", [128, EL, CAP], F32))
        hps = ctx.enter_context(nc.psum_tensor("ex_hps", [128, EL, S4, CAP], F32))
        yps = ctx.enter_context(nc.psum_tensor("ex_yps", [128, 2, 512], F32))
        w1 = ctx.enter_context(nc.sbuf_tensor("ex_w1", [128, EL, S4, 128], F32))
        w2 = ctx.enter_context(nc.sbuf_tensor("ex_w2", [128, EL, S4, 32], F32))
        b1 = ctx.enter_context(nc.sbuf_tensor("ex_b1", [128, E * S4], F32))
        b2 = ctx.enter_context(nc.sbuf_tensor("ex_b2", [1, E * C], F32))
        idx = ctx.enter_context(nc.sbuf_tensor("ex_idx", [CAP, EL], U32))
        xg = ctx.enter_context(nc.sbuf_tensor("ex_xg", [CAP, EL, C], F32))
        xgt = ctx.enter_context(nc.sbuf_tensor("ex_xgt", [128, EL, CAP], F32))
        h = ctx.enter_context(nc.sbuf_tensor("ex_h", [128, EL, S4, CAP], F32))
        y = ctx.enter_context(nc.sbuf_tensor("ex_y", [CAP, EL, C], F32))
        block = ctx.enter_context(nc.Block())

        @block.sync
        def _(sp):
            sp.dma_start(b1[:], b1d).then_inc(biases, 16)
            sp.dma_start(b2[:], b2d).then_inc(biases, 16)
            with sp.Fori(0, IT) as i:
                for a in range(EL):
                    sp.wait_ge(S["yps"][a], i)
                    sp.dma_start(w1[:, a], w1d[i * EL + a].rearrange("s d m -> d s m")).then_inc(S["w"][a], 16)
                    sp.dma_start(w2[:, a], w2d[i * EL + a].rearrange("s m k -> m s k")).then_inc(S["w"][a], 16)

        @block.gpsimd
        def _(g):
            with g.Fori(0, IT) as i:
                for a in range(EL):
                    g.wait_ge(S["fetched"][a], 16 * i)
                    g.wait_ge(S["added"][a], 16 * i)
                    g.nop(nofuse=True)
                    g.tensor_copy(idx[:, a:a + 1], IDX[:, bass.ds(i * EL + a, 1)]).then_inc(S["idx"][a], 1)
                for a in range(EL):
                    g.wait_ge(S["tps"][a], i)
                    g.wait_ge(S["idx"][a], i + 1)
                    g.nop(nofuse=True)
                    g.indirect_dma_start(xg[:, a, :], None, Xt,
                                         bass.IndirectOffsetOnAxis(ap=idx[:, a:a + 1], axis=0)
                                         ).then_inc(S["fetched"][a], 16)
                for a in range(EL):
                    g.wait_ge(S["y"][a], i + 1)
                    if a:
                        g.wait_ge(S["added"][a - 1], 16 * (i + 1))
                    else:
                        g.wait_ge(S["added"][EL - 1], 16 * i)
                    g.nop(nofuse=True)
                    g.indirect_dma_start(Acc, bass.IndirectOffsetOnAxis(ap=idx[:, a:a + 1], axis=0),
                                         y[:, a, :], None, compute_op=ALU.add).then_inc(S["added"][a], 16)
            g.wait_ge(S["added"][EL - 1], 16 * IT)

        @block.tensor
        def _(pe):
            with pe.Fori(0, IT) as i:
                for a in range(EL):
                    pe.wait_ge(S["fetched"][a], 16 * (i + 1))
                    pe.wait_ge(S["xgt"][a], i)
                    if a:
                        pe.wait_ge(S["xgt"][a - 1], i + 1)
                    else:
                        pe.wait_ge(S["xgt"][EL - 1], i)
                    pe.transpose(tps[:, a, :], xg[:, a, :], cst("ident")).then_inc(S["tps"][a], 1)
                for a in range(EL):
                    pe.wait_ge(S["xgt"][a], i + 1)
                    pe.wait_ge(S["w"][a], 32 * (i + 1))
                    pe.wait_ge(S["h"][a], i)
                    for s in range(S4):
                        last = pe.matmul(hps[:, a, s, :], w1[:, a, s, :], xgt[:, a, :], start=True, stop=True)
                    last.then_inc(S["hps"][a], 1)
                pe.wait_ge(biases, 32)
                for a in range(EL):
                    pe.wait_ge(S["h"][a], i + 1)
                    if a >= 2:
                        pe.wait_ge(S["y"][a - 2], i + 1)
                    else:
                        pe.wait_ge(S["y"][a + 2], i)
                    out = yps[:, a % 2, 0:C]
                    pe.matmul(out, cst("ones")[0:1, :], b2[0:1, bass.ds((i * EL + a) * C, C)],
                              start=True, stop=False, skip_group_check=True)
                    for s in range(S4):
                        last = pe.matmul(out[:, 32 * s:32 * s + 32], h[:, a, s, :], w2[:, a, s, :],
                                         start=False, stop=(s == S4 - 1), skip_group_check=True)
                    last.then_inc(S["yps"][a], 1)

        @block.scalar
        def _(act):
            act.wait_ge(biases, 32)
            with act.Fori(0, IT) as i:
                for a in range(EL):
                    act.wait_ge(S["hps"][a], i + 1)
                    act.wait_ge(S["yps"][a], i)
                    for s in range(S4):
                        last = act.activation(h[:, a, s, :], hps[:, a, s, :], ACT.Gelu,
                                              bias=b1[:, bass.ds((i * EL + a) * S4 + s, 1)])
                    last.then_inc(S["h"][a], 1)

        @block.vector
        def _(v):
            with v.Fori(0, IT) as i:
                for a in range(EL):
                    v.wait_ge(S["tps"][a], i + 1)
                    v.wait_ge(S["hps"][a], i)
                    v.tensor_copy(xgt[:, a, :], tps[:, a, :]).then_inc(S["xgt"][a], 1)
                for a in range(EL):
                    v.wait_ge(S["yps"][a], i + 1)
                    v.wait_ge(S["added"][a], 16 * i)
                    v.tensor_scalar(y[:, a, :], yps[:, a % 2, 0:C], WGT[:, bass.ds(i * EL + a, 1)], None,
                                    ALU.mult).then_inc(S["y"][a], 1)


def collect_phase(nc, K):
    GX, cst, Acc = K["GX"], K["cst"], K["Acc"]
    Av = Acc.rearrange("(b j p) c -> b p j c", p=128, j=NB)
    with ExitStack() as ctx:
        S = sems(nc, ctx, "co", "loaded tps g", LANES)
        tps = ctx.enter_context(nc.psum_tensor("co_tps", [128, LANES, T], F32))
        acc = ctx.enter_context(nc.sbuf_tensor("co_acc", [128, LANES, NB, C], F32))
        block = ctx.enter_context(nc.Block())

        @block.sync
        def _(sp):
            with sp.Fori(0, B // LANES) as i:
                for a in range(LANES):
                    sp.wait_ge(S["tps"][a], i)
                    sp.dma_start(acc[:, a], Av[i * LANES + a]).then_inc(S["loaded"][a], 16)

        @block.tensor
        def _(pe):
            with pe.Fori(0, B // LANES) as i:
                for a in range(LANES):
                    pe.wait_ge(S["loaded"][a], 16 * (i + 1))
                    pe.wait_ge(S["g"][a], i)
                    for j in range(NB):
                        last = pe.transpose(tps[:, a, j * 128:(j + 1) * 128], acc[:, a, j, :], cst("ident"))
                    last.then_inc(S["tps"][a], 1)

        @block.scalar
        def _(act):
            with act.Fori(0, B // LANES) as i:
                for a in range(LANES):
                    act.wait_ge(S["tps"][a], i + 1)
                    act.activation(GX[:, bass.ds((i * LANES + a) * T, T)], tps[:, a, :], ACT.Copy).then_inc(S["g"][a], 1)


KEYS_AT = {0: 0, 1: T, 3: T + 384, 2: 2 * T}
SPAN = 2 * T + 256


def choose_phase(nc, K):
    XN, cst, W, Sd, Gd = K["XN"], K["cst"], K["w1"], K["Sd"], K["Gd"]
    IT = B // LANES
    PER = 128 // E1
    with ExitStack() as ctx:
        S = sems(nc, ctx, "ch", "logps score", LANES)
        P = sems(nc, ctx, "chp", "out back thr0 cand count total keep thr gt need eqn off rank ok sel gate stored")
        lps = ctx.enter_context(nc.psum_tensor("ch_lps", [128, LANES, T], F32))
        tot = ctx.enter_context(nc.psum_tensor("ch_tot", [128, 1], F32))
        rows = ctx.enter_context(nc.sbuf_tensor("ch_rows", [E1, NT], F32))
        sc = ctx.enter_context(nc.sbuf_tensor("ch_sc", [128, NT // PER], F32))
        m = ctx.enter_context(nc.sbuf_tensor("ch_m", [128, 3, NT // PER], F32))
        thr = ctx.enter_context(nc.sbuf_tensor("ch_thr", [128, 1], F32))
        cand = ctx.enter_context(nc.sbuf_tensor("ch_cand", [128, 1], F32))
        cnt = ctx.enter_context(nc.sbuf_tensor("ch_cnt", [128, 1], F32))
        keep = ctx.enter_context(nc.sbuf_tensor("ch_keep", [128, 1], U32))
        need = ctx.enter_context(nc.sbuf_tensor("ch_need", [128, 1], F32))
        block = ctx.enter_context(nc.Block())

        @block.tensor
        def _(pe):
            with pe.Fori(0, IT) as i:
                for a in range(LANES):
                    pe.wait_ge(S["score"][a], i)
                    pe.matmul(lps[0:E1, a, :], W("gate"), XN[:, bass.ds((i * LANES + a) * T, T)],
                              start=True, stop=True).then_inc(S["logps"][a], 1)
            for n in range(BITS + 1):
                pe.wait_ge(P["count"], n + 1)
                pe.matmul(tot[:], cst("exsum"), cnt[:], start=True, stop=True).then_inc(P["total"], 1)
            pe.wait_ge(P["eqn"], 1)
            pe.wait_ge(P["need"], 1)
            pe.matmul(tot[:], cst("exbefore"), cnt[:], start=True, stop=True).then_inc(P["off"], 1)

        @block.scalar
        def _(act):
            with act.Fori(0, IT) as i:
                for a in range(LANES):
                    act.wait_ge(S["logps"][a], i + 1)
                    act.activation(rows[:, bass.ds((i * LANES + a) * T, T)], lps[0:E1, a, :],
                                   ACT.Sigmoid).then_inc(S["score"][a], 1)

        @block.sync
        def _(sp):
            for a in range(LANES):
                sp.wait_ge(S["score"][a], IT)
            sp.dma_start(Sd, rows[:]).then_inc(P["out"], 16)
            sp.wait_ge(P["out"], 16)
            sp.dma_start(sc[:], Sd.rearrange("e (p t) -> (e p) t", p=PER)).then_inc(P["back"], 16)
            sp.wait_ge(P["gate"], 1)
            sp.dma_start(Gd.rearrange("e (p t) -> (e p) t", p=PER), m[:, 0, :]).then_inc(P["stored"], 16)
            sp.wait_ge(P["stored"], 16)

        @block.vector
        def _(v):
            v.memset(thr[:], 0.0).then_inc(P["thr0"], 1)
            v.wait_ge(P["thr0"], 1)
            v.wait_ge(P["back"], 16)
            for n in range(BITS):
                bit = 1 << (BITS - 1 - n)
                v.wait_ge(P["thr"], n)
                v.tensor_scalar(cand[:].bitcast(I32), thr[:].bitcast(I32), bit, None,
                                ALU.bitwise_or).then_inc(P["cand"], 1)
                v.wait_ge(P["cand"], n + 1)
                v.tensor_scalar(m[:, 0, :], sc[:], cand[:, 0:1], None, ALU.is_ge, ALU.add,
                                accum_out=cnt[:]).then_inc(P["count"], 1)
                v.wait_ge(P["total"], n + 1)
                v.tensor_scalar(keep[:], tot[:], float(CAP1), None, ALU.is_ge).then_inc(P["keep"], 1)
                v.wait_ge(P["keep"], n + 1)
                v.copy_predicated(thr[:], keep[:], cand[:]).then_inc(P["thr"], 1)
            v.wait_ge(P["thr"], BITS)
            v.tensor_scalar(m[:, 0, :], sc[:], thr[:, 0:1], None, ALU.is_gt, ALU.add,
                            accum_out=cnt[:]).then_inc(P["count"], 1)
            v.wait_ge(P["total"], BITS + 1)
            v.tensor_scalar(need[:], tot[:], -1.0, float(CAP1), ALU.mult, ALU.add).then_inc(P["need"], 1)
            v.tensor_scalar(m[:, 1, :], sc[:], thr[:, 0:1], None, ALU.is_equal, ALU.add,
                            accum_out=cnt[:]).then_inc(P["eqn"], 1)
            v.wait_ge(P["eqn"], 1)
            v.wait_ge(P["off"], 1)
            v.tensor_tensor_scan(m[:, 2, :], cst("onerow")[:, 0:NT // PER], m[:, 1, :], 0.0, ALU.mult,
                                 ALU.add).then_inc(P["rank"], 1)
            v.wait_ge(P["rank"], 1)
            v.tensor_scalar(need[:], need[:], tot[:, 0:1], None, ALU.subtract).then_inc(P["rank"], 1)
            v.wait_ge(P["rank"], 2)
            v.scalar_tensor_tensor(out=m[:, 2, :], in0=m[:, 2, :], scalar=need[:, 0:1], in1=m[:, 1, :],
                                   op0=ALU.is_le, op1=ALU.mult).then_inc(P["ok"], 1)
            v.wait_ge(P["ok"], 1)
            v.tensor_tensor(m[:, 2, :], m[:, 2, :], m[:, 0, :], ALU.add).then_inc(P["sel"], 1)
            v.wait_ge(P["sel"], 1)
            v.tensor_tensor(m[:, 0, :], m[:, 2, :], sc[:], ALU.mult).then_inc(P["gate"], 1)


def ffn1_phase(nc, K):
    XN, GX, W, Gd = K["XN"], K["GX"], K["w1"], K["Gd"]
    F = 4
    with ExitStack() as ctx:
        S = sems(nc, ctx, "f1", "gates used x")
        H = sems(nc, ctx, "f1h", "ps act yps t", E1)
        w1 = ctx.enter_context(nc.sbuf_tensor("f1_w1s", [128, E1, F * 128], F32))
        w2 = ctx.enter_context(nc.sbuf_tensor("f1_w2s", [128, E1, F, C], F32))
        hps = ctx.enter_context(nc.psum_tensor("f1_hps", [128, F, T], F32))
        yps = ctx.enter_context(nc.psum_tensor("f1_yps", [128, 2, T], F32))
        h = ctx.enter_context(nc.sbuf_tensor("f1_h", [128, 2, F, T], F32))
        g = ctx.enter_context(nc.sbuf_tensor("f1_g", [128, E1, T], F32))
        t = ctx.enter_context(nc.sbuf_tensor("f1_t", [128, T], F32))
        HB = [sems(nc, ctx, f"f1b{f}", "ps act", E1) for f in range(F)]
        loaded = sems(nc, ctx, "f1l", "loaded")["loaded"]
        block = ctx.enter_context(nc.Block())

        @block.sync
        def _(sp):
            sp.dma_start(w1[:], K["A"]["f1_w1"].rearrange("e d f -> d e f")).then_inc(loaded, 16)
            sp.dma_start(w2[:], K["A"]["f1_w2"].rearrange("e (f p) c -> p e f c", p=128)).then_inc(loaded, 16)
            with sp.Fori(0, B) as i:
                sp.wait_ge(S["x"], i)
                for e in range(E1):
                    sp.dma_start(g[:, e, :], Gd[e:e + 1, bass.ds(i * T, T)].to_broadcast([128, T])
                                 ).then_inc(S["gates"], 16)

        @block.tensor
        def _(pe):
            pe.wait_ge(loaded, 32)

            def down(i, e):
                if e >= 2:
                    pe.wait_ge(H["t"][e - 2], i + 1)
                else:
                    pe.wait_ge(H["t"][e + E1 - 2], i)
                for f in range(F):
                    pe.wait_ge(HB[f]["act"][e], i + 1)
                    last = pe.matmul(yps[:, e % 2, :], w2[:, e, f, :], h[:, e % 2, f, :],
                                     start=(f == 0), stop=(f == F - 1))
                last.then_inc(H["yps"][e], 1)

            with pe.Fori(0, B) as i:
                for e in range(E1):
                    for f in range(F):
                        if e:
                            pe.wait_ge(HB[f]["act"][e - 1], i + 1)
                        else:
                            pe.wait_ge(HB[f]["act"][E1 - 1], i)
                        pe.matmul(hps[:, f, :], w1[:, e, f * 128:(f + 1) * 128], XN[:, bass.ds(i * T, T)],
                                  start=True, stop=True).then_inc(HB[f]["ps"][e], 1)
                    if e:
                        down(i, e - 1)
                down(i, E1 - 1)

        @block.scalar
        def _(act):
            with act.Fori(0, B) as i:
                for e in range(E1):
                    if e >= 2:
                        act.wait_ge(H["yps"][e - 2], i + 1)
                    else:
                        act.wait_ge(H["yps"][e + E1 - 2], i)
                    for f in range(F):
                        act.wait_ge(HB[f]["ps"][e], i + 1)
                        act.activation(h[:, e % 2, f, :], hps[:, f, :], ACT.Gelu,
                                       bias=W("ffb1")[:, e * F + f:e * F + f + 1]).then_inc(HB[f]["act"][e], 1)

        @block.vector
        def _(v):
            with v.Fori(0, B) as i:
                v.wait_ge(S["gates"], 16 * E1 * (i + 1))
                for e in range(E1):
                    out = GX[:, bass.ds(i * T, T)] if e == 0 else t[:]
                    v.wait_ge(H["yps"][e], i + 1)
                    v.scalar_tensor_tensor(out=out, in0=yps[:, e % 2, :], scalar=W("ffb2")[:, e:e + 1],
                                           in1=g[:, e, :], op0=ALU.add, op1=ALU.mult).then_inc(H["t"][e], 1)
                    v.wait_ge(H["t"][e], i + 1)
                    if e:
                        v.tensor_tensor(GX[:, bass.ds(i * T, T)], GX[:, bass.ds(i * T, T)], t[:],
                                        ALU.add).then_inc(H["act"][e], 1)
                        v.wait_ge(H["act"][e], i + 1)
                v.nop().then_inc(S["x"], 1)


QUERIES_AT = {3: 0, 2: T, 0: T + 384, 1: 2 * T}


def inertia_phase(nc, K):
    XN, SX, GX, cst, W = K["XN"], K["SX"], K["GX"], K["cst"], K["w2"]
    ITERS, F = 8, 4
    IT = B // LANES
    with ExitStack() as ctx:
        S = sems(nc, ctx, "in", "x2 v0 mean cent sq var std rstd gained n "
                 "x3 mean2 cent2 sq2 var2 std2 rstd2 gained2 n2 ops out", LANES)
        R = [sems(nc, ctx, f"inr{k}", "pre u t v xs", LANES) for k in range(ITERS)]
        HF = [sems(nc, ctx, f"inf{f}", "ps h", LANES) for f in range(F)]
        ps = ctx.enter_context(nc.psum_tensor("in_ps", [128, LANES, 4, T], F32))
        sb = lambda name, *n: ctx.enter_context(nc.sbuf_tensor("in_" + name, [128, LANES, *n, T], F32))
        x2, xs, vel, tmp, u, h = sb("x2"), sb("xs"), sb("vel"), sb("tmp"), sb("u"), sb("h", F)
        block = ctx.enter_context(nc.Block())

        def row(i, a):
            return bass.ds((i * LANES + a) * T, T)

        @block.tensor
        def _(pe):
            with pe.Fori(0, IT) as i:
                for a in range(LANES):
                    pe.wait_ge(S["x2"][a], i + 1)
                    pe.wait_ge(S["out"][a], i)
                    pe.matmul(ps[:, a, 0, :], cst("mean"), x2[:, a, :], start=True, stop=True).then_inc(S["mean"][a], 1)
                for a in range(LANES):
                    pe.wait_ge(S["sq"][a], i + 1)
                    pe.matmul(ps[:, a, 1, :], cst("mean"), u[:, a, :], start=True, stop=True).then_inc(S["var"][a], 1)
                for k in range(ITERS):
                    for a in range(LANES):
                        if k:
                            pe.wait_ge(R[k - 1]["u"][a], i + 1)
                        pe.matmul(ps[:, a, 2, :], W("w_ctx"), GX[:, row(i, a)], start=True, stop=False)
                        if k:
                            pe.wait_ge(R[k - 1]["xs"][a], i + 1)
                        else:
                            pe.wait_ge(S["n"][a], i + 1)
                        pe.matmul(ps[:, a, 2, :], W("w_x"), xs[:, a, :], start=False,
                                  stop=True).then_inc(R[k]["pre"][a], 1)
                for a in range(LANES):
                    pe.wait_ge(S["x3"][a], i + 1)
                    pe.matmul(ps[:, a, 0, :], cst("mean"), x2[:, a, :], start=True, stop=True).then_inc(S["mean2"][a], 1)
                for a in range(LANES):
                    pe.wait_ge(S["sq2"][a], i + 1)
                    pe.matmul(ps[:, a, 1, :], cst("mean"), u[:, a, :], start=True, stop=True).then_inc(S["var2"][a], 1)
                for a in range(LANES):
                    pe.wait_ge(S["n2"][a], i + 1)
                    for f in range(F):
                        pe.matmul(ps[:, a, f, :], W("ff_w1")[:, f * 128:(f + 1) * 128], xs[:, a, :],
                                  start=True, stop=True).then_inc(HF[f]["ps"][a], 1)
                for a in range(LANES):
                    for f in range(F):
                        pe.wait_ge(HF[f]["h"][a], i + 1)
                        last = pe.matmul(ps[:, a, 0, :], W("ff_w2")[:, f * C:(f + 1) * C], h[:, a, f, :],
                                         start=(f == 0), stop=(f == F - 1))
                    last.then_inc(S["ops"][a], 1)

        @block.scalar
        def _(act):
            with act.Fori(0, IT) as i:
                for a in range(LANES):
                    act.wait_ge(S["cent"][a], i + 1)
                    act.activation(u[:, a, :], xs[:, a, :], ACT.Square).then_inc(S["sq"][a], 1)
                for a in range(LANES):
                    act.wait_ge(S["var"][a], i + 1)
                    act.activation(tmp[:, a, :], ps[:, a, 1, :], ACT.Sqrt, bias=cst("eps")).then_inc(S["std"][a], 1)
                for k in range(ITERS):
                    for a in range(LANES):
                        act.wait_ge(R[k]["pre"][a], i + 1)
                        if k:
                            act.wait_ge(R[k - 1]["v"][a], i + 1)
                        act.activation(u[:, a, :], ps[:, a, 2, :], ACT.Tanh, bias=W("b_inl")).then_inc(R[k]["u"][a], 1)
                for a in range(LANES):
                    act.wait_ge(S["cent2"][a], i + 1)
                    act.activation(u[:, a, :], xs[:, a, :], ACT.Square).then_inc(S["sq2"][a], 1)
                for a in range(LANES):
                    act.wait_ge(S["var2"][a], i + 1)
                    act.activation(tmp[:, a, :], ps[:, a, 1, :], ACT.Sqrt, bias=cst("eps")).then_inc(S["std2"][a], 1)
                for a in range(LANES):
                    for f in range(F):
                        act.wait_ge(HF[f]["ps"][a], i + 1)
                        act.activation(h[:, a, f, :], ps[:, a, f, :], ACT.Gelu,
                                       bias=W("ff_b1")[:, f:f + 1]).then_inc(HF[f]["h"][a], 1)

        @block.vector
        def _(v):
            def norm(i, tag, gain, shift):
                for a in range(LANES):
                    v.wait_ge(S["mean" + tag][a], i + 1)
                    v.tensor_tensor(xs[:, a, :], x2[:, a, :], ps[:, a, 0, :], ALU.subtract).then_inc(S["cent" + tag][a], 1)
                for a in range(LANES):
                    v.wait_ge(S["std" + tag][a], i + 1)
                    v.reciprocal(tmp[:, a, :], tmp[:, a, :]).then_inc(S["rstd" + tag][a], 1)
                    v.wait_ge(S["rstd" + tag][a], i + 1)
                    v.scalar_tensor_tensor(out=xs[:, a, :], in0=xs[:, a, :], scalar=W(gain), in1=tmp[:, a, :],
                                           op0=ALU.mult, op1=ALU.mult).then_inc(S["gained" + tag][a], 1)
                    v.wait_ge(S["gained" + tag][a], i + 1)
                    v.tensor_scalar(xs[:, a, :], xs[:, a, :], W(shift), None, ALU.add).then_inc(S["n" + tag][a], 1)

            with v.Fori(0, IT) as i:
                for a in range(LANES):
                    v.tensor_tensor(x2[:, a, :], XN[:, row(i, a)], GX[:, row(i, a)], ALU.add).then_inc(S["x2"][a], 1)
                    v.memset(vel[:, a, :], 0.0).then_inc(S["v0"][a], 1)
                for a in range(LANES):
                    v.wait_ge(S["x2"][a], i + 1)
                    v.wait_ge(S["v0"][a], i + 1)
                norm(i, "", "g1", "b1")
                for k in range(ITERS):
                    for a in range(LANES):
                        if k:
                            v.wait_ge(R[k - 1]["xs"][a], i + 1)
                        else:
                            v.wait_ge(S["n"][a], i + 1)
                        v.scalar_tensor_tensor(out=tmp[:, a, :], in0=vel[:, a, :], scalar=0.9, in1=xs[:, a, :],
                                               op0=ALU.mult, op1=ALU.subtract).then_inc(R[k]["t"][a], 1)
                    for a in range(LANES):
                        v.wait_ge(R[k]["t"][a], i + 1)
                        v.wait_ge(R[k]["u"][a], i + 1)
                        v.tensor_tensor(vel[:, a, :], tmp[:, a, :], u[:, a, :], ALU.add).then_inc(R[k]["v"][a], 1)
                        v.wait_ge(R[k]["v"][a], i + 1)
                        v.scalar_tensor_tensor(out=xs[:, a, :], in0=vel[:, a, :], scalar=0.01, in1=xs[:, a, :],
                                               op0=ALU.mult, op1=ALU.add).then_inc(R[k]["xs"][a], 1)
                for a in range(LANES):
                    v.wait_ge(R[ITERS - 1]["xs"][a], i + 1)
                    v.tensor_tensor(x2[:, a, :], x2[:, a, :], xs[:, a, :], ALU.add).then_inc(S["x3"][a], 1)
                norm(i, "2", "g2", "b2")
                for a in range(LANES):
                    v.wait_ge(S["ops"][a], i + 1)
                    v.scalar_tensor_tensor(out=SX[:, row(i, a)], in0=ps[:, a, 0, :], scalar=W("ff_b2"),
                                           in1=x2[:, a, :], op0=ALU.add, op1=ALU.add).then_inc(S["out"][a], 1)
                for a in range(LANES):
                    v.wait_ge(S["out"][a], i + 1)


def gated_mlp_phase(nc, K):
    XN, GX, W = K["XN"], K["GX"], K["w2f"]
    F = 4
    with ExitStack() as ctx:
        S = sems(nc, ctx, "gm", "ops out")
        L = [sems(nc, ctx, f"gm{n}", "ps sb", F) for n in range(4)]
        
        ps = ctx.enter_context(nc.psum_tensor("gm_ps", [128, 8, T], F32))
        a1 = ctx.enter_context(nc.sbuf_tensor("gm_a1", [128, F, T], F32))
        h0 = ctx.enter_context(nc.sbuf_tensor("gm_h0", [128, F, T], F32))
        h1 = ctx.enter_context(nc.sbuf_tensor("gm_h1", [128, F, T], F32))
        h2 = ctx.enter_context(nc.sbuf_tensor("gm_h2", [128, F, T], F32))
        block = ctx.enter_context(nc.Block())

        @block.tensor
        def _(pe):
            with pe.Fori(0, B) as i:
                x = XN[:, bass.ds(i * T, T)]
                for f in range(F):
                    pe.wait_ge(S["out"] if f == 0 else L[2]["sb"][f], i)
                    pe.matmul(ps[:, f, :], W("w1")[:, f * 128:(f + 1) * 128], x, start=True,
                              stop=True).then_inc(L[0]["ps"][f], 1)
                    pe.wait_ge(L[3]["sb"][f], i)
                    pe.matmul(ps[:, 4 + f, :], W("w2")[:, f * 128:(f + 1) * 128], x, start=True,
                              stop=True).then_inc(L[1]["ps"][f], 1)
                for n, w, src, ready in ((2, "h1", h0, L[1]["sb"]), (3, "h2", h1, L[2]["sb"])):
                    for f in range(F):
                        pe.wait_ge(L[n - 2]["sb"][f], i + 1)
                        for j in range(F):
                            pe.wait_ge(ready[j], i + 1)
                            last = pe.matmul(ps[:, 4 * (n % 2) + f, :],
                                             W(w)[:, j * 512 + f * 128:j * 512 + (f + 1) * 128], src[:, j, :],
                                             start=(j == 0), stop=(j == F - 1))
                        last.then_inc(L[n]["ps"][f], 1)
                for j in range(F):
                    pe.wait_ge(L[3]["sb"][j], i + 1)
                    last = pe.matmul(ps[:, 0, :], W("w3")[:, j * C:(j + 1) * C], h2[:, j, :],
                                     start=(j == 0), stop=(j == F - 1))
                last.then_inc(S["ops"], 1)

        @block.scalar
        def _(act):
            with act.Fori(0, B) as i:
                for f in range(F):
                    act.wait_ge(L[0]["ps"][f], i + 1)
                    act.wait_ge(L[1]["sb"][f], i)
                    act.activation(a1[:, f, :], ps[:, f, :], ACT.Silu, scale=W("s1")[:, f:f + 1]).then_inc(L[0]["sb"][f], 1)
                for n, dst, sc in ((2, h1, "sh1"), (3, h2, "sh2")):
                    for f in range(F):
                        act.wait_ge(L[n]["ps"][f], i + 1)
                        if n == 2:
                            act.wait_ge(L[3]["ps"][F - 1], i)
                        else:
                            act.wait_ge(S["ops"], i)
                        act.activation(dst[:, f, :], ps[:, 4 * (n % 2) + f, :], ACT.Gelu,
                                       scale=W(sc)[:, f:f + 1]).then_inc(L[n]["sb"][f], 1)

        @block.vector
        def _(v):
            with v.Fori(0, B) as i:
                for f in range(F):
                    v.wait_ge(L[1]["ps"][f], i + 1)
                    v.wait_ge(L[0]["sb"][f], i + 1)
                    v.wait_ge(L[2]["ps"][F - 1], i)
                    v.scalar_tensor_tensor(out=h0[:, f, :], in0=ps[:, 4 + f, :], scalar=W("s2")[:, f:f + 1],
                                           in1=a1[:, f, :], op0=ALU.mult, op1=ALU.mult).then_inc(L[1]["sb"][f], 1)
                v.wait_ge(S["ops"], i + 1)
                v.tensor_scalar(GX[:, bass.ds(i * T, T)], ps[:, 0, :], W("s3"), None, ALU.mult).then_inc(S["out"], 1)


TERMS = ((0, 0), (0, 1), (1, 0), (0, 2), (2, 0), (1, 1))


def split_phase(nc, K, tag, src, wq, wk, wv, tiles, dim, bias=None, qscale=1.0):
    X, VA, Pd = K[src], K["VA"], K["Pd"]
    H = 16
    D = VA.shape[-1] - 1
    N = 2 * tiles
    with ExitStack() as ctx:
        S = sems(nc, ctx, tag, "xs vps v ones")
        U = [sems(nc, ctx, f"{tag}{a}", "ps f hi r1 mid lo stored", N) for a in range(1)][0]
        ps = ctx.enter_context(nc.psum_tensor(tag + "_ps", [128, N, T], F32))
        vps = ctx.enter_context(nc.psum_tensor(tag + "_vps", [128, NB, C], F32))
        xs = ctx.enter_context(nc.sbuf_tensor(tag + "_xs", [128, T], F32))
        f = ctx.enter_context(nc.sbuf_tensor(tag + "_f", [128, N, T], F32))
        r = ctx.enter_context(nc.sbuf_tensor(tag + "_r", [128, N, T], F32))
        p = ctx.enter_context(nc.sbuf_tensor(tag + "_p", [128, N, 3, T], BF16))
        block = ctx.enter_context(nc.Block())

        @block.tensor
        def _(pe):
            with pe.Fori(0, B) as i:
                pe.wait_ge(S["xs"], i + 1)
                for n in range(N):
                    pe.wait_ge(U["f"][n], i)
                    w = (wq if n < tiles else wk)[:, (n % tiles) * 128:(n % tiles + 1) * 128]
                    pe.matmul(ps[:, n, :], w, xs[:], start=True, stop=True).then_inc(U["ps"][n], 1)
                pe.wait_ge(S["v"], i)
                for j in range(NB):
                    last = pe.matmul(vps[:, j, :], xs[:, j * 128:(j + 1) * 128], wv, start=True, stop=True)
                last.then_inc(S["vps"], 1)

        @block.scalar
        def _(act):
            with act.Fori(0, B) as i:
                for n in range(N):
                    act.wait_ge(U["ps"][n], i + 1)
                    act.wait_ge(U["r1"][n], i)
                    act.activation(f[:, n, :], ps[:, n, :], ACT.Identity, scale=qscale if n < tiles else 1.0,
                                   bias=0.0 if bias is None else bias[:, n:n + 1]).then_inc(U["f"][n], 1)
                    act.wait_ge(U["f"][n], i + 1)
                    act.wait_ge(U["stored"][n], 16 * i)
                    act.activation(p[:, n, 0, :], f[:, n, :], ACT.Copy).then_inc(U["hi"][n], 1)
                for n in range(N):
                    act.wait_ge(U["r1"][n], i + 1)
                    act.activation(p[:, n, 1, :], r[:, n, :], ACT.Copy).then_inc(U["mid"][n], 1)

        @block.vector
        def _(v):
            v.memset(VA[:], 1.0).then_inc(S["ones"], 1)
            v.wait_ge(S["ones"], 1)
            with v.Fori(0, B) as i:
                v.wait_ge(S["vps"], i)
                v.tensor_copy(xs[:], X[:, bass.ds(i * T, T)]).then_inc(S["xs"], 1)
                for n in range(N):
                    v.wait_ge(U["hi"][n], i + 1)
                    v.wait_ge(U["lo"][n], i)
                    v.tensor_tensor(r[:, n, :], f[:, n, :], p[:, n, 0, :], ALU.subtract).then_inc(U["r1"][n], 1)
                v.wait_ge(S["vps"], i + 1)
                out = VA[:, bass.ds(i * NB, NB), :, 0:D]
                got = vps[:].rearrange("p j (h d) -> p j h d", h=H)
                if bias is None:
                    v.tensor_copy(out, got).then_inc(S["v"], 1)
                else:
                    v.tensor_tensor(out, got, K["w2"]("v_b_row").rearrange("p (h d) -> p h d", h=H).unsqueeze(
                        1).to_broadcast([128, NB, H, D]), ALU.add).then_inc(S["v"], 1)
                for n in range(N):
                    v.wait_ge(U["mid"][n], i + 1)
                    v.tensor_tensor(p[:, n, 2, :], r[:, n, :], p[:, n, 1, :], ALU.subtract).then_inc(U["lo"][n], 1)

        @block.sync
        def _(sp):
            with sp.Fori(0, B) as i:
                for n in range(N):
                    sp.wait_ge(U["lo"][n], i + 1)
                    sp.dma_start(Pd[i, n // tiles, :, (n % tiles) * 128:(n % tiles + 1) * 128].rearrange("c r t -> r c t"),
                                 p[:, n]).then_inc(U["stored"][n], 16)
            for n in range(N):
                sp.wait_ge(U["stored"][n], 16 * B)


def load_stacks(sp, Pd, row, first, n, qs, ks, loaded, D):
    for at, (pq, pk) in enumerate(TERMS):
        for side, part, dst in ((0, pq, qs), (1, pk, ks)):
            src = Pd[row, side, part, first * D:(first + n) * D]
            sp.dma_start(dst[at * D:(at + 1) * D], src.rearrange("(h d) t -> d h t", d=D)).then_inc(loaded, 16)


GROUPS, GH = 4, 4


def open_bank(pe, K, bank):
    pe.matmul(bank, K["zero"][:, 0:128], K["zero"][:], start=True, stop=False, skip_group_check=True)


def causal_phase(nc, K, tag, dst, D, softmax):
    VA, Pd, cst, out = K["VA"], K["Pd"], K["cst"], K[dst]
    H, DV = GROUPS * GH, 8
    R = len(TERMS) * D + (2 if softmax else 0)
    LOADS = 16 * (2 * len(TERMS) + (1 if softmax else 0))
    SC = (float(1 / np.sqrt(D)),) if softmax else (0.25 * 0.5 ** 0.5,)
    with ExitStack() as ctx:
        S = sems(nc, ctx, tag, "ones den num dsb rec y")
        G = sems(nc, ctx, tag + "g", "loaded out va", GROUPS)
        HD = sems(nc, ctx, tag + "h", "score power masked av", H)
        ps = ctx.enter_context(nc.psum_tensor(tag + "_ps", [128, 2, 3 * T], F32))
        O = ctx.enter_context(nc.psum_tensor(tag + "_o", [128, 2, T], F32))
        qs = ctx.enter_context(nc.sbuf_tensor(tag + "_qs", [R, GROUPS, GH, T], BF16))
        ks = ctx.enter_context(nc.sbuf_tensor(tag + "_ks", [R, GROUPS, GH, T], BF16))
        va = ctx.enter_context(nc.sbuf_tensor(tag + "_va", [128, NB, H, DV + 1], F32))
        vc = ctx.enter_context(nc.sbuf_tensor(tag + "_vc", [128, NB, H, DV], F32))
        pw = ctx.enter_context(nc.sbuf_tensor(tag + "_pw", [128, 2, 3, T], F32))
        osb = ctx.enter_context(nc.sbuf_tensor(tag + "_osb", [128, GROUPS, T], F32))
        rec = ctx.enter_context(nc.sbuf_tensor(tag + "_rec", [128, T], F32))
        block = ctx.enter_context(nc.Block())
        weights = HD["power"] if softmax else HD["masked"]

        @block.sync
        def _(sp):
            if softmax:
                sp.wait_ge(S["ones"], 1)
            with sp.Fori(0, B) as i:
                for g in range(GROUPS):
                    sp.wait_ge(HD["score"][GH * g + GH - 1], i)
                    load_stacks(sp, Pd, i, g * GH, GH, qs[:, g], ks[:, g], G["loaded"][g], D)
                    if softmax:
                        sp.dma_start(qs[R - 2:R, g], K["Md"][i, :, g * GH:(g + 1) * GH]).then_inc(G["loaded"][g], 16)

        @block.tensor
        def _(pe):
            def scores(i, h):
                g = h // GH
                if h % GH == 0:
                    pe.wait_ge(G["loaded"][g], LOADS * (i + 1))
                if h >= 2:
                    pe.wait_ge(HD["power"][h - 2], i + 1)
                else:
                    pe.wait_ge(HD["power"][h + H - 2], i)
                for jk in range(NB):
                    at, n = KEYS_AT[jk], T - 128 * jk
                    k, q = ks[:, g, h % GH, jk * 128:(jk + 1) * 128], qs[:, g, h % GH, jk * 128:T]
                    if softmax:
                        pe.matmul(ps[:, h % 2, at:at + 128], K["cb"]("identb"), K["cb"]("neg_across"),
                                  start=True, stop=False)
                        last = pe.matmul(ps[:, h % 2, at:at + 128], k, q[:, 0:128], start=False, stop=True)
                        if n > 128:
                            last = pe.matmul(ps[:, h % 2, at + 128:at + n], k, q[:, 128:n], start=True, stop=True)
                    else:
                        last = pe.matmul(ps[:, h % 2, at:at + n], k, q, start=True, stop=True)
                last.then_inc(HD["score"][h], 1)

            def values(i, h):
                g = h // GH
                if h % GH == 0:
                    if g >= 2:
                        pe.wait_ge(G["out"][g - 2], i + 1)
                    else:
                        pe.wait_ge(S["dsb" if g == 0 else "y"], i)
                    open_bank(pe, K, O[:, g % 2, :])
                pe.wait_ge(G["va"][g], i + 1)
                pe.wait_ge(weights[h], i + 1)
                for jk in range(NB):
                    at, n = KEYS_AT[jk], T - 128 * jk
                    last = pe.matmul(O[32 * (h % GH):32 * (h % GH) + DV + 1, g % 2, jk * 128:T], va[:, jk, h, :],
                                     pw[:, h % 2, at // T, at % T:at % T + n], start=False,
                                     stop=(h % GH == GH - 1 and jk == NB - 1), skip_group_check=True)
                last.then_inc(HD["av"][h], 1)

            def turn(i, last):
                for h in range(H):
                    if h + 1 < H:
                        scores(i, h + 1)
                    elif not last:
                        scores(i + 1, 0)
                    values(i, h)
                for g in range(GROUPS):
                    pe.wait_ge(G["out"][g], i + 1)
                if not softmax:
                    pe.matmul(O[:, 0, :], cst("ones")[0:1, :], cst("halfcount"), start=True, stop=False)
                for g in range(GROUPS):
                    last = pe.matmul(O[:, 0, :], cst("close_den")[:, g * 128:(g + 1) * 128], osb[:, g, :],
                                     start=(softmax and g == 0), stop=(g == GROUPS - 1))
                last.then_inc(S["den"], 1)
                for g in range(GROUPS):
                    last = pe.matmul(O[:, 1, :], cst("close")[:, g * 128:(g + 1) * 128], osb[:, g, :],
                                     start=(g == 0), stop=(softmax and g == GROUPS - 1), skip_group_check=True)
                if not softmax:
                    for jk in range(NB):
                        last = pe.matmul(O[:, 1, jk * 128:T], vc[:, jk].rearrange("p h d -> p (h d)"), cst("halfwide")[:, 0:T - 128 * jk],
                                         start=False, stop=(jk == NB - 1), skip_group_check=True)
                last.then_inc(S["num"], 1)

            scores(0, 0)
            with pe.Fori(0, B - 1) as i:
                turn(i, False)
            turn(B - 1, True)

        @block.scalar
        def _(act):
            with act.Fori(0, B) as i:
                for h in range(H):
                    act.wait_ge(HD["score"][h], i + 1)
                    if h >= 2:
                        act.wait_ge(HD["av"][h - 2], i + 1)
                    else:
                        act.wait_ge(HD["av"][h + H - 2], i)
                    act.activation(pw[:, h % 2].rearrange("p g x -> p (g x)")[:, 0:SPAN], ps[:, h % 2, 0:SPAN],
                                   ACT.Exp if softmax else ACT.Square, scale=SC[0],
                                   bias=0.0 if softmax else cst("rhalf")).then_inc(HD["power"][h], 1)

        @block.gpsimd
        def _(gp):
            with gp.Fori(0, B) as i:
                for g in range(GROUPS):
                    gp.wait_ge(HD["av"][GH * g + GH - 1], i)
                    gp.wait_ge(S["num"], i)
                    gp.nop(nofuse=True)
                    if not softmax:
                        gp.tensor_copy(vc[:, :, g * GH:(g + 1) * GH, :],
                                       VA[:, bass.ds(i * NB, NB), g * GH:(g + 1) * GH, 0:DV])
                    gp.tensor_copy(va[:, :, g * GH:(g + 1) * GH, :],
                                   VA[:, bass.ds(i * NB, NB), g * GH:(g + 1) * GH, :]).then_inc(G["va"][g], 1)

        @block.vector
        def _(v):
            if softmax:
                v.memset(ks[:], 1.0).then_inc(S["ones"], 1)
            with v.Fori(0, B) as i:
                def evacuate(g):
                    v.wait_ge(HD["av"][GH * g + GH - 1], i + 1)
                    v.wait_ge(S["num"], i)
                    v.tensor_copy(osb[:, g, :], O[:, g % 2, :]).then_inc(G["out"][g], 1)

                for h in range(H):
                    if not softmax:
                        v.wait_ge(HD["power"][h], i + 1)
                        v.tensor_tensor(pw[:, h % 2, :, 0:128], pw[:, h % 2, :, 0:128],
                                        cst("tri").unsqueeze(1).to_broadcast([128, 3, 128]), ALU.mult)
                        v.tensor_tensor(pw[:, h % 2, 1, 384:512], pw[:, h % 2, 1, 384:512], cst("tri"),
                                        ALU.mult).then_inc(HD["masked"][h], 1)
                    if h % GH == 1 and h > GH:
                        evacuate(h // GH - 1)
                evacuate(GROUPS - 1)
                v.wait_ge(S["den"], i + 1)
                v.wait_ge(S["y"], i)
                v.tensor_scalar(rec[:], O[:, 0, :], 0.0 if softmax else 1e-12, None, ALU.add).then_inc(S["dsb"], 1)
                v.wait_ge(S["dsb"], i + 1)
                v.reciprocal(rec[:], rec[:]).then_inc(S["rec"], 1)
                v.wait_ge(S["rec"], i + 1)
                v.wait_ge(S["num"], i + 1)
                v.tensor_tensor(out[:, bass.ds(i * T, T)], O[:, 1, :], rec[:], ALU.mult).then_inc(S["y"], 1)


def maxima_phase(nc, K):
    Pd, Md, cst, cb = K["Pd"], K["Md"], K["cst"], K["cb"]
    H, D = GROUPS * GH, 8
    R = len(TERMS) * D
    LOADS = 16 * 2 * len(TERMS)
    with ExitStack() as ctx:
        S = sems(nc, ctx, "mx", "tps hi mid stored")
        G = sems(nc, ctx, "mxg", "loaded", GROUPS)["loaded"]
        HD = sems(nc, ctx, "mxh", "far top", H)
        ps = ctx.enter_context(nc.psum_tensor("mx_ps", [128, 2, 3 * T], F32))
        tps = ctx.enter_context(nc.psum_tensor("mx_tps", [H, T], F32))
        qs = ctx.enter_context(nc.sbuf_tensor("mx_qs", [R, GROUPS, GH, T], BF16))
        ks = ctx.enter_context(nc.sbuf_tensor("mx_ks", [R, GROUPS, GH, T], BF16))
        mx = ctx.enter_context(nc.sbuf_tensor("mx_mx", [128, NB, H], F32))
        parts = ctx.enter_context(nc.sbuf_tensor("mx_parts", [H, 2, T], BF16))
        block = ctx.enter_context(nc.Block())

        @block.sync
        def _(sp):
            with sp.Fori(0, B) as i:
                for g in range(GROUPS):
                    sp.wait_ge(HD["far"][GH * g + GH - 1], i)
                    load_stacks(sp, Pd, i, g * GH, GH, qs[:, g], ks[:, g], G[g], D)

        @block.tensor
        def _(pe):
            with pe.Fori(0, B) as i:
                for h in range(H):
                    g = h // GH
                    if h % GH == 0:
                        pe.wait_ge(G[g], LOADS * (i + 1))
                    if h >= 2:
                        pe.wait_ge(HD["top"][h - 2], i + 1)
                    else:
                        pe.wait_ge(HD["top"][h + H - 2], i)
                    for jq in range(NB):
                        at, n = QUERIES_AT[jq], 128 * (jq + 1)
                        q, k = qs[:, g, h % GH, jq * 128:(jq + 1) * 128], ks[:, g, h % GH, :]
                        if jq:
                            pe.matmul(ps[:, h % 2, at:at + n - 128], q, k[:, 0:n - 128], start=True, stop=True)
                        pe.matmul(ps[:, h % 2, at + n - 128:at + n], cb("identb"), cb("neg_down"),
                                  start=True, stop=False)
                        last = pe.matmul(ps[:, h % 2, at + n - 128:at + n], q, k[:, n - 128:n],
                                         start=False, stop=True)
                    last.then_inc(HD["far"][h], 1)
                pe.wait_ge(HD["top"][H - 1], i + 1)
                pe.wait_ge(S["mid"], i)
                for j in range(NB):
                    last = pe.transpose(tps[:, j * 128:(j + 1) * 128], mx[:, j, :], cst("ident"))
                last.then_inc(S["tps"], 1)

        @block.vector
        def _(v):
            with v.Fori(0, B) as i:
                v.wait_ge(S["tps"], i)
                for h in range(H):
                    v.wait_ge(HD["far"][h], i + 1)
                    for jq in range(NB):
                        at = QUERIES_AT[jq]
                        last = v.tensor_reduce(mx[:, jq, h:h + 1], ps[:, h % 2, at:at + 128 * (jq + 1)], AX.X,
                                               ALU.max, negate=True)
                    last.then_inc(HD["top"][h], 1)
                v.wait_ge(S["tps"], i + 1)
                v.wait_ge(S["stored"], 16 * i)
                v.tensor_copy(parts[:, 0, :], tps[:]).then_inc(S["hi"], 1)
                v.wait_ge(S["hi"], i + 1)
                v.tensor_tensor(parts[:, 1, :], tps[:], parts[:, 0, :], ALU.subtract).then_inc(S["mid"], 1)

        @block.scalar
        def _(act):
            with act.Fori(0, B) as i:
                act.wait_ge(S["mid"], i + 1)
                act.dma_start(Md[i].rearrange("n h t -> h n t"), parts[:]).then_inc(S["stored"], 16)
            act.wait_ge(S["stored"], 16 * B)


def project_phase(nc, K, tag, name, w, bias=0.0):
    X = K[name]
    L = 4
    with ExitStack() as ctx:
        S = sems(nc, ctx, tag, "ps out", L)
        ps = ctx.enter_context(nc.psum_tensor(tag + "_ps", [128, L, T], F32))
        block = ctx.enter_context(nc.Block())

        @block.tensor
        def _(pe):
            with pe.Fori(0, B // L) as i:
                for a in range(L):
                    pe.wait_ge(S["out"][a], i)
                    pe.matmul(ps[:, a, :], w, X[:, bass.ds((i * L + a) * T, T)],
                              start=True, stop=True).then_inc(S["ps"][a], 1)

        @block.scalar
        def _(act):
            with act.Fori(0, B // L) as i:
                for a in range(L):
                    act.wait_ge(S["ps"][a], i + 1)
                    act.activation(X[:, bass.ds((i * L + a) * T, T)], ps[:, a, :], ACT.Identity,
                                   bias=bias).then_inc(S["out"][a], 1)


def column_attention_phase(nc, K):
    GX, VA, Pd, cst = K["GX"], K["VA"], K["Pd"], K["cst"]
    H, D = GROUPS * GH, 8
    R = len(TERMS) * D
    AHEAD = 2
    CLOSE = 2
    LOADS = 16 * 2 * len(TERMS)
    with ExitStack() as ctx:
        S = sems(nc, ctx, "ca", "num y")
        G = sems(nc, ctx, "cag", "loaded out", GROUPS)
        U = sems(nc, ctx, "cau", "score top exp", NB)
        V = sems(nc, ctx, "cav", "value", 2 * NB)
        HD = sems(nc, ctx, "cah", "rz vz", H)
        ps = ctx.enter_context(nc.psum_tensor("ca_ps", [128, NB, T], F32))
        O = ctx.enter_context(nc.psum_tensor("ca_o", [128, 2, T], F32))
        nps = ctx.enter_context(nc.psum_tensor("ca_num", [128, T], F32))
        qs = ctx.enter_context(nc.sbuf_tensor("ca_qs", [R, GROUPS, GH, T], BF16))
        ks = ctx.enter_context(nc.sbuf_tensor("ca_ks", [R, GROUPS, GH, T], BF16))
        pw = ctx.enter_context(nc.sbuf_tensor("ca_pw", [128, 2, NB, T], F32))
        mx = ctx.enter_context(nc.sbuf_tensor("ca_mx", [128, H, NB], F32))
        z = ctx.enter_context(nc.sbuf_tensor("ca_z", [128, H, NB], F32))
        vs = ctx.enter_context(nc.sbuf_tensor("ca_vs", [128, 2, NB, D], F32))
        osb = ctx.enter_context(nc.sbuf_tensor("ca_osb", [128, GROUPS, T], F32))
        block = ctx.enter_context(nc.Block())

        @block.sync
        def _(sp):
            with sp.Fori(0, B) as i:
                for g in range(GROUPS):
                    sp.wait_ge(G["out"][g], i)
                    load_stacks(sp, Pd, i, g * GH, GH, qs[:, g], ks[:, g], G["loaded"][g], D)

        @block.tensor
        def _(pe):
            def score(i, h, jk):
                if h % GH == 0 and jk == 0:
                    pe.wait_ge(G["loaded"][h // GH], LOADS * (i + 1))
                pe.wait_ge(U["exp"][jk], i * H + h)
                pe.matmul(ps[:, jk, :], ks[:, h // GH, h % GH, jk * 128:(jk + 1) * 128],
                          qs[:, h // GH, h % GH, :], start=True, stop=True).then_inc(U["score"][jk], 1)

            def value(i, h, jk):
                g = h // GH
                if jk == 0:
                    if h % GH == 0:
                        if g >= 2:
                            pe.wait_ge(G["out"][g - 2], i + 1)
                        else:
                            pe.wait_ge(G["out"][g + 2], i)
                        open_bank(pe, K, O[:, g % 2, :])
                    pe.wait_ge(HD["vz"][h], i + 1)
                last = h % GH == GH - 1 and jk == NB - 1
                pe.matmul(O[32 * (h % GH):32 * (h % GH) + D, g % 2, :], vs[:, h % 2, jk, :],
                          pw[:, h % 2, jk, :], start=False, stop=last, skip_group_check=True
                          ).then_inc(V["value"][h % 2 * NB + jk], 1)

            def close(i):
                for g in range(GROUPS):
                    pe.wait_ge(G["out"][g], i + 1)
                    last = pe.matmul(nps[:], cst("close")[:, g * 128:(g + 1) * 128], osb[:, g, :],
                                     start=(g == 0), stop=(g == GROUPS - 1))
                last.then_inc(S["num"], 1)

            def turn(i, first, last):
                for h in range(H):
                    for jk in range(NB):
                        if h + AHEAD < H:
                            score(i, h + AHEAD, jk)
                        elif not last:
                            score(i + 1, h + AHEAD - H, jk)
                        value(i, h, jk)
                    if h == CLOSE and not first:
                        pe.wait_ge(S["y"], i - 1)
                        close(i - 1)

            for h in range(AHEAD):
                for jk in range(NB):
                    score(0, h, jk)
            turn(0, True, False)
            with pe.Fori(1, B - 1) as i:
                turn(i, False, False)
            turn(B - 1, False, True)
            pe.wait_ge(S["y"], B - 1)
            close(B - 1)

        @block.scalar
        def _(act):
            with act.Fori(0, B) as i:
                for h in range(H):
                    for jk in range(NB):
                        act.wait_ge(V["value"][h % 2 * NB + jk], i * (H // 2) + h // 2)
                        act.wait_ge(U["top"][jk], i * H + h + 1)
                        act.activation(pw[:, h % 2, jk, :], ps[:, jk, :], ACT.Exp,
                                       bias=mx[:, h, jk:jk + 1], accum_out=z[:, h, jk:jk + 1]).then_inc(U["exp"][jk], 1)

        @block.vector
        def _(v):
            def weigh(i, h):
                v.wait_ge(U["exp"][NB - 1], i * H + h + 1)
                v.reciprocal(z[:, h, :], z[:, h, :]).then_inc(HD["rz"][h], 1)
                v.wait_ge(HD["rz"][h], i + 1)
                v.wait_ge(V["value"][h % 2 * NB + NB - 1], i * (H // 2) + h // 2)
                v.tensor_tensor(vs[:, h % 2], VA[:, bass.ds(i * NB, NB), h, 0:D],
                                z[:, h, :].unsqueeze(2).to_broadcast([128, NB, D]), ALU.mult).then_inc(HD["vz"][h], 1)

            def evacuate(i, g):
                h = GH * g + GH - 1
                v.wait_ge(V["value"][h % 2 * NB + NB - 1], i * (H // 2) + h // 2 + 1)
                v.wait_ge(S["num"], i)
                v.tensor_copy(osb[:, g, :], O[:, g % 2, :]).then_inc(G["out"][g], 1)

            def close(i):
                v.wait_ge(S["num"], i + 1)
                v.tensor_copy(GX[:, bass.ds(i * T, T)], nps[:]).then_inc(S["y"], 1)

            def turn(i, first):
                for h in range(H):
                    for jk in range(NB):
                        v.wait_ge(U["score"][jk], i * H + h + 1)
                        v.tensor_reduce(mx[:, h, jk:jk + 1], ps[:, jk, :], AX.X,
                                        ALU.max, negate=True).then_inc(U["top"][jk], 1)
                        if h and jk == 1:
                            weigh(i, h - 1)
                    g = (h - AHEAD - 1) // GH
                    if (h - AHEAD) % GH == 0 and (h > AHEAD or not first):
                        evacuate(i if g >= 0 else i - 1, g % GROUPS)
                    if h == CLOSE + AHEAD + 1 and not first:
                        close(i - 1)
                weigh(i, H - 1)

            turn(0, True)
            with v.Fori(1, B) as i:
                turn(i, False)
            evacuate(B - 1, GROUPS - 1)
            close(B - 1)


def l2_gelu_phase(nc, K):
    GX, cst, W = K["GX"], K["cst"], K["w3"]
    IT = B // LANES
    with ExitStack() as ctx:
        S = sems(nc, ctx, "lg", "z z1 sq ss std rs n w w1 sq2 ss2 std2 rs2 n2 out", LANES)
        ps = ctx.enter_context(nc.psum_tensor("lg_ps", [128, LANES, 4, T], F32))
        z = ctx.enter_context(nc.sbuf_tensor("lg_z", [128, LANES, T], F32))
        sq = ctx.enter_context(nc.sbuf_tensor("lg_sq", [128, LANES, T], F32))
        block = ctx.enter_context(nc.Block())

        def row(i, a):
            return bass.ds((i * LANES + a) * T, T)

        @block.tensor
        def _(pe):
            with pe.Fori(0, IT) as i:
                for a in range(LANES):
                    pe.wait_ge(S["z1"][a], i)
                    pe.matmul(ps[:, a, 0, :], W("wo"), GX[:, row(i, a)], start=True, stop=True).then_inc(S["z"][a], 1)
                for a in range(LANES):
                    pe.wait_ge(S["sq"][a], i + 1)
                    pe.wait_ge(S["std"][a], i)
                    pe.matmul(ps[:, a, 1, :], cst("ones"), sq[:, a, :], start=True, stop=True).then_inc(S["ss"][a], 1)
                for a in range(LANES):
                    pe.wait_ge(S["n"][a], i + 1)
                    pe.wait_ge(S["w1"][a], i)
                    pe.matmul(ps[:, a, 2, :], W("wff"), z[:, a, :], start=True, stop=True).then_inc(S["w"][a], 1)
                for a in range(LANES):
                    pe.wait_ge(S["sq2"][a], i + 1)
                    pe.wait_ge(S["std2"][a], i)
                    pe.matmul(ps[:, a, 3, :], cst("ones"), sq[:, a, :], start=True, stop=True).then_inc(S["ss2"][a], 1)

        @block.scalar
        def _(act):
            with act.Fori(0, IT) as i:
                for tag, src in (("", "z1"), ("2", "w1")):
                    for a in range(LANES):
                        act.wait_ge(S[src][a], i + 1)
                        act.activation(sq[:, a, :], z[:, a, :], ACT.Square).then_inc(S["sq" + tag][a], 1)
                    for a in range(LANES):
                        act.wait_ge(S["ss" + tag][a], i + 1)
                        act.activation(sq[:, a, :], ps[:, a, 3 if tag else 1, :], ACT.Sqrt,
                                       bias=cst("tiny")).then_inc(S["std" + tag][a], 1)
                for a in range(LANES):
                    act.wait_ge(S["n2"][a], i + 1)
                    act.activation(GX[:, row(i, a)], z[:, a, :], ACT.Gelu).then_inc(S["out"][a], 1)

        @block.vector
        def _(v):
            with v.Fori(0, IT) as i:
                for tag, src, dst, nd in (("", "z", "z1", "n"), ("2", "w", "w1", "n2")):
                    for a in range(LANES):
                        v.wait_ge(S[src][a], i + 1)
                        if not tag:
                            v.wait_ge(S["out"][a], i)
                        v.tensor_copy(z[:, a, :], ps[:, a, 2 if tag else 0, :]).then_inc(S[dst][a], 1)
                    for a in range(LANES):
                        v.wait_ge(S["std" + tag][a], i + 1)
                        v.reciprocal(sq[:, a, :], sq[:, a, :]).then_inc(S["rs" + tag][a], 1)
                        v.wait_ge(S["rs" + tag][a], i + 1)
                        v.tensor_tensor(z[:, a, :], z[:, a, :], sq[:, a, :], ALU.mult).then_inc(S[nd][a], 1)


def ssm_rows_phase(nc, K):
    XN, cst, W, Rd, COL = K["XN"], K["cst"], K["w3a"], K["Rd"], K["COL"]
    HB = B * 4
    with ExitStack() as ctx:
        S = sems(nc, ctx, "sr", "ps z az ez lz sp a1 adt ell sub gam bd beta cps col stored sp2")
        ps = ctx.enter_context(nc.psum_tensor("sr_ps", [HB, 3, T], F32))
        cps = ctx.enter_context(nc.psum_tensor("sr_cps", [128, 3, NB, HB], F32))
        z = ctx.enter_context(nc.sbuf_tensor("sr_z", [HB, 2, T], F32))
        e = ctx.enter_context(nc.sbuf_tensor("sr_e", [HB, 2, T], F32))
        q = ctx.enter_context(nc.sbuf_tensor("sr_q", [HB, 6, T], F32))
        block = ctx.enter_context(nc.Block())

        @block.tensor
        def _(pe):
            for n in range(3):
                for b in range(B):
                    last = pe.matmul(ps[:, n, :], W("rows")[:, (n * B + b) * HB:(n * B + b + 1) * HB],
                                     XN[:, b * T:(b + 1) * T], start=(b == 0), stop=(b == B - 1))
            last.then_inc(S["ps"], 1)
            pe.wait_ge(S["ell"], 1)
            pe.wait_ge(S["gam"], 1)
            pe.wait_ge(S["bd"], 1)
            for n in range(3):
                for j in range(NB):
                    last = pe.transpose(cps[:, n, j, :], q[:, n, j * 128:(j + 1) * 128], cst("ident")[0:HB, 0:HB])
            last.then_inc(S["cps"], 1)

        @block.scalar
        def _(act):
            act.wait_ge(S["ps"], 1)
            act.activation(q[:, 5, :], ps[:, 2, :], ACT.Sigmoid).then_inc(S["beta"], 1)
            act.wait_ge(S["z"], 1)
            act.activation(e[:], z[:], ACT.Abs).then_inc(S["az"], 1)
            act.wait_ge(S["az"], 1)
            act.activation(e[:], e[:], ACT.Exp, scale=-1.0).then_inc(S["ez"], 1)
            act.wait_ge(S["ez"], 1)
            act.activation(e[:], e[:], ACT.Ln, bias=1.0).then_inc(S["lz"], 1)

        @block.vector
        def _(v):
            v.wait_ge(S["ps"], 1)
            v.wait_ge(S["beta"], 1)
            v.tensor_scalar(z[:, 0, :], ps[:, 0, :], W("dt_bias"), None, ALU.add)
            v.tensor_copy(z[:, 1, :], ps[:, 1, :]).then_inc(S["z"], 1)
            v.wait_ge(S["z"], 1)
            v.wait_ge(S["lz"], 1)
            v.scalar_tensor_tensor(out=q[:, 3:5, :], in0=z[:], scalar=0.0, in1=e[:],
                                   op0=ALU.max, op1=ALU.add).then_inc(S["sp"], 1)
            v.wait_ge(S["sp"], 1)
            v.tensor_scalar(q[:, 4, :], q[:, 4, :], -1.0, -1e-4, ALU.mult, ALU.min).then_inc(S["a1"], 1)
            v.wait_ge(S["a1"], 1)
            v.tensor_tensor(q[:, 4, :], q[:, 4, :], q[:, 3, :], ALU.mult).then_inc(S["adt"], 1)
            v.wait_ge(S["adt"], 1)
            v.tensor_tensor_scan(q[:, 0, :], cst("onerow")[0:HB], q[:, 4, :], 0.0, ALU.mult, ALU.add).then_inc(S["ell"], 1)
            v.tensor_tensor(q[:, 2, :], q[:, 5, :], q[:, 3, :], ALU.mult).then_inc(S["bd"], 1)
            v.tensor_tensor(e[:, 0, 0:T - 1], q[:, 5, 0:T - 1], q[:, 5, 1:T], ALU.subtract)
            v.tensor_copy(e[:, 0, T - 1:T], q[:, 5, T - 1:T]).then_inc(S["sub"], 1)
            v.wait_ge(S["sub"], 1)
            v.scalar_tensor_tensor(out=q[:, 1, :], in0=e[:, 0, :], scalar=1.0, in1=q[:, 3, :],
                                   op0=ALU.add, op1=ALU.mult).then_inc(S["gam"], 1)
            v.wait_ge(S["cps"], 1)
            v.tensor_copy(COL[:], cps[:]).then_inc(S["col"], 1)
            v.wait_ge(S["col"], 1)

        @block.sync
        def _(sp):
            sp.wait_ge(S["ell"], 1)
            sp.dma_start(Rd[0], q[:, 3, :]).then_inc(S["stored"], 16)
            sp.dma_start(Rd[1], q[:, 0, :]).then_inc(S["stored"], 16)
            sp.wait_ge(S["stored"], 32)


def ssm_phase(nc, K):
    XN, SX, cst, W, Rd, COL = K["XN"], K["SX"], K["cst"], K["w3a"], K["Rd"], K["COL"]
    H = 4
    TWO_PI_HI, TWO_PI_LO = 6.28125, float(2 * np.pi - 6.28125)
    MAGIC = 1.5 * 2.0 ** 23
    Q_, K_ = 0, 1
    with ExitStack() as ctx:
        S = sems(nc, ctx, "ss", "xs rows pj1 ev1 pj2 ev2a ev2b xt sq ms std rs norm nturn rev at th n n1 c1 c2 clamp "
                 "sin abs cos cosm y2 yz sps s colj")
        HD = sems(nc, ctx, "sh", "cps b0 t1 t2 turned qk dd dec m0 m1 m2 dm a y", H)
        ps = ctx.enter_context(nc.psum_tensor("ss_ps", [128, 8, T], F32))
        sb = lambda name, *n: ctx.enter_context(nc.sbuf_tensor("ss_" + name, [128, *n], F32))
        xs, zs, xf, bc, rot = sb("xs", T), sb("zs", 2, T), sb("xf", 2, T), sb("bc", 2, T), sb("rot", 2, T)
        sq, xt, ang, th = sb("sq", 2, T), sb("xt", NB, 256), sb("ang", T), sb("th", 3, T)
        dtb, ellb = sb("dtb", T), sb("ellb", H, T)
        tb, t2, t3 = sb("tb", 2, T), sb("t2", 2, T), sb("t3", 2, T)
        kq, dec, aw = sb("kq", 2, 2, T), sb("dec", 2, 3, T), sb("aw", 3, T)
        mm = sb("mm", 2, NB, 128)
        y = sb("y", 2, T)
        block = ctx.enter_context(nc.Block())

        @block.sync
        def _(sp):
            with sp.Fori(0, B) as i:
                sp.wait_ge(S["at"], i)
                sp.wait_ge(HD["dd"][H - 1], i)
                for h in range(H):
                    sp.dma_start(dtb[32 * h:32 * h + 32, :], Rd[0, bass.ds(i * H + h, 1), :].to_broadcast([32, T])
                                 ).then_inc(S["rows"], 16)
                    sp.dma_start(ellb[:, h, :], Rd[1, bass.ds(i * H + h, 1), :].to_broadcast([128, T])
                                 ).then_inc(S["rows"], 16)

        @block.tensor
        def _(pe):
            with pe.Fori(0, B) as i:
                pe.wait_ge(S["s"], i)
                pe.wait_ge(S["xs"], i + 1)
                for n in range(7):
                    last = pe.matmul(ps[:, n, :], W("in")[:, n * 128:(n + 1) * 128], xs[:], start=True, stop=True)
                last.then_inc(S["pj1"], 1)
                pe.wait_ge(S["ev1"], i + 1)
                pe.wait_ge(S["ev2a"], i + 1)
                for j in range(NB):
                    last = pe.matmul(ps[:, j // 2, (j % 2) * 256:(j % 2) * 256 + 256], xs[:, j * 128:(j + 1) * 128],
                                     W("in")[:, 256:512], start=True, stop=True)
                last.then_inc(S["pj2"], 1)
                pe.wait_ge(S["sq"], i + 1)
                for n in range(2):
                    last = pe.matmul(ps[:, 4 + n, :], cst("mean"), sq[:, n, :], start=True, stop=True)
                last.then_inc(S["ms"], 1)
                pe.wait_ge(S["norm"], i + 1)
                for n in range(2):
                    last = pe.matmul(ps[:, 2 + n, :], cst("rot"), bc[:, n, :], start=True, stop=True)
                last.then_inc(S["nturn"], 1)
                pe.wait_ge(S["rev"], i + 1)
                pe.wait_ge(S["xt"], i + 1)
                pe.wait_ge(S["cosm"], i + 1)
                pe.wait_ge(S["sin"], i + 1)

                def spread(h):
                    if h:
                        pe.wait_ge(HD["t2"][h - 1], i + 1)
                    for n in range(2):
                        last = pe.matmul(ps[:, 3 + n, :], cst(("spread", "spread_sin")[n])[:, h * 128:(h + 1) * 128],
                                         th[:, 1 + n, :],
                                         start=True, stop=True)
                    last.then_inc(HD["cps"][h], 1)

                spread(0)
                for h in range(H):
                    if h + 1 < H:
                        spread(h + 1)
                    pe.wait_ge(HD["turned"][h], i + 1)
                    if h:
                        pe.wait_ge(HD["a"][h - 1], i + 1)
                    for jk in range(NB):
                        at, n = KEYS_AT[jk], T - 128 * jk
                        last = pe.matmul(ps[:, at // T, at % T:at % T + n], kq[:, h % 2, K_, jk * 128:(jk + 1) * 128],
                                         kq[:, h % 2, Q_, jk * 128:T], start=True, stop=True)
                    last.then_inc(HD["qk"][h], 1)
                    pe.wait_ge(HD["a"][h], i + 1)
                    r = slice(64 * (h % 2), 64 * (h % 2) + 64)
                    for jk in range(NB):
                        at, n = KEYS_AT[jk], T - 128 * jk
                        last = pe.matmul(ps[r, 5 + h // 2, jk * 128:T], xt[:, jk, h * 64:(h + 1) * 64],
                                         aw[:, at // T, at % T:at % T + n], start=(jk == 0), stop=(jk == NB - 1))
                    last.then_inc(HD["y"][h], 1)
                pe.wait_ge(S["yz"], i + 1)
                for n in range(2):
                    last = pe.matmul(ps[:, 7, :], W("out")[:, n * C:(n + 1) * C], y[:, n, :],
                                     start=(n == 0), stop=(n == 1))
                last.then_inc(S["sps"], 1)

        @block.scalar
        def _(act):
            with act.Fori(0, B) as i:
                act.wait_ge(S["pj1"], i + 1)
                act.wait_ge(S["yz"], i)
                act.activation(zs[:], ps[:, 0:2, :], ACT.Silu)
                act.activation(ang[:], ps[:, 6, :], ACT.Copy)
                act.wait_ge(S["y2"], i)
                act.activation(xf[:], ps[:, 2:4, :], ACT.Copy).then_inc(S["ev1"], 1)
                act.wait_ge(S["ev2a"], i + 1)
                act.activation(sq[:], bc[:], ACT.Square).then_inc(S["sq"], 1)
                act.wait_ge(S["pj2"], i + 1)
                act.activation(xt[:].rearrange("p j f -> p (j f)"), ps[:, 0:2, :].rearrange("p n t -> p (n t)"),
                               ACT.Copy).then_inc(S["xt"], 1)
                act.wait_ge(S["ms"], i + 1)
                act.activation(sq[:], ps[:, 4:6, :], ACT.Sqrt, bias=cst("eps")).then_inc(S["std"], 1)
                act.wait_ge(S["clamp"], i + 1)
                act.activation(th[:, 2, :], th[:, 0, :], ACT.Sin).then_inc(S["sin"], 1)
                act.activation(th[:, 1, :], th[:, 0, :], ACT.Abs).then_inc(S["abs"], 1)
                act.wait_ge(S["abs"], i + 1)
                act.activation(th[:, 1, :], th[:, 1, :], ACT.Sin, scale=-1.0, bias=cst("halfpi")).then_inc(S["cos"], 1)
                act.wait_ge(S["nturn"], i + 1)
                act.activation(rot[:], ps[:, 2:4, :], ACT.Copy).then_inc(S["rev"], 1)
                for h in range(H):
                    act.wait_ge(HD["dd"][h], i + 1)
                    for g, n in ((0, T), (1, T), (2, 256)):
                        last = act.activation(dec[:, h % 2, g, 0:n], dec[:, h % 2, g, 0:n], ACT.Exp)
                    last.then_inc(HD["dec"][h], 1)
                act.wait_ge(S["sps"], i + 1)
                act.activation(SX[:, bass.ds(i * T, T)], ps[:, 7, :], ACT.Copy).then_inc(S["s"], 1)

        @block.gpsimd
        def _(g):
            with g.Fori(0, B) as i:
                for h in range(H):
                    for n, c, src in ((0, 1, "stri"), (1, 2, "ident")):
                        if n == 0:
                            if h >= 1:
                                g.wait_ge(HD["dm"][h - 1], i + 1)
                            else:
                                g.wait_ge(HD["dm"][H - 1], i)
                        last = g.tensor_tensor(mm[:, n], cst(src).unsqueeze(1).to_broadcast([128, NB, 128]),
                                               COL[:, c, :, bass.ds(i * H + h, 1)].to_broadcast([128, NB, 128]),
                                               ALU.mult)
                    last.then_inc(HD["m1"][h], 1)
                    g.wait_ge(HD["m1"][h], i + 1)
                    g.tensor_tensor(mm[:, 0], mm[:, 0], mm[:, 1], ALU.add).then_inc(HD["m2"][h], 1)
                    g.wait_ge(HD["m2"][h], i + 1)
                    g.wait_ge(HD["dec"][h], i + 1)
                    for jk in range(NB):
                        at = KEYS_AT[jk]
                        d = dec[:, h % 2, at // T, at % T:at % T + 128]
                        last = g.tensor_tensor(d, d, mm[:, 0, jk, :], ALU.mult)
                    last.then_inc(HD["dm"][h], 1)

        @block.vector
        def _(v):
            with v.Fori(0, B) as i:
                v.wait_ge(S["pj2"], i)
                v.tensor_copy(xs[:], XN[:, bass.ds(i * T, T)]).then_inc(S["xs"], 1)
                v.wait_ge(S["pj1"], i + 1)
                v.wait_ge(S["nturn"], i)
                v.tensor_copy(bc[:], ps[:, 4:6, :]).then_inc(S["ev2a"], 1)
                v.wait_ge(S["ev1"], i + 1)
                v.wait_ge(S["rows"], 16 * 2 * H * (i + 1))
                v.tensor_tensor(ang[:], ang[:], dtb[:], ALU.mult).then_inc(S["at"], 1)
                v.wait_ge(S["at"], i + 1)
                v.tensor_tensor_scan(th[:, 0, :], cst("onerow"), ang[:], 0.0, ALU.mult, ALU.add).then_inc(S["th"], 1)
                v.wait_ge(S["th"], i + 1)
                v.wait_ge(HD["cps"][H - 1], i)
                v.tensor_scalar(th[:, 1, :], th[:, 0, :], float(1 / (2 * np.pi)), MAGIC, ALU.mult,
                                ALU.add).then_inc(S["n"], 1)
                v.wait_ge(S["n"], i + 1)
                v.tensor_scalar(th[:, 1, :], th[:, 1, :], MAGIC, None, ALU.subtract).then_inc(S["n1"], 1)
                v.wait_ge(S["n1"], i + 1)
                v.scalar_tensor_tensor(out=th[:, 0, :], in0=th[:, 1, :], scalar=-TWO_PI_HI, in1=th[:, 0, :],
                                       op0=ALU.mult, op1=ALU.add).then_inc(S["c1"], 1)
                v.wait_ge(S["c1"], i + 1)
                v.scalar_tensor_tensor(out=th[:, 0, :], in0=th[:, 1, :], scalar=-TWO_PI_LO, in1=th[:, 0, :],
                                       op0=ALU.mult, op1=ALU.add).then_inc(S["c2"], 1)
                v.wait_ge(S["c2"], i + 1)
                v.tensor_scalar(th[:, 0, :], th[:, 0, :], 3.1415925, -3.1415925, ALU.min,
                                ALU.max).then_inc(S["clamp"], 1)
                v.wait_ge(S["std"], i + 1)
                v.reciprocal(sq[:], sq[:]).then_inc(S["rs"], 1)
                v.wait_ge(S["rs"], i + 1)
                for n in range(2):
                    last = v.scalar_tensor_tensor(out=bc[:, n, :], in0=bc[:, n, :], scalar=W("bc_w")[:, n:n + 1],
                                                  in1=sq[:, n, :], op0=ALU.mult, op1=ALU.mult)
                last.then_inc(S["norm"], 1)
                v.wait_ge(S["cos"], i + 1)
                v.tensor_scalar(th[:, 1, :], th[:, 1, :], 1.0, None, ALU.subtract).then_inc(S["cosm"], 1)
                v.wait_ge(S["norm"], i + 1)
                v.wait_ge(S["rev"], i + 1)
                for h in range(H):
                    v.wait_ge(HD["cps"][h], i + 1)
                    if h >= 2:
                        v.wait_ge(HD["qk"][h - 2], i + 1)
                    if h:
                        v.wait_ge(HD["turned"][h - 1], i + 1)
                    for n in range(2):
                        last = v.tensor_scalar(tb[:, n, :], bc[:, n, :], W("bc_b")[:, n * H + h:n * H + h + 1], None,
                                               ALU.add)
                    last.then_inc(HD["b0"][h], 1)
                    v.wait_ge(HD["b0"][h], i + 1)
                    for n in range(2):
                        v.scalar_tensor_tensor(out=t2[:, n, :], in0=ps[:, 3, :], scalar=1.0, in1=tb[:, n, :],
                                               op0=ALU.add, op1=ALU.mult)
                        last = v.scalar_tensor_tensor(out=t3[:, n, :], in0=rot[:, n, :],
                                                      scalar=W("bc_rb")[:, n * H + h:n * H + h + 1], in1=ps[:, 4, :],
                                                      op0=ALU.add, op1=ALU.mult)
                    last.then_inc(HD["t2"][h], 1)
                    v.wait_ge(HD["t2"][h], i + 1)
                    for n in range(2):
                        last = v.tensor_tensor(kq[:, h % 2, K_ if n == 0 else Q_, :], t2[:, n, :], t3[:, n, :], ALU.add)
                    last.then_inc(HD["turned"][h], 1)
                    if h >= 2:
                        v.wait_ge(HD["a"][h - 2], i + 1)
                    for jk in range(NB):
                        at, n = KEYS_AT[jk], T - 128 * jk
                        last = v.tensor_scalar(dec[:, h % 2, at // T, at % T:at % T + n], ellb[:, h, jk * 128:T],
                                               COL[:, 0, jk, bass.ds(i * H + h, 1)], 0.0, ALU.subtract, ALU.min)
                    last.then_inc(HD["dd"][h], 1)
                    v.wait_ge(HD["qk"][h], i + 1)
                    v.wait_ge(HD["dm"][h], i + 1)
                    if h:
                        v.wait_ge(HD["y"][h - 1], i + 1)
                    for jk in range(NB):
                        at, n = KEYS_AT[jk], T - 128 * jk
                        g, o = at // T, at % T
                        last = v.tensor_tensor(aw[:, g, o:o + 128], ps[:, g, o:o + 128], dec[:, h % 2, g, o:o + 128],
                                               ALU.mult)
                        if n > 128:
                            last = v.scalar_tensor_tensor(
                                out=aw[:, g, o + 128:o + n], in0=ps[:, g, o + 128:o + n],
                                scalar=COL[:, 1, jk, bass.ds(i * H + h, 1)], in1=dec[:, h % 2, g, o + 128:o + n],
                                op0=ALU.mult, op1=ALU.mult)
                    last.then_inc(HD["a"][h], 1)
                v.wait_ge(HD["y"][H - 1], i + 1)
                v.wait_ge(S["sps"], i)
                for n in range(2):
                    last = v.scalar_tensor_tensor(out=y[:, n, :], in0=xf[:, n, :], scalar=W("d")[:, n:n + 1],
                                                  in1=ps[:, 5 + n, :], op0=ALU.mult, op1=ALU.add)
                last.then_inc(S["y2"], 1)
                v.wait_ge(S["y2"], i + 1)
                v.tensor_tensor(y[:], y[:], zs[:], ALU.mult).then_inc(S["yz"], 1)


def rows_at(places, n):
    out = np.zeros((n, places[0][1].shape[1]), np.float32)
    for at, a in places:
        out[at:at + a.shape[0]] = a
    return out


def col(a):
    return np.reshape(a, (-1, 1))


def w0_parts(I):
    L = lambda n: I["L0_attn_" + n]
    return {
        "maa_x": col(L("time_maa_x")), "maa": L("time_maa").reshape(4, C).T,
        "maa_w1": L("time_maa_w1").T,
        "maa_w2": L("time_maa_w2").transpose(0, 2, 1).reshape(128, C),
        "receptance": L("receptance").T, "gate_w1": L("gate_w1").T, "gate_w2": L("gate_w2").T,
        "key_w": L("key_w").T, "value": L("value").T, "output": L("output").T,
        "kkk_mk_w1": rows_at([(0, L("time_kkk_w1")), (32, L("mk_w1"))], 64).T,
        "kkk_w2": rows_at([(0, L("time_kkk_w2").T)], 32),
        "mk_w2": rows_at([(32, L("mk_w2").T)], 64),
        "decay_aaa_ma_w1": rows_at([(0, L("time_decay_w1")), (64, L("time_aaa_w1")), (96, L("ma_w1"))], 128).T,
        "decay_w2": L("time_decay_w2").T,
        "aaa_w2": rows_at([(64, L("time_aaa_w2").T)], 96),
        "ma_w2": rows_at([(96, L("ma_w2").T)], 128),
        "decay": col(L("time_decay")), "aaaaa": col(L("time_aaaaa")), "misc_a": col(L("time_misc_a")),
        "misc_k": col(L("time_misc_k")), "ln_w": col(L("ln_w")), "ln_b": col(L("ln_b")),
        "faaaa": col(L("time_faaaa")), "router": I["L0_ffn_Wr"].T,
    }


def w1_parts(I):
    return {
        "q": I["L1_attn_Wq"].T, "k": I["L1_attn_Wk"].T,
        "v": I["L1_attn_Wv"].T, "o": I["L1_attn_Wo"].T, "gate": I["L1_ffn_Wg"],
        "ffb1": I["L1_ffn_b1"].reshape(-1, 128).T, "ffb2": I["L1_ffn_b2"].T,
    }


def w2_parts(I):
    L = lambda n: I["L2_attn_" + n]
    w, b = L("qkv_w"), L("qkv_b")
    return {
        "q": w[:, 0:C], "k": w[:, C:2 * C], "qk_b": b[0:2 * C].reshape(2, C).T,
        "v": w[:, 2 * C:], "v_b_row": np.broadcast_to(b[2 * C:], (128, C)),
        "o": L("out_w"), "o_b": col(L("out_b")), "g_attn": col(L("g_attn")), "b_attn": col(L("b_attn")),
        "g1": col(L("g1")), "b1": col(L("b1")), "g2": col(L("g2")), "b2": col(L("b2")),
        "w_ctx": L("w_ctx"), "w_x": L("w_x"), "b_inl": col(L("b_inl")),
        "ff_w1": L("ff_w1"), "ff_b1": L("ff_b1").reshape(4, 128).T,
        "ff_w2": L("ff_w2").reshape(4, 128, C).transpose(1, 0, 2).reshape(128, 4 * C), "ff_b2": col(L("ff_b2")),
    }


def w2f_parts(I):
    L = lambda n: I["L2_ffn_" + n]
    wide = lambda w: w.T.reshape(4, 128, -1).transpose(1, 0, 2).reshape(128, -1)
    cols = lambda b: b.reshape(4, 128).T
    return {
        "w1": L("w1_w").T, "w2": L("w2_w").T, "h1": wide(L("h1_w")), "h2": wide(L("h2_w")), "w3": wide(L("w3_w")),
        "s1": cols(L("w1_s")), "s2": cols(L("w2_s")), "sh1": cols(L("h1_s")), "sh2": cols(L("h2_s")),
        "s3": col(L("w3_s")),
    }


def w3f_parts(I):
    L = lambda n: I["L3_ffn_" + n]
    return {"q": L("Wq"), "k": L("Wk"), "v": L("Wv"), "wo": L("Wo"), "wff": L("Wff")}


def w3a_parts(I):
    L = lambda n: I["L3_attn_" + n]
    w = L("W_in")
    o = np.cumsum([0, 256, 256, 128, 128, 4, 4, 4, 32])
    z, x, bb, cc, dt, aa, trap, ang = [w[:, o[n]:o[n + 1]] for n in range(8)]
    rows = np.zeros((C, 3, B, B, 4), np.float32)
    for n, part in enumerate((dt, aa, trap)):
        for b in range(B):
            rows[:, n, b, b] = part

    def turned(a):
        return np.concatenate([a[..., 32:64], a[..., 0:32], np.zeros_like(a[..., 64:])], -1)

    return {
        "in": np.concatenate([z, x, bb, cc, ang, ang, ang, ang], 1), "rows": rows.reshape(C, -1),
        "out": L("W_out").reshape(2, 128, C).transpose(1, 0, 2).reshape(128, 2 * C),
        "dt_bias": col(np.broadcast_to(L("dt_bias"), (B, 4))), "bc_w": np.stack([L("B_norm_w"), L("C_norm_w")], 1),
        "bc_b": np.concatenate([L("B_bias"), L("C_bias")]).T,
        "bc_rb": turned(np.concatenate([L("B_bias"), L("C_bias")])).T,
        "d": np.repeat(L("D"), 64).reshape(2, 128).T,
    }


def constb_parts():
    i = np.arange(128)
    return {
        "identb": np.eye(128, dtype=np.float32),
        "neg_down": np.where(i[None] > i[:, None], -1e30, 0).astype(np.float32),
        "neg_across": np.where(i[:, None] > i[None], -1e30, 0).astype(np.float32),
    }


def closing(first, n):
    out = np.zeros((128, GROUPS, 128), np.float32)
    for g in range(GROUPS):
        for h in range(GH):
            for d in range(8):
                out[32 * h + first + (d if n > 1 else 0), g, 8 * (g * GH + h) + d] = 1
    return out.reshape(128, GROUPS * 128)


def const_parts():
    i = np.arange(128)
    return {
        "ident": np.eye(128, dtype=np.float32),
        "mean": np.full((128, 128), 1 / C, np.float32),
        "ones": np.ones((128, 128), np.float32),
        "headsum": (i[:, None] // 8 == i[None] // 8).astype(np.float32),
        "tri": (i[:, None] <= i[None]).astype(np.float32),
        "headmean": (i[:, None] // 8 == i[None] // 8).astype(np.float32) / 8,
        "exsum": (i[:, None] // 16 == i[None] // 16).astype(np.float32),
        "exbefore": ((i[:, None] // 16 == i[None] // 16) & (i[:, None] < i[None])).astype(np.float32),
        "onerow": np.ones((128, 512), np.float32),
        "stri": (i[:, None] < i[None]).astype(np.float32),
        "rot": ((i[:, None] < 64) & (i[None] < 64) & (i[:, None] == (i[None] + 32) % 64)).astype(np.float32),
        "spread": np.concatenate([((i[:, None] // 32 == h) & (i[None] < 64) & (i[:, None] % 32 == i[None] % 32))
                                  .astype(np.float32) for h in range(4)], 1),
        "spread_sin": np.concatenate([((i[:, None] // 32 == h) & (i[None] < 64) & (i[:, None] % 32 == i[None] % 32))
                                      * np.where(i[None] < 32, -1, 1).astype(np.float32) for h in range(4)], 1),
        "halfpi": np.full((128, 1), np.pi / 2, np.float32),
        "halfwide": np.concatenate([0.5 * (i[:, None] <= i[None]), np.full((128, T - 128), 0.5)], 1
                                   ).astype(np.float32),
        "halfcount": 0.5 * np.arange(1, T + 1, dtype=np.float32)[None],
        "close": closing(0, 8), "close_den": closing(8, 1),
        "rhalf": np.full((128, 1), 0.5 ** 0.5, np.float32),
        "eps": np.full((128, 1), 1e-5, np.float32),
        "gn_eps": np.full((128, 1), 0.00064, np.float32),
        "mhalf": np.full((128, 1), -0.5, np.float32),
        "tiny": np.full((128, 1), 1e-24, np.float32),
    }


def pack(parts):
    at, place, cols = 0, {}, []
    for n, a in parts.items():
        full = np.zeros((128, a.shape[1]), np.float32)
        full[:a.shape[0]] = a
        place[n] = (at, a.shape[0], a.shape[1])
        at += a.shape[1]
        cols.append(full)
    return np.concatenate(cols, 1), place


def view(tile, place):
    def get(name):
        at, rows, n = place[name]
        return tile[0:rows, at:at + n]
    return get


def update_phase(nc, K, layer, out=None):
    X, SX, GX = K["X"], K["SX"], K["GX"]
    PARTS = 4
    N = NT // PARTS
    with ExitStack() as ctx:
        S = sems(nc, ctx, f"u{layer}", "gate prod added stored", 1)
        block = ctx.enter_context(nc.Block())

        @block.scalar
        def _(act):
            for n in range(PARTS):
                p = slice(n * N, (n + 1) * N)
                act.activation(GX[:, p], GX[:, p], ACT.Silu).then_inc(S["gate"], 1)

        @block.vector
        def _(v):
            for n in range(PARTS):
                p = slice(n * N, (n + 1) * N)
                v.wait_ge(S["gate"], n + 1)
                v.tensor_tensor(SX[:, p], SX[:, p], GX[:, p], ALU.mult).then_inc(S["prod"], 1)
                v.wait_ge(S["prod"], n + 1)
                v.tensor_tensor(X[:, p], X[:, p], SX[:, p], ALU.add).then_inc(S["added"], 1)

        if out is not None:
            @block.sync
            def _(sp):
                for n in range(PARTS):
                    p = slice(n * N, (n + 1) * N)
                    sp.wait_ge(S["added"], n + 1)
                    sp.dma_start(out[:, p], X[:, p]).then_inc(S["stored"], 16)
                sp.wait_ge(S["stored"], 16 * PARTS)


def load_phase(nc, tag, pairs):
    with ExitStack() as ctx:
        loaded = sems(nc, ctx, "ld" + tag, "loaded")["loaded"]
        block = ctx.enter_context(nc.Block())

        @block.sync
        def _(sp):
            for dst, src in pairs:
                sp.dma_start(dst, src).then_inc(loaded, 16)
            sp.wait_ge(loaded, 16 * len(pairs))


def zero_phase(nc, zero):
    with nc.Block() as block:
        @block.vector
        def _(v):
            v.memset(zero[:], 0.0)


def convert_phase(nc, dst, src):
    with nc.Block() as block:
        @block.vector
        def _(v):
            v.tensor_copy(dst, src)


def network(nc, A, out, places):
    with ExitStack() as ctx:
        K = {"A": A}
        for n in ("X", "XN", "SX", "GX"):
            K[n] = ctx.enter_context(nc.sbuf_tensor(n, [128, NT], F32))

        def weights(scope, name):
            n = places[name][1]
            tile = scope.enter_context(nc.sbuf_tensor("w_" + name, [128, n], F32))
            K[name] = view(tile, places[name][0])
            return tile[:], A[name]

        def scratch(name, shape, dtype):
            K[name] = nc.dram_tensor(name, shape, dtype, kind="Internal").ap()

        def tile(scope, name, shape, dtype, layer=""):
            K[name] = scope.enter_context(nc.sbuf_tensor(name + layer, shape, dtype))

        tile(ctx, "zero", [1, T], BF16)
        zero_phase(nc, K["zero"])
        first = [weights(ctx, "cst"), (K["X"][:], A["x"])]
        with ExitStack() as layer:
            load_phase(nc, "0", first + [weights(layer, "w0")])
            norm_phase(nc, K, "0")
            scratch("Qd", [8, B, 128, T], F32)
            scratch("Yd", [128, B, T], F32)
            rwkv_pre_phase(nc, K)
            rwkv_scan_phase(nc, K)
            rwkv_out_phase(nc, K)
            scratch("Xt", [NT, C], F32)
            scratch("Acc", [NT, C], F32)
            tile(layer, "IDX", [128, E], U32)
            tile(layer, "WGT", [128, E], F32)
            route_phase(nc, K)
            experts_phase(nc, K)
            collect_phase(nc, K)
        update_phase(nc, K, "0")
        with ExitStack() as layer:
            load_phase(nc, "1", [weights(layer, "w1")])
            norm_phase(nc, K, "1")
            scratch("Pd1", [B, 2, 3, 2 * C, T], BF16)
            K["Pd"] = K["Pd1"]
            tile(layer, "VA", [128, NT // 128, 16, 9], F32, "1")
            split_phase(nc, K, "s1", "XN", K["w1"]("q"), K["w1"]("k"), K["w1"]("v"), 2, 16)
            causal_phase(nc, K, "ta", "SX", 16, False)
            project_phase(nc, K, "tp", "SX", K["w1"]("o"))
            scratch("Sd", [E1, NT], F32)
            scratch("Gd", [E1, NT], F32)
            choose_phase(nc, K)
            ffn1_phase(nc, K)
        update_phase(nc, K, "1")
        with ExitStack() as layer:
            load_phase(nc, "2", [weights(layer, "w2"), weights(layer, "cb_f32")])
            n = places["cb_f32"][1]
            tile(layer, "cb_tile", [128, n], BF16)
            K["cb"] = view(K["cb_tile"], places["cb_f32"][0])
            norm_phase(nc, K, "2")
            at = {p: K["cb"](p) for p in places["cb_f32"][0]}
            for p in at:
                convert_phase(nc, at[p], K["cb_f32"](p))
            norm_phase(nc, K, "2a", "XN", "SX", K["w2"]("g_attn"), K["w2"]("b_attn"))
            scratch("Pd", [B, 2, 3, C, T], BF16)
            scratch("Md", [B, 2, 16, T], BF16)
            tile(layer, "VA", [128, NT // 128, 16, 9], F32, "2")
            split_phase(nc, K, "s2", "SX", K["w2"]("q"), K["w2"]("k"), K["w2"]("v"), 1, 8, K["w2"]("qk_b"))
            maxima_phase(nc, K)
            causal_phase(nc, K, "at", "GX", 8, True)
            project_phase(nc, K, "ap", "GX", K["w2"]("o"), K["w2"]("o_b"))
            inertia_phase(nc, K)
        with ExitStack() as layer:
            load_phase(nc, "2f", [weights(layer, "w2f")])
            gated_mlp_phase(nc, K)
        update_phase(nc, K, "2")
        with ExitStack() as layer:
            load_phase(nc, "3", [weights(layer, "w3")])
            norm_phase(nc, K, "3")
            tile(layer, "VA", [128, NT // 128, 16, 9], F32, "3")
            split_phase(nc, K, "s3", "XN", K["w3"]("q"), K["w3"]("k"), K["w3"]("v"), 1, 8, qscale=float(1 / np.sqrt(C)))
            column_attention_phase(nc, K)
            l2_gelu_phase(nc, K)
        with ExitStack() as layer:
            load_phase(nc, "3a", [weights(layer, "w3a")])
            scratch("Rd", [2, B * 4, T], F32)
            tile(layer, "COL", [128, 3, NB, B * 4], F32)
            ssm_rows_phase(nc, K)
            ssm_phase(nc, K)
        update_phase(nc, K, "3", out)


def kernel(**inputs):
    import numpy as _np
    import concourse.bacc as _bacc
    from concourse import mybir as _mybir
    from concourse.bass_utils import run_bass_kernel_spmd as _run

    I = {n: _np.asarray(a) for n, a in inputs.items()}
    arrays, places = {}, {}
    for name, parts in (("cst", const_parts()), ("cb_f32", constb_parts()), ("w0", w0_parts(I)), ("w1", w1_parts(I)),
                        ("w2", w2_parts(I)), ("w2f", w2f_parts(I)), ("w3", w3f_parts(I)), ("w3a", w3a_parts(I))):
        a, place = pack(parts)
        arrays[name] = a
        places[name] = (place, a.shape[1])
    arrays["x"] = I["L0_attn_x"].reshape(NT, C).T
    arrays["e_w1"], arrays["e_w2"] = I["L0_ffn_W1"], I["L0_ffn_W2"]
    arrays["e_b1"] = I["L0_ffn_b1"].transpose(2, 0, 1).reshape(128, -1)
    arrays["e_b2"] = I["L0_ffn_b2"].reshape(1, -1)
    arrays["f1_w1"], arrays["f1_w2"] = I["L1_ffn_W1"], I["L1_ffn_W2"]
    arrays = {n: _np.ascontiguousarray(a) for n, a in arrays.items()}

    nc = _bacc.Bacc("TRN2", target_bir_lowering=False, num_devices=1)
    A = {n: nc.dram_tensor(n, a.shape, _mybir.dt.from_np(a.dtype), kind="ExternalInput").ap()
         for n, a in arrays.items()}
    out = nc.dram_tensor("out", (C, NT), F32, kind="ExternalOutput").ap()
    network(nc, A, out, places)
    r = _run(nc, [arrays], core_ids=[0])
    return _np.ascontiguousarray(r.results[0]["out"].T).reshape(B, T, C)
```

```python
from contextlib import ExitStack

import numpy as np

import concourse.bass as bass
from concourse import mybir

F32 = mybir.dt.float32
BF16 = mybir.dt.bfloat16
U32 = mybir.dt.uint32
I32 = mybir.dt.int32
ALU = mybir.AluOpType
ACT = mybir.ActivationFunctionType
AX = mybir.AxisListType

B, T, C = 8, 512, 128
NT = B * T
NB = T // 128
E, CAP, S4 = 48, 128, 4
E1, CAP1, BITS = 8, 1024, 30
LANES = 2


def sems(nc, ctx, tag, names, lanes=1):
    made = {n: [nc.alloc_semaphore(f"{tag}_{n}{a}") for a in range(lanes)] for n in names.split()}
    ctx.callback(clear, nc, [s for lane in made.values() for s in lane])
    return made if lanes > 1 else {n: s[0] for n, s in made.items()}


def clear(nc, used):
    nc.clear_and_free_semaphores(used)
    nc.all_engine_barrier()


def norm_phase(nc, K, layer, src="X", dst="XN", gain=None, shift=None):
    X, XN, cst = K[src], K[dst], K["cst"]
    L = 4
    with ExitStack() as ctx:
        S = sems(nc, ctx, f"n{layer}", "mean cent sq var std rstd gained xn", L)
        ps = ctx.enter_context(nc.psum_tensor(f"n{layer}_ps", [128, 2 * L, T], F32))
        xc = ctx.enter_context(nc.sbuf_tensor(f"n{layer}_xc", [128, L, T], F32))
        sq = ctx.enter_context(nc.sbuf_tensor(f"n{layer}_sq", [128, L, T], F32))
        block = ctx.enter_context(nc.Block())

        @block.tensor
        def _(pe):
            with pe.Fori(0, B // L) as i:
                n = i * L
                for a in range(L):
                    pe.wait_ge(S["cent"][a], i)
                    pe.matmul(ps[:, a, :], cst("mean"), X[:, bass.ds((n + a) * T, T)],
                              start=True, stop=True).then_inc(S["mean"][a], 1)
                for a in range(L):
                    pe.wait_ge(S["sq"][a], i + 1)
                    pe.wait_ge(S["std"][a], i)
                    pe.matmul(ps[:, L + a, :], cst("mean"), sq[:, a, :],
                              start=True, stop=True).then_inc(S["var"][a], 1)

        @block.vector
        def _(v):
            with v.Fori(0, B // L) as i:
                n = i * L
                for a in range(L):
                    v.wait_ge(S["mean"][a], i + 1)
                    v.wait_ge(S["xn"][a], i)
                    v.tensor_tensor(xc[:, a, :], X[:, bass.ds((n + a) * T, T)], ps[:, a, :],
                                    ALU.subtract).then_inc(S["cent"][a], 1)
                for a in range(L):
                    v.wait_ge(S["rstd"][a], i + 1)
                    if gain is None:
                        v.tensor_tensor(XN[:, bass.ds((n + a) * T, T)], xc[:, a, :], sq[:, a, :],
                                        ALU.mult).then_inc(S["xn"][a], 1)
                        continue
                    v.scalar_tensor_tensor(out=xc[:, a, :], in0=xc[:, a, :], scalar=gain, in1=sq[:, a, :],
                                           op0=ALU.mult, op1=ALU.mult).then_inc(S["gained"][a], 1)
                    v.wait_ge(S["gained"][a], i + 1)
                    v.tensor_scalar(XN[:, bass.ds((n + a) * T, T)], xc[:, a, :], shift, None,
                                    ALU.add).then_inc(S["xn"][a], 1)

        @block.scalar
        def _(act):
            with act.Fori(0, B // L) as i:
                n = i * L
                for a in range(L):
                    act.wait_ge(S["cent"][a], i + 1)
                    act.wait_ge(S["xn"][a], i)
                    act.activation(sq[:, a, :], xc[:, a, :], ACT.Square).then_inc(S["sq"][a], 1)
                for a in range(L):
                    act.wait_ge(S["var"][a], i + 1)
                    act.activation(sq[:, a, :], ps[:, L + a, :], ACT.Ln,
                                   bias=cst("eps")).then_inc(S["std"][a], 1)
                for a in range(L):
                    act.wait_ge(S["std"][a], i + 1)
                    act.activation(sq[:, a, :], sq[:, a, :], ACT.Exp, scale=-0.5).then_inc(S["rstd"][a], 1)


def rwkv_pre_phase(nc, K):
    XN, cst, W, Qd = K["XN"], K["cst"], K["w0"], K["Qd"]
    KK, EW, BB, KV, VV, RR, BON, GG = range(8)
    with ExitStack() as ctx:
        S = sems(nc, ctx, "rp", "diff xxx mixps mix delta xf lowps lowr low hips hev kksq z "
                 "lateps a ma mk nrm az ez lz w ew wm km f1 f2 k2 kn rn kkn b vps v k3 rk bonps q stored", LANES)
        ps = ctx.enter_context(nc.psum_tensor("rp_ps", [128, LANES, 4, T], F32))
        sb = lambda name, n: ctx.enter_context(nc.sbuf_tensor("rp_" + name, [128, LANES, n, T], F32))
        xp = ctx.enter_context(nc.sbuf_tensor("rp_xp", [128, LANES, T], F32))
        xf = sb("xf", 4)
        t = sb("t", 6)
        q = sb("q", 8)
        P = sems(nc, ctx, "rpp", "best at taken kept")
        block = ctx.enter_context(nc.Block())
        IT = B // LANES

        ROUNDS = CAP // 8 // IT

        def row(i, a):
            return bass.ds((i * LANES + a) * T, T)

        @block.vector
        def _(v):
            with v.Fori(0, IT) as i:
                for a in range(LANES):
                    x = XN[:, row(i, a)]
                    v.wait_ge(S["rk"][a], i)
                    v.wait_ge(S["xf"][a], i)
                    v.tensor_tensor(xp[:, a, 1:T], XN[:, bass.ds((i * LANES + a) * T, T - 1)],
                                    XN[:, bass.ds((i * LANES + a) * T + 1, T - 1)], ALU.subtract)
                    v.tensor_scalar(xp[:, a, 0:1], XN[:, bass.ds((i * LANES + a) * T, 1)], -1.0, None,
                                    ALU.mult).then_inc(S["diff"][a], 1)
                    v.wait_ge(S["diff"][a], i + 1)
                    v.wait_ge(S["mixps"][a], i)
                    v.wait_ge(S["stored"][a], 16 * i)
                    v.scalar_tensor_tensor(out=t[:, a, 0, :], in0=xp[:, a, :], scalar=W("maa_x"), in1=x,
                                           op0=ALU.mult, op1=ALU.add).then_inc(S["xxx"][a], 1)
                best_eight(v, K, P, i * ROUNDS)
                for a in range(LANES):
                    x = XN[:, row(i, a)]
                    v.wait_ge(S["delta"][a], i + 1)
                    for f in range(4):
                        last = v.scalar_tensor_tensor(out=t[:, a, 1 + f, :], in0=ps[:, a, f, :],
                                                      scalar=W("maa")[:, f:f + 1], in1=xp[:, a, :],
                                                      op0=ALU.add, op1=ALU.mult)
                    last.then_inc(S["f1"][a], 1)
                    v.wait_ge(S["f1"][a], 2 * i + 1)
                    for f in range(4):
                        last = v.tensor_tensor(xf[:, a, f, :], t[:, a, 1 + f, :], x, ALU.add)
                    last.then_inc(S["xf"][a], 1)
                for a in range(LANES):
                    v.wait_ge(S["lowps"][a], i + 1)
                    v.tensor_copy(q[:, a, RR, :], ps[:, a, 0, :]).then_inc(S["lowr"][a], 1)
                best_eight(v, K, P, i * ROUNDS + 1)
                for a in range(LANES):
                    v.wait_ge(S["hips"][a], i + 1)
                    v.tensor_copy(q[:, a, GG, :], ps[:, a, 0, :])
                    v.tensor_copy(q[:, a, KV, :], ps[:, a, 1, :])
                    v.tensor_scalar(t[:, a, 0, :], ps[:, a, 3, :], W("decay"), None,
                                    ALU.add).then_inc(S["z"][a], 1)
                    v.tensor_copy(q[:, a, KK, :], ps[:, a, 2, :]).then_inc(S["hev"][a], 1)
                for r in range(2, ROUNDS):
                    best_eight(v, K, P, i * ROUNDS + r)
                for a in range(LANES):
                    v.wait_ge(S["lz"][a], i + 1)
                    v.scalar_tensor_tensor(out=t[:, a, 0, :], in0=t[:, a, 0, :], scalar=0.0, in1=t[:, a, 1, :],
                                           op0=ALU.min, op1=ALU.subtract).then_inc(S["w"][a], 1)
                    v.wait_ge(S["mk"][a], i + 1)
                    v.wait_ge(S["w"][a], i + 1)
                    v.scalar_tensor_tensor(out=t[:, a, 2, :], in0=t[:, a, 0, :], scalar=-0.5, in1=t[:, a, 5, :],
                                           op0=ALU.add, op1=ALU.mult).then_inc(S["wm"][a], 1)
                    v.scalar_tensor_tensor(out=t[:, a, 1, :], in0=t[:, a, 4, :], scalar=-1.0, in1=t[:, a, 3, :],
                                           op0=ALU.add, op1=ALU.mult).then_inc(S["f1"][a], 1)
                    v.wait_ge(S["f1"][a], 2 * i + 2)
                    v.tensor_tensor(t[:, a, 1, :], t[:, a, 4, :], t[:, a, 1, :],
                                    ALU.subtract).then_inc(S["f2"][a], 1)
                    v.wait_ge(S["f2"][a], i + 1)
                    v.tensor_tensor(q[:, a, KV, :], q[:, a, KV, :], t[:, a, 1, :],
                                    ALU.mult).then_inc(S["k2"][a], 1)
                    v.wait_ge(S["km"][a], i + 1)
                    v.wait_ge(S["k2"][a], i + 1)
                    v.tensor_tensor(q[:, a, KV, :], q[:, a, KV, :], t[:, a, 2, :],
                                    ALU.mult).then_inc(S["k3"][a], 1)
                    v.wait_ge(S["k3"][a], i + 1)
                    v.scalar_tensor_tensor(out=t[:, a, 1, :], in0=q[:, a, RR, :], scalar=W("faaaa"),
                                           in1=q[:, a, KV, :], op0=ALU.mult, op1=ALU.mult).then_inc(S["rk"][a], 1)
                    v.wait_ge(S["nrm"][a], i + 1)
                    v.reciprocal(t[:, a, 2, :], xf[:, a, 1, :]).then_inc(S["rn"][a], 1)
                    v.wait_ge(S["rn"][a], i + 1)
                    v.tensor_tensor(q[:, a, KK, :], q[:, a, KK, :], t[:, a, 2, :],
                                    ALU.mult).then_inc(S["kkn"][a], 1)
                    v.wait_ge(S["kkn"][a], i + 1)
                    v.scalar_tensor_tensor(out=q[:, a, BB, :], in0=q[:, a, KK, :], scalar=-1.0, in1=t[:, a, 3, :],
                                           op0=ALU.mult, op1=ALU.mult)
                    v.wait_ge(S["vps"][a], i + 1)
                    v.tensor_copy(q[:, a, VV, :], ps[:, a, 0, :]).then_inc(S["v"][a], 1)
                    v.wait_ge(S["v"][a], i + 1)
                    v.wait_ge(S["bonps"][a], i + 1)
                    v.tensor_tensor(q[:, a, BON, :], ps[:, a, 1, :], q[:, a, VV, :],
                                    ALU.mult).then_inc(S["q"][a], 1)

        @block.tensor
        def _(pe):
            with pe.Fori(0, IT) as i:
                for a in range(LANES):
                    pe.wait_ge(S["xxx"][a], i + 1)
                    pe.wait_ge(S["q"][a], i)
                    pe.matmul(ps[:, a, 0, :], W("maa_w1"), t[:, a, 0, :],
                              start=True, stop=True).then_inc(S["mixps"][a], 1)
                for a in range(LANES):
                    pe.wait_ge(S["mix"][a], i + 1)
                    for f in range(4):
                        r = slice(32 * f, 32 * f + 32)
                        last = pe.matmul(ps[:, a, f, :], W("maa_w2")[r, :], xf[r, a, 0, :], start=True, stop=True)
                    last.then_inc(S["delta"][a], 1)
                for a in range(LANES):
                    pe.wait_ge(S["xf"][a], i + 1)
                    pe.matmul(ps[:, a, 0, :], W("receptance"), xf[:, a, 0, :], start=True, stop=True)
                    pe.matmul(ps[:, a, 1, :], W("gate_w1"), xf[:, a, 0, :], start=True, stop=True)
                    pe.matmul(ps[0:64, a, 2, :], W("kkk_mk_w1"), xf[:, a, 2, :], start=True, stop=True)
                    pe.matmul(ps[:, a, 3, :], W("decay_aaa_ma_w1"), xf[:, a, 1, :],
                              start=True, stop=True).then_inc(S["lowps"][a], 1)
                for a in range(LANES):
                    pe.wait_ge(S["low"][a], i + 1)
                    pe.wait_ge(S["lowr"][a], i + 1)
                    pe.matmul(ps[:, a, 0, :], W("gate_w2"), t[:, a, 1, :], start=True, stop=True)
                    pe.matmul(ps[:, a, 1, :], W("key_w"), xf[:, a, 2, :], start=True, stop=True)
                    pe.matmul(ps[:, a, 2, :], W("key_w"), xf[:, a, 2, :], start=True, stop=False)
                    pe.matmul(ps[:, a, 2, :], W("kkk_w2"), t[0:32, a, 2, :], start=False, stop=True)
                    pe.matmul(ps[:, a, 3, :], W("decay_w2"), t[0:64, a, 3, :],
                              start=True, stop=True).then_inc(S["hips"][a], 1)
                for a in range(LANES):
                    pe.wait_ge(S["hev"][a], i + 1)
                    pe.wait_ge(S["kksq"][a], i + 1)
                    pe.matmul(ps[:, a, 0, :], W("aaa_w2")[64:96, :], t[64:96, a, 3, :], start=True, stop=True)
                    pe.matmul(ps[:, a, 1, :], W("ma_w2")[96:128, :], t[96:128, a, 3, :], start=True, stop=True)
                    pe.matmul(ps[:, a, 3, :], W("mk_w2")[32:64, :], t[32:64, a, 2, :], start=True, stop=True)
                    pe.matmul(ps[:, a, 2, :], cst("headsum"), xf[:, a, 0, :],
                              start=True, stop=True).then_inc(S["lateps"][a], 1)
                for a in range(LANES):
                    pe.wait_ge(S["a"][a], i + 1)
                    pe.matmul(ps[:, a, 0, :], W("value"), xf[:, a, 3, :],
                              start=True, stop=True).then_inc(S["vps"][a], 1)
                    pe.wait_ge(S["rk"][a], i + 1)
                    pe.matmul(ps[:, a, 1, :], cst("headsum"), t[:, a, 1, :],
                              start=True, stop=True).then_inc(S["bonps"][a], 1)

        @block.scalar
        def _(act):
            with act.Fori(0, IT) as i:
                for a in range(LANES):
                    act.wait_ge(S["mixps"][a], i + 1)
                    act.wait_ge(S["vps"][a], i)
                    act.activation(xf[:, a, 0, :], ps[:, a, 0, :], ACT.Tanh).then_inc(S["mix"][a], 1)
                for a in range(LANES):
                    act.wait_ge(S["lowps"][a], i + 1)
                    act.activation(t[:, a, 1, :], ps[:, a, 1, :], ACT.Tanh)
                    act.activation(t[0:32, a, 2, :], ps[0:32, a, 2, :], ACT.Tanh)
                    act.activation(t[32:64, a, 2, :], ps[32:64, a, 2, :], ACT.Copy)
                    act.activation(t[0:64, a, 3, :], ps[0:64, a, 3, :], ACT.Tanh)
                    act.activation(t[64:128, a, 3, :], ps[64:128, a, 3, :], ACT.Copy).then_inc(S["low"][a], 1)
                for a in range(LANES):
                    act.wait_ge(S["hev"][a], i + 1)
                    act.activation(xf[:, a, 0, :], q[:, a, KK, :], ACT.Square).then_inc(S["kksq"][a], 1)
                for a in range(LANES):
                    act.wait_ge(S["lateps"][a], i + 1)
                    act.activation(t[:, a, 3, :], ps[:, a, 0, :], ACT.Sigmoid, bias=W("aaaaa")).then_inc(S["a"][a], 1)
                    act.activation(t[:, a, 4, :], ps[:, a, 1, :], ACT.Sigmoid, bias=W("misc_a"))
                    act.activation(t[:, a, 5, :], ps[:, a, 3, :], ACT.Sigmoid, bias=W("misc_k")).then_inc(S["mk"][a], 1)
                for a in range(LANES):
                    act.activation(xf[:, a, 1, :], ps[:, a, 2, :], ACT.Sqrt, bias=cst("tiny")).then_inc(S["nrm"][a], 1)
                for a in range(LANES):
                    act.wait_ge(S["z"][a], i + 1)
                    act.activation(t[:, a, 1, :], t[:, a, 0, :], ACT.Abs).then_inc(S["az"][a], 1)
                    act.wait_ge(S["az"][a], i + 1)
                    act.activation(t[:, a, 1, :], t[:, a, 1, :], ACT.Exp, scale=-1.0).then_inc(S["ez"][a], 1)
                    act.wait_ge(S["ez"][a], i + 1)
                    act.activation(t[:, a, 1, :], t[:, a, 1, :], ACT.Ln, bias=1.0).then_inc(S["lz"][a], 1)
                for a in range(LANES):
                    act.wait_ge(S["w"][a], i + 1)
                    act.activation(q[:, a, EW, :], t[:, a, 0, :], ACT.Exp, bias=cst("mhalf")).then_inc(S["ew"][a], 1)
                    act.wait_ge(S["wm"][a], i + 1)
                    act.activation(t[:, a, 2, :], t[:, a, 2, :], ACT.Exp).then_inc(S["km"][a], 1)

        @block.sync
        def _(sp):
            with sp.Fori(0, IT) as i:
                for a in range(LANES):
                    sp.wait_ge(S["q"][a], i + 1)
                    sp.wait_ge(S["ew"][a], i + 1)
                    sp.dma_start(Qd[:, i * LANES + a].rearrange("q c t -> c q t"), q[:, a]).then_inc(S["stored"][a], 16)
            for a in range(LANES):
                sp.wait_ge(S["stored"][a], 16 * IT)


def scan_and_experts_phase(nc, K):
    cst, Xt, Acc, IDX, WGT = K["cst"], K["Xt"], K["Acc"], K["IDX"], K["WGT"]
    w1d, w2d, b1d, b2d = K["A"]["e_w1"], K["A"]["e_w2"], K["A"]["e_b1"], K["A"]["e_b2"]
    Qd, Yd = K["Qd"], K["Yd"]
    H, N = 16, 8
    Qh = Qd.rearrange("q b (h n) t -> q (b h) n t", n=N)
    CH = 32
    IT = T // CH // LANES
    KK, EW, BB, KV, VV, RR = range(6)
    EL = E // IT
    EG = EL // LANES
    M = N // 2
    HALVES = (slice(0, M), slice(M, N))
    with ExitStack() as ctx:
        S = sems(nc, ctx, "rs", "loaded vk steps yprod y stored", LANES)
        zeroed = sems(nc, ctx, "rs", "zeroed")["zeroed"]
        F = [sems(nc, ctx, f"rsf{n}", "folded", LANES)["folded"] for n in range(2)]
        chain = sems(nc, ctx, "rsc", "chain", 2)["chain"]
        land = ctx.enter_context(nc.sbuf_tensor("rs_land", [128, LANES, 6, N, CH], F32))
        vk = ctx.enter_context(nc.sbuf_tensor("rs_vk", [128, LANES, CH, N, N], F32))
        hist = ctx.enter_context(nc.sbuf_tensor("rs_hist", [128, LANES, CH, N, N], F32))
        yp = ctx.enter_context(nc.sbuf_tensor("rs_yp", [128, CH, N, N], F32))
        y = ctx.enter_context(nc.sbuf_tensor("rs_y", [128, LANES, N, CH], F32))
        prod = ctx.enter_context(nc.sbuf_tensor("rs_prod", [128, 2, 2, M, N], F32))
        sab = ctx.enter_context(nc.sbuf_tensor("rs_sab", [128, N], F32))
        outer = ctx.enter_context(nc.sbuf_tensor("rs_outer", [128, N, N], F32))
        X = sems(nc, ctx, "ex", "w xg idx fetched tps xgt hps h yps y added", EL)
        biases = sems(nc, ctx, "exb", "biases")["biases"]
        tps = ctx.enter_context(nc.psum_tensor("ex_tps", [128, 2, T], F32))
        hps = ctx.enter_context(nc.psum_tensor("ex_hps", [128, EG, S4, CAP], F32))
        yps = ctx.enter_context(nc.psum_tensor("ex_yps", [128, 2, 512], F32))
        w1 = ctx.enter_context(nc.sbuf_tensor("ex_w1", [128, EL, S4, 128], F32))
        w2 = ctx.enter_context(nc.sbuf_tensor("ex_w2", [128, EL, S4, 32], F32))
        b1 = ctx.enter_context(nc.sbuf_tensor("ex_b1", [128, E * S4], F32))
        b2 = ctx.enter_context(nc.sbuf_tensor("ex_b2", [1, EL, C], F32))
        idx = ctx.enter_context(nc.sbuf_tensor("ex_idx", [CAP, EL], U32))
        xg = ctx.enter_context(nc.sbuf_tensor("ex_xg", [CAP, EL, C], F32))
        xgt = ctx.enter_context(nc.sbuf_tensor("ex_xgt", [128, EL, CAP], F32))
        h = ctx.enter_context(nc.sbuf_tensor("ex_h", [128, EG, S4, CAP], F32))
        ye = ctx.enter_context(nc.sbuf_tensor("ex_y", [CAP, EL, C], F32))
        block = ctx.enter_context(nc.Block())

        def load(sp, i, a):
            for q in range(6):
                sp.dma_start(land[:, a, q], Qh[q, :, :, bass.ds((i * LANES + a) * CH, CH)]).then_inc(S["loaded"][a], 16)

        @block.sync
        def _(sp):
            sp.dma_start(b1[:], b1d).then_inc(biases, 16)
            with sp.Fori(0, IT) as i:
                for a in range(LANES):
                    sp.wait_ge(S["steps"][a], i)
                    sp.wait_ge(S["yprod"][a], i)
                    load(sp, i, a)
                    for e in range(a * EG, (a + 1) * EG):
                        sp.wait_ge(X["yps"][e], i)
                        sp.dma_start(w1[:, e], w1d[i * EL + e].rearrange("s d m -> d s m")).then_inc(X["w"][e], 16)
                        sp.dma_start(w2[:, e], w2d[i * EL + e].rearrange("s m k -> m s k")).then_inc(X["w"][e], 16)
                        sp.dma_start(b2[:, e], b2d[0:1, bass.ds((i * EL + e) * C, C)]).then_inc(X["w"][e], 16)

        @block.gpsimd
        def _(g):
            def pairs(i, a):
                g.wait_ge(S["loaded"][a], 96 * (i + 1))
                g.wait_ge(S["steps"][a], i)
                kt = land[:, a, KV].rearrange("p n t -> p t n")
                vt = land[:, a, VV].rearrange("p n t -> p t n")
                for n in range(N):
                    last = g.tensor_tensor(vk[:, a, :, n, :], kt, vt[:, :, n:n + 1].to_broadcast([128, CH, N]),
                                           ALU.mult)
                last.then_inc(S["vk"][a], 1)

            def outputs(i, a):
                g.wait_ge(S["steps"][a], i + 1)
                g.wait_ge(S["stored"][a], 16 * i)
                g.wait_ge(S["y"][1 - a], i + a)
                rt = land[:, a, RR].rearrange("p n t -> p t n")
                for n in range(N):
                    last = g.tensor_tensor(yp[:, :, n, :], hist[:, a, :, n, :], rt, ALU.mult)
                last.then_inc(S["yprod"][a], 1)
                g.wait_ge(S["yprod"][a], i + 1)
                yt = y[:, a].rearrange("p n t -> p t n")
                for half, step in ((4, 0), (2, 1), (1, 2)):
                    out = yt if half == 1 else yp[:, :, :, 0:half]
                    if step:
                        g.wait_ge(F[step - 1][a], i + 1)
                    if half == 1:
                        out = yt.unsqueeze(3)
                    g.tensor_tensor(out, yp[:, :, :, 0:half], yp[:, :, :, half:2 * half],
                                    ALU.add).then_inc(S["y"][a] if half == 1 else F[step][a], 1)

            def fetch(i, a):
                for e in range(a * EG, (a + 1) * EG):
                    g.wait_ge(X["added"][e], 16 * i)
                    g.nop(nofuse=True)
                    g.tensor_copy(idx[:, e:e + 1], IDX[:, bass.ds(i * EL + e, 1)]).then_inc(X["idx"][e], 1)
                for e in range(a * EG, (a + 1) * EG):
                    g.wait_ge(X["tps"][e], i)
                    g.wait_ge(X["idx"][e], i + 1)
                    g.nop(nofuse=True)
                    g.indirect_dma_start(xg[:, e, :], None, Xt,
                                         bass.IndirectOffsetOnAxis(ap=idx[:, e:e + 1], axis=0)
                                         ).then_inc(X["fetched"][e], 16)

            def add(i, e):
                g.wait_ge(X["y"][e], i + 1)
                if e:
                    g.wait_ge(X["added"][e - 1], 16 * (i + 1))
                else:
                    g.wait_ge(X["added"][EL - 1], 16 * i)
                g.nop(nofuse=True)
                g.indirect_dma_start(Acc, bass.IndirectOffsetOnAxis(ap=idx[:, e:e + 1], axis=0),
                                     ye[:, e, :], None, compute_op=ALU.add).then_inc(X["added"][e], 16)

            def chunk(i, a, last):
                if not last:
                    pairs(i + a, 1 - a)
                add(i, a * EG)
                outputs(i, a)
                add(i, a * EG + 1)
                if not last:
                    fetch(i + a, 1 - a)
                add(i, a * EG + 2)

            fetch(0, 0)
            pairs(0, 0)
            with g.Fori(0, IT - 1) as i:
                chunk(i, 0, False)
                chunk(i, 1, False)
            chunk(IT - 1, 0, False)
            chunk(IT - 1, 1, True)
            g.wait_ge(X["added"][EL - 1], 16 * IT)

        @block.tensor
        def _(pe):
            with pe.Fori(0, IT) as i:
                for a in range(LANES):
                    group = range(a * EG, (a + 1) * EG)
                    for e in group:
                        pe.wait_ge(X["fetched"][e], 16 * (i + 1))
                        if e >= 2:
                            pe.wait_ge(X["xgt"][e - 2], i + 1)
                        else:
                            pe.wait_ge(X["xgt"][e + EL - 2], i)
                        pe.transpose(tps[:, e % 2, 0:CAP], xg[:, e, :], cst("ident")).then_inc(X["tps"][e], 1)
                        pe.wait_ge(X["xgt"][e], i + 1)
                        pe.wait_ge(X["w"][e], 48 * (i + 1))
                        if e >= EG:
                            pe.wait_ge(X["h"][e - EG], i + 1)
                        else:
                            pe.wait_ge(X["h"][e + EG], i)
                        for s in range(S4):
                            last = pe.matmul(hps[:, e % EG, s, :], w1[:, e, s, :], xgt[:, e, :], start=True, stop=True)
                        last.then_inc(X["hps"][e], 1)
                    for e in group:
                        pe.wait_ge(X["h"][e], i + 1)
                        if e >= 2:
                            pe.wait_ge(X["y"][e - 2], i + 1)
                        else:
                            pe.wait_ge(X["y"][e + EL - 2], i)
                        out = yps[:, e % 2, 0:C]
                        pe.matmul(out, cst("ones")[0:1, :], b2[0:1, e, :], start=True, stop=False,
                                  skip_group_check=True)
                        for s in range(S4):
                            last = pe.matmul(out[:, 32 * s:32 * s + 32], h[:, e % EG, s, :], w2[:, e, s, :],
                                             start=False, stop=(s == S4 - 1), skip_group_check=True)
                        last.then_inc(X["yps"][e], 1)

        @block.vector
        def _(v):
            v.memset(hist[:, LANES - 1, CH - 1], 0.0).then_inc(zeroed, 1)
            v.wait_ge(zeroed, 1)
            with v.Fori(0, IT) as i:
                for a in range(LANES):
                    v.wait_ge(S["vk"][a], i + 1)
                    v.wait_ge(S["loaded"][a], 96 * (i + 1))
                    v.wait_ge(S["yprod"][a], i)
                    for t in range(CH):
                        prev = hist[:, a, t - 1] if t else hist[:, (a - 1) % LANES, CH - 1]
                        new = hist[:, a, t]
                        for c, r in enumerate(HALVES):
                            if t:
                                v.wait_ge(chain[c], 4 * t)
                            v.tensor_tensor(prod[:, c], prev[:, r].unsqueeze(1).to_broadcast([128, 2, M, N]),
                                            land[:, a, 0:2, :, t].unsqueeze(2).to_broadcast([128, 2, M, N]),
                                            ALU.mult).then_inc(chain[c], 1)
                        for c, r in enumerate(HALVES):
                            v.wait_ge(chain[c], 4 * t + 1)
                            v.tensor_reduce(sab[:, r], prod[:, c, 0], AX.X, ALU.add).then_inc(chain[c], 1)
                        v.tensor_tensor(new.rearrange("p (c v) k -> p c v k", c=2), prod[:, :, 1],
                                        vk[:, a, t].rearrange("p (c v) k -> p c v k", c=2), ALU.add)
                        for c, r in enumerate(HALVES):
                            v.wait_ge(chain[c], 4 * t + 2)
                            v.tensor_tensor(outer[:, r], sab[:, r].unsqueeze(2).to_broadcast([128, M, N]),
                                            land[:, a, BB, :, t].unsqueeze(1).to_broadcast([128, M, N]),
                                            ALU.mult).then_inc(chain[c], 1)
                        for c, r in enumerate(HALVES):
                            v.wait_ge(chain[c], 4 * t + 3)
                            v.tensor_tensor(new[:, r], new[:, r], outer[:, r], ALU.add).then_inc(chain[c], 1)
                    for c in range(2):
                        v.wait_ge(chain[c], 4 * CH)
                        v.sem_clear(chain[c])
                    v.nop().then_inc(S["steps"][a], 1)

        @block.scalar
        def _(act):
            act.wait_ge(biases, 16)
            with act.Fori(0, IT) as i:
                for a in range(LANES):
                    group = range(a * EG, (a + 1) * EG)
                    for e in group:
                        act.wait_ge(X["tps"][e], i + 1)
                        act.wait_ge(X["hps"][e], i)
                        act.activation(xgt[:, e, :], tps[:, e % 2, 0:CAP], ACT.Copy).then_inc(X["xgt"][e], 1)
                    for e in group:
                        act.wait_ge(X["hps"][e], i + 1)
                        if e >= EG:
                            act.wait_ge(X["yps"][e - EG], i + 1)
                        else:
                            act.wait_ge(X["yps"][e + EG], i)
                        for s in range(S4):
                            last = act.activation(h[:, e % EG, s, :], hps[:, e % EG, s, :], ACT.Gelu,
                                                  bias=b1[:, bass.ds((i * EL + e) * S4 + s, 1)])
                        last.then_inc(X["h"][e], 1)
                    for e in group:
                        act.wait_ge(X["yps"][e], i + 1)
                        act.wait_ge(X["added"][e], 16 * i)
                        act.activation(ye[:, e, :], yps[:, e % 2, 0:C], ACT.Copy,
                                       scale=WGT[:, bass.ds(i * EL + e, 1)]).then_inc(X["y"][e], 1)
                    act.wait_ge(S["y"][a], i + 1)
                    act.dma_start(Yd[:, :, bass.ds((i * LANES + a) * CH, CH)], y[:, a]).then_inc(S["stored"][a], 16)
            for a in range(LANES):
                act.wait_ge(S["stored"][a], 16 * IT)


def rwkv_out_phase(nc, K):
    SX, cst, W, Qd, Yd = K["SX"], K["cst"], K["w0"], K["Qd"], K["Yd"]
    Yv = Yd.rearrange("(b h) v t -> b (h v) t", b=B)
    IT = B // LANES
    with ExitStack() as ctx:
        S = sems(nc, ctx, "ro", "loaded mean cent sq var std rstd yn ynb yb o sps s", LANES)
        ps = ctx.enter_context(nc.psum_tensor("ro_ps", [128, LANES, 3, T], F32))
        y = ctx.enter_context(nc.sbuf_tensor("ro_y", [128, LANES, 3, T], F32))
        sq = ctx.enter_context(nc.sbuf_tensor("ro_sq", [128, LANES, T], F32))
        block = ctx.enter_context(nc.Block())

        @block.sync
        def _(sp):
            with sp.Fori(0, IT) as i:
                for a in range(LANES):
                    sp.wait_ge(S["sps"][a], i)
                    sp.dma_start(y[:, a, 0, :], Yv[i * LANES + a]).then_inc(S["loaded"][a], 16)
                    sp.dma_start(y[:, a, 1:3, :], Qd[6:8, i * LANES + a].rearrange("q c t -> c q t")).then_inc(S["loaded"][a], 16)

        @block.tensor
        def _(pe):
            with pe.Fori(0, IT) as i:
                for a in range(LANES):
                    pe.wait_ge(S["loaded"][a], 32 * (i + 1))
                    pe.wait_ge(S["cent"][a], i)
                    pe.matmul(ps[:, a, 0, :], cst("headmean"), y[:, a, 0, :],
                              start=True, stop=True).then_inc(S["mean"][a], 1)
                for a in range(LANES):
                    pe.wait_ge(S["sq"][a], i + 1)
                    pe.wait_ge(S["std"][a], i)
                    pe.matmul(ps[:, a, 1, :], cst("headmean"), sq[:, a, :],
                              start=True, stop=True).then_inc(S["var"][a], 1)
                for a in range(LANES):
                    pe.wait_ge(S["o"][a], i + 1)
                    pe.wait_ge(S["s"][a], i)
                    pe.matmul(ps[:, a, 2, :], W("output"), y[:, a, 0, :],
                              start=True, stop=True).then_inc(S["sps"][a], 1)

        @block.scalar
        def _(act):
            with act.Fori(0, IT) as i:
                for a in range(LANES):
                    act.wait_ge(S["cent"][a], i + 1)
                    act.wait_ge(S["yn"][a], i)
                    act.activation(sq[:, a, :], y[:, a, 0, :], ACT.Square).then_inc(S["sq"][a], 1)
                for a in range(LANES):
                    act.wait_ge(S["var"][a], i + 1)
                    act.activation(sq[:, a, :], ps[:, a, 1, :], ACT.Sqrt, bias=cst("gn_eps")).then_inc(S["std"][a], 1)
                for a in range(LANES):
                    act.wait_ge(S["sps"][a], i + 1)
                    act.activation(SX[:, bass.ds((i * LANES + a) * T, T)], ps[:, a, 2, :], ACT.Copy).then_inc(S["s"][a], 1)

        @block.vector
        def _(v):
            with v.Fori(0, IT) as i:
                for a in range(LANES):
                    v.wait_ge(S["mean"][a], i + 1)
                    v.tensor_tensor(y[:, a, 0, :], y[:, a, 0, :], ps[:, a, 0, :], ALU.subtract).then_inc(S["cent"][a], 1)
                for a in range(LANES):
                    v.wait_ge(S["std"][a], i + 1)
                    v.reciprocal(sq[:, a, :], sq[:, a, :]).then_inc(S["rstd"][a], 1)
                    v.wait_ge(S["rstd"][a], i + 1)
                    v.tensor_tensor(y[:, a, 0, :], y[:, a, 0, :], sq[:, a, :], ALU.mult).then_inc(S["yn"][a], 1)
                    v.wait_ge(S["yn"][a], i + 1)
                    v.tensor_scalar(y[:, a, 0, :], y[:, a, 0, :], W("ln_w"), W("ln_b"), ALU.mult, ALU.add).then_inc(S["ynb"][a], 1)
                    v.wait_ge(S["ynb"][a], i + 1)
                    v.tensor_tensor(y[:, a, 0, :], y[:, a, 0, :], y[:, a, 1, :], ALU.add).then_inc(S["yb"][a], 1)
                    v.wait_ge(S["yb"][a], i + 1)
                    v.tensor_tensor(y[:, a, 0, :], y[:, a, 0, :], y[:, a, 2, :], ALU.mult).then_inc(S["o"][a], 1)


def route_phase(nc, K):
    XN, cst, W, Xt, Acc, LOG = K["XN"], K["cst"], K["w0"], K["Xt"], K["Acc"], K["LOG"]
    IT = B // 2
    Xv = Xt.rearrange("(b j p) c -> b p j c", p=128, j=NB)
    with ExitStack() as ctx:
        S = sems(nc, ctx, "rt", "xs logps logit tps tok stored", 2)
        P = sems(nc, ctx, "rtp", "zero zeroed blank")
        lps = ctx.enter_context(nc.psum_tensor("rt_lps", [128, 2, T], F32))
        tps = ctx.enter_context(nc.psum_tensor("rt_tps", [128, 2, NB, C], F32))
        xs = ctx.enter_context(nc.sbuf_tensor("rt_xs", [128, 2, T], F32))
        tok = ctx.enter_context(nc.sbuf_tensor("rt_tok", [128, 2, NB, C], F32))
        zero = ctx.enter_context(nc.sbuf_tensor("rt_zero", [128, NT // 128 * C], F32))
        block = ctx.enter_context(nc.Block())
        half = lambda a: slice(64 * a, 64 * a + E)

        @block.tensor
        def _(pe):
            with pe.Fori(0, IT) as i:
                for a in range(2):
                    pe.wait_ge(S["xs"][a], i + 1)
                    pe.wait_ge(S["logit"][a], i)
                    pe.wait_ge(S["tok"][a], i)
                    pe.matmul(lps[half(a), a, :], W("router"), xs[:, a, :],
                              start=True, stop=True).then_inc(S["logps"][a], 1)
                    for j in range(NB):
                        last = pe.transpose(tps[:, a, j, :], xs[:, a, j * 128:(j + 1) * 128], cst("ident"))
                    last.then_inc(S["tps"][a], 1)

        @block.scalar
        def _(act):
            act.wait_ge(P["blank"], 1)
            with act.Fori(0, IT) as i:
                for a in range(2):
                    act.wait_ge(S["tps"][a], i)
                    act.activation(xs[:, a, :], XN[:, bass.ds((a * IT + i) * T, T)],
                                   ACT.Copy).then_inc(S["xs"][a], 1)
                for a in range(2):
                    act.wait_ge(S["logps"][a], i + 1)
                    act.activation(LOG[half(a), bass.ds(i * T, T)], lps[half(a), a, :],
                                   ACT.Copy).then_inc(S["logit"][a], 1)

        @block.vector
        def _(v):
            v.memset(LOG[32:64], 0.0).then_inc(P["blank"], 1)
            v.memset(zero[:], 0.0).then_inc(P["zero"], 1)
            with v.Fori(0, IT) as i:
                for a in range(2):
                    v.wait_ge(S["tps"][a], i + 1)
                    v.wait_ge(S["stored"][a], 16 * i)
                    v.tensor_copy(tok[:, a], tps[:, a]).then_inc(S["tok"][a], 1)

        @block.sync
        def _(sp):
            sp.wait_ge(P["zero"], 1)
            sp.dma_start(Acc.rearrange("(p r) c -> p (r c)", p=128), zero[:]).then_inc(P["zeroed"], 16)
            with sp.Fori(0, IT) as i:
                for a in range(2):
                    sp.wait_ge(S["tok"][a], i + 1)
                    sp.dma_start(Xv[a * IT + i], tok[:, a]).then_inc(S["stored"][a], 16)
            sp.wait_ge(P["zeroed"], 16)
            for a in range(2):
                sp.wait_ge(S["stored"][a], 16 * IT)


def best_eight(v, K, P, r):
    LOG, best, at, top, where = K["LOG"], K["BEST"], K["AT"], K["TOP"], K["WHERE"]
    eight = bass.ds(r * 8, 8)
    v.wait_ge(P["taken"], r)
    v.wait_ge(P["kept"], r)
    v.nop(nofuse=True)
    v.max(top[:], LOG[:]).then_inc(P["best"], 1)
    v.wait_ge(P["best"], r + 1)
    v.nop(nofuse=True)
    v.max_index(where[:], top[:], LOG[:]).then_inc(P["at"], 1)
    v.wait_ge(P["at"], r + 1)
    v.nop(nofuse=True)
    v.match_replace(LOG[:], top[:], LOG[:], -3.0e38).then_inc(P["taken"], 1)
    v.tensor_copy(best[:, eight], top[:])
    v.tensor_copy(at[:, eight], where[:]).then_inc(P["kept"], 1)


def choice_phase(nc, K):
    cst, IDX, WGT, best, at = K["cst"], K["IDX"], K["WGT"], K["BEST"], K["AT"]
    H = K["LOG"].shape[0]
    half = lambda a: slice(64 * a, 64 * a + E)
    with ExitStack() as ctx:
        P = sems(nc, ctx, "ch", "atf turned side flipped at2 val first diff gated rows neg e rsum w cols idx")
        tps = ctx.enter_context(nc.psum_tensor("ch_tps", [128, 2, H], F32))
        fps = ctx.enter_context(nc.psum_tensor("ch_fps", [128, 2, E], F32))
        rps = ctx.enter_context(nc.psum_tensor("ch_rps", [E, CAP], F32))
        wps = ctx.enter_context(nc.psum_tensor("ch_wps", [128, E], F32))
        atf = ctx.enter_context(nc.sbuf_tensor("ch_atf", [H, CAP], F32))
        t = ctx.enter_context(nc.sbuf_tensor("ch_t", [128, 2, H], F32))
        val = ctx.enter_context(nc.sbuf_tensor("ch_val", [128, E], F32))
        first = ctx.enter_context(nc.sbuf_tensor("ch_first", [128, E], F32))
        second = ctx.enter_context(nc.sbuf_tensor("ch_second", [128, E], F32))
        diff = ctx.enter_context(nc.sbuf_tensor("ch_diff", [128, E], F32))
        w = ctx.enter_context(nc.sbuf_tensor("ch_w", [E, CAP], F32))
        small = ctx.enter_context(nc.sbuf_tensor("ch_small", [E, 3], F32))
        block = ctx.enter_context(nc.Block())

        @block.tensor
        def _(pe):
            pe.wait_ge(P["atf"], 1)
            pe.transpose(tps[:, 0, :], best[:], cst("ident")[0:H, 0:H])
            pe.transpose(tps[:, 1, :], atf[:], cst("ident")[0:H, 0:H]).then_inc(P["turned"], 1)
            pe.wait_ge(P["side"], 1)
            for n in range(2):
                last = pe.matmul(fps[:, n, :], cst("flip"), t[:, n, half(1)], start=True, stop=True)
            last.then_inc(P["flipped"], 1)
            pe.wait_ge(P["val"], 1)
            pe.transpose(rps[:], val[:], cst("ident")).then_inc(P["rows"], 1)
            pe.wait_ge(P["w"], 1)
            pe.transpose(wps[:], w[:], cst("ident")[0:E, 0:E]).then_inc(P["cols"], 1)

        @block.scalar
        def _(act):
            act.wait_ge(P["neg"], 1)
            act.activation(w[:], rps[:], ACT.Exp, bias=small[:, 0:1], accum_out=small[:, 1:2]).then_inc(P["e"], 1)

        @block.vector
        def _(v):
            v.tensor_copy(atf[:], at[:]).then_inc(P["atf"], 1)
            v.wait_ge(P["turned"], 1)
            v.tensor_copy(t[:], tps[:]).then_inc(P["side"], 1)
            v.wait_ge(P["flipped"], 1)
            v.tensor_tensor(first[:], t[:, 0, half(0)], fps[:, 0, :], ALU.is_ge).then_inc(P["first"], 1)
            v.tensor_tensor(val[:], t[:, 0, half(0)], fps[:, 0, :], ALU.max).then_inc(P["val"], 1)
            v.tensor_scalar(second[:], fps[:, 1, :], float(NT // 2), None, ALU.add).then_inc(P["at2"], 1)
            v.wait_ge(P["at2"], 1)
            v.tensor_tensor(diff[:], t[:, 1, half(0)], second[:], ALU.subtract).then_inc(P["diff"], 1)
            v.wait_ge(P["first"], 1)
            v.wait_ge(P["diff"], 1)
            v.tensor_tensor(diff[:], diff[:], first[:], ALU.mult).then_inc(P["gated"], 1)
            v.wait_ge(P["gated"], 1)
            v.tensor_tensor(IDX[:], second[:], diff[:], ALU.add).then_inc(P["idx"], 1)
            v.wait_ge(P["rows"], 1)
            v.tensor_reduce(small[:, 0:1], rps[:], AX.X, ALU.max, negate=True).then_inc(P["neg"], 1)
            v.wait_ge(P["e"], 1)
            v.reciprocal(small[:, 2:3], small[:, 1:2]).then_inc(P["rsum"], 1)
            v.wait_ge(P["rsum"], 1)
            v.tensor_scalar(w[:], w[:], small[:, 2:3], None, ALU.mult).then_inc(P["w"], 1)
            v.wait_ge(P["cols"], 1)
            v.tensor_copy(WGT[:], wps[:])


def collect_phase(nc, K):
    GX, cst, Acc = K["GX"], K["cst"], K["Acc"]
    Av = Acc.rearrange("(b j p) c -> b p j c", p=128, j=NB)
    with ExitStack() as ctx:
        S = sems(nc, ctx, "co", "loaded tps g", LANES)
        tps = ctx.enter_context(nc.psum_tensor("co_tps", [128, LANES, T], F32))
        acc = ctx.enter_context(nc.sbuf_tensor("co_acc", [128, LANES, NB, C], F32))
        block = ctx.enter_context(nc.Block())

        @block.sync
        def _(sp):
            with sp.Fori(0, B // LANES) as i:
                for a in range(LANES):
                    sp.wait_ge(S["tps"][a], i)
                    sp.dma_start(acc[:, a], Av[i * LANES + a]).then_inc(S["loaded"][a], 16)

        @block.tensor
        def _(pe):
            with pe.Fori(0, B // LANES) as i:
                for a in range(LANES):
                    pe.wait_ge(S["loaded"][a], 16 * (i + 1))
                    pe.wait_ge(S["g"][a], i)
                    for j in range(NB):
                        last = pe.transpose(tps[:, a, j * 128:(j + 1) * 128], acc[:, a, j, :], cst("ident"))
                    last.then_inc(S["tps"][a], 1)

        @block.scalar
        def _(act):
            with act.Fori(0, B // LANES) as i:
                for a in range(LANES):
                    act.wait_ge(S["tps"][a], i + 1)
                    act.activation(GX[:, bass.ds((i * LANES + a) * T, T)], tps[:, a, :], ACT.Copy).then_inc(S["g"][a], 1)


KEYS_AT = {0: 0, 1: T, 3: T + 384, 2: 2 * T}
SPAN = 2 * T + 256


def choose_phase(nc, K):
    XN, cst, W, Sd, Gd = K["XN"], K["cst"], K["w1"], K["Sd"], K["Gd"]
    IT = B // LANES
    PER = 128 // E1
    with ExitStack() as ctx:
        S = sems(nc, ctx, "ch", "logps score", LANES)
        P = sems(nc, ctx, "chp", "out back thr0 cand count total keep thr gt need eqn off rank ok sel gate stored")
        lps = ctx.enter_context(nc.psum_tensor("ch_lps", [128, LANES, T], F32))
        tot = ctx.enter_context(nc.psum_tensor("ch_tot", [128, 1], F32))
        rows = ctx.enter_context(nc.sbuf_tensor("ch_rows", [E1, NT], F32))
        sc = ctx.enter_context(nc.sbuf_tensor("ch_sc", [128, NT // PER], F32))
        m = ctx.enter_context(nc.sbuf_tensor("ch_m", [128, 3, NT // PER], F32))
        thr = ctx.enter_context(nc.sbuf_tensor("ch_thr", [128, 1], F32))
        cand = ctx.enter_context(nc.sbuf_tensor("ch_cand", [128, 1], F32))
        cnt = ctx.enter_context(nc.sbuf_tensor("ch_cnt", [128, 1], F32))
        keep = ctx.enter_context(nc.sbuf_tensor("ch_keep", [128, 1], U32))
        need = ctx.enter_context(nc.sbuf_tensor("ch_need", [128, 1], F32))
        block = ctx.enter_context(nc.Block())

        @block.tensor
        def _(pe):
            with pe.Fori(0, IT) as i:
                for a in range(LANES):
                    pe.wait_ge(S["score"][a], i)
                    pe.matmul(lps[0:E1, a, :], W("gate"), XN[:, bass.ds((i * LANES + a) * T, T)],
                              start=True, stop=True).then_inc(S["logps"][a], 1)
            for n in range(BITS + 1):
                pe.wait_ge(P["count"], n + 1)
                pe.matmul(tot[:], cst("exsum"), cnt[:], start=True, stop=True).then_inc(P["total"], 1)
            pe.wait_ge(P["eqn"], 1)
            pe.wait_ge(P["need"], 1)
            pe.matmul(tot[:], cst("exbefore"), cnt[:], start=True, stop=True).then_inc(P["off"], 1)

        @block.scalar
        def _(act):
            with act.Fori(0, IT) as i:
                for a in range(LANES):
                    act.wait_ge(S["logps"][a], i + 1)
                    act.activation(rows[:, bass.ds((i * LANES + a) * T, T)], lps[0:E1, a, :],
                                   ACT.Sigmoid).then_inc(S["score"][a], 1)

        @block.sync
        def _(sp):
            for a in range(LANES):
                sp.wait_ge(S["score"][a], IT)
            sp.dma_start(Sd, rows[:]).then_inc(P["out"], 16)
            sp.wait_ge(P["out"], 16)
            sp.dma_start(sc[:], Sd.rearrange("e (p t) -> (e p) t", p=PER)).then_inc(P["back"], 16)
            sp.wait_ge(P["gate"], 1)
            sp.dma_start(Gd.rearrange("e (p t) -> (e p) t", p=PER), m[:, 0, :]).then_inc(P["stored"], 16)
            sp.wait_ge(P["stored"], 16)

        @block.vector
        def _(v):
            v.memset(thr[:], 0.0).then_inc(P["thr0"], 1)
            v.wait_ge(P["thr0"], 1)
            v.wait_ge(P["back"], 16)
            for n in range(BITS):
                bit = 1 << (BITS - 1 - n)
                v.wait_ge(P["thr"], n)
                v.tensor_scalar(cand[:].bitcast(I32), thr[:].bitcast(I32), bit, None,
                                ALU.bitwise_or).then_inc(P["cand"], 1)
                v.wait_ge(P["cand"], n + 1)
                v.tensor_scalar(m[:, 0, :], sc[:], cand[:, 0:1], None, ALU.is_ge, ALU.add,
                                accum_out=cnt[:]).then_inc(P["count"], 1)
                v.wait_ge(P["total"], n + 1)
                v.tensor_scalar(keep[:], tot[:], float(CAP1), None, ALU.is_ge).then_inc(P["keep"], 1)
                v.wait_ge(P["keep"], n + 1)
                v.copy_predicated(thr[:], keep[:], cand[:]).then_inc(P["thr"], 1)
            v.wait_ge(P["thr"], BITS)
            v.tensor_scalar(m[:, 0, :], sc[:], thr[:, 0:1], None, ALU.is_gt, ALU.add,
                            accum_out=cnt[:]).then_inc(P["count"], 1)
            v.wait_ge(P["total"], BITS + 1)
            v.tensor_scalar(need[:], tot[:], -1.0, float(CAP1), ALU.mult, ALU.add).then_inc(P["need"], 1)
            v.tensor_scalar(m[:, 1, :], sc[:], thr[:, 0:1], None, ALU.is_equal, ALU.add,
                            accum_out=cnt[:]).then_inc(P["eqn"], 1)
            v.wait_ge(P["eqn"], 1)
            v.wait_ge(P["off"], 1)
            v.tensor_tensor_scan(m[:, 2, :], cst("onerow")[:, 0:NT // PER], m[:, 1, :], 0.0, ALU.mult,
                                 ALU.add).then_inc(P["rank"], 1)
            v.wait_ge(P["rank"], 1)
            v.tensor_scalar(need[:], need[:], tot[:, 0:1], None, ALU.subtract).then_inc(P["rank"], 1)
            v.wait_ge(P["rank"], 2)
            v.scalar_tensor_tensor(out=m[:, 2, :], in0=m[:, 2, :], scalar=need[:, 0:1], in1=m[:, 1, :],
                                   op0=ALU.is_le, op1=ALU.mult).then_inc(P["ok"], 1)
            v.wait_ge(P["ok"], 1)
            v.tensor_tensor(m[:, 2, :], m[:, 2, :], m[:, 0, :], ALU.add).then_inc(P["sel"], 1)
            v.wait_ge(P["sel"], 1)
            v.tensor_tensor(m[:, 0, :], m[:, 2, :], sc[:], ALU.mult).then_inc(P["gate"], 1)


def ffn1_phase(nc, K):
    XN, GX, W, Gd = K["XN"], K["GX"], K["w1"], K["Gd"]
    F = 4
    with ExitStack() as ctx:
        S = sems(nc, ctx, "f1", "gates used x")
        H = sems(nc, ctx, "f1h", "ps act yps t", E1)
        w1 = ctx.enter_context(nc.sbuf_tensor("f1_w1s", [128, E1, F * 128], F32))
        w2 = ctx.enter_context(nc.sbuf_tensor("f1_w2s", [128, E1, F, C], F32))
        hps = ctx.enter_context(nc.psum_tensor("f1_hps", [128, F, T], F32))
        yps = ctx.enter_context(nc.psum_tensor("f1_yps", [128, 2, T], F32))
        h = ctx.enter_context(nc.sbuf_tensor("f1_h", [128, 2, F, T], F32))
        g = ctx.enter_context(nc.sbuf_tensor("f1_g", [128, E1, T], F32))
        t = ctx.enter_context(nc.sbuf_tensor("f1_t", [128, T], F32))
        HB = [sems(nc, ctx, f"f1b{f}", "ps act", E1) for f in range(F)]
        loaded = sems(nc, ctx, "f1l", "loaded")["loaded"]
        block = ctx.enter_context(nc.Block())

        @block.sync
        def _(sp):
            sp.dma_start(w1[:], K["A"]["f1_w1"].rearrange("e d f -> d e f")).then_inc(loaded, 16)
            sp.dma_start(w2[:], K["A"]["f1_w2"].rearrange("e (f p) c -> p e f c", p=128)).then_inc(loaded, 16)
            with sp.Fori(0, B) as i:
                sp.wait_ge(S["x"], i)
                for e in range(E1):
                    sp.dma_start(g[:, e, :], Gd[e:e + 1, bass.ds(i * T, T)].to_broadcast([128, T])
                                 ).then_inc(S["gates"], 16)

        @block.tensor
        def _(pe):
            pe.wait_ge(loaded, 32)

            def down(i, e):
                if e >= 2:
                    pe.wait_ge(H["t"][e - 2], i + 1)
                else:
                    pe.wait_ge(H["t"][e + E1 - 2], i)
                for f in range(F):
                    pe.wait_ge(HB[f]["act"][e], i + 1)
                    last = pe.matmul(yps[:, e % 2, :], w2[:, e, f, :], h[:, e % 2, f, :],
                                     start=(f == 0), stop=(f == F - 1))
                last.then_inc(H["yps"][e], 1)

            with pe.Fori(0, B) as i:
                for e in range(E1):
                    for f in range(F):
                        if e:
                            pe.wait_ge(HB[f]["act"][e - 1], i + 1)
                        else:
                            pe.wait_ge(HB[f]["act"][E1 - 1], i)
                        pe.matmul(hps[:, f, :], w1[:, e, f * 128:(f + 1) * 128], XN[:, bass.ds(i * T, T)],
                                  start=True, stop=True).then_inc(HB[f]["ps"][e], 1)
                    if e:
                        down(i, e - 1)
                down(i, E1 - 1)

        @block.scalar
        def _(act):
            with act.Fori(0, B) as i:
                for e in range(E1):
                    if e >= 2:
                        act.wait_ge(H["yps"][e - 2], i + 1)
                    else:
                        act.wait_ge(H["yps"][e + E1 - 2], i)
                    for f in range(F):
                        act.wait_ge(HB[f]["ps"][e], i + 1)
                        act.activation(h[:, e % 2, f, :], hps[:, f, :], ACT.Gelu,
                                       bias=W("ffb1")[:, e * F + f:e * F + f + 1]).then_inc(HB[f]["act"][e], 1)

        @block.vector
        def _(v):
            with v.Fori(0, B) as i:
                v.wait_ge(S["gates"], 16 * E1 * (i + 1))
                for e in range(E1):
                    out = GX[:, bass.ds(i * T, T)] if e == 0 else t[:]
                    v.wait_ge(H["yps"][e], i + 1)
                    v.scalar_tensor_tensor(out=out, in0=yps[:, e % 2, :], scalar=W("ffb2")[:, e:e + 1],
                                           in1=g[:, e, :], op0=ALU.add, op1=ALU.mult).then_inc(H["t"][e], 1)
                    v.wait_ge(H["t"][e], i + 1)
                    if e:
                        v.tensor_tensor(GX[:, bass.ds(i * T, T)], GX[:, bass.ds(i * T, T)], t[:],
                                        ALU.add).then_inc(H["act"][e], 1)
                        v.wait_ge(H["act"][e], i + 1)
                v.nop().then_inc(S["x"], 1)


QUERIES_AT = {3: 0, 2: T, 0: T + 384, 1: 2 * T}


def inertia_phase(nc, K):
    XN, SX, GX, cst, W = K["XN"], K["SX"], K["GX"], K["cst"], K["w2"]
    ITERS, F = 8, 4
    L = 4
    IT = B // L
    with ExitStack() as ctx:
        S = sems(nc, ctx, "in", "x2 v0 mean cent sq var std rstd gained n "
                 "x3 mean2 cent2 sq2 var2 std2 rstd2 gained2 n2 out", L)
        small = sems(nc, ctx, "inw", "w")["w"]
        R = sems(nc, ctx, "inr", "pre u t v xs", L)
        HF = sems(nc, ctx, "inf", "ps h used", L)
        ps = ctx.enter_context(nc.psum_tensor("in_ps", [128, L, 2, T], F32))
        sb = lambda name, *n: ctx.enter_context(nc.sbuf_tensor("in_" + name, [128, L, *n, T], F32))
        x2, xs, vel, tmp, u, h = sb("x2"), sb("xs"), sb("vel"), sb("tmp"), sb("u"), sb("h", 2)
        step_x = ctx.enter_context(nc.sbuf_tensor("in_step_x", [128, 128], F32))
        block = ctx.enter_context(nc.Block())

        def row(i, a):
            return bass.ds((i * L + a) * T, T)

        @block.tensor
        def _(pe):
            with pe.Fori(0, IT) as i:
                for a in range(L):
                    pe.wait_ge(S["x2"][a], i + 1)
                    pe.wait_ge(S["out"][a], i)
                    pe.matmul(ps[:, a, 0, :], cst("mean"), x2[:, a, :], start=True, stop=True).then_inc(S["mean"][a], 1)
                for a in range(L):
                    pe.wait_ge(S["sq"][a], i + 1)
                    pe.matmul(ps[:, a, 1, :], cst("mean"), u[:, a, :], start=True, stop=True).then_inc(S["var"][a], 1)
                for k in range(ITERS):
                    for a in range(L):
                        if k:
                            pe.wait_ge(R["u"][a], i * ITERS + k)
                            pe.wait_ge(R["v"][a], i * ITERS + k)
                            pe.matmul(ps[:, a, 0, :], step_x[:], vel[:, a, :], start=False,
                                      stop=(k == ITERS - 1), skip_group_check=True).then_inc(R["pre"][a], 1)
                            continue
                        pe.matmul(ps[:, a, 0, :], W("w_ctx"), GX[:, row(i, a)], start=True, stop=False,
                                  skip_group_check=True)
                        pe.wait_ge(S["n"][a], i + 1)
                        pe.wait_ge(small, 1)
                        pe.matmul(ps[:, a, 0, :], W("w_x"), xs[:, a, :], start=False, stop=False,
                                  skip_group_check=True).then_inc(R["pre"][a], 1)
                for a in range(L):
                    pe.wait_ge(S["x3"][a], i + 1)
                    pe.matmul(ps[:, a, 0, :], cst("mean"), x2[:, a, :], start=True, stop=True).then_inc(S["mean2"][a], 1)
                for a in range(L):
                    pe.wait_ge(S["sq2"][a], i + 1)
                    pe.matmul(ps[:, a, 1, :], cst("mean"), u[:, a, :], start=True, stop=True).then_inc(S["var2"][a], 1)
                for f in range(F + 1):
                    for a in range(L):
                        if f < F:
                            if f == 0:
                                pe.wait_ge(S["n2"][a], i + 1)
                            else:
                                pe.wait_ge(HF["h"][a], i * F + f)
                            pe.matmul(ps[:, a, 0, :], W("ff_w1")[:, f * 128:(f + 1) * 128], xs[:, a, :],
                                      start=True, stop=True).then_inc(HF["ps"][a], 1)
                        if f:
                            pe.wait_ge(HF["h"][a], i * F + f)
                            last = pe.matmul(ps[:, a, 1, :], W("ff_w2")[:, (f - 1) * C:f * C], h[:, a, (f - 1) % 2, :],
                                             start=(f == 1), stop=(f == F))
                            last.then_inc(HF["used"][a], 1)

        @block.scalar
        def _(act):
            with act.Fori(0, IT) as i:
                for a in range(L):
                    act.wait_ge(S["cent"][a], i + 1)
                    act.activation(u[:, a, :], xs[:, a, :], ACT.Square).then_inc(S["sq"][a], 1)
                for a in range(L):
                    act.wait_ge(S["var"][a], i + 1)
                    act.activation(tmp[:, a, :], ps[:, a, 1, :], ACT.Ln, bias=cst("eps")).then_inc(S["std"][a], 1)
                for a in range(L):
                    act.wait_ge(S["std"][a], i + 1)
                    act.activation(tmp[:, a, :], tmp[:, a, :], ACT.Exp, scale=-0.5).then_inc(S["rstd"][a], 1)
                for k in range(ITERS):
                    for a in range(L):
                        act.wait_ge(R["pre"][a], i * ITERS + k + 1)
                        act.wait_ge(R["v"][a], i * ITERS + k)
                        act.activation(u[:, a, :], ps[:, a, 0, :], ACT.Tanh, bias=W("b_inl")).then_inc(R["u"][a], 1)
                for a in range(L):
                    act.wait_ge(S["cent2"][a], i + 1)
                    act.activation(u[:, a, :], xs[:, a, :], ACT.Square).then_inc(S["sq2"][a], 1)
                for a in range(L):
                    act.wait_ge(S["var2"][a], i + 1)
                    act.activation(tmp[:, a, :], ps[:, a, 1, :], ACT.Ln, bias=cst("eps")).then_inc(S["std2"][a], 1)
                for a in range(L):
                    act.wait_ge(S["std2"][a], i + 1)
                    act.activation(tmp[:, a, :], tmp[:, a, :], ACT.Exp, scale=-0.5).then_inc(S["rstd2"][a], 1)
                for f in range(F):
                    for a in range(L):
                        act.wait_ge(HF["ps"][a], i * F + f + 1)
                        if f >= 2:
                            act.wait_ge(HF["used"][a], i * F + f - 1)
                        else:
                            act.wait_ge(HF["used"][a], i * F)
                        act.activation(h[:, a, f % 2, :], ps[:, a, 0, :], ACT.Gelu,
                                       bias=W("ff_b1")[:, f:f + 1]).then_inc(HF["h"][a], 1)

        @block.vector
        def _(v):
            def norm(i, tag, gain, shift):
                for a in range(L):
                    v.wait_ge(S["mean" + tag][a], i + 1)
                    v.tensor_tensor(xs[:, a, :], x2[:, a, :], ps[:, a, 0, :], ALU.subtract).then_inc(S["cent" + tag][a], 1)
                for a in range(L):
                    v.wait_ge(S["rstd" + tag][a], i + 1)
                    v.scalar_tensor_tensor(out=xs[:, a, :], in0=xs[:, a, :], scalar=W(gain), in1=tmp[:, a, :],
                                           op0=ALU.mult, op1=ALU.mult).then_inc(S["gained" + tag][a], 1)
                    v.wait_ge(S["gained" + tag][a], i + 1)
                    v.tensor_scalar(xs[:, a, :], xs[:, a, :], W(shift), None, ALU.add).then_inc(S["n" + tag][a], 1)

            v.tensor_scalar(step_x[:], W("w_x"), 0.01, None, ALU.mult).then_inc(small, 1)
            with v.Fori(0, IT) as i:
                for a in range(L):
                    v.tensor_tensor(x2[:, a, :], XN[:, row(i, a)], GX[:, row(i, a)], ALU.add).then_inc(S["x2"][a], 1)
                    v.memset(vel[:, a, :], 0.0).then_inc(S["v0"][a], 1)
                for a in range(L):
                    v.wait_ge(S["x2"][a], i + 1)
                    v.wait_ge(S["v0"][a], i + 1)
                norm(i, "", "g1", "b1")
                for k in range(ITERS):
                    for a in range(L):
                        if k:
                            v.wait_ge(R["xs"][a], i * ITERS + k)
                        else:
                            v.wait_ge(S["n"][a], i + 1)
                        v.scalar_tensor_tensor(out=tmp[:, a, :], in0=vel[:, a, :], scalar=0.9, in1=xs[:, a, :],
                                               op0=ALU.mult, op1=ALU.subtract).then_inc(R["t"][a], 1)
                    for a in range(L):
                        v.wait_ge(R["t"][a], i * ITERS + k + 1)
                        v.wait_ge(R["u"][a], i * ITERS + k + 1)
                        if k:
                            v.wait_ge(R["pre"][a], i * ITERS + k + 1)
                        v.tensor_tensor(vel[:, a, :], tmp[:, a, :], u[:, a, :], ALU.add).then_inc(R["v"][a], 1)
                        v.wait_ge(R["v"][a], i * ITERS + k + 1)
                        v.scalar_tensor_tensor(out=xs[:, a, :], in0=vel[:, a, :], scalar=0.01, in1=xs[:, a, :],
                                               op0=ALU.mult, op1=ALU.add).then_inc(R["xs"][a], 1)
                for a in range(L):
                    v.wait_ge(R["xs"][a], i * ITERS + ITERS)
                    v.tensor_tensor(x2[:, a, :], x2[:, a, :], xs[:, a, :], ALU.add).then_inc(S["x3"][a], 1)
                norm(i, "2", "g2", "b2")
                for a in range(L):
                    v.wait_ge(HF["used"][a], i * F + F)
                    v.scalar_tensor_tensor(out=SX[:, row(i, a)], in0=ps[:, a, 1, :], scalar=W("ff_b2"),
                                           in1=x2[:, a, :], op0=ALU.add, op1=ALU.add).then_inc(S["out"][a], 1)
                for a in range(L):
                    v.wait_ge(S["out"][a], i + 1)


def gated_mlp_phase(nc, K):
    XN, GX, W = K["XN"], K["GX"], K["w2f"]
    F = 4
    with ExitStack() as ctx:
        S = sems(nc, ctx, "gm", "ops out")
        L = [sems(nc, ctx, f"gm{n}", "ps sb", F) for n in range(4)]
        
        ps = ctx.enter_context(nc.psum_tensor("gm_ps", [128, 8, T], F32))
        a1 = ctx.enter_context(nc.sbuf_tensor("gm_a1", [128, F, T], F32))
        h0 = ctx.enter_context(nc.sbuf_tensor("gm_h0", [128, F, T], F32))
        h1 = ctx.enter_context(nc.sbuf_tensor("gm_h1", [128, F, T], F32))
        h2 = ctx.enter_context(nc.sbuf_tensor("gm_h2", [128, F, T], F32))
        block = ctx.enter_context(nc.Block())

        @block.tensor
        def _(pe):
            with pe.Fori(0, B) as i:
                x = XN[:, bass.ds(i * T, T)]
                for f in range(F):
                    pe.wait_ge(S["out"] if f == 0 else L[2]["sb"][f], i)
                    pe.matmul(ps[:, f, :], W("w1")[:, f * 128:(f + 1) * 128], x, start=True,
                              stop=True).then_inc(L[0]["ps"][f], 1)
                    pe.wait_ge(L[3]["sb"][f], i)
                    pe.matmul(ps[:, 4 + f, :], W("w2")[:, f * 128:(f + 1) * 128], x, start=True,
                              stop=True).then_inc(L[1]["ps"][f], 1)
                for n, w, src, ready in ((2, "h1", h0, L[1]["sb"]), (3, "h2", h1, L[2]["sb"])):
                    for f in range(F):
                        pe.wait_ge(L[n - 2]["sb"][f], i + 1)
                        for j in range(F):
                            pe.wait_ge(ready[j], i + 1)
                            last = pe.matmul(ps[:, 4 * (n % 2) + f, :],
                                             W(w)[:, j * 512 + f * 128:j * 512 + (f + 1) * 128], src[:, j, :],
                                             start=(j == 0), stop=(j == F - 1))
                        last.then_inc(L[n]["ps"][f], 1)
                for j in range(F):
                    pe.wait_ge(L[3]["sb"][j], i + 1)
                    last = pe.matmul(ps[:, 0, :], W("w3")[:, j * C:(j + 1) * C], h2[:, j, :],
                                     start=(j == 0), stop=(j == F - 1))
                last.then_inc(S["ops"], 1)

        @block.scalar
        def _(act):
            with act.Fori(0, B) as i:
                for f in range(F):
                    act.wait_ge(L[0]["ps"][f], i + 1)
                    act.wait_ge(L[1]["sb"][f], i)
                    act.activation(a1[:, f, :], ps[:, f, :], ACT.Silu, scale=W("s1")[:, f:f + 1]).then_inc(L[0]["sb"][f], 1)
                for n, dst, sc in ((2, h1, "sh1"), (3, h2, "sh2")):
                    for f in range(F):
                        act.wait_ge(L[n]["ps"][f], i + 1)
                        if n == 2:
                            act.wait_ge(L[3]["ps"][F - 1], i)
                        else:
                            act.wait_ge(S["ops"], i)
                        act.activation(dst[:, f, :], ps[:, 4 * (n % 2) + f, :], ACT.Gelu,
                                       scale=W(sc)[:, f:f + 1]).then_inc(L[n]["sb"][f], 1)

        @block.vector
        def _(v):
            with v.Fori(0, B) as i:
                for f in range(F):
                    v.wait_ge(L[1]["ps"][f], i + 1)
                    v.wait_ge(L[0]["sb"][f], i + 1)
                    v.wait_ge(L[2]["ps"][F - 1], i)
                    v.scalar_tensor_tensor(out=h0[:, f, :], in0=ps[:, 4 + f, :], scalar=W("s2")[:, f:f + 1],
                                           in1=a1[:, f, :], op0=ALU.mult, op1=ALU.mult).then_inc(L[1]["sb"][f], 1)
                v.wait_ge(S["ops"], i + 1)
                v.tensor_scalar(GX[:, bass.ds(i * T, T)], ps[:, 0, :], W("s3"), None, ALU.mult).then_inc(S["out"], 1)


TERMS = ((0, 0), (0, 1), (1, 0), (0, 2), (2, 0), (1, 1))


def split_phase(nc, K, tag, src, wq, wk, wv, tiles, dim, bias=None, qscale=1.0):
    X, VA, Pd = K[src], K["VA"], K["Pd"]
    H = 16
    D = VA.shape[-1] - 1
    N = 2 * tiles
    with ExitStack() as ctx:
        S = sems(nc, ctx, tag, "xs vps v ones")
        U = [sems(nc, ctx, f"{tag}{a}", "ps f hi r1 mid lo stored", N) for a in range(1)][0]
        ps = ctx.enter_context(nc.psum_tensor(tag + "_ps", [128, N, T], F32))
        vps = ctx.enter_context(nc.psum_tensor(tag + "_vps", [128, NB, C], F32))
        xs = ctx.enter_context(nc.sbuf_tensor(tag + "_xs", [128, T], F32))
        f = ctx.enter_context(nc.sbuf_tensor(tag + "_f", [128, N, T], F32))
        r = ctx.enter_context(nc.sbuf_tensor(tag + "_r", [128, N, T], F32))
        p = ctx.enter_context(nc.sbuf_tensor(tag + "_p", [128, N, 3, T], BF16))
        block = ctx.enter_context(nc.Block())

        @block.tensor
        def _(pe):
            with pe.Fori(0, B) as i:
                pe.wait_ge(S["xs"], i + 1)
                for n in range(N):
                    pe.wait_ge(U["f"][n], i)
                    w = (wq if n < tiles else wk)[:, (n % tiles) * 128:(n % tiles + 1) * 128]
                    pe.matmul(ps[:, n, :], w, xs[:], start=True, stop=True).then_inc(U["ps"][n], 1)
                pe.wait_ge(S["v"], i)
                for j in range(NB):
                    last = pe.matmul(vps[:, j, :], xs[:, j * 128:(j + 1) * 128], wv, start=True, stop=True)
                last.then_inc(S["vps"], 1)

        @block.scalar
        def _(act):
            with act.Fori(0, B) as i:
                for n in range(N):
                    act.wait_ge(U["ps"][n], i + 1)
                    act.wait_ge(U["r1"][n], i)
                    act.activation(f[:, n, :], ps[:, n, :], ACT.Identity, scale=qscale if n < tiles else 1.0,
                                   bias=0.0 if bias is None else bias[:, n:n + 1]).then_inc(U["f"][n], 1)
                    act.wait_ge(U["f"][n], i + 1)
                    act.wait_ge(U["stored"][n], 16 * i)
                    act.activation(p[:, n, 0, :], f[:, n, :], ACT.Copy).then_inc(U["hi"][n], 1)
                for n in range(N):
                    act.wait_ge(U["r1"][n], i + 1)
                    act.activation(p[:, n, 1, :], r[:, n, :], ACT.Copy).then_inc(U["mid"][n], 1)

        @block.vector
        def _(v):
            v.memset(VA[:], 1.0).then_inc(S["ones"], 1)
            v.wait_ge(S["ones"], 1)
            with v.Fori(0, B) as i:
                v.wait_ge(S["vps"], i)
                v.tensor_copy(xs[:], X[:, bass.ds(i * T, T)]).then_inc(S["xs"], 1)
                for n in range(N):
                    v.wait_ge(U["hi"][n], i + 1)
                    v.wait_ge(U["lo"][n], i)
                    v.tensor_tensor(r[:, n, :], f[:, n, :], p[:, n, 0, :], ALU.subtract).then_inc(U["r1"][n], 1)
                v.wait_ge(S["vps"], i + 1)
                out = VA[:, bass.ds(i * NB, NB), :, 0:D]
                got = vps[:].rearrange("p j (h d) -> p j h d", h=H)
                if bias is None:
                    v.tensor_copy(out, got).then_inc(S["v"], 1)
                else:
                    v.tensor_tensor(out, got, K["w2"]("v_b_row").rearrange("p (h d) -> p h d", h=H).unsqueeze(
                        1).to_broadcast([128, NB, H, D]), ALU.add).then_inc(S["v"], 1)
                for n in range(N):
                    v.wait_ge(U["mid"][n], i + 1)
                    v.tensor_tensor(p[:, n, 2, :], r[:, n, :], p[:, n, 1, :], ALU.subtract).then_inc(U["lo"][n], 1)

        @block.sync
        def _(sp):
            with sp.Fori(0, B) as i:
                for n in range(N):
                    sp.wait_ge(U["lo"][n], i + 1)
                    sp.dma_start(Pd[i, n // tiles, :, (n % tiles) * 128:(n % tiles + 1) * 128].rearrange("c r t -> r c t"),
                                 p[:, n]).then_inc(U["stored"][n], 16)
            for n in range(N):
                sp.wait_ge(U["stored"][n], 16 * B)


def load_stacks(sp, Pd, row, first, n, qs, ks, loaded, D):
    for at, (pq, pk) in enumerate(TERMS):
        for side, part, dst in ((0, pq, qs), (1, pk, ks)):
            src = Pd[row, side, part, first * D:(first + n) * D]
            sp.dma_start(dst[at * D:(at + 1) * D], src.rearrange("(h d) t -> d h t", d=D)).then_inc(loaded, 16)


GROUPS, GH = 4, 4


def open_bank(pe, K, bank):
    pe.matmul(bank, K["zero"][:, 0:128], K["zero"][:], start=True, stop=False, skip_group_check=True)


def causal_phase(nc, K, tag, dst, D, softmax):
    VA, Pd, cst, out = K["VA"], K["Pd"], K["cst"], K[dst]
    H, DV = GROUPS * GH, 8
    R = len(TERMS) * D + (2 if softmax else 0)
    LOADS = 16 * (2 * len(TERMS) + (1 if softmax else 0))
    SC = (float(1 / np.sqrt(D)),) if softmax else (0.25 * 0.5 ** 0.5,)
    with ExitStack() as ctx:
        S = sems(nc, ctx, tag, "ones den num dsb rec y")
        G = sems(nc, ctx, tag + "g", "loaded out va", GROUPS)
        HD = sems(nc, ctx, tag + "h", "score power masked av", H)
        ps = ctx.enter_context(nc.psum_tensor(tag + "_ps", [128, 2, 3 * T], F32))
        O = ctx.enter_context(nc.psum_tensor(tag + "_o", [128, 2, T], F32))
        qs = ctx.enter_context(nc.sbuf_tensor(tag + "_qs", [R, GROUPS, GH, T], BF16))
        ks = ctx.enter_context(nc.sbuf_tensor(tag + "_ks", [R, GROUPS, GH, T], BF16))
        va = ctx.enter_context(nc.sbuf_tensor(tag + "_va", [128, NB, H, DV + 1], F32))
        vc = ctx.enter_context(nc.sbuf_tensor(tag + "_vc", [128, NB, H, DV], F32))
        pw = ctx.enter_context(nc.sbuf_tensor(tag + "_pw", [128, 2, 3, T], F32))
        osb = ctx.enter_context(nc.sbuf_tensor(tag + "_osb", [128, GROUPS, T], F32))
        rec = ctx.enter_context(nc.sbuf_tensor(tag + "_rec", [128, T], F32))
        block = ctx.enter_context(nc.Block())
        weights = HD["power"] if softmax else HD["masked"]

        @block.sync
        def _(sp):
            if softmax:
                sp.wait_ge(S["ones"], 1)
            with sp.Fori(0, B) as i:
                for g in range(GROUPS):
                    sp.wait_ge(HD["score"][GH * g + GH - 1], i)
                    load_stacks(sp, Pd, i, g * GH, GH, qs[:, g], ks[:, g], G["loaded"][g], D)
                    if softmax:
                        sp.dma_start(qs[R - 2:R, g], K["Md"][i, :, g * GH:(g + 1) * GH]).then_inc(G["loaded"][g], 16)

        @block.tensor
        def _(pe):
            def scores(i, h):
                g = h // GH
                if h % GH == 0:
                    pe.wait_ge(G["loaded"][g], LOADS * (i + 1))
                if h >= 2:
                    pe.wait_ge(HD["power"][h - 2], i + 1)
                else:
                    pe.wait_ge(HD["power"][h + H - 2], i)
                for jk in range(NB):
                    at, n = KEYS_AT[jk], T - 128 * jk
                    k, q = ks[:, g, h % GH, jk * 128:(jk + 1) * 128], qs[:, g, h % GH, jk * 128:T]
                    if softmax:
                        pe.matmul(ps[:, h % 2, at:at + 128], K["cb"]("identb"), K["cb"]("neg_across"),
                                  start=True, stop=False)
                        last = pe.matmul(ps[:, h % 2, at:at + 128], k, q[:, 0:128], start=False, stop=True)
                        if n > 128:
                            last = pe.matmul(ps[:, h % 2, at + 128:at + n], k, q[:, 128:n], start=True, stop=True)
                    else:
                        last = pe.matmul(ps[:, h % 2, at:at + n], k, q, start=True, stop=True)
                last.then_inc(HD["score"][h], 1)

            def values(i, h):
                g = h // GH
                if h % GH == 0:
                    if g >= 2:
                        pe.wait_ge(G["out"][g - 2], i + 1)
                    else:
                        pe.wait_ge(S["dsb" if g == 0 else "y"], i)
                    open_bank(pe, K, O[:, g % 2, :])
                pe.wait_ge(G["va"][g], i + 1)
                pe.wait_ge(weights[h], i + 1)
                for jk in range(NB):
                    at, n = KEYS_AT[jk], T - 128 * jk
                    last = pe.matmul(O[32 * (h % GH):32 * (h % GH) + DV + 1, g % 2, jk * 128:T], va[:, jk, h, :],
                                     pw[:, h % 2, at // T, at % T:at % T + n], start=False,
                                     stop=(h % GH == GH - 1 and jk == NB - 1), skip_group_check=True)
                last.then_inc(HD["av"][h], 1)

            def turn(i, last):
                for h in range(H):
                    if h + 1 < H:
                        scores(i, h + 1)
                    elif not last:
                        scores(i + 1, 0)
                    values(i, h)
                for g in range(GROUPS):
                    pe.wait_ge(G["out"][g], i + 1)
                if not softmax:
                    pe.matmul(O[:, 0, :], cst("ones")[0:1, :], cst("halfcount"), start=True, stop=False)
                for g in range(GROUPS):
                    last = pe.matmul(O[:, 0, :], cst("close_den")[:, g * 128:(g + 1) * 128], osb[:, g, :],
                                     start=(softmax and g == 0), stop=(g == GROUPS - 1))
                last.then_inc(S["den"], 1)
                for g in range(GROUPS):
                    last = pe.matmul(O[:, 1, :], cst("close")[:, g * 128:(g + 1) * 128], osb[:, g, :],
                                     start=(g == 0), stop=(softmax and g == GROUPS - 1), skip_group_check=True)
                if not softmax:
                    for jk in range(NB):
                        last = pe.matmul(O[:, 1, jk * 128:T], vc[:, jk].rearrange("p h d -> p (h d)"), cst("halfwide")[:, 0:T - 128 * jk],
                                         start=False, stop=(jk == NB - 1), skip_group_check=True)
                last.then_inc(S["num"], 1)

            scores(0, 0)
            with pe.Fori(0, B - 1) as i:
                turn(i, False)
            turn(B - 1, True)

        @block.scalar
        def _(act):
            with act.Fori(0, B) as i:
                for h in range(H):
                    act.wait_ge(HD["score"][h], i + 1)
                    if h >= 2:
                        act.wait_ge(HD["av"][h - 2], i + 1)
                    else:
                        act.wait_ge(HD["av"][h + H - 2], i)
                    act.activation(pw[:, h % 2].rearrange("p g x -> p (g x)")[:, 0:SPAN], ps[:, h % 2, 0:SPAN],
                                   ACT.Exp if softmax else ACT.Square, scale=SC[0],
                                   bias=0.0 if softmax else cst("rhalf")).then_inc(HD["power"][h], 1)

        @block.gpsimd
        def _(gp):
            with gp.Fori(0, B) as i:
                for g in range(GROUPS):
                    gp.wait_ge(HD["av"][GH * g + GH - 1], i)
                    gp.wait_ge(S["num"], i)
                    gp.nop(nofuse=True)
                    if not softmax:
                        gp.tensor_copy(vc[:, :, g * GH:(g + 1) * GH, :],
                                       VA[:, bass.ds(i * NB, NB), g * GH:(g + 1) * GH, 0:DV])
                    gp.tensor_copy(va[:, :, g * GH:(g + 1) * GH, :],
                                   VA[:, bass.ds(i * NB, NB), g * GH:(g + 1) * GH, :]).then_inc(G["va"][g], 1)

        @block.vector
        def _(v):
            if softmax:
                v.memset(ks[:], 1.0).then_inc(S["ones"], 1)
            with v.Fori(0, B) as i:
                def evacuate(g):
                    v.wait_ge(HD["av"][GH * g + GH - 1], i + 1)
                    v.wait_ge(S["num"], i)
                    v.tensor_copy(osb[:, g, :], O[:, g % 2, :]).then_inc(G["out"][g], 1)

                for h in range(H):
                    if not softmax:
                        v.wait_ge(HD["power"][h], i + 1)
                        v.tensor_tensor(pw[:, h % 2, :, 0:128], pw[:, h % 2, :, 0:128],
                                        cst("tri").unsqueeze(1).to_broadcast([128, 3, 128]), ALU.mult)
                        v.tensor_tensor(pw[:, h % 2, 1, 384:512], pw[:, h % 2, 1, 384:512], cst("tri"),
                                        ALU.mult).then_inc(HD["masked"][h], 1)
                    if h % GH == 1 and h > GH:
                        evacuate(h // GH - 1)
                evacuate(GROUPS - 1)
                v.wait_ge(S["den"], i + 1)
                v.wait_ge(S["y"], i)
                v.tensor_scalar(rec[:], O[:, 0, :], 0.0 if softmax else 1e-12, None, ALU.add).then_inc(S["dsb"], 1)
                v.wait_ge(S["dsb"], i + 1)
                v.reciprocal(rec[:], rec[:]).then_inc(S["rec"], 1)
                v.wait_ge(S["rec"], i + 1)
                v.wait_ge(S["num"], i + 1)
                v.tensor_tensor(out[:, bass.ds(i * T, T)], O[:, 1, :], rec[:], ALU.mult).then_inc(S["y"], 1)


def maxima_phase(nc, K):
    Pd, Md, cst, cb = K["Pd"], K["Md"], K["cst"], K["cb"]
    H, D = GROUPS * GH, 8
    R = len(TERMS) * D
    LOADS = 16 * 2 * len(TERMS)
    with ExitStack() as ctx:
        S = sems(nc, ctx, "mx", "tps hi mid stored")
        G = sems(nc, ctx, "mxg", "loaded", GROUPS)["loaded"]
        HD = sems(nc, ctx, "mxh", "far top", H)
        ps = ctx.enter_context(nc.psum_tensor("mx_ps", [128, 2, 3 * T], F32))
        tps = ctx.enter_context(nc.psum_tensor("mx_tps", [H, T], F32))
        qs = ctx.enter_context(nc.sbuf_tensor("mx_qs", [R, GROUPS, GH, T], BF16))
        ks = ctx.enter_context(nc.sbuf_tensor("mx_ks", [R, GROUPS, GH, T], BF16))
        mx = ctx.enter_context(nc.sbuf_tensor("mx_mx", [128, NB, H], F32))
        parts = ctx.enter_context(nc.sbuf_tensor("mx_parts", [H, 2, T], BF16))
        block = ctx.enter_context(nc.Block())

        @block.sync
        def _(sp):
            with sp.Fori(0, B) as i:
                for g in range(GROUPS):
                    sp.wait_ge(HD["far"][GH * g + GH - 1], i)
                    load_stacks(sp, Pd, i, g * GH, GH, qs[:, g], ks[:, g], G[g], D)

        @block.tensor
        def _(pe):
            with pe.Fori(0, B) as i:
                for h in range(H):
                    g = h // GH
                    if h % GH == 0:
                        pe.wait_ge(G[g], LOADS * (i + 1))
                    if h >= 2:
                        pe.wait_ge(HD["top"][h - 2], i + 1)
                    else:
                        pe.wait_ge(HD["top"][h + H - 2], i)
                    for jq in range(NB):
                        at, n = QUERIES_AT[jq], 128 * (jq + 1)
                        q, k = qs[:, g, h % GH, jq * 128:(jq + 1) * 128], ks[:, g, h % GH, :]
                        if jq:
                            pe.matmul(ps[:, h % 2, at:at + n - 128], q, k[:, 0:n - 128], start=True, stop=True)
                        pe.matmul(ps[:, h % 2, at + n - 128:at + n], cb("identb"), cb("neg_down"),
                                  start=True, stop=False)
                        last = pe.matmul(ps[:, h % 2, at + n - 128:at + n], q, k[:, n - 128:n],
                                         start=False, stop=True)
                    last.then_inc(HD["far"][h], 1)
                pe.wait_ge(HD["top"][H - 1], i + 1)
                pe.wait_ge(S["mid"], i)
                for j in range(NB):
                    last = pe.transpose(tps[:, j * 128:(j + 1) * 128], mx[:, j, :], cst("ident"))
                last.then_inc(S["tps"], 1)

        @block.vector
        def _(v):
            with v.Fori(0, B) as i:
                v.wait_ge(S["tps"], i)
                for h in range(H):
                    v.wait_ge(HD["far"][h], i + 1)
                    for jq in range(NB):
                        at = QUERIES_AT[jq]
                        last = v.tensor_reduce(mx[:, jq, h:h + 1], ps[:, h % 2, at:at + 128 * (jq + 1)], AX.X,
                                               ALU.max, negate=True)
                    last.then_inc(HD["top"][h], 1)
                v.wait_ge(S["tps"], i + 1)
                v.wait_ge(S["stored"], 16 * i)
                v.tensor_copy(parts[:, 0, :], tps[:]).then_inc(S["hi"], 1)
                v.wait_ge(S["hi"], i + 1)
                v.tensor_tensor(parts[:, 1, :], tps[:], parts[:, 0, :], ALU.subtract).then_inc(S["mid"], 1)

        @block.scalar
        def _(act):
            with act.Fori(0, B) as i:
                act.wait_ge(S["mid"], i + 1)
                act.dma_start(Md[i].rearrange("n h t -> h n t"), parts[:]).then_inc(S["stored"], 16)
            act.wait_ge(S["stored"], 16 * B)


def project_phase(nc, K, tag, name, w, bias=0.0):
    X = K[name]
    L = 4
    with ExitStack() as ctx:
        S = sems(nc, ctx, tag, "ps out", L)
        ps = ctx.enter_context(nc.psum_tensor(tag + "_ps", [128, L, T], F32))
        block = ctx.enter_context(nc.Block())

        @block.tensor
        def _(pe):
            with pe.Fori(0, B // L) as i:
                for a in range(L):
                    pe.wait_ge(S["out"][a], i)
                    pe.matmul(ps[:, a, :], w, X[:, bass.ds((i * L + a) * T, T)],
                              start=True, stop=True).then_inc(S["ps"][a], 1)

        @block.scalar
        def _(act):
            with act.Fori(0, B // L) as i:
                for a in range(L):
                    act.wait_ge(S["ps"][a], i + 1)
                    act.activation(X[:, bass.ds((i * L + a) * T, T)], ps[:, a, :], ACT.Identity,
                                   bias=bias).then_inc(S["out"][a], 1)


def column_attention_phase(nc, K):
    GX, VA, Pd, cst = K["GX"], K["VA"], K["Pd"], K["cst"]
    H, D = GROUPS * GH, 8
    R = len(TERMS) * D
    AHEAD = 2
    CLOSE = 2
    LOADS = 16 * 2 * len(TERMS)
    with ExitStack() as ctx:
        S = sems(nc, ctx, "ca", "num y")
        G = sems(nc, ctx, "cag", "loaded out", GROUPS)
        U = sems(nc, ctx, "cau", "score top exp", NB)
        V = sems(nc, ctx, "cav", "value", 2 * NB)
        HD = sems(nc, ctx, "cah", "rz vz", H)
        ps = ctx.enter_context(nc.psum_tensor("ca_ps", [128, NB, T], F32))
        O = ctx.enter_context(nc.psum_tensor("ca_o", [128, 2, T], F32))
        nps = ctx.enter_context(nc.psum_tensor("ca_num", [128, T], F32))
        qs = ctx.enter_context(nc.sbuf_tensor("ca_qs", [R, GROUPS, GH, T], BF16))
        ks = ctx.enter_context(nc.sbuf_tensor("ca_ks", [R, GROUPS, GH, T], BF16))
        pw = ctx.enter_context(nc.sbuf_tensor("ca_pw", [128, 2, NB, T], F32))
        mx = ctx.enter_context(nc.sbuf_tensor("ca_mx", [128, H, NB], F32))
        z = ctx.enter_context(nc.sbuf_tensor("ca_z", [128, H, NB], F32))
        vs = ctx.enter_context(nc.sbuf_tensor("ca_vs", [128, 2, NB, D], F32))
        osb = ctx.enter_context(nc.sbuf_tensor("ca_osb", [128, GROUPS, T], F32))
        block = ctx.enter_context(nc.Block())

        @block.sync
        def _(sp):
            with sp.Fori(0, B) as i:
                for g in range(GROUPS):
                    sp.wait_ge(G["out"][g], i)
                    load_stacks(sp, Pd, i, g * GH, GH, qs[:, g], ks[:, g], G["loaded"][g], D)

        @block.tensor
        def _(pe):
            def score(i, h, jk):
                if h % GH == 0 and jk == 0:
                    pe.wait_ge(G["loaded"][h // GH], LOADS * (i + 1))
                pe.wait_ge(U["exp"][jk], i * H + h)
                pe.matmul(ps[:, jk, :], ks[:, h // GH, h % GH, jk * 128:(jk + 1) * 128],
                          qs[:, h // GH, h % GH, :], start=True, stop=True).then_inc(U["score"][jk], 1)

            def value(i, h, jk):
                g = h // GH
                if jk == 0:
                    if h % GH == 0:
                        if g >= 2:
                            pe.wait_ge(G["out"][g - 2], i + 1)
                        else:
                            pe.wait_ge(G["out"][g + 2], i)
                        open_bank(pe, K, O[:, g % 2, :])
                    pe.wait_ge(HD["vz"][h], i + 1)
                last = h % GH == GH - 1 and jk == NB - 1
                pe.matmul(O[32 * (h % GH):32 * (h % GH) + D, g % 2, :], vs[:, h % 2, jk, :],
                          pw[:, h % 2, jk, :], start=False, stop=last, skip_group_check=True
                          ).then_inc(V["value"][h % 2 * NB + jk], 1)

            def close(i):
                for g in range(GROUPS):
                    pe.wait_ge(G["out"][g], i + 1)
                    last = pe.matmul(nps[:], cst("close")[:, g * 128:(g + 1) * 128], osb[:, g, :],
                                     start=(g == 0), stop=(g == GROUPS - 1))
                last.then_inc(S["num"], 1)

            def turn(i, first, last):
                for h in range(H):
                    for jk in range(NB):
                        if h + AHEAD < H:
                            score(i, h + AHEAD, jk)
                        elif not last:
                            score(i + 1, h + AHEAD - H, jk)
                        value(i, h, jk)
                    if h == CLOSE and not first:
                        pe.wait_ge(S["y"], i - 1)
                        close(i - 1)

            for h in range(AHEAD):
                for jk in range(NB):
                    score(0, h, jk)
            turn(0, True, False)
            with pe.Fori(1, B - 1) as i:
                turn(i, False, False)
            turn(B - 1, False, True)
            pe.wait_ge(S["y"], B - 1)
            close(B - 1)

        @block.scalar
        def _(act):
            with act.Fori(0, B) as i:
                for h in range(H):
                    for jk in range(NB):
                        act.wait_ge(V["value"][h % 2 * NB + jk], i * (H // 2) + h // 2)
                        act.wait_ge(U["top"][jk], i * H + h + 1)
                        act.activation(pw[:, h % 2, jk, :], ps[:, jk, :], ACT.Exp,
                                       bias=mx[:, h, jk:jk + 1], accum_out=z[:, h, jk:jk + 1]).then_inc(U["exp"][jk], 1)

        @block.vector
        def _(v):
            def weigh(i, h):
                v.wait_ge(U["exp"][NB - 1], i * H + h + 1)
                v.reciprocal(z[:, h, :], z[:, h, :]).then_inc(HD["rz"][h], 1)
                v.wait_ge(HD["rz"][h], i + 1)
                v.wait_ge(V["value"][h % 2 * NB + NB - 1], i * (H // 2) + h // 2)
                v.tensor_tensor(vs[:, h % 2], VA[:, bass.ds(i * NB, NB), h, 0:D],
                                z[:, h, :].unsqueeze(2).to_broadcast([128, NB, D]), ALU.mult).then_inc(HD["vz"][h], 1)

            def evacuate(i, g):
                h = GH * g + GH - 1
                v.wait_ge(V["value"][h % 2 * NB + NB - 1], i * (H // 2) + h // 2 + 1)
                v.wait_ge(S["num"], i)
                v.tensor_copy(osb[:, g, :], O[:, g % 2, :]).then_inc(G["out"][g], 1)

            def close(i):
                v.wait_ge(S["num"], i + 1)
                v.tensor_copy(GX[:, bass.ds(i * T, T)], nps[:]).then_inc(S["y"], 1)

            def turn(i, first):
                for h in range(H):
                    for jk in range(NB):
                        v.wait_ge(U["score"][jk], i * H + h + 1)
                        v.tensor_reduce(mx[:, h, jk:jk + 1], ps[:, jk, :], AX.X,
                                        ALU.max, negate=True).then_inc(U["top"][jk], 1)
                        if h and jk == 1:
                            weigh(i, h - 1)
                    g = (h - AHEAD - 1) // GH
                    if (h - AHEAD) % GH == 0 and (h > AHEAD or not first):
                        evacuate(i if g >= 0 else i - 1, g % GROUPS)
                    if h == CLOSE + AHEAD + 1 and not first:
                        close(i - 1)
                weigh(i, H - 1)

            turn(0, True)
            with v.Fori(1, B) as i:
                turn(i, False)
            evacuate(B - 1, GROUPS - 1)
            close(B - 1)


def l2_gelu_phase(nc, K):
    GX, cst, W = K["GX"], K["cst"], K["w3"]
    L = 4
    IT = B // L
    with ExitStack() as ctx:
        S = sems(nc, ctx, "lg", "z z1 sq ss std rs n w w1 sq2 ss2 std2 rs2 n2 out", L)
        ps = ctx.enter_context(nc.psum_tensor("lg_ps", [128, L, 2, T], F32))
        z = ctx.enter_context(nc.sbuf_tensor("lg_z", [128, L, T], F32))
        sq = ctx.enter_context(nc.sbuf_tensor("lg_sq", [128, L, T], F32))
        block = ctx.enter_context(nc.Block())

        def row(i, a):
            return bass.ds((i * L + a) * T, T)

        @block.tensor
        def _(pe):
            with pe.Fori(0, IT) as i:
                for a in range(L):
                    pe.wait_ge(S["z1"][a], i)
                    pe.matmul(ps[:, a, 0, :], W("wo"), GX[:, row(i, a)], start=True, stop=True).then_inc(S["z"][a], 1)
                for a in range(L):
                    pe.wait_ge(S["sq"][a], i + 1)
                    pe.wait_ge(S["std"][a], i)
                    pe.matmul(ps[:, a, 1, :], cst("ones"), sq[:, a, :], start=True, stop=True).then_inc(S["ss"][a], 1)
                for a in range(L):
                    pe.wait_ge(S["n"][a], i + 1)
                    pe.wait_ge(S["w1"][a], i)
                    pe.matmul(ps[:, a, 0, :], W("wff"), z[:, a, :], start=True, stop=True).then_inc(S["w"][a], 1)
                for a in range(L):
                    pe.wait_ge(S["sq2"][a], i + 1)
                    pe.wait_ge(S["std2"][a], i)
                    pe.matmul(ps[:, a, 1, :], cst("ones"), sq[:, a, :], start=True, stop=True).then_inc(S["ss2"][a], 1)

        @block.scalar
        def _(act):
            with act.Fori(0, IT) as i:
                for tag, src in (("", "z1"), ("2", "w1")):
                    for a in range(L):
                        act.wait_ge(S[src][a], i + 1)
                        act.activation(sq[:, a, :], z[:, a, :], ACT.Square).then_inc(S["sq" + tag][a], 1)
                    for a in range(L):
                        act.wait_ge(S["ss" + tag][a], i + 1)
                        act.activation(sq[:, a, :], ps[:, a, 1, :], ACT.Ln,
                                       bias=cst("tiny")).then_inc(S["std" + tag][a], 1)
                    for a in range(L):
                        act.wait_ge(S["std" + tag][a], i + 1)
                        act.activation(sq[:, a, :], sq[:, a, :], ACT.Exp, scale=-0.5).then_inc(S["rs" + tag][a], 1)
                for a in range(L):
                    act.wait_ge(S["n2"][a], i + 1)
                    act.activation(GX[:, row(i, a)], z[:, a, :], ACT.Gelu).then_inc(S["out"][a], 1)

        @block.vector
        def _(v):
            with v.Fori(0, IT) as i:
                for tag, src, dst, nd in (("", "z", "z1", "n"), ("2", "w", "w1", "n2")):
                    for a in range(L):
                        v.wait_ge(S[src][a], i + 1)
                        if not tag:
                            v.wait_ge(S["out"][a], i)
                        v.tensor_copy(z[:, a, :], ps[:, a, 0, :]).then_inc(S[dst][a], 1)
                    for a in range(L):
                        v.wait_ge(S["rs" + tag][a], i + 1)
                        v.tensor_tensor(z[:, a, :], z[:, a, :], sq[:, a, :], ALU.mult).then_inc(S[nd][a], 1)


def ssm_rows_phase(nc, K):
    XN, cst, W, Rd, COL = K["XN"], K["cst"], K["w3a"], K["Rd"], K["COL"]
    HB = B * 4
    with ExitStack() as ctx:
        S = sems(nc, ctx, "sr", "ps z az ez lz sp a1 adt ell sub gam bd beta cps col stored sp2")
        ps = ctx.enter_context(nc.psum_tensor("sr_ps", [HB, 3, T], F32))
        cps = ctx.enter_context(nc.psum_tensor("sr_cps", [128, 3, NB, HB], F32))
        z = ctx.enter_context(nc.sbuf_tensor("sr_z", [HB, 2, T], F32))
        e = ctx.enter_context(nc.sbuf_tensor("sr_e", [HB, 2, T], F32))
        q = ctx.enter_context(nc.sbuf_tensor("sr_q", [HB, 6, T], F32))
        block = ctx.enter_context(nc.Block())

        @block.tensor
        def _(pe):
            for n in range(3):
                for b in range(B):
                    last = pe.matmul(ps[:, n, :], W("rows")[:, (n * B + b) * HB:(n * B + b + 1) * HB],
                                     XN[:, b * T:(b + 1) * T], start=(b == 0), stop=(b == B - 1))
            last.then_inc(S["ps"], 1)
            pe.wait_ge(S["ell"], 1)
            pe.wait_ge(S["gam"], 1)
            pe.wait_ge(S["bd"], 1)
            for n in range(3):
                for j in range(NB):
                    last = pe.transpose(cps[:, n, j, :], q[:, n, j * 128:(j + 1) * 128], cst("ident")[0:HB, 0:HB])
            last.then_inc(S["cps"], 1)

        @block.scalar
        def _(act):
            act.wait_ge(S["ps"], 1)
            act.activation(q[:, 5, :], ps[:, 2, :], ACT.Sigmoid).then_inc(S["beta"], 1)
            act.wait_ge(S["z"], 1)
            act.activation(e[:], z[:], ACT.Abs).then_inc(S["az"], 1)
            act.wait_ge(S["az"], 1)
            act.activation(e[:], e[:], ACT.Exp, scale=-1.0).then_inc(S["ez"], 1)
            act.wait_ge(S["ez"], 1)
            act.activation(e[:], e[:], ACT.Ln, bias=1.0).then_inc(S["lz"], 1)

        @block.vector
        def _(v):
            v.wait_ge(S["ps"], 1)
            v.wait_ge(S["beta"], 1)
            v.tensor_scalar(z[:, 0, :], ps[:, 0, :], W("dt_bias"), None, ALU.add)
            v.tensor_copy(z[:, 1, :], ps[:, 1, :]).then_inc(S["z"], 1)
            v.wait_ge(S["z"], 1)
            v.wait_ge(S["lz"], 1)
            v.scalar_tensor_tensor(out=q[:, 3:5, :], in0=z[:], scalar=0.0, in1=e[:],
                                   op0=ALU.max, op1=ALU.add).then_inc(S["sp"], 1)
            v.wait_ge(S["sp"], 1)
            v.tensor_scalar(q[:, 4, :], q[:, 4, :], -1.0, -1e-4, ALU.mult, ALU.min).then_inc(S["a1"], 1)
            v.wait_ge(S["a1"], 1)
            v.tensor_tensor(q[:, 4, :], q[:, 4, :], q[:, 3, :], ALU.mult).then_inc(S["adt"], 1)
            v.wait_ge(S["adt"], 1)
            v.tensor_tensor_scan(q[:, 0, :], cst("onerow")[0:HB], q[:, 4, :], 0.0, ALU.mult, ALU.add).then_inc(S["ell"], 1)
            v.tensor_tensor(q[:, 2, :], q[:, 5, :], q[:, 3, :], ALU.mult).then_inc(S["bd"], 1)
            v.tensor_tensor(e[:, 0, 0:T - 1], q[:, 5, 0:T - 1], q[:, 5, 1:T], ALU.subtract)
            v.tensor_copy(e[:, 0, T - 1:T], q[:, 5, T - 1:T]).then_inc(S["sub"], 1)
            v.wait_ge(S["sub"], 1)
            v.scalar_tensor_tensor(out=q[:, 1, :], in0=e[:, 0, :], scalar=1.0, in1=q[:, 3, :],
                                   op0=ALU.add, op1=ALU.mult).then_inc(S["gam"], 1)
            v.wait_ge(S["cps"], 1)
            v.tensor_copy(COL[:], cps[:]).then_inc(S["col"], 1)
            v.wait_ge(S["col"], 1)

        @block.sync
        def _(sp):
            sp.wait_ge(S["ell"], 1)
            sp.dma_start(Rd[0], q[:, 3, :]).then_inc(S["stored"], 16)
            sp.dma_start(Rd[1], q[:, 0, :]).then_inc(S["stored"], 16)
            sp.wait_ge(S["stored"], 32)


def ssm_phase(nc, K):
    XN, SX, cst, W, Rd, COL = K["XN"], K["SX"], K["cst"], K["w3a"], K["Rd"], K["COL"]
    H = 4
    TWO_PI_HI, TWO_PI_LO = 6.28125, float(2 * np.pi - 6.28125)
    MAGIC = 1.5 * 2.0 ** 23
    Q_, K_ = 0, 1
    with ExitStack() as ctx:
        S = sems(nc, ctx, "ss", "xs rows pj1 ev1 pj2 ev2a ev2b xt sq ms std rs norm nturn rev at th n n1 c1 c2 clamp "
                 "sin abs cos cosm y2 yz sps s colj")
        HD = sems(nc, ctx, "sh", "cps b0 t1 t2 turned qk dd dec m0 m1 m2 dm a y", H)
        ps = ctx.enter_context(nc.psum_tensor("ss_ps", [128, 8, T], F32))
        sb = lambda name, *n: ctx.enter_context(nc.sbuf_tensor("ss_" + name, [128, *n], F32))
        xs, zs, xf, bc, rot = sb("xs", T), sb("zs", 2, T), sb("xf", 2, T), sb("bc", 2, T), sb("rot", 2, T)
        sq, xt, ang, th = sb("sq", 2, T), sb("xt", NB, 256), sb("ang", T), sb("th", 3, T)
        dtb, ellb = sb("dtb", T), sb("ellb", H, T)
        tb, t2, t3 = sb("tb", 2, T), sb("t2", 2, T), sb("t3", 2, T)
        kq, dec, aw = sb("kq", 2, 2, T), sb("dec", 2, 3, T), sb("aw", 2, 3, T)
        mm, own = sb("mm", H, NB, 128), sb("own", NB, 128)
        y = sb("y", 2, T)
        block = ctx.enter_context(nc.Block())

        @block.sync
        def _(sp):
            with sp.Fori(0, B) as i:
                sp.wait_ge(S["at"], i)
                sp.wait_ge(HD["dd"][H - 1], i)
                for h in range(H):
                    sp.dma_start(dtb[32 * h:32 * h + 32, :], Rd[0, bass.ds(i * H + h, 1), :].to_broadcast([32, T])
                                 ).then_inc(S["rows"], 16)
                    sp.dma_start(ellb[:, h, :], Rd[1, bass.ds(i * H + h, 1), :].to_broadcast([128, T])
                                 ).then_inc(S["rows"], 16)

        @block.tensor
        def _(pe):
            with pe.Fori(0, B) as i:
                pe.wait_ge(S["s"], i)
                pe.wait_ge(S["xs"], i + 1)
                for n in range(7):
                    last = pe.matmul(ps[:, n, :], W("in")[:, n * 128:(n + 1) * 128], xs[:], start=True, stop=True)
                last.then_inc(S["pj1"], 1)
                pe.wait_ge(S["ev1"], i + 1)
                pe.wait_ge(S["ev2a"], i + 1)
                for j in range(NB):
                    last = pe.matmul(ps[:, j // 2, (j % 2) * 256:(j % 2) * 256 + 256], xs[:, j * 128:(j + 1) * 128],
                                     W("in")[:, 256:512], start=True, stop=True)
                last.then_inc(S["pj2"], 1)
                pe.wait_ge(S["sq"], i + 1)
                for n in range(2):
                    last = pe.matmul(ps[:, 4 + n, :], cst("mean"), sq[:, n, :], start=True, stop=True)
                last.then_inc(S["ms"], 1)
                pe.wait_ge(S["norm"], i + 1)
                for n in range(2):
                    last = pe.matmul(ps[:, 2 + n, :], cst("rot"), bc[:, n, :], start=True, stop=True)
                last.then_inc(S["nturn"], 1)
                pe.wait_ge(S["rev"], i + 1)
                pe.wait_ge(S["xt"], i + 1)
                pe.wait_ge(S["cosm"], i + 1)
                pe.wait_ge(S["sin"], i + 1)

                def spread(h):
                    if h:
                        pe.wait_ge(HD["t2"][h - 1], i + 1)
                    for n in range(2):
                        last = pe.matmul(ps[:, 3 + n, :], cst(("spread", "spread_sin")[n])[:, h * 128:(h + 1) * 128],
                                         th[:, 1 + n, :],
                                         start=True, stop=True)
                    last.then_inc(HD["cps"][h], 1)

                def products(h):
                    pe.wait_ge(HD["turned"][h], i + 1)
                    if h:
                        pe.wait_ge(HD["a"][h - 1], i + 1)
                    for jk in range(NB):
                        at, n = KEYS_AT[jk], T - 128 * jk
                        last = pe.matmul(ps[:, at // T, at % T:at % T + n], kq[:, h % 2, K_, jk * 128:(jk + 1) * 128],
                                         kq[:, h % 2, Q_, jk * 128:T], start=True, stop=True)
                    last.then_inc(HD["qk"][h], 1)

                def outputs(h):
                    pe.wait_ge(HD["a"][h], i + 1)
                    r = slice(64 * (h % 2), 64 * (h % 2) + 64)
                    for jk in range(NB):
                        at, n = KEYS_AT[jk], T - 128 * jk
                        last = pe.matmul(ps[r, 5 + h // 2, jk * 128:T], xt[:, jk, h * 64:(h + 1) * 64],
                                         aw[:, h % 2, at // T, at % T:at % T + n], start=(jk == 0), stop=(jk == NB - 1))
                    last.then_inc(HD["y"][h], 1)

                spread(0)
                spread(1)
                for h in range(H):
                    products(h)
                    if h:
                        outputs(h - 1)
                    if h + 2 < H:
                        spread(h + 2)
                outputs(H - 1)
                pe.wait_ge(S["yz"], i + 1)
                for n in range(2):
                    last = pe.matmul(ps[:, 7, :], W("out")[:, n * C:(n + 1) * C], y[:, n, :],
                                     start=(n == 0), stop=(n == 1))
                last.then_inc(S["sps"], 1)

        @block.scalar
        def _(act):
            with act.Fori(0, B) as i:
                act.wait_ge(S["pj1"], i + 1)
                act.wait_ge(S["yz"], i)
                act.activation(zs[:], ps[:, 0:2, :], ACT.Silu)
                act.activation(ang[:], ps[:, 6, :], ACT.Copy)
                act.wait_ge(S["y2"], i)
                act.activation(xf[:], ps[:, 2:4, :], ACT.Copy).then_inc(S["ev1"], 1)
                act.wait_ge(S["ev2a"], i + 1)
                act.activation(sq[:], bc[:], ACT.Square).then_inc(S["sq"], 1)
                act.wait_ge(S["pj2"], i + 1)
                act.activation(xt[:].rearrange("p j f -> p (j f)"), ps[:, 0:2, :].rearrange("p n t -> p (n t)"),
                               ACT.Copy).then_inc(S["xt"], 1)
                act.wait_ge(S["ms"], i + 1)
                act.activation(sq[:], ps[:, 4:6, :], ACT.Ln, bias=cst("eps")).then_inc(S["std"], 1)
                act.wait_ge(S["std"], i + 1)
                act.activation(sq[:], sq[:], ACT.Exp, scale=-0.5).then_inc(S["rs"], 1)
                act.wait_ge(S["clamp"], i + 1)
                act.activation(th[:, 2, :], th[:, 0, :], ACT.Sin).then_inc(S["sin"], 1)
                act.activation(th[:, 1, :], th[:, 0, :], ACT.Abs).then_inc(S["abs"], 1)
                act.wait_ge(S["abs"], i + 1)
                act.activation(th[:, 1, :], th[:, 1, :], ACT.Sin, scale=-1.0, bias=cst("halfpi")).then_inc(S["cos"], 1)
                act.wait_ge(S["nturn"], i + 1)
                act.activation(rot[:], ps[:, 2:4, :], ACT.Copy).then_inc(S["rev"], 1)

                def biased(h):
                    if h:
                        act.wait_ge(HD["t2"][h - 1], i + 1)
                    for n in range(2):
                        last = act.activation(tb[:, n, :], bc[:, n, :], ACT.Identity,
                                              bias=W("bc_b")[:, n * H + h:n * H + h + 1])
                    last.then_inc(HD["b0"][h], 1)

                act.wait_ge(S["norm"], i + 1)
                biased(0)
                for h in range(H):
                    if h + 1 < H:
                        biased(h + 1)
                    act.wait_ge(HD["dd"][h], i + 1)
                    for g, n in ((0, T), (1, T), (2, 256)):
                        last = act.activation(dec[:, h % 2, g, 0:n], dec[:, h % 2, g, 0:n], ACT.Exp)
                    last.then_inc(HD["dec"][h], 1)
                act.wait_ge(S["sps"], i + 1)
                act.activation(SX[:, bass.ds(i * T, T)], ps[:, 7, :], ACT.Copy).then_inc(S["s"], 1)

        @block.gpsimd
        def _(g):
            with g.Fori(0, B) as i:
                def turned(h):
                    g.wait_ge(HD["t2"][h], i + 1)
                    if h >= 2:
                        g.wait_ge(HD["qk"][h - 2], i + 1)
                    for n in range(2):
                        last = g.tensor_tensor(kq[:, h % 2, K_ if n == 0 else Q_, :], t2[:, n, :], t3[:, n, :], ALU.add)
                    last.then_inc(HD["turned"][h], 1)

                g.wait_ge(HD["dm"][H - 1], i)
                for h in range(H):
                    for n, c, src in ((0, 1, "stri"), (1, 2, "ident")):
                        if n and h:
                            g.wait_ge(HD["m2"][h - 1], i + 1)
                        last = g.tensor_tensor(mm[:, h] if n == 0 else own[:],
                                               cst(src).unsqueeze(1).to_broadcast([128, NB, 128]),
                                               COL[:, c, :, bass.ds(i * H + h, 1)].to_broadcast([128, NB, 128]),
                                               ALU.mult)
                    last.then_inc(HD["m1"][h], 1)
                    g.wait_ge(HD["m1"][h], i + 1)
                    g.tensor_tensor(mm[:, h], mm[:, h], own[:], ALU.add).then_inc(HD["m2"][h], 1)
                g.wait_ge(HD["m2"][H - 1], i + 1)
                turned(0)
                for h in range(H):
                    g.wait_ge(HD["dec"][h], i + 1)
                    for jk in range(NB):
                        at = KEYS_AT[jk]
                        d = dec[:, h % 2, at // T, at % T:at % T + 128]
                        last = g.tensor_tensor(d, d, mm[:, h, jk, :], ALU.mult)
                    last.then_inc(HD["dm"][h], 1)
                    if h + 1 < H:
                        turned(h + 1)

        @block.vector
        def _(v):
            with v.Fori(0, B) as i:
                v.wait_ge(S["pj2"], i)
                v.tensor_copy(xs[:], XN[:, bass.ds(i * T, T)]).then_inc(S["xs"], 1)
                v.wait_ge(S["pj1"], i + 1)
                v.wait_ge(S["nturn"], i)
                v.tensor_copy(bc[:], ps[:, 4:6, :]).then_inc(S["ev2a"], 1)
                v.wait_ge(S["ev1"], i + 1)
                v.wait_ge(S["rows"], 16 * 2 * H * (i + 1))
                v.tensor_tensor(ang[:], ang[:], dtb[:], ALU.mult).then_inc(S["at"], 1)
                v.wait_ge(S["at"], i + 1)
                v.tensor_tensor_scan(th[:, 0, :], cst("onerow"), ang[:], 0.0, ALU.mult, ALU.add).then_inc(S["th"], 1)
                v.wait_ge(S["th"], i + 1)
                v.wait_ge(HD["cps"][H - 1], i)
                v.tensor_scalar(th[:, 1, :], th[:, 0, :], float(1 / (2 * np.pi)), MAGIC, ALU.mult,
                                ALU.add).then_inc(S["n"], 1)
                v.wait_ge(S["n"], i + 1)
                v.tensor_scalar(th[:, 1, :], th[:, 1, :], MAGIC, None, ALU.subtract).then_inc(S["n1"], 1)
                v.wait_ge(S["n1"], i + 1)
                v.scalar_tensor_tensor(out=th[:, 0, :], in0=th[:, 1, :], scalar=-TWO_PI_HI, in1=th[:, 0, :],
                                       op0=ALU.mult, op1=ALU.add).then_inc(S["c1"], 1)
                v.wait_ge(S["c1"], i + 1)
                v.scalar_tensor_tensor(out=th[:, 0, :], in0=th[:, 1, :], scalar=-TWO_PI_LO, in1=th[:, 0, :],
                                       op0=ALU.mult, op1=ALU.add).then_inc(S["c2"], 1)
                v.wait_ge(S["c2"], i + 1)
                v.tensor_scalar(th[:, 0, :], th[:, 0, :], 3.1415925, -3.1415925, ALU.min,
                                ALU.max).then_inc(S["clamp"], 1)
                v.wait_ge(S["rs"], i + 1)
                for n in range(2):
                    last = v.scalar_tensor_tensor(out=bc[:, n, :], in0=bc[:, n, :], scalar=W("bc_w")[:, n:n + 1],
                                                  in1=sq[:, n, :], op0=ALU.mult, op1=ALU.mult)
                last.then_inc(S["norm"], 1)
                v.wait_ge(S["cos"], i + 1)
                v.tensor_scalar(th[:, 1, :], th[:, 1, :], 1.0, None, ALU.subtract).then_inc(S["cosm"], 1)
                v.wait_ge(S["norm"], i + 1)
                v.wait_ge(S["rev"], i + 1)

                def prepare(h):
                    v.wait_ge(HD["cps"][h], i + 1)
                    if h:
                        v.wait_ge(HD["turned"][h - 1], i + 1)
                    v.wait_ge(HD["b0"][h], i + 1)
                    for n in range(2):
                        v.scalar_tensor_tensor(out=t2[:, n, :], in0=ps[:, 3, :], scalar=1.0, in1=tb[:, n, :],
                                               op0=ALU.add, op1=ALU.mult)
                        last = v.scalar_tensor_tensor(out=t3[:, n, :], in0=rot[:, n, :],
                                                      scalar=W("bc_rb")[:, n * H + h:n * H + h + 1], in1=ps[:, 4, :],
                                                      op0=ALU.add, op1=ALU.mult)
                    last.then_inc(HD["t2"][h], 1)
                    if h >= 2:
                        v.wait_ge(HD["a"][h - 2], i + 1)
                    for jk in range(NB):
                        at, n = KEYS_AT[jk], T - 128 * jk
                        last = v.tensor_scalar(dec[:, h % 2, at // T, at % T:at % T + n], ellb[:, h, jk * 128:T],
                                               COL[:, 0, jk, bass.ds(i * H + h, 1)], 0.0, ALU.subtract, ALU.min)
                    last.then_inc(HD["dd"][h], 1)

                def weigh(h):
                    v.wait_ge(HD["qk"][h], i + 1)
                    v.wait_ge(HD["dm"][h], i + 1)
                    if h >= 2:
                        v.wait_ge(HD["y"][h - 2], i + 1)
                    for jk in range(NB):
                        at, n = KEYS_AT[jk], T - 128 * jk
                        g, o = at // T, at % T
                        last = v.tensor_tensor(aw[:, h % 2, g, o:o + 128], ps[:, g, o:o + 128], dec[:, h % 2, g, o:o + 128],
                                               ALU.mult)
                        if n > 128:
                            last = v.scalar_tensor_tensor(
                                out=aw[:, h % 2, g, o + 128:o + n], in0=ps[:, g, o + 128:o + n],
                                scalar=COL[:, 1, jk, bass.ds(i * H + h, 1)], in1=dec[:, h % 2, g, o + 128:o + n],
                                op0=ALU.mult, op1=ALU.mult)
                    last.then_inc(HD["a"][h], 1)

                prepare(0)
                for h in range(H):
                    if h + 1 < H:
                        prepare(h + 1)
                    weigh(h)
                v.wait_ge(HD["y"][H - 1], i + 1)
                v.wait_ge(S["sps"], i)
                for n in range(2):
                    last = v.scalar_tensor_tensor(out=y[:, n, :], in0=xf[:, n, :], scalar=W("d")[:, n:n + 1],
                                                  in1=ps[:, 5 + n, :], op0=ALU.mult, op1=ALU.add)
                last.then_inc(S["y2"], 1)
                v.wait_ge(S["y2"], i + 1)
                v.tensor_tensor(y[:], y[:], zs[:], ALU.mult).then_inc(S["yz"], 1)


def rows_at(places, n):
    out = np.zeros((n, places[0][1].shape[1]), np.float32)
    for at, a in places:
        out[at:at + a.shape[0]] = a
    return out


def col(a):
    return np.reshape(a, (-1, 1))


def w0_parts(I):
    L = lambda n: I["L0_attn_" + n]
    return {
        "maa_x": col(L("time_maa_x")), "maa": L("time_maa").reshape(4, C).T,
        "maa_w1": L("time_maa_w1").T,
        "maa_w2": L("time_maa_w2").transpose(0, 2, 1).reshape(128, C),
        "receptance": L("receptance").T, "gate_w1": L("gate_w1").T, "gate_w2": L("gate_w2").T,
        "key_w": L("key_w").T, "value": L("value").T, "output": L("output").T,
        "kkk_mk_w1": rows_at([(0, L("time_kkk_w1")), (32, L("mk_w1"))], 64).T,
        "kkk_w2": rows_at([(0, L("time_kkk_w2").T)], 32),
        "mk_w2": rows_at([(32, L("mk_w2").T)], 64),
        "decay_aaa_ma_w1": rows_at([(0, L("time_decay_w1")), (64, L("time_aaa_w1")), (96, L("ma_w1"))], 128).T,
        "decay_w2": L("time_decay_w2").T,
        "aaa_w2": rows_at([(64, L("time_aaa_w2").T)], 96),
        "ma_w2": rows_at([(96, L("ma_w2").T)], 128),
        "decay": col(L("time_decay")), "aaaaa": col(L("time_aaaaa")), "misc_a": col(L("time_misc_a")),
        "misc_k": col(L("time_misc_k")), "ln_w": col(L("ln_w")), "ln_b": col(L("ln_b")),
        "faaaa": col(L("time_faaaa")), "router": I["L0_ffn_Wr"].T,
    }


def w1_parts(I):
    return {
        "q": I["L1_attn_Wq"].T, "k": I["L1_attn_Wk"].T,
        "v": I["L1_attn_Wv"].T, "o": I["L1_attn_Wo"].T, "gate": I["L1_ffn_Wg"],
        "ffb1": I["L1_ffn_b1"].reshape(-1, 128).T, "ffb2": I["L1_ffn_b2"].T,
    }


def w2_parts(I):
    L = lambda n: I["L2_attn_" + n]
    w, b = L("qkv_w"), L("qkv_b")
    return {
        "q": w[:, 0:C], "k": w[:, C:2 * C], "qk_b": b[0:2 * C].reshape(2, C).T,
        "v": w[:, 2 * C:], "v_b_row": np.broadcast_to(b[2 * C:], (128, C)),
        "o": L("out_w"), "o_b": col(L("out_b")), "g_attn": col(L("g_attn")), "b_attn": col(L("b_attn")),
        "g1": col(L("g1")), "b1": col(L("b1")), "g2": col(L("g2")), "b2": col(L("b2")),
        "w_ctx": L("w_ctx"), "w_x": L("w_x"), "b_inl": col(L("b_inl")),
        "ff_w1": L("ff_w1"), "ff_b1": L("ff_b1").reshape(4, 128).T,
        "ff_w2": L("ff_w2").reshape(4, 128, C).transpose(1, 0, 2).reshape(128, 4 * C), "ff_b2": col(L("ff_b2")),
    }


def w2f_parts(I):
    L = lambda n: I["L2_ffn_" + n]
    wide = lambda w: w.T.reshape(4, 128, -1).transpose(1, 0, 2).reshape(128, -1)
    cols = lambda b: b.reshape(4, 128).T
    return {
        "w1": L("w1_w").T, "w2": L("w2_w").T, "h1": wide(L("h1_w")), "h2": wide(L("h2_w")), "w3": wide(L("w3_w")),
        "s1": cols(L("w1_s")), "s2": cols(L("w2_s")), "sh1": cols(L("h1_s")), "sh2": cols(L("h2_s")),
        "s3": col(L("w3_s")),
    }


def w3f_parts(I):
    L = lambda n: I["L3_ffn_" + n]
    return {"q": L("Wq"), "k": L("Wk"), "v": L("Wv"), "wo": L("Wo"), "wff": L("Wff")}


def w3a_parts(I):
    L = lambda n: I["L3_attn_" + n]
    w = L("W_in")
    o = np.cumsum([0, 256, 256, 128, 128, 4, 4, 4, 32])
    z, x, bb, cc, dt, aa, trap, ang = [w[:, o[n]:o[n + 1]] for n in range(8)]
    rows = np.zeros((C, 3, B, B, 4), np.float32)
    for n, part in enumerate((dt, aa, trap)):
        for b in range(B):
            rows[:, n, b, b] = part

    def turned(a):
        return np.concatenate([a[..., 32:64], a[..., 0:32], np.zeros_like(a[..., 64:])], -1)

    return {
        "in": np.concatenate([z, x, bb, cc, ang, ang, ang, ang], 1), "rows": rows.reshape(C, -1),
        "out": L("W_out").reshape(2, 128, C).transpose(1, 0, 2).reshape(128, 2 * C),
        "dt_bias": col(np.broadcast_to(L("dt_bias"), (B, 4))), "bc_w": np.stack([L("B_norm_w"), L("C_norm_w")], 1),
        "bc_b": np.concatenate([L("B_bias"), L("C_bias")]).T,
        "bc_rb": turned(np.concatenate([L("B_bias"), L("C_bias")])).T,
        "d": np.repeat(L("D"), 64).reshape(2, 128).T,
    }


def constb_parts():
    i = np.arange(128)
    return {
        "identb": np.eye(128, dtype=np.float32),
        "neg_down": np.where(i[None] > i[:, None], -1e30, 0).astype(np.float32),
        "neg_across": np.where(i[:, None] > i[None], -1e30, 0).astype(np.float32),
    }


def closing(first, n):
    out = np.zeros((128, GROUPS, 128), np.float32)
    for g in range(GROUPS):
        for h in range(GH):
            for d in range(8):
                out[32 * h + first + (d if n > 1 else 0), g, 8 * (g * GH + h) + d] = 1
    return out.reshape(128, GROUPS * 128)


def const_parts():
    i = np.arange(128)
    return {
        "ident": np.eye(128, dtype=np.float32),
        "mean": np.full((128, 128), 1 / C, np.float32),
        "ones": np.ones((128, 128), np.float32),
        "headsum": (i[:, None] // 8 == i[None] // 8).astype(np.float32),
        "tri": (i[:, None] <= i[None]).astype(np.float32),
        "headmean": (i[:, None] // 8 == i[None] // 8).astype(np.float32) / 8,
        "exsum": (i[:, None] // 16 == i[None] // 16).astype(np.float32),
        "exbefore": ((i[:, None] // 16 == i[None] // 16) & (i[:, None] < i[None])).astype(np.float32),
        "onerow": np.ones((128, 512), np.float32),
        "stri": (i[:, None] < i[None]).astype(np.float32),
        "rot": ((i[:, None] < 64) & (i[None] < 64) & (i[:, None] == (i[None] + 32) % 64)).astype(np.float32),
        "spread": np.concatenate([((i[:, None] // 32 == h) & (i[None] < 64) & (i[:, None] % 32 == i[None] % 32))
                                  .astype(np.float32) for h in range(4)], 1),
        "spread_sin": np.concatenate([((i[:, None] // 32 == h) & (i[None] < 64) & (i[:, None] % 32 == i[None] % 32))
                                      * np.where(i[None] < 32, -1, 1).astype(np.float32) for h in range(4)], 1),
        "halfpi": np.full((128, 1), np.pi / 2, np.float32),
        "halfwide": np.concatenate([0.5 * (i[:, None] <= i[None]), np.full((128, T - 128), 0.5)], 1
                                   ).astype(np.float32),
        "halfcount": 0.5 * np.arange(1, T + 1, dtype=np.float32)[None],
        "close": closing(0, 8), "close_den": closing(8, 1),
        "flip": np.eye(128, dtype=np.float32)[::-1],
        "rhalf": np.full((128, 1), 0.5 ** 0.5, np.float32),
        "eps": np.full((128, 1), 1e-5, np.float32),
        "gn_eps": np.full((128, 1), 0.00064, np.float32),
        "mhalf": np.full((128, 1), -0.5, np.float32),
        "tiny": np.full((128, 1), 1e-24, np.float32),
    }


def pack(parts):
    at, place, cols = 0, {}, []
    for n, a in parts.items():
        full = np.zeros((128, a.shape[1]), np.float32)
        full[:a.shape[0]] = a
        place[n] = (at, a.shape[0], a.shape[1])
        at += a.shape[1]
        cols.append(full)
    return np.concatenate(cols, 1), place


def view(tile, place):
    def get(name):
        at, rows, n = place[name]
        return tile[0:rows, at:at + n]
    return get


def update_phase(nc, K, layer, out=None):
    X, SX, GX = K["X"], K["SX"], K["GX"]
    PARTS = 4
    N = NT // PARTS
    with ExitStack() as ctx:
        S = sems(nc, ctx, f"u{layer}", "gate prod added stored", 1)
        block = ctx.enter_context(nc.Block())

        @block.scalar
        def _(act):
            for n in range(PARTS):
                p = slice(n * N, (n + 1) * N)
                act.activation(GX[:, p], GX[:, p], ACT.Silu).then_inc(S["gate"], 1)

        @block.vector
        def _(v):
            for n in range(PARTS):
                p = slice(n * N, (n + 1) * N)
                v.wait_ge(S["gate"], n + 1)
                v.tensor_tensor(SX[:, p], SX[:, p], GX[:, p], ALU.mult).then_inc(S["prod"], 1)
                v.wait_ge(S["prod"], n + 1)
                v.tensor_tensor(X[:, p], X[:, p], SX[:, p], ALU.add).then_inc(S["added"], 1)

        if out is not None:
            @block.sync
            def _(sp):
                for n in range(PARTS):
                    p = slice(n * N, (n + 1) * N)
                    sp.wait_ge(S["added"], n + 1)
                    sp.dma_start(out[:, p], X[:, p]).then_inc(S["stored"], 16)
                sp.wait_ge(S["stored"], 16 * PARTS)


def load_phase(nc, tag, pairs):
    with ExitStack() as ctx:
        loaded = sems(nc, ctx, "ld" + tag, "loaded")["loaded"]
        block = ctx.enter_context(nc.Block())

        @block.sync
        def _(sp):
            for dst, src in pairs:
                sp.dma_start(dst, src).then_inc(loaded, 16)
            sp.wait_ge(loaded, 16 * len(pairs))


def zero_phase(nc, zero):
    with nc.Block() as block:
        @block.vector
        def _(v):
            v.memset(zero[:], 0.0)


def convert_phase(nc, dst, src):
    with nc.Block() as block:
        @block.vector
        def _(v):
            v.tensor_copy(dst, src)


def network(nc, A, out, places):
    with ExitStack() as ctx:
        K = {"A": A}
        for n in ("X", "XN", "SX", "GX"):
            K[n] = ctx.enter_context(nc.sbuf_tensor(n, [128, NT], F32))

        def weights(scope, name):
            n = places[name][1]
            tile = scope.enter_context(nc.sbuf_tensor("w_" + name, [128, n], F32))
            K[name] = view(tile, places[name][0])
            return tile[:], A[name]

        def scratch(name, shape, dtype):
            K[name] = nc.dram_tensor(name, shape, dtype, kind="Internal").ap()

        def tile(scope, name, shape, dtype, layer=""):
            K[name] = scope.enter_context(nc.sbuf_tensor(name + layer, shape, dtype))

        tile(ctx, "zero", [1, T], BF16)
        zero_phase(nc, K["zero"])
        first = [weights(ctx, "cst"), (K["X"][:], A["x"])]
        with ExitStack() as layer:
            load_phase(nc, "0", first + [weights(layer, "w0")])
            norm_phase(nc, K, "0")
            scratch("Qd", [8, B, 128, T], F32)
            scratch("Yd", [128, B, T], F32)
            scratch("Xt", [NT, C], F32)
            scratch("Acc", [NT, C], F32)
            tile(layer, "IDX", [128, E], U32)
            tile(layer, "WGT", [128, E], F32)
            with ExitStack() as choice:
                H = 64 + E
                tile(choice, "LOG", [H, NT // 2], F32)
                tile(choice, "BEST", [H, CAP], F32)
                tile(choice, "AT", [H, CAP], U32)
                tile(choice, "TOP", [H, 8], F32)
                tile(choice, "WHERE", [H, 8], U32)
                route_phase(nc, K)
                rwkv_pre_phase(nc, K)
                choice_phase(nc, K)
            scan_and_experts_phase(nc, K)
            rwkv_out_phase(nc, K)
            collect_phase(nc, K)
        update_phase(nc, K, "0")
        with ExitStack() as layer:
            load_phase(nc, "1", [weights(layer, "w1")])
            norm_phase(nc, K, "1")
            scratch("Pd1", [B, 2, 3, 2 * C, T], BF16)
            K["Pd"] = K["Pd1"]
            tile(layer, "VA", [128, NT // 128, 16, 9], F32, "1")
            split_phase(nc, K, "s1", "XN", K["w1"]("q"), K["w1"]("k"), K["w1"]("v"), 2, 16)
            causal_phase(nc, K, "ta", "SX", 16, False)
            project_phase(nc, K, "tp", "SX", K["w1"]("o"))
            scratch("Sd", [E1, NT], F32)
            scratch("Gd", [E1, NT], F32)
            choose_phase(nc, K)
            ffn1_phase(nc, K)
        update_phase(nc, K, "1")
        with ExitStack() as layer:
            load_phase(nc, "2", [weights(layer, "w2"), weights(layer, "cb_f32")])
            n = places["cb_f32"][1]
            tile(layer, "cb_tile", [128, n], BF16)
            K["cb"] = view(K["cb_tile"], places["cb_f32"][0])
            norm_phase(nc, K, "2")
            at = {p: K["cb"](p) for p in places["cb_f32"][0]}
            for p in at:
                convert_phase(nc, at[p], K["cb_f32"](p))
            norm_phase(nc, K, "2a", "XN", "SX", K["w2"]("g_attn"), K["w2"]("b_attn"))
            scratch("Pd", [B, 2, 3, C, T], BF16)
            scratch("Md", [B, 2, 16, T], BF16)
            tile(layer, "VA", [128, NT // 128, 16, 9], F32, "2")
            split_phase(nc, K, "s2", "SX", K["w2"]("q"), K["w2"]("k"), K["w2"]("v"), 1, 8, K["w2"]("qk_b"))
            maxima_phase(nc, K)
            causal_phase(nc, K, "at", "GX", 8, True)
            project_phase(nc, K, "ap", "GX", K["w2"]("o"), K["w2"]("o_b"))
            inertia_phase(nc, K)
        with ExitStack() as layer:
            load_phase(nc, "2f", [weights(layer, "w2f")])
            gated_mlp_phase(nc, K)
        update_phase(nc, K, "2")
        with ExitStack() as layer:
            load_phase(nc, "3", [weights(layer, "w3")])
            norm_phase(nc, K, "3")
            tile(layer, "VA", [128, NT // 128, 16, 9], F32, "3")
            split_phase(nc, K, "s3", "XN", K["w3"]("q"), K["w3"]("k"), K["w3"]("v"), 1, 8, qscale=float(1 / np.sqrt(C)))
            column_attention_phase(nc, K)
            l2_gelu_phase(nc, K)
        with ExitStack() as layer:
            load_phase(nc, "3a", [weights(layer, "w3a")])
            scratch("Rd", [2, B * 4, T], F32)
            tile(layer, "COL", [128, 3, NB, B * 4], F32)
            ssm_rows_phase(nc, K)
            ssm_phase(nc, K)
        update_phase(nc, K, "3", out)


def kernel(**inputs):
    import numpy as _np
    import concourse.bacc as _bacc
    from concourse import mybir as _mybir
    from concourse.bass_utils import run_bass_kernel_spmd as _run

    I = {n: _np.asarray(a) for n, a in inputs.items()}
    arrays, places = {}, {}
    for name, parts in (("cst", const_parts()), ("cb_f32", constb_parts()), ("w0", w0_parts(I)), ("w1", w1_parts(I)),
                        ("w2", w2_parts(I)), ("w2f", w2f_parts(I)), ("w3", w3f_parts(I)), ("w3a", w3a_parts(I))):
        a, place = pack(parts)
        arrays[name] = a
        places[name] = (place, a.shape[1])
    arrays["x"] = I["L0_attn_x"].reshape(NT, C).T
    arrays["e_w1"], arrays["e_w2"] = I["L0_ffn_W1"], I["L0_ffn_W2"]
    arrays["e_b1"] = I["L0_ffn_b1"].transpose(2, 0, 1).reshape(128, -1)
    arrays["e_b2"] = I["L0_ffn_b2"].reshape(1, -1)
    arrays["f1_w1"], arrays["f1_w2"] = I["L1_ffn_W1"], I["L1_ffn_W2"]
    arrays = {n: _np.ascontiguousarray(a) for n, a in arrays.items()}

    nc = _bacc.Bacc("TRN2", target_bir_lowering=False, num_devices=1)
    A = {n: nc.dram_tensor(n, a.shape, _mybir.dt.from_np(a.dtype), kind="ExternalInput").ap()
         for n, a in arrays.items()}
    out = nc.dram_tensor("out", (C, NT), F32, kind="ExternalOutput").ap()
    network(nc, A, out, places)
    r = _run(nc, [arrays], core_ids=[0])
    return _np.ascontiguousarray(r.results[0]["out"].T).reshape(B, T, C)
```

```python
from contextlib import ExitStack

import numpy as np

import concourse.bass as bass
from concourse import mybir

F32 = mybir.dt.float32
BF16 = mybir.dt.bfloat16
U32 = mybir.dt.uint32
I32 = mybir.dt.int32
ALU = mybir.AluOpType
ACT = mybir.ActivationFunctionType
AX = mybir.AxisListType

B, T, C = 8, 512, 128
NT = B * T
NB = T // 128
E, CAP, S4 = 48, 128, 4
E1, CAP1, BITS = 8, 1024, 30
LANES = 2


def sems(nc, ctx, tag, names, lanes=1):
    made = {n: [nc.alloc_semaphore(f"{tag}_{n}{a}") for a in range(lanes)] for n in names.split()}
    ctx.callback(clear, nc, [s for lane in made.values() for s in lane])
    return made if lanes > 1 else {n: s[0] for n, s in made.items()}


def clear(nc, used):
    nc.clear_and_free_semaphores(used)
    nc.all_engine_barrier()


def norm_phase(nc, K, layer, src="X", dst="XN", gain=None, shift=None):
    X, XN, cst = K[src], K[dst], K["cst"]
    L = 4
    with ExitStack() as ctx:
        S = sems(nc, ctx, f"n{layer}", "mean cent sq var std rstd gained xn", L)
        ps = ctx.enter_context(nc.psum_tensor(f"n{layer}_ps", [128, 2 * L, T], F32))
        xc = ctx.enter_context(nc.sbuf_tensor(f"n{layer}_xc", [128, L, T], F32))
        sq = ctx.enter_context(nc.sbuf_tensor(f"n{layer}_sq", [128, L, T], F32))
        block = ctx.enter_context(nc.Block())

        @block.tensor
        def _(pe):
            with pe.Fori(0, B // L) as i:
                n = i * L
                for a in range(L):
                    pe.wait_ge(S["cent"][a], i)
                    pe.matmul(ps[:, a, :], cst("mean"), X[:, bass.ds((n + a) * T, T)],
                              start=True, stop=True).then_inc(S["mean"][a], 1)
                for a in range(L):
                    pe.wait_ge(S["sq"][a], i + 1)
                    pe.wait_ge(S["std"][a], i)
                    pe.matmul(ps[:, L + a, :], cst("mean"), sq[:, a, :],
                              start=True, stop=True).then_inc(S["var"][a], 1)

        @block.vector
        def _(v):
            with v.Fori(0, B // L) as i:
                n = i * L
                for a in range(L):
                    v.wait_ge(S["mean"][a], i + 1)
                    v.wait_ge(S["xn"][a], i)
                    v.tensor_tensor(xc[:, a, :], X[:, bass.ds((n + a) * T, T)], ps[:, a, :],
                                    ALU.subtract).then_inc(S["cent"][a], 1)
                for a in range(L):
                    v.wait_ge(S["rstd"][a], i + 1)
                    if gain is None:
                        v.tensor_tensor(XN[:, bass.ds((n + a) * T, T)], xc[:, a, :], sq[:, a, :],
                                        ALU.mult).then_inc(S["xn"][a], 1)
                        continue
                    v.scalar_tensor_tensor(out=xc[:, a, :], in0=xc[:, a, :], scalar=gain, in1=sq[:, a, :],
                                           op0=ALU.mult, op1=ALU.mult).then_inc(S["gained"][a], 1)
                    v.wait_ge(S["gained"][a], i + 1)
                    v.tensor_scalar(XN[:, bass.ds((n + a) * T, T)], xc[:, a, :], shift, None,
                                    ALU.add).then_inc(S["xn"][a], 1)

        @block.scalar
        def _(act):
            with act.Fori(0, B // L) as i:
                n = i * L
                for a in range(L):
                    act.wait_ge(S["cent"][a], i + 1)
                    act.wait_ge(S["xn"][a], i)
                    act.activation(sq[:, a, :], xc[:, a, :], ACT.Square).then_inc(S["sq"][a], 1)
                for a in range(L):
                    act.wait_ge(S["var"][a], i + 1)
                    act.activation(sq[:, a, :], ps[:, L + a, :], ACT.Ln,
                                   bias=cst("eps")).then_inc(S["std"][a], 1)
                for a in range(L):
                    act.wait_ge(S["std"][a], i + 1)
                    act.activation(sq[:, a, :], sq[:, a, :], ACT.Exp, scale=-0.5).then_inc(S["rstd"][a], 1)


def rwkv_pre_phase(nc, K):
    XN, cst, W, Qd = K["XN"], K["cst"], K["w0"], K["Qd"]
    KK, EW, BB, KV, VV, RR, BON, GG = range(8)
    with ExitStack() as ctx:
        S = sems(nc, ctx, "rp", "diff xxx mixps mix delta xf lowps lowr low hips hev kksq z "
                 "lateps a ma mk nrm az ez lz w ew wm km f1 f2 k2 kn rn kkn b vps v k3 rk bonps q stored", LANES)
        ps = ctx.enter_context(nc.psum_tensor("rp_ps", [128, LANES, 4, T], F32))
        sb = lambda name, n: ctx.enter_context(nc.sbuf_tensor("rp_" + name, [128, LANES, n, T], F32))
        xp = ctx.enter_context(nc.sbuf_tensor("rp_xp", [128, LANES, T], F32))
        xf = sb("xf", 4)
        t = sb("t", 6)
        q = sb("q", 8)
        P = sems(nc, ctx, "rpp", "best at taken kept")
        block = ctx.enter_context(nc.Block())
        IT = B // LANES

        ROUNDS = CAP // 8 // IT

        def row(i, a):
            return bass.ds((i * LANES + a) * T, T)

        @block.vector
        def _(v):
            with v.Fori(0, IT) as i:
                for a in range(LANES):
                    x = XN[:, row(i, a)]
                    v.wait_ge(S["rk"][a], i)
                    v.wait_ge(S["xf"][a], i)
                    v.tensor_tensor(xp[:, a, 1:T], XN[:, bass.ds((i * LANES + a) * T, T - 1)],
                                    XN[:, bass.ds((i * LANES + a) * T + 1, T - 1)], ALU.subtract)
                    v.tensor_scalar(xp[:, a, 0:1], XN[:, bass.ds((i * LANES + a) * T, 1)], -1.0, None,
                                    ALU.mult).then_inc(S["diff"][a], 1)
                    v.wait_ge(S["diff"][a], i + 1)
                    v.wait_ge(S["mixps"][a], i)
                    v.wait_ge(S["stored"][a], 16 * i)
                    v.scalar_tensor_tensor(out=t[:, a, 0, :], in0=xp[:, a, :], scalar=W("maa_x"), in1=x,
                                           op0=ALU.mult, op1=ALU.add).then_inc(S["xxx"][a], 1)
                best_eight(v, K, P, i * ROUNDS)
                for a in range(LANES):
                    x = XN[:, row(i, a)]
                    v.wait_ge(S["delta"][a], i + 1)
                    for f in range(4):
                        last = v.scalar_tensor_tensor(out=t[:, a, 1 + f, :], in0=ps[:, a, f, :],
                                                      scalar=W("maa")[:, f:f + 1], in1=xp[:, a, :],
                                                      op0=ALU.add, op1=ALU.mult)
                    last.then_inc(S["f1"][a], 1)
                    v.wait_ge(S["f1"][a], 2 * i + 1)
                    for f in range(4):
                        last = v.tensor_tensor(xf[:, a, f, :], t[:, a, 1 + f, :], x, ALU.add)
                    last.then_inc(S["xf"][a], 1)
                for a in range(LANES):
                    v.wait_ge(S["lowps"][a], i + 1)
                    v.tensor_copy(q[:, a, RR, :], ps[:, a, 0, :]).then_inc(S["lowr"][a], 1)
                best_eight(v, K, P, i * ROUNDS + 1)
                for a in range(LANES):
                    v.wait_ge(S["hips"][a], i + 1)
                    v.tensor_copy(q[:, a, GG, :], ps[:, a, 0, :])
                    v.tensor_copy(q[:, a, KV, :], ps[:, a, 1, :])
                    v.tensor_scalar(t[:, a, 0, :], ps[:, a, 3, :], W("decay"), None,
                                    ALU.add).then_inc(S["z"][a], 1)
                    v.tensor_copy(q[:, a, KK, :], ps[:, a, 2, :]).then_inc(S["hev"][a], 1)
                for r in range(2, ROUNDS):
                    best_eight(v, K, P, i * ROUNDS + r)
                for a in range(LANES):
                    v.wait_ge(S["lz"][a], i + 1)
                    v.scalar_tensor_tensor(out=t[:, a, 0, :], in0=t[:, a, 0, :], scalar=0.0, in1=t[:, a, 1, :],
                                           op0=ALU.min, op1=ALU.subtract).then_inc(S["w"][a], 1)
                    v.wait_ge(S["mk"][a], i + 1)
                    v.wait_ge(S["w"][a], i + 1)
                    v.scalar_tensor_tensor(out=t[:, a, 2, :], in0=t[:, a, 0, :], scalar=-0.5, in1=t[:, a, 5, :],
                                           op0=ALU.add, op1=ALU.mult).then_inc(S["wm"][a], 1)
                    v.scalar_tensor_tensor(out=t[:, a, 1, :], in0=t[:, a, 4, :], scalar=-1.0, in1=t[:, a, 3, :],
                                           op0=ALU.add, op1=ALU.mult).then_inc(S["f1"][a], 1)
                    v.wait_ge(S["f1"][a], 2 * i + 2)
                    v.tensor_tensor(t[:, a, 1, :], t[:, a, 4, :], t[:, a, 1, :],
                                    ALU.subtract).then_inc(S["f2"][a], 1)
                    v.wait_ge(S["f2"][a], i + 1)
                    v.tensor_tensor(q[:, a, KV, :], q[:, a, KV, :], t[:, a, 1, :],
                                    ALU.mult).then_inc(S["k2"][a], 1)
                    v.wait_ge(S["km"][a], i + 1)
                    v.wait_ge(S["k2"][a], i + 1)
                    v.tensor_tensor(q[:, a, KV, :], q[:, a, KV, :], t[:, a, 2, :],
                                    ALU.mult).then_inc(S["k3"][a], 1)
                    v.wait_ge(S["k3"][a], i + 1)
                    v.scalar_tensor_tensor(out=t[:, a, 1, :], in0=q[:, a, RR, :], scalar=W("faaaa"),
                                           in1=q[:, a, KV, :], op0=ALU.mult, op1=ALU.mult).then_inc(S["rk"][a], 1)
                    v.wait_ge(S["rn"][a], i + 1)
                    v.tensor_tensor(q[:, a, KK, :], q[:, a, KK, :], xf[:, a, 1, :],
                                    ALU.mult).then_inc(S["kkn"][a], 1)
                    v.wait_ge(S["kkn"][a], i + 1)
                    v.scalar_tensor_tensor(out=q[:, a, BB, :], in0=q[:, a, KK, :], scalar=-1.0, in1=t[:, a, 3, :],
                                           op0=ALU.mult, op1=ALU.mult)
                    v.wait_ge(S["vps"][a], i + 1)
                    v.tensor_copy(q[:, a, VV, :], ps[:, a, 0, :]).then_inc(S["v"][a], 1)
                    v.wait_ge(S["v"][a], i + 1)
                    v.wait_ge(S["bonps"][a], i + 1)
                    v.tensor_tensor(q[:, a, BON, :], ps[:, a, 1, :], q[:, a, VV, :],
                                    ALU.mult).then_inc(S["q"][a], 1)

        @block.tensor
        def _(pe):
            with pe.Fori(0, IT) as i:
                for a in range(LANES):
                    pe.wait_ge(S["xxx"][a], i + 1)
                    pe.wait_ge(S["q"][a], i)
                    pe.matmul(ps[:, a, 0, :], W("maa_w1"), t[:, a, 0, :],
                              start=True, stop=True).then_inc(S["mixps"][a], 1)
                for a in range(LANES):
                    pe.wait_ge(S["mix"][a], i + 1)
                    for f in range(4):
                        r = slice(32 * f, 32 * f + 32)
                        last = pe.matmul(ps[:, a, f, :], W("maa_w2")[r, :], xf[r, a, 0, :], start=True, stop=True)
                    last.then_inc(S["delta"][a], 1)
                for a in range(LANES):
                    pe.wait_ge(S["xf"][a], i + 1)
                    pe.matmul(ps[:, a, 0, :], W("receptance"), xf[:, a, 0, :], start=True, stop=True)
                    pe.matmul(ps[:, a, 1, :], W("gate_w1"), xf[:, a, 0, :], start=True, stop=True)
                    pe.matmul(ps[0:64, a, 2, :], W("kkk_mk_w1"), xf[:, a, 2, :], start=True, stop=True)
                    pe.matmul(ps[:, a, 3, :], W("decay_aaa_ma_w1"), xf[:, a, 1, :],
                              start=True, stop=True).then_inc(S["lowps"][a], 1)
                for a in range(LANES):
                    pe.wait_ge(S["low"][a], i + 1)
                    pe.wait_ge(S["lowr"][a], i + 1)
                    pe.matmul(ps[:, a, 0, :], W("gate_w2"), t[:, a, 1, :], start=True, stop=True)
                    pe.matmul(ps[:, a, 1, :], W("key_w"), xf[:, a, 2, :], start=True, stop=True)
                    pe.matmul(ps[:, a, 2, :], W("key_w"), xf[:, a, 2, :], start=True, stop=False)
                    pe.matmul(ps[:, a, 2, :], W("kkk_w2"), t[0:32, a, 2, :], start=False, stop=True)
                    pe.matmul(ps[:, a, 3, :], W("decay_w2"), t[0:64, a, 3, :],
                              start=True, stop=True).then_inc(S["hips"][a], 1)
                for a in range(LANES):
                    pe.wait_ge(S["hev"][a], i + 1)
                    pe.wait_ge(S["kksq"][a], i + 1)
                    pe.matmul(ps[:, a, 0, :], W("aaa_w2")[64:96, :], t[64:96, a, 3, :], start=True, stop=True)
                    pe.matmul(ps[:, a, 1, :], W("ma_w2")[96:128, :], t[96:128, a, 3, :], start=True, stop=True)
                    pe.matmul(ps[:, a, 3, :], W("mk_w2")[32:64, :], t[32:64, a, 2, :], start=True, stop=True)
                    pe.matmul(ps[:, a, 2, :], cst("headsum"), xf[:, a, 0, :],
                              start=True, stop=True).then_inc(S["lateps"][a], 1)
                for a in range(LANES):
                    pe.wait_ge(S["a"][a], i + 1)
                    pe.matmul(ps[:, a, 0, :], W("value"), xf[:, a, 3, :],
                              start=True, stop=True).then_inc(S["vps"][a], 1)
                    pe.wait_ge(S["rk"][a], i + 1)
                    pe.matmul(ps[:, a, 1, :], cst("headsum"), t[:, a, 1, :],
                              start=True, stop=True).then_inc(S["bonps"][a], 1)

        @block.scalar
        def _(act):
            with act.Fori(0, IT) as i:
                for a in range(LANES):
                    act.wait_ge(S["mixps"][a], i + 1)
                    act.wait_ge(S["vps"][a], i)
                    act.activation(xf[:, a, 0, :], ps[:, a, 0, :], ACT.Tanh).then_inc(S["mix"][a], 1)
                for a in range(LANES):
                    act.wait_ge(S["lowps"][a], i + 1)
                    act.activation(t[:, a, 1, :], ps[:, a, 1, :], ACT.Tanh)
                    act.activation(t[0:32, a, 2, :], ps[0:32, a, 2, :], ACT.Tanh)
                    act.activation(t[32:64, a, 2, :], ps[32:64, a, 2, :], ACT.Copy)
                    act.activation(t[0:64, a, 3, :], ps[0:64, a, 3, :], ACT.Tanh)
                    act.activation(t[64:128, a, 3, :], ps[64:128, a, 3, :], ACT.Copy).then_inc(S["low"][a], 1)
                for a in range(LANES):
                    act.wait_ge(S["hev"][a], i + 1)
                    act.activation(xf[:, a, 0, :], q[:, a, KK, :], ACT.Square).then_inc(S["kksq"][a], 1)
                for a in range(LANES):
                    act.wait_ge(S["lateps"][a], i + 1)
                    act.activation(t[:, a, 3, :], ps[:, a, 0, :], ACT.Sigmoid, bias=W("aaaaa")).then_inc(S["a"][a], 1)
                    act.activation(t[:, a, 4, :], ps[:, a, 1, :], ACT.Sigmoid, bias=W("misc_a"))
                    act.activation(t[:, a, 5, :], ps[:, a, 3, :], ACT.Sigmoid, bias=W("misc_k")).then_inc(S["mk"][a], 1)
                for a in range(LANES):
                    act.activation(xf[:, a, 1, :], ps[:, a, 2, :], ACT.Ln, bias=cst("tiny")).then_inc(S["nrm"][a], 1)
                for a in range(LANES):
                    act.wait_ge(S["z"][a], i + 1)
                    act.activation(t[:, a, 1, :], t[:, a, 0, :], ACT.Abs).then_inc(S["az"][a], 1)
                    act.wait_ge(S["az"][a], i + 1)
                    act.activation(t[:, a, 1, :], t[:, a, 1, :], ACT.Exp, scale=-1.0).then_inc(S["ez"][a], 1)
                    act.wait_ge(S["nrm"][a], i + 1)
                    act.activation(xf[:, a, 1, :], xf[:, a, 1, :], ACT.Exp, scale=-0.5).then_inc(S["rn"][a], 1)
                    act.wait_ge(S["ez"][a], i + 1)
                    act.activation(t[:, a, 1, :], t[:, a, 1, :], ACT.Ln, bias=1.0).then_inc(S["lz"][a], 1)
                for a in range(LANES):
                    act.wait_ge(S["w"][a], i + 1)
                    act.activation(q[:, a, EW, :], t[:, a, 0, :], ACT.Exp, bias=cst("mhalf")).then_inc(S["ew"][a], 1)
                    act.wait_ge(S["wm"][a], i + 1)
                    act.activation(t[:, a, 2, :], t[:, a, 2, :], ACT.Exp).then_inc(S["km"][a], 1)

        @block.sync
        def _(sp):
            with sp.Fori(0, IT) as i:
                for a in range(LANES):
                    sp.wait_ge(S["q"][a], i + 1)
                    sp.wait_ge(S["ew"][a], i + 1)
                    sp.dma_start(Qd[:, i * LANES + a].rearrange("q c t -> c q t"), q[:, a]).then_inc(S["stored"][a], 16)
            for a in range(LANES):
                sp.wait_ge(S["stored"][a], 16 * IT)


def scan_and_experts_phase(nc, K):
    cst, Xt, Acc, IDX, WGT = K["cst"], K["Xt"], K["Acc"], K["IDX"], K["WGT"]
    w1d, w2d, b1d, b2d = K["A"]["e_w1"], K["A"]["e_w2"], K["A"]["e_b1"], K["A"]["e_b2"]
    Qd, Yd = K["Qd"], K["Yd"]
    H, N = 16, 8
    Qh = Qd.rearrange("q b (h n) t -> q (b h) n t", n=N)
    CH = 32
    IT = T // CH // LANES
    KK, EW, BB, KV, VV, RR = range(6)
    EL = E // IT
    EG = EL // LANES
    with ExitStack() as ctx:
        S = sems(nc, ctx, "rs", "loaded vk steps yprod y stored", LANES)
        zeroed = sems(nc, ctx, "rs", "zeroed")["zeroed"]
        F = [sems(nc, ctx, f"rsf{n}", "folded", LANES)["folded"] for n in range(2)]
        chain = sems(nc, ctx, "rsc", "chain")["chain"]
        Q = sems(nc, ctx, "rsb", "bk b0 b1 beta", LANES)
        rest = ctx.enter_context(nc.sbuf_tensor("rs_rest", [128, 2, N, N], F32))
        r = ctx.enter_context(nc.sbuf_tensor("rs_r", [128, N], F32))
        bk = ctx.enter_context(nc.sbuf_tensor("rs_bk", [128, N, CH], F32))
        beta = ctx.enter_context(nc.sbuf_tensor("rs_beta", [128, LANES, CH], F32))
        land = ctx.enter_context(nc.sbuf_tensor("rs_land", [128, LANES, 6, N, CH], F32))
        vk = ctx.enter_context(nc.sbuf_tensor("rs_vk", [128, LANES, CH, N, N], F32))
        hist = ctx.enter_context(nc.sbuf_tensor("rs_hist", [128, LANES, CH, N, N], F32))
        yp = ctx.enter_context(nc.sbuf_tensor("rs_yp", [128, CH, N, N], F32))
        y = ctx.enter_context(nc.sbuf_tensor("rs_y", [128, LANES, N, CH], F32))
        prod = ctx.enter_context(nc.sbuf_tensor("rs_prod", [128, 2, N, N], F32))
        sab = ctx.enter_context(nc.sbuf_tensor("rs_sab", [128, N], F32))
        before = ctx.enter_context(nc.sbuf_tensor("rs_before", [128, N, N], F32))
        outer = ctx.enter_context(nc.sbuf_tensor("rs_outer", [128, N, N], F32))
        X = sems(nc, ctx, "ex", "w xg idx fetched tps xgt hps h yps y added", EL)
        biases = sems(nc, ctx, "exb", "biases")["biases"]
        tps = ctx.enter_context(nc.psum_tensor("ex_tps", [128, 2, T], F32))
        hps = ctx.enter_context(nc.psum_tensor("ex_hps", [128, EG, S4, CAP], F32))
        yps = ctx.enter_context(nc.psum_tensor("ex_yps", [128, 2, 512], F32))
        w1 = ctx.enter_context(nc.sbuf_tensor("ex_w1", [128, EL, S4, 128], F32))
        w2 = ctx.enter_context(nc.sbuf_tensor("ex_w2", [128, EL, S4, 32], F32))
        b1 = ctx.enter_context(nc.sbuf_tensor("ex_b1", [128, E * S4], F32))
        b2 = ctx.enter_context(nc.sbuf_tensor("ex_b2", [1, EL, C], F32))
        idx = ctx.enter_context(nc.sbuf_tensor("ex_idx", [CAP, EL], U32))
        xg = ctx.enter_context(nc.sbuf_tensor("ex_xg", [CAP, EL, C], F32))
        xgt = ctx.enter_context(nc.sbuf_tensor("ex_xgt", [128, EL, CAP], F32))
        h = ctx.enter_context(nc.sbuf_tensor("ex_h", [128, EG, S4, CAP], F32))
        ye = ctx.enter_context(nc.sbuf_tensor("ex_y", [CAP, EL, C], F32))
        block = ctx.enter_context(nc.Block())

        def load(sp, i, a):
            for q in range(6):
                sp.dma_start(land[:, a, q], Qh[q, :, :, bass.ds((i * LANES + a) * CH, CH)]).then_inc(S["loaded"][a], 16)

        @block.sync
        def _(sp):
            sp.dma_start(b1[:], b1d).then_inc(biases, 16)
            with sp.Fori(0, IT) as i:
                for a in range(LANES):
                    sp.wait_ge(Q["beta"][1 - a], i + a)
                    sp.wait_ge(S["steps"][a], i)
                    sp.wait_ge(S["yprod"][a], i)
                    load(sp, i, a)
                    for e in range(a * EG, (a + 1) * EG):
                        sp.wait_ge(X["yps"][e], i)
                        sp.dma_start(w1[:, e], w1d[i * EL + e].rearrange("s d m -> d s m")).then_inc(X["w"][e], 16)
                        sp.dma_start(w2[:, e], w2d[i * EL + e].rearrange("s m k -> m s k")).then_inc(X["w"][e], 16)
                        sp.dma_start(b2[:, e], b2d[0:1, bass.ds((i * EL + e) * C, C)]).then_inc(X["w"][e], 16)

        @block.gpsimd
        def _(g):
            def pairs(i, a):
                g.wait_ge(S["loaded"][a], 96 * (i + 1))
                g.wait_ge(S["steps"][a], i)
                kt = land[:, a, KV].rearrange("p n t -> p t n")
                vt = land[:, a, VV].rearrange("p n t -> p t n")
                for n in range(N):
                    last = g.tensor_tensor(vk[:, a, :, n, :], kt, vt[:, :, n:n + 1].to_broadcast([128, CH, N]),
                                           ALU.mult)
                last.then_inc(S["vk"][a], 1)

            def products(i, a, first):
                g.wait_ge(Q["beta"][1 - a], i + a)
                kk, b, b_last = land[:, a, KK], land[:, a, BB], land[:, 1 - a, BB, :, CH - 1:CH]
                if first:
                    g.wait_ge(zeroed, 1)
                else:
                    g.tensor_tensor(bk[:, :, 0:1], kk[:, :, 0:1], b_last, ALU.mult)
                g.tensor_tensor(bk[:, :, 1:CH], kk[:, :, 1:CH], b[:, :, 0:CH - 1], ALU.mult).then_inc(Q["bk"][a], 1)
                g.wait_ge(Q["bk"][a], i + 1)
                g.tensor_tensor(bk[:, 0:4], bk[:, 0:4], bk[:, 4:8], ALU.add).then_inc(Q["b0"][a], 1)
                g.wait_ge(Q["b0"][a], i + 1)
                g.tensor_tensor(bk[:, 0:2], bk[:, 0:2], bk[:, 2:4], ALU.add).then_inc(Q["b1"][a], 1)
                g.wait_ge(Q["b1"][a], i + 1)
                g.tensor_tensor(beta[:, a, :], bk[:, 0, :], bk[:, 1, :], ALU.add).then_inc(Q["beta"][a], 1)

            def outputs(i, a):
                g.wait_ge(S["steps"][a], i + 1)
                g.wait_ge(S["stored"][a], 16 * i)
                g.wait_ge(S["y"][1 - a], i + a)
                rt = land[:, a, RR].rearrange("p n t -> p t n")
                for n in range(N):
                    last = g.tensor_tensor(yp[:, :, n, :], hist[:, a, :, n, :], rt, ALU.mult)
                last.then_inc(S["yprod"][a], 1)
                g.wait_ge(S["yprod"][a], i + 1)
                yt = y[:, a].rearrange("p n t -> p t n")
                for half, step in ((4, 0), (2, 1), (1, 2)):
                    out = yt if half == 1 else yp[:, :, :, 0:half]
                    if step:
                        g.wait_ge(F[step - 1][a], i + 1)
                    if half == 1:
                        out = yt.unsqueeze(3)
                    g.tensor_tensor(out, yp[:, :, :, 0:half], yp[:, :, :, half:2 * half],
                                    ALU.add).then_inc(S["y"][a] if half == 1 else F[step][a], 1)

            def fetch(i, a):
                for e in range(a * EG, (a + 1) * EG):
                    g.wait_ge(X["added"][e], 16 * i)
                    g.nop(nofuse=True)
                    g.tensor_copy(idx[:, e:e + 1], IDX[:, bass.ds(i * EL + e, 1)]).then_inc(X["idx"][e], 1)
                for e in range(a * EG, (a + 1) * EG):
                    g.wait_ge(X["tps"][e], i)
                    g.wait_ge(X["idx"][e], i + 1)
                    g.nop(nofuse=True)
                    g.indirect_dma_start(xg[:, e, :], None, Xt,
                                         bass.IndirectOffsetOnAxis(ap=idx[:, e:e + 1], axis=0)
                                         ).then_inc(X["fetched"][e], 16)

            def add(i, e):
                g.wait_ge(X["y"][e], i + 1)
                if e:
                    g.wait_ge(X["added"][e - 1], 16 * (i + 1))
                else:
                    g.wait_ge(X["added"][EL - 1], 16 * i)
                g.nop(nofuse=True)
                g.indirect_dma_start(Acc, bass.IndirectOffsetOnAxis(ap=idx[:, e:e + 1], axis=0),
                                     ye[:, e, :], None, compute_op=ALU.add).then_inc(X["added"][e], 16)

            def chunk(i, a, last):
                if not last:
                    pairs(i + a, 1 - a)
                    products(i + a, 1 - a, False)
                add(i, a * EG)
                outputs(i, a)
                add(i, a * EG + 1)
                if not last:
                    fetch(i + a, 1 - a)
                add(i, a * EG + 2)

            fetch(0, 0)
            pairs(0, 0)
            products(0, 0, True)
            with g.Fori(0, IT - 1) as i:
                chunk(i, 0, False)
                chunk(i, 1, False)
            chunk(IT - 1, 0, False)
            chunk(IT - 1, 1, True)
            g.wait_ge(X["added"][EL - 1], 16 * IT)

        @block.tensor
        def _(pe):
            with pe.Fori(0, IT) as i:
                for a in range(LANES):
                    group = range(a * EG, (a + 1) * EG)
                    for e in group:
                        pe.wait_ge(X["fetched"][e], 16 * (i + 1))
                        if e >= 2:
                            pe.wait_ge(X["xgt"][e - 2], i + 1)
                        else:
                            pe.wait_ge(X["xgt"][e + EL - 2], i)
                        pe.transpose(tps[:, e % 2, 0:CAP], xg[:, e, :], cst("ident")).then_inc(X["tps"][e], 1)
                        pe.wait_ge(X["xgt"][e], i + 1)
                        pe.wait_ge(X["w"][e], 48 * (i + 1))
                        if e >= EG:
                            pe.wait_ge(X["h"][e - EG], i + 1)
                        else:
                            pe.wait_ge(X["h"][e + EG], i)
                        for s in range(S4):
                            last = pe.matmul(hps[:, e % EG, s, :], w1[:, e, s, :], xgt[:, e, :], start=True, stop=True)
                        last.then_inc(X["hps"][e], 1)
                    for e in group:
                        pe.wait_ge(X["h"][e], i + 1)
                        if e >= 2:
                            pe.wait_ge(X["y"][e - 2], i + 1)
                        else:
                            pe.wait_ge(X["y"][e + EL - 2], i)
                        out = yps[:, e % 2, 0:C]
                        pe.matmul(out, cst("ones")[0:1, :], b2[0:1, e, :], start=True, stop=False,
                                  skip_group_check=True)
                        for s in range(S4):
                            last = pe.matmul(out[:, 32 * s:32 * s + 32], h[:, e % EG, s, :], w2[:, e, s, :],
                                             start=False, stop=(s == S4 - 1), skip_group_check=True)
                        last.then_inc(X["yps"][e], 1)

        @block.vector
        def _(v):
            v.memset(rest[:, 1], 0.0)
            v.memset(outer[:], 0.0)
            v.memset(sab[:], 0.0)
            v.memset(bk[:], 0.0).then_inc(zeroed, 1)
            v.wait_ge(zeroed, 1)
            with v.Fori(0, IT) as i:
                for a in range(LANES):
                    v.wait_ge(S["vk"][a], i + 1)
                    v.wait_ge(Q["beta"][a], i + 1)
                    v.wait_ge(S["loaded"][a], 96 * (i + 1))
                    v.wait_ge(S["yprod"][a], i)
                    KKM, ADD, RED, EWM, SAB, REST, OUTER = range(1, 8)
                    for t in range(CH):
                        prev = hist[:, a, t - 1] if t else before[:]
                        c = 7 * t
                        if t:
                            v.wait_ge(chain, c - 7 + REST)
                        v.tensor_tensor(prod[:, 0], rest[:, (t + 1) % 2],
                                        land[:, a, KK, :, t].unsqueeze(1).to_broadcast([128, N, N]),
                                        ALU.mult).then_inc(chain, 1)
                        if t:
                            v.wait_ge(chain, c - 7 + OUTER)
                        v.tensor_tensor(prev, rest[:, (t + 1) % 2], outer[:], ALU.add).then_inc(chain, 1)
                        v.wait_ge(chain, c + KKM)
                        v.tensor_reduce(r[:], prod[:, 0], AX.X, ALU.add).then_inc(chain, 1)
                        v.wait_ge(chain, c + ADD)
                        v.tensor_tensor(prod[:, 1], prev, land[:, a, EW, :, t].unsqueeze(1).to_broadcast([128, N, N]),
                                        ALU.mult).then_inc(chain, 1)
                        v.wait_ge(chain, c + RED)
                        v.scalar_tensor_tensor(out=sab[:], in0=sab[:], scalar=beta[:, a, t:t + 1], in1=r[:],
                                               op0=ALU.mult, op1=ALU.add).then_inc(chain, 1)
                        v.wait_ge(chain, c + EWM)
                        v.tensor_tensor(rest[:, t % 2], prod[:, 1], vk[:, a, t], ALU.add).then_inc(chain, 1)
                        v.wait_ge(chain, c + SAB)
                        v.tensor_tensor(outer[:], sab[:].unsqueeze(2).to_broadcast([128, N, N]),
                                        land[:, a, BB, :, t].unsqueeze(1).to_broadcast([128, N, N]),
                                        ALU.mult).then_inc(chain, 1)
                    v.wait_ge(chain, 7 * CH)
                    v.tensor_tensor(hist[:, a, CH - 1], rest[:, (CH - 1) % 2], outer[:], ALU.add).then_inc(chain, 1)
                    v.wait_ge(chain, 7 * CH + 1)
                    v.sem_clear(chain)
                    v.nop().then_inc(S["steps"][a], 1)

        @block.scalar
        def _(act):
            act.wait_ge(biases, 16)
            with act.Fori(0, IT) as i:
                for a in range(LANES):
                    group = range(a * EG, (a + 1) * EG)
                    for e in group:
                        act.wait_ge(X["tps"][e], i + 1)
                        act.wait_ge(X["hps"][e], i)
                        act.activation(xgt[:, e, :], tps[:, e % 2, 0:CAP], ACT.Copy).then_inc(X["xgt"][e], 1)
                    for e in group:
                        act.wait_ge(X["hps"][e], i + 1)
                        if e >= EG:
                            act.wait_ge(X["yps"][e - EG], i + 1)
                        else:
                            act.wait_ge(X["yps"][e + EG], i)
                        for s in range(S4):
                            last = act.activation(h[:, e % EG, s, :], hps[:, e % EG, s, :], ACT.Gelu,
                                                  bias=b1[:, bass.ds((i * EL + e) * S4 + s, 1)])
                        last.then_inc(X["h"][e], 1)
                    for e in group:
                        act.wait_ge(X["yps"][e], i + 1)
                        act.wait_ge(X["added"][e], 16 * i)
                        act.activation(ye[:, e, :], yps[:, e % 2, 0:C], ACT.Copy,
                                       scale=WGT[:, bass.ds(i * EL + e, 1)]).then_inc(X["y"][e], 1)
                    act.wait_ge(S["y"][a], i + 1)
                    act.dma_start(Yd[:, :, bass.ds((i * LANES + a) * CH, CH)], y[:, a]).then_inc(S["stored"][a], 16)
            for a in range(LANES):
                act.wait_ge(S["stored"][a], 16 * IT)


def rwkv_out_phase(nc, K):
    SX, cst, W, Qd, Yd = K["SX"], K["cst"], K["w0"], K["Qd"], K["Yd"]
    Yv = Yd.rearrange("(b h) v t -> b (h v) t", b=B)
    L = 4
    IT = B // L
    with ExitStack() as ctx:
        S = sems(nc, ctx, "ro", "loaded mean cent sq var std rstd yn ynb yb o sps s", L)
        ps = ctx.enter_context(nc.psum_tensor("ro_ps", [128, L, 2, T], F32))
        y = ctx.enter_context(nc.sbuf_tensor("ro_y", [128, L, 3, T], F32))
        sq = ctx.enter_context(nc.sbuf_tensor("ro_sq", [128, L, T], F32))
        block = ctx.enter_context(nc.Block())

        @block.sync
        def _(sp):
            with sp.Fori(0, IT) as i:
                for a in range(L):
                    sp.wait_ge(S["sps"][a], i)
                    sp.dma_start(y[:, a, 0, :], Yv[i * L + a]).then_inc(S["loaded"][a], 16)
                    sp.dma_start(y[:, a, 1:3, :], Qd[6:8, i * L + a].rearrange("q c t -> c q t")).then_inc(S["loaded"][a], 16)

        @block.tensor
        def _(pe):
            with pe.Fori(0, IT) as i:
                for a in range(L):
                    pe.wait_ge(S["loaded"][a], 32 * (i + 1))
                    pe.wait_ge(S["s"][a], i)
                    pe.matmul(ps[:, a, 0, :], cst("headmean"), y[:, a, 0, :],
                              start=True, stop=True).then_inc(S["mean"][a], 1)
                for a in range(L):
                    pe.wait_ge(S["sq"][a], i + 1)
                    pe.wait_ge(S["std"][a], i)
                    pe.matmul(ps[:, a, 1, :], cst("headmean"), sq[:, a, :],
                              start=True, stop=True).then_inc(S["var"][a], 1)
                for a in range(L):
                    pe.wait_ge(S["o"][a], i + 1)
                    pe.matmul(ps[:, a, 0, :], W("output"), y[:, a, 0, :],
                              start=True, stop=True).then_inc(S["sps"][a], 1)

        @block.scalar
        def _(act):
            with act.Fori(0, IT) as i:
                for a in range(L):
                    act.wait_ge(S["cent"][a], i + 1)
                    act.wait_ge(S["yn"][a], i)
                    act.activation(sq[:, a, :], y[:, a, 0, :], ACT.Square).then_inc(S["sq"][a], 1)
                for a in range(L):
                    act.wait_ge(S["var"][a], i + 1)
                    act.activation(sq[:, a, :], ps[:, a, 1, :], ACT.Ln, bias=cst("gn_eps")).then_inc(S["std"][a], 1)
                for a in range(L):
                    act.wait_ge(S["std"][a], i + 1)
                    act.activation(sq[:, a, :], sq[:, a, :], ACT.Exp, scale=-0.5).then_inc(S["rstd"][a], 1)
                for a in range(L):
                    act.wait_ge(S["sps"][a], i + 1)
                    act.activation(SX[:, bass.ds((i * L + a) * T, T)], ps[:, a, 0, :], ACT.Copy).then_inc(S["s"][a], 1)

        @block.vector
        def _(v):
            with v.Fori(0, IT) as i:
                for a in range(L):
                    v.wait_ge(S["mean"][a], i + 1)
                    v.tensor_tensor(y[:, a, 0, :], y[:, a, 0, :], ps[:, a, 0, :], ALU.subtract).then_inc(S["cent"][a], 1)
                for a in range(L):
                    v.wait_ge(S["rstd"][a], i + 1)
                    v.tensor_tensor(y[:, a, 0, :], y[:, a, 0, :], sq[:, a, :], ALU.mult).then_inc(S["yn"][a], 1)
                    v.wait_ge(S["yn"][a], i + 1)
                    v.tensor_scalar(y[:, a, 0, :], y[:, a, 0, :], W("ln_w"), W("ln_b"), ALU.mult, ALU.add).then_inc(S["ynb"][a], 1)
                    v.wait_ge(S["ynb"][a], i + 1)
                    v.tensor_tensor(y[:, a, 0, :], y[:, a, 0, :], y[:, a, 1, :], ALU.add).then_inc(S["yb"][a], 1)
                    v.wait_ge(S["yb"][a], i + 1)
                    v.tensor_tensor(y[:, a, 0, :], y[:, a, 0, :], y[:, a, 2, :], ALU.mult).then_inc(S["o"][a], 1)


def route_phase(nc, K):
    XN, cst, W, Xt, Acc, LOG = K["XN"], K["cst"], K["w0"], K["Xt"], K["Acc"], K["LOG"]
    IT = B // 2
    Xv = Xt.rearrange("(b j p) c -> b p j c", p=128, j=NB)
    with ExitStack() as ctx:
        S = sems(nc, ctx, "rt", "xs logps logit tps tok stored", 2)
        P = sems(nc, ctx, "rtp", "zero zeroed blank")
        lps = ctx.enter_context(nc.psum_tensor("rt_lps", [128, 2, T], F32))
        tps = ctx.enter_context(nc.psum_tensor("rt_tps", [128, 2, NB, C], F32))
        xs = ctx.enter_context(nc.sbuf_tensor("rt_xs", [128, 2, T], F32))
        tok = ctx.enter_context(nc.sbuf_tensor("rt_tok", [128, 2, NB, C], F32))
        zero = ctx.enter_context(nc.sbuf_tensor("rt_zero", [128, NT // 128 * C], F32))
        block = ctx.enter_context(nc.Block())
        half = lambda a: slice(64 * a, 64 * a + E)

        @block.tensor
        def _(pe):
            with pe.Fori(0, IT) as i:
                for a in range(2):
                    pe.wait_ge(S["xs"][a], i + 1)
                    pe.wait_ge(S["logit"][a], i)
                    pe.wait_ge(S["tok"][a], i)
                    pe.matmul(lps[half(a), a, :], W("router"), xs[:, a, :],
                              start=True, stop=True).then_inc(S["logps"][a], 1)
                    for j in range(NB):
                        last = pe.transpose(tps[:, a, j, :], xs[:, a, j * 128:(j + 1) * 128], cst("ident"))
                    last.then_inc(S["tps"][a], 1)

        @block.scalar
        def _(act):
            act.wait_ge(P["blank"], 1)
            with act.Fori(0, IT) as i:
                for a in range(2):
                    act.wait_ge(S["tps"][a], i)
                    act.activation(xs[:, a, :], XN[:, bass.ds((a * IT + i) * T, T)],
                                   ACT.Copy).then_inc(S["xs"][a], 1)
                for a in range(2):
                    act.wait_ge(S["logps"][a], i + 1)
                    act.activation(LOG[half(a), bass.ds(i * T, T)], lps[half(a), a, :],
                                   ACT.Copy).then_inc(S["logit"][a], 1)

        @block.vector
        def _(v):
            v.memset(LOG[32:64], 0.0).then_inc(P["blank"], 1)
            v.memset(zero[:], 0.0).then_inc(P["zero"], 1)
            with v.Fori(0, IT) as i:
                for a in range(2):
                    v.wait_ge(S["tps"][a], i + 1)
                    v.wait_ge(S["stored"][a], 16 * i)
                    v.tensor_copy(tok[:, a], tps[:, a]).then_inc(S["tok"][a], 1)

        @block.sync
        def _(sp):
            sp.wait_ge(P["zero"], 1)
            sp.dma_start(Acc.rearrange("(p r) c -> p (r c)", p=128), zero[:]).then_inc(P["zeroed"], 16)
            with sp.Fori(0, IT) as i:
                for a in range(2):
                    sp.wait_ge(S["tok"][a], i + 1)
                    sp.dma_start(Xv[a * IT + i], tok[:, a]).then_inc(S["stored"][a], 16)
            sp.wait_ge(P["zeroed"], 16)
            for a in range(2):
                sp.wait_ge(S["stored"][a], 16 * IT)


def best_eight(v, K, P, r):
    LOG, best, at, top, where = K["LOG"], K["BEST"], K["AT"], K["TOP"], K["WHERE"]
    eight = bass.ds(r * 8, 8)
    v.wait_ge(P["taken"], r)
    v.wait_ge(P["kept"], r)
    v.nop(nofuse=True)
    v.max(top[:], LOG[:]).then_inc(P["best"], 1)
    v.wait_ge(P["best"], r + 1)
    v.nop(nofuse=True)
    v.max_index(where[:], top[:], LOG[:]).then_inc(P["at"], 1)
    v.wait_ge(P["at"], r + 1)
    v.nop(nofuse=True)
    v.match_replace(LOG[:], top[:], LOG[:], -3.0e38).then_inc(P["taken"], 1)
    v.tensor_copy(best[:, eight], top[:])
    v.tensor_copy(at[:, eight], where[:]).then_inc(P["kept"], 1)


def choice_phase(nc, K):
    cst, IDX, WGT, best, at = K["cst"], K["IDX"], K["WGT"], K["BEST"], K["AT"]
    H = K["LOG"].shape[0]
    half = lambda a: slice(64 * a, 64 * a + E)
    with ExitStack() as ctx:
        P = sems(nc, ctx, "ch", "atf turned side flipped at2 val first diff gated rows neg e rsum w cols idx")
        tps = ctx.enter_context(nc.psum_tensor("ch_tps", [128, 2, H], F32))
        fps = ctx.enter_context(nc.psum_tensor("ch_fps", [128, 2, E], F32))
        rps = ctx.enter_context(nc.psum_tensor("ch_rps", [E, CAP], F32))
        wps = ctx.enter_context(nc.psum_tensor("ch_wps", [128, E], F32))
        atf = ctx.enter_context(nc.sbuf_tensor("ch_atf", [H, CAP], F32))
        t = ctx.enter_context(nc.sbuf_tensor("ch_t", [128, 2, H], F32))
        val = ctx.enter_context(nc.sbuf_tensor("ch_val", [128, E], F32))
        first = ctx.enter_context(nc.sbuf_tensor("ch_first", [128, E], F32))
        second = ctx.enter_context(nc.sbuf_tensor("ch_second", [128, E], F32))
        diff = ctx.enter_context(nc.sbuf_tensor("ch_diff", [128, E], F32))
        w = ctx.enter_context(nc.sbuf_tensor("ch_w", [E, CAP], F32))
        small = ctx.enter_context(nc.sbuf_tensor("ch_small", [E, 3], F32))
        block = ctx.enter_context(nc.Block())

        @block.tensor
        def _(pe):
            pe.wait_ge(P["atf"], 1)
            pe.transpose(tps[:, 0, :], best[:], cst("ident")[0:H, 0:H])
            pe.transpose(tps[:, 1, :], atf[:], cst("ident")[0:H, 0:H]).then_inc(P["turned"], 1)
            pe.wait_ge(P["side"], 1)
            for n in range(2):
                last = pe.matmul(fps[:, n, :], cst("flip"), t[:, n, half(1)], start=True, stop=True)
            last.then_inc(P["flipped"], 1)
            pe.wait_ge(P["val"], 1)
            pe.transpose(rps[:], val[:], cst("ident")).then_inc(P["rows"], 1)
            pe.wait_ge(P["w"], 1)
            pe.transpose(wps[:], w[:], cst("ident")[0:E, 0:E]).then_inc(P["cols"], 1)

        @block.scalar
        def _(act):
            act.wait_ge(P["neg"], 1)
            act.activation(w[:], rps[:], ACT.Exp, bias=small[:, 0:1], accum_out=small[:, 1:2]).then_inc(P["e"], 1)

        @block.vector
        def _(v):
            v.tensor_copy(atf[:], at[:]).then_inc(P["atf"], 1)
            v.wait_ge(P["turned"], 1)
            v.tensor_copy(t[:], tps[:]).then_inc(P["side"], 1)
            v.wait_ge(P["flipped"], 1)
            v.tensor_tensor(first[:], t[:, 0, half(0)], fps[:, 0, :], ALU.is_ge).then_inc(P["first"], 1)
            v.tensor_tensor(val[:], t[:, 0, half(0)], fps[:, 0, :], ALU.max).then_inc(P["val"], 1)
            v.tensor_scalar(second[:], fps[:, 1, :], float(NT // 2), None, ALU.add).then_inc(P["at2"], 1)
            v.wait_ge(P["at2"], 1)
            v.tensor_tensor(diff[:], t[:, 1, half(0)], second[:], ALU.subtract).then_inc(P["diff"], 1)
            v.wait_ge(P["first"], 1)
            v.wait_ge(P["diff"], 1)
            v.tensor_tensor(diff[:], diff[:], first[:], ALU.mult).then_inc(P["gated"], 1)
            v.wait_ge(P["gated"], 1)
            v.tensor_tensor(IDX[:], second[:], diff[:], ALU.add).then_inc(P["idx"], 1)
            v.wait_ge(P["rows"], 1)
            v.tensor_reduce(small[:, 0:1], rps[:], AX.X, ALU.max, negate=True).then_inc(P["neg"], 1)
            v.wait_ge(P["e"], 1)
            v.reciprocal(small[:, 2:3], small[:, 1:2]).then_inc(P["rsum"], 1)
            v.wait_ge(P["rsum"], 1)
            v.tensor_scalar(w[:], w[:], small[:, 2:3], None, ALU.mult).then_inc(P["w"], 1)
            v.wait_ge(P["cols"], 1)
            v.tensor_copy(WGT[:], wps[:])


def collect_phase(nc, K):
    GX, cst, Acc = K["GX"], K["cst"], K["Acc"]
    Av = Acc.rearrange("(b j p) c -> b p j c", p=128, j=NB)
    with ExitStack() as ctx:
        S = sems(nc, ctx, "co", "loaded tps g", LANES)
        tps = ctx.enter_context(nc.psum_tensor("co_tps", [128, LANES, T], F32))
        acc = ctx.enter_context(nc.sbuf_tensor("co_acc", [128, LANES, NB, C], F32))
        block = ctx.enter_context(nc.Block())

        @block.sync
        def _(sp):
            with sp.Fori(0, B // LANES) as i:
                for a in range(LANES):
                    sp.wait_ge(S["tps"][a], i)
                    sp.dma_start(acc[:, a], Av[i * LANES + a]).then_inc(S["loaded"][a], 16)

        @block.tensor
        def _(pe):
            with pe.Fori(0, B // LANES) as i:
                for a in range(LANES):
                    pe.wait_ge(S["loaded"][a], 16 * (i + 1))
                    pe.wait_ge(S["g"][a], i)
                    for j in range(NB):
                        last = pe.transpose(tps[:, a, j * 128:(j + 1) * 128], acc[:, a, j, :], cst("ident"))
                    last.then_inc(S["tps"][a], 1)

        @block.scalar
        def _(act):
            with act.Fori(0, B // LANES) as i:
                for a in range(LANES):
                    act.wait_ge(S["tps"][a], i + 1)
                    act.activation(GX[:, bass.ds((i * LANES + a) * T, T)], tps[:, a, :], ACT.Copy).then_inc(S["g"][a], 1)


KEYS_AT = {0: 0, 1: T, 3: T + 384, 2: 2 * T}
SPAN = 2 * T + 256


def choose_phase(nc, K):
    XN, cst, W, Sd, Gd = K["XN"], K["cst"], K["w1"], K["Sd"], K["Gd"]
    IT = B // LANES
    PER = 128 // E1
    with ExitStack() as ctx:
        S = sems(nc, ctx, "ch", "logps score", LANES)
        P = sems(nc, ctx, "chp", "out back thr0 cand count total keep thr gt need eqn off rank ok sel gate stored")
        lps = ctx.enter_context(nc.psum_tensor("ch_lps", [128, LANES, T], F32))
        tot = ctx.enter_context(nc.psum_tensor("ch_tot", [128, 1], F32))
        rows = ctx.enter_context(nc.sbuf_tensor("ch_rows", [E1, NT], F32))
        sc = ctx.enter_context(nc.sbuf_tensor("ch_sc", [128, NT // PER], F32))
        m = ctx.enter_context(nc.sbuf_tensor("ch_m", [128, 3, NT // PER], F32))
        thr = ctx.enter_context(nc.sbuf_tensor("ch_thr", [128, 1], F32))
        cand = ctx.enter_context(nc.sbuf_tensor("ch_cand", [128, 1], F32))
        cnt = ctx.enter_context(nc.sbuf_tensor("ch_cnt", [128, 1], F32))
        keep = ctx.enter_context(nc.sbuf_tensor("ch_keep", [128, 1], U32))
        need = ctx.enter_context(nc.sbuf_tensor("ch_need", [128, 1], F32))
        block = ctx.enter_context(nc.Block())

        @block.tensor
        def _(pe):
            with pe.Fori(0, IT) as i:
                for a in range(LANES):
                    pe.wait_ge(S["score"][a], i)
                    pe.matmul(lps[0:E1, a, :], W("gate"), XN[:, bass.ds((i * LANES + a) * T, T)],
                              start=True, stop=True).then_inc(S["logps"][a], 1)
            for n in range(BITS + 1):
                pe.wait_ge(P["count"], n + 1)
                pe.matmul(tot[:], cst("exsum"), cnt[:], start=True, stop=True).then_inc(P["total"], 1)
            pe.wait_ge(P["eqn"], 1)
            pe.wait_ge(P["need"], 1)
            pe.matmul(tot[:], cst("exbefore"), cnt[:], start=True, stop=True).then_inc(P["off"], 1)

        @block.scalar
        def _(act):
            with act.Fori(0, IT) as i:
                for a in range(LANES):
                    act.wait_ge(S["logps"][a], i + 1)
                    act.activation(rows[:, bass.ds((i * LANES + a) * T, T)], lps[0:E1, a, :],
                                   ACT.Sigmoid).then_inc(S["score"][a], 1)

        @block.sync
        def _(sp):
            for a in range(LANES):
                sp.wait_ge(S["score"][a], IT)
            sp.dma_start(Sd, rows[:]).then_inc(P["out"], 16)
            sp.wait_ge(P["out"], 16)
            sp.dma_start(sc[:], Sd.rearrange("e (p t) -> (e p) t", p=PER)).then_inc(P["back"], 16)
            sp.wait_ge(P["gate"], 1)
            sp.dma_start(Gd.rearrange("e (p t) -> (e p) t", p=PER), m[:, 0, :]).then_inc(P["stored"], 16)
            sp.wait_ge(P["stored"], 16)

        @block.vector
        def _(v):
            v.memset(thr[:], 0.0).then_inc(P["thr0"], 1)
            v.wait_ge(P["thr0"], 1)
            v.wait_ge(P["back"], 16)
            for n in range(BITS):
                bit = 1 << (BITS - 1 - n)
                v.wait_ge(P["thr"], n)
                v.tensor_scalar(cand[:].bitcast(I32), thr[:].bitcast(I32), bit, None,
                                ALU.bitwise_or).then_inc(P["cand"], 1)
                v.wait_ge(P["cand"], n + 1)
                v.tensor_scalar(m[:, 0, :], sc[:], cand[:, 0:1], None, ALU.is_ge, ALU.add,
                                accum_out=cnt[:]).then_inc(P["count"], 1)
                v.wait_ge(P["total"], n + 1)
                v.tensor_scalar(keep[:], tot[:], float(CAP1), None, ALU.is_ge).then_inc(P["keep"], 1)
                v.wait_ge(P["keep"], n + 1)
                v.copy_predicated(thr[:], keep[:], cand[:]).then_inc(P["thr"], 1)
            v.wait_ge(P["thr"], BITS)
            v.tensor_scalar(m[:, 0, :], sc[:], thr[:, 0:1], None, ALU.is_gt, ALU.add,
                            accum_out=cnt[:]).then_inc(P["count"], 1)
            v.wait_ge(P["total"], BITS + 1)
            v.tensor_scalar(need[:], tot[:], -1.0, float(CAP1), ALU.mult, ALU.add).then_inc(P["need"], 1)
            v.tensor_scalar(m[:, 1, :], sc[:], thr[:, 0:1], None, ALU.is_equal, ALU.add,
                            accum_out=cnt[:]).then_inc(P["eqn"], 1)
            v.wait_ge(P["eqn"], 1)
            v.wait_ge(P["off"], 1)
            v.tensor_tensor_scan(m[:, 2, :], cst("onerow")[:, 0:NT // PER], m[:, 1, :], 0.0, ALU.mult,
                                 ALU.add).then_inc(P["rank"], 1)
            v.wait_ge(P["rank"], 1)
            v.tensor_scalar(need[:], need[:], tot[:, 0:1], None, ALU.subtract).then_inc(P["rank"], 1)
            v.wait_ge(P["rank"], 2)
            v.scalar_tensor_tensor(out=m[:, 2, :], in0=m[:, 2, :], scalar=need[:, 0:1], in1=m[:, 1, :],
                                   op0=ALU.is_le, op1=ALU.mult).then_inc(P["ok"], 1)
            v.wait_ge(P["ok"], 1)
            v.tensor_tensor(m[:, 2, :], m[:, 2, :], m[:, 0, :], ALU.add).then_inc(P["sel"], 1)
            v.wait_ge(P["sel"], 1)
            v.tensor_tensor(m[:, 0, :], m[:, 2, :], sc[:], ALU.mult).then_inc(P["gate"], 1)


def ffn1_phase(nc, K):
    XN, GX, W, Gd = K["XN"], K["GX"], K["w1"], K["Gd"]
    F = 4
    with ExitStack() as ctx:
        S = sems(nc, ctx, "f1", "gates used x")
        H = sems(nc, ctx, "f1h", "ps act yps t", E1)
        w1 = ctx.enter_context(nc.sbuf_tensor("f1_w1s", [128, E1, F * 128], F32))
        w2 = ctx.enter_context(nc.sbuf_tensor("f1_w2s", [128, E1, F, C], F32))
        hps = ctx.enter_context(nc.psum_tensor("f1_hps", [128, F, T], F32))
        yps = ctx.enter_context(nc.psum_tensor("f1_yps", [128, 2, T], F32))
        h = ctx.enter_context(nc.sbuf_tensor("f1_h", [128, 2, F, T], F32))
        g = ctx.enter_context(nc.sbuf_tensor("f1_g", [128, E1, T], F32))
        t = ctx.enter_context(nc.sbuf_tensor("f1_t", [128, T], F32))
        HB = [sems(nc, ctx, f"f1b{f}", "ps act", E1) for f in range(F)]
        loaded = sems(nc, ctx, "f1l", "loaded")["loaded"]
        block = ctx.enter_context(nc.Block())

        @block.sync
        def _(sp):
            sp.dma_start(w1[:], K["A"]["f1_w1"].rearrange("e d f -> d e f")).then_inc(loaded, 16)
            sp.dma_start(w2[:], K["A"]["f1_w2"].rearrange("e (f p) c -> p e f c", p=128)).then_inc(loaded, 16)
            with sp.Fori(0, B) as i:
                sp.wait_ge(S["x"], i)
                for e in range(E1):
                    sp.dma_start(g[:, e, :], Gd[e:e + 1, bass.ds(i * T, T)].to_broadcast([128, T])
                                 ).then_inc(S["gates"], 16)

        @block.tensor
        def _(pe):
            pe.wait_ge(loaded, 32)

            def down(i, e):
                if e >= 2:
                    pe.wait_ge(H["t"][e - 2], i + 1)
                else:
                    pe.wait_ge(H["t"][e + E1 - 2], i)
                for f in range(F):
                    pe.wait_ge(HB[f]["act"][e], i + 1)
                    last = pe.matmul(yps[:, e % 2, :], w2[:, e, f, :], h[:, e % 2, f, :],
                                     start=(f == 0), stop=(f == F - 1))
                last.then_inc(H["yps"][e], 1)

            with pe.Fori(0, B) as i:
                for e in range(E1):
                    for f in range(F):
                        if e:
                            pe.wait_ge(HB[f]["act"][e - 1], i + 1)
                        else:
                            pe.wait_ge(HB[f]["act"][E1 - 1], i)
                        pe.matmul(hps[:, f, :], w1[:, e, f * 128:(f + 1) * 128], XN[:, bass.ds(i * T, T)],
                                  start=True, stop=True).then_inc(HB[f]["ps"][e], 1)
                    if e:
                        down(i, e - 1)
                down(i, E1 - 1)

        @block.scalar
        def _(act):
            with act.Fori(0, B) as i:
                for e in range(E1):
                    if e >= 2:
                        act.wait_ge(H["yps"][e - 2], i + 1)
                    else:
                        act.wait_ge(H["yps"][e + E1 - 2], i)
                    for f in range(F):
                        act.wait_ge(HB[f]["ps"][e], i + 1)
                        act.activation(h[:, e % 2, f, :], hps[:, f, :], ACT.Gelu,
                                       bias=W("ffb1")[:, e * F + f:e * F + f + 1]).then_inc(HB[f]["act"][e], 1)

        @block.vector
        def _(v):
            with v.Fori(0, B) as i:
                v.wait_ge(S["gates"], 16 * E1 * (i + 1))
                for e in range(E1):
                    out = GX[:, bass.ds(i * T, T)] if e == 0 else t[:]
                    v.wait_ge(H["yps"][e], i + 1)
                    v.scalar_tensor_tensor(out=out, in0=yps[:, e % 2, :], scalar=W("ffb2")[:, e:e + 1],
                                           in1=g[:, e, :], op0=ALU.add, op1=ALU.mult).then_inc(H["t"][e], 1)
                    v.wait_ge(H["t"][e], i + 1)
                    if e:
                        v.tensor_tensor(GX[:, bass.ds(i * T, T)], GX[:, bass.ds(i * T, T)], t[:],
                                        ALU.add).then_inc(H["act"][e], 1)
                        v.wait_ge(H["act"][e], i + 1)
                v.nop().then_inc(S["x"], 1)


QUERIES_AT = {3: 0, 2: T, 0: T + 384, 1: 2 * T}


def inertia_phase(nc, K):
    XN, SX, cst, W = K["XN"], K["SX"], K["cst"], K["w2"]
    ITERS, F = 8, 4
    L = 4
    IT = B // L
    with ExitStack() as ctx:
        S = sems(nc, ctx, "in", "x2 v0 mean cent sq var std rstd gained n "
                 "x3 mean2 cent2 sq2 var2 std2 rstd2 gained2 n2 out", L)
        small = sems(nc, ctx, "inw", "w")["w"]
        R = sems(nc, ctx, "inr", "pre u t v xs", L)
        HF = sems(nc, ctx, "inf", "ps h used", L)
        ps = ctx.enter_context(nc.psum_tensor("in_ps", [128, L, 2, T], F32))
        sb = lambda name, *n: ctx.enter_context(nc.sbuf_tensor("in_" + name, [128, L, *n, T], F32))
        x2, xs, vel, tmp, u, h = sb("x2"), sb("xs"), sb("vel"), sb("tmp"), sb("u"), sb("h", 2)
        step_x = ctx.enter_context(nc.sbuf_tensor("in_step_x", [128, 128], F32))
        block = ctx.enter_context(nc.Block())

        def row(i, a):
            return bass.ds((i * L + a) * T, T)

        @block.tensor
        def _(pe):
            with pe.Fori(0, IT) as i:
                for a in range(L):
                    pe.wait_ge(S["x2"][a], i + 1)
                    pe.wait_ge(S["out"][a], i)
                    pe.matmul(ps[:, a, 0, :], cst("mean"), x2[:, a, :], start=True, stop=True).then_inc(S["mean"][a], 1)
                for a in range(L):
                    pe.wait_ge(S["sq"][a], i + 1)
                    pe.matmul(ps[:, a, 1, :], cst("mean"), u[:, a, :], start=True, stop=True).then_inc(S["var"][a], 1)
                for k in range(ITERS):
                    for a in range(L):
                        if k:
                            pe.wait_ge(R["u"][a], i * ITERS + k)
                            pe.wait_ge(R["v"][a], i * ITERS + k)
                            pe.matmul(ps[:, a, 0, :], step_x[:], vel[:, a, :], start=False,
                                      stop=(k == ITERS - 1), skip_group_check=True).then_inc(R["pre"][a], 1)
                            continue
                        pe.matmul(ps[:, a, 0, :], W("w_ctx"), SX[:, row(i, a)], start=True, stop=False,
                                  skip_group_check=True)
                        pe.wait_ge(S["n"][a], i + 1)
                        pe.wait_ge(small, 1)
                        pe.matmul(ps[:, a, 0, :], W("w_x"), xs[:, a, :], start=False, stop=False,
                                  skip_group_check=True).then_inc(R["pre"][a], 1)
                for a in range(L):
                    pe.wait_ge(S["x3"][a], i + 1)
                    pe.matmul(ps[:, a, 0, :], cst("mean"), x2[:, a, :], start=True, stop=True).then_inc(S["mean2"][a], 1)
                for a in range(L):
                    pe.wait_ge(S["sq2"][a], i + 1)
                    pe.matmul(ps[:, a, 1, :], cst("mean"), u[:, a, :], start=True, stop=True).then_inc(S["var2"][a], 1)
                for f in range(F + 1):
                    for a in range(L):
                        if f < F:
                            if f == 0:
                                pe.wait_ge(S["n2"][a], i + 1)
                            else:
                                pe.wait_ge(HF["h"][a], i * F + f)
                            pe.matmul(ps[:, a, 0, :], W("ff_w1")[:, f * 128:(f + 1) * 128], xs[:, a, :],
                                      start=True, stop=True).then_inc(HF["ps"][a], 1)
                        if f:
                            pe.wait_ge(HF["h"][a], i * F + f)
                            last = pe.matmul(ps[:, a, 1, :], W("ff_w2")[:, (f - 1) * C:f * C], h[:, a, (f - 1) % 2, :],
                                             start=(f == 1), stop=(f == F))
                            last.then_inc(HF["used"][a], 1)

        @block.scalar
        def _(act):
            with act.Fori(0, IT) as i:
                for a in range(L):
                    act.wait_ge(S["cent"][a], i + 1)
                    act.activation(u[:, a, :], xs[:, a, :], ACT.Square).then_inc(S["sq"][a], 1)
                for a in range(L):
                    act.wait_ge(S["var"][a], i + 1)
                    act.activation(tmp[:, a, :], ps[:, a, 1, :], ACT.Ln, bias=cst("eps")).then_inc(S["std"][a], 1)
                for a in range(L):
                    act.wait_ge(S["std"][a], i + 1)
                    act.activation(tmp[:, a, :], tmp[:, a, :], ACT.Exp, scale=-0.5).then_inc(S["rstd"][a], 1)
                for k in range(ITERS):
                    for a in range(L):
                        act.wait_ge(R["pre"][a], i * ITERS + k + 1)
                        act.wait_ge(R["v"][a], i * ITERS + k)
                        act.activation(u[:, a, :], ps[:, a, 0, :], ACT.Tanh, bias=W("b_inl")).then_inc(R["u"][a], 1)
                for a in range(L):
                    act.wait_ge(S["cent2"][a], i + 1)
                    act.activation(u[:, a, :], xs[:, a, :], ACT.Square).then_inc(S["sq2"][a], 1)
                for a in range(L):
                    act.wait_ge(S["var2"][a], i + 1)
                    act.activation(tmp[:, a, :], ps[:, a, 1, :], ACT.Ln, bias=cst("eps")).then_inc(S["std2"][a], 1)
                for a in range(L):
                    act.wait_ge(S["std2"][a], i + 1)
                    act.activation(tmp[:, a, :], tmp[:, a, :], ACT.Exp, scale=-0.5).then_inc(S["rstd2"][a], 1)
                for f in range(F):
                    for a in range(L):
                        act.wait_ge(HF["ps"][a], i * F + f + 1)
                        if f >= 2:
                            act.wait_ge(HF["used"][a], i * F + f - 1)
                        else:
                            act.wait_ge(HF["used"][a], i * F)
                        act.activation(h[:, a, f % 2, :], ps[:, a, 0, :], ACT.Gelu,
                                       bias=W("ff_b1")[:, f:f + 1]).then_inc(HF["h"][a], 1)

        @block.vector
        def _(v):
            def norm(i, tag, gain, shift):
                for a in range(L):
                    v.wait_ge(S["mean" + tag][a], i + 1)
                    v.tensor_tensor(xs[:, a, :], x2[:, a, :], ps[:, a, 0, :], ALU.subtract).then_inc(S["cent" + tag][a], 1)
                for a in range(L):
                    v.wait_ge(S["rstd" + tag][a], i + 1)
                    v.scalar_tensor_tensor(out=xs[:, a, :], in0=xs[:, a, :], scalar=W(gain), in1=tmp[:, a, :],
                                           op0=ALU.mult, op1=ALU.mult).then_inc(S["gained" + tag][a], 1)
                    v.wait_ge(S["gained" + tag][a], i + 1)
                    v.tensor_scalar(xs[:, a, :], xs[:, a, :], W(shift), None, ALU.add).then_inc(S["n" + tag][a], 1)

            v.tensor_scalar(step_x[:], W("w_x"), 0.01, None, ALU.mult).then_inc(small, 1)
            with v.Fori(0, IT) as i:
                for a in range(L):
                    v.tensor_tensor(x2[:, a, :], XN[:, row(i, a)], SX[:, row(i, a)], ALU.add).then_inc(S["x2"][a], 1)
                    v.memset(vel[:, a, :], 0.0).then_inc(S["v0"][a], 1)
                for a in range(L):
                    v.wait_ge(S["x2"][a], i + 1)
                    v.wait_ge(S["v0"][a], i + 1)
                norm(i, "", "g1", "b1")
                for k in range(ITERS):
                    for a in range(L):
                        if k:
                            v.wait_ge(R["xs"][a], i * ITERS + k)
                        else:
                            v.wait_ge(S["n"][a], i + 1)
                        v.scalar_tensor_tensor(out=tmp[:, a, :], in0=vel[:, a, :], scalar=0.9, in1=xs[:, a, :],
                                               op0=ALU.mult, op1=ALU.subtract).then_inc(R["t"][a], 1)
                    for a in range(L):
                        v.wait_ge(R["t"][a], i * ITERS + k + 1)
                        v.wait_ge(R["u"][a], i * ITERS + k + 1)
                        if k:
                            v.wait_ge(R["pre"][a], i * ITERS + k + 1)
                        v.tensor_tensor(vel[:, a, :], tmp[:, a, :], u[:, a, :], ALU.add).then_inc(R["v"][a], 1)
                        v.wait_ge(R["v"][a], i * ITERS + k + 1)
                        v.scalar_tensor_tensor(out=xs[:, a, :], in0=vel[:, a, :], scalar=0.01, in1=xs[:, a, :],
                                               op0=ALU.mult, op1=ALU.add).then_inc(R["xs"][a], 1)
                for a in range(L):
                    v.wait_ge(R["xs"][a], i * ITERS + ITERS)
                    v.tensor_tensor(x2[:, a, :], x2[:, a, :], xs[:, a, :], ALU.add).then_inc(S["x3"][a], 1)
                norm(i, "2", "g2", "b2")
                for a in range(L):
                    v.wait_ge(HF["used"][a], i * F + F)
                    v.scalar_tensor_tensor(out=SX[:, row(i, a)], in0=ps[:, a, 1, :], scalar=W("ff_b2"),
                                           in1=x2[:, a, :], op0=ALU.add, op1=ALU.add).then_inc(S["out"][a], 1)
                for a in range(L):
                    v.wait_ge(S["out"][a], i + 1)


TERMS = ((0, 0), (0, 1), (1, 0), (0, 2), (2, 0), (1, 1))


def split_phase(nc, K, tag, src, wq, wk, wv, tiles, dim, bias=None, qscale=1.0):
    X, VA, Pd = K[src], K["VA"], K["Pd"]
    H = 16
    D = VA.shape[-1] - 1
    N = 2 * tiles
    with ExitStack() as ctx:
        S = sems(nc, ctx, tag, "xs vps v ones")
        U = [sems(nc, ctx, f"{tag}{a}", "ps f hi r1 mid lo stored", N) for a in range(1)][0]
        ps = ctx.enter_context(nc.psum_tensor(tag + "_ps", [128, N, T], F32))
        vps = ctx.enter_context(nc.psum_tensor(tag + "_vps", [128, NB, C], F32))
        xs = ctx.enter_context(nc.sbuf_tensor(tag + "_xs", [128, T], F32))
        f = ctx.enter_context(nc.sbuf_tensor(tag + "_f", [128, N, T], F32))
        r = ctx.enter_context(nc.sbuf_tensor(tag + "_r", [128, N, T], F32))
        p = ctx.enter_context(nc.sbuf_tensor(tag + "_p", [128, N, 3, T], BF16))
        block = ctx.enter_context(nc.Block())

        @block.tensor
        def _(pe):
            with pe.Fori(0, B) as i:
                for n in range(N):
                    pe.wait_ge(U["f"][n], i)
                    w = (wq if n < tiles else wk)[:, (n % tiles) * 128:(n % tiles + 1) * 128]
                    pe.matmul(ps[:, n, :], w, X[:, bass.ds(i * T, T)], start=True, stop=True).then_inc(U["ps"][n], 1)
                pe.wait_ge(S["v"], i)
                pe.wait_ge(S["xs"], i + 1)
                for j in range(NB):
                    last = pe.matmul(vps[:, j, :], xs[:, j * 128:(j + 1) * 128], wv, start=True, stop=True)
                last.then_inc(S["vps"], 1)

        @block.scalar
        def _(act):
            with act.Fori(0, B) as i:
                for n in range(N):
                    act.wait_ge(U["ps"][n], i + 1)
                    act.wait_ge(U["r1"][n], i)
                    act.activation(f[:, n, :], ps[:, n, :], ACT.Identity, scale=qscale if n < tiles else 1.0,
                                   bias=0.0 if bias is None else bias[:, n:n + 1]).then_inc(U["f"][n], 1)
                    act.wait_ge(U["f"][n], i + 1)
                    act.wait_ge(U["stored"][n], 16 * i)
                    act.activation(p[:, n, 0, :], f[:, n, :], ACT.Copy).then_inc(U["hi"][n], 1)
                for n in range(N):
                    act.wait_ge(U["r1"][n], i + 1)
                    act.activation(p[:, n, 1, :], r[:, n, :], ACT.Copy).then_inc(U["mid"][n], 1)

        @block.vector
        def _(v):
            v.memset(VA[:], 1.0).then_inc(S["ones"], 1)
            v.wait_ge(S["ones"], 1)
            with v.Fori(0, B) as i:
                v.wait_ge(S["vps"], i)
                v.tensor_copy(xs[:], X[:, bass.ds(i * T, T)]).then_inc(S["xs"], 1)
                for n in range(N):
                    v.wait_ge(U["hi"][n], i + 1)
                    v.wait_ge(U["lo"][n], i)
                    v.tensor_tensor(r[:, n, :], f[:, n, :], p[:, n, 0, :], ALU.subtract).then_inc(U["r1"][n], 1)
                v.wait_ge(S["vps"], i + 1)
                out = VA[:, bass.ds(i * NB, NB), :, 0:D]
                got = vps[:].rearrange("p j (h d) -> p j h d", h=H)
                if bias is None:
                    v.tensor_copy(out, got).then_inc(S["v"], 1)
                else:
                    v.tensor_tensor(out, got, K["w2"]("v_b_row").rearrange("p (h d) -> p h d", h=H).unsqueeze(
                        1).to_broadcast([128, NB, H, D]), ALU.add).then_inc(S["v"], 1)
                for n in range(N):
                    v.wait_ge(U["mid"][n], i + 1)
                    v.tensor_tensor(p[:, n, 2, :], r[:, n, :], p[:, n, 1, :], ALU.subtract).then_inc(U["lo"][n], 1)

        @block.sync
        def _(sp):
            with sp.Fori(0, B) as i:
                for n in range(N):
                    sp.wait_ge(U["lo"][n], i + 1)
                    sp.dma_start(Pd[i, n // tiles, :, (n % tiles) * 128:(n % tiles + 1) * 128].rearrange("c r t -> r c t"),
                                 p[:, n]).then_inc(U["stored"][n], 16)
            for n in range(N):
                sp.wait_ge(U["stored"][n], 16 * B)


def load_stacks(sp, Pd, row, first, n, qs, ks, loaded, D):
    for at, (pq, pk) in enumerate(TERMS):
        for side, part, dst in ((0, pq, qs), (1, pk, ks)):
            src = Pd[row, side, part, first * D:(first + n) * D]
            sp.dma_start(dst[at * D:(at + 1) * D], src.rearrange("(h d) t -> d h t", d=D)).then_inc(loaded, 16)


GROUPS, GH = 4, 4


def open_bank(pe, K, bank):
    pe.matmul(bank, K["zero"][:, 0:128], K["zero"][:], start=True, stop=False, skip_group_check=True)


def causal_phase(nc, K, tag, dst, D, softmax):
    VA, Pd, cst, out = K["VA"], K["Pd"], K["cst"], K[dst]
    H, DV = GROUPS * GH, 8
    BUF = 4
    R = len(TERMS) * D + (2 if softmax else 0)
    LOADS = 16 * (2 * len(TERMS) + (1 if softmax else 0))
    SC = (float(1 / np.sqrt(D)),) if softmax else (0.25 * 0.5 ** 0.5,)
    with ExitStack() as ctx:
        S = sems(nc, ctx, tag, "ones ready count half vc sums vsum den rec num y")
        G = sems(nc, ctx, tag + "g", "loaded out va num_placed den_placed", GROUPS)
        HD = sems(nc, ctx, tag + "h", "score power masked av", H)
        ps = ctx.enter_context(nc.psum_tensor(tag + "_ps", [128, 2, 3 * T], F32))
        O = ctx.enter_context(nc.psum_tensor(tag + "_o", [128, 2, T], F32))
        qs = ctx.enter_context(nc.sbuf_tensor(tag + "_qs", [R, GROUPS, GH, T], BF16))
        ks = ctx.enter_context(nc.sbuf_tensor(tag + "_ks", [R, GROUPS, GH, T], BF16))
        va = ctx.enter_context(nc.sbuf_tensor(tag + "_va", [128, NB, H, 2 * DV], F32))
        vc = ctx.enter_context(nc.sbuf_tensor(tag + "_vc", [128, NB, H, DV], F32))
        pw = ctx.enter_context(nc.sbuf_tensor(tag + "_pw", [128, BUF, 3, T], F32))
        osb = ctx.enter_context(nc.sbuf_tensor(tag + "_osb", [128, GROUPS, T], F32))
        row = lambda name: ctx.enter_context(nc.sbuf_tensor(tag + "_" + name, [128, T], F32))
        num, den, rec = row("num"), row("den"), row("rec")
        vsum, half = (None, None) if softmax else (row("vsum"), row("half"))
        block = ctx.enter_context(nc.Block())
        weights = HD["power"] if softmax else HD["masked"]

        @block.sync
        def _(sp):
            if softmax:
                sp.wait_ge(S["ones"], 1)
            def load(i, g):
                sp.wait_ge(HD["score"][GH * g + GH - 1], i)
                load_stacks(sp, Pd, i, g * GH, GH, qs[:, g], ks[:, g], G["loaded"][g], D)
                if softmax:
                    sp.dma_start(qs[R - 2:R, g], K["Md"][i, :, g * GH:(g + 1) * GH]).then_inc(G["loaded"][g], 16)

            def place(i, g):
                sp.wait_ge(S["y"], i)
                sp.nop(nofuse=True)
                sp.wait_ge(G["out"][g], i + 1)
                sp.nop(nofuse=True)
                for a in range(GH):
                    h = g * GH + a
                    sp.dma_start(num[h * DV:(h + 1) * DV, :],
                                 osb[32 * a:32 * a + DV, g, :]).then_inc(G["num_placed"][g], 16)

            for g in range(GROUPS):
                load(0, g)
            with sp.Fori(1, B) as i:
                for g in range(GROUPS):
                    load(i, g)
                    place(i - 1, g)
            for g in range(GROUPS):
                place(B - 1, g)

        @block.tensor
        def _(pe):
            def scores(i, h):
                g = h // GH
                if h % GH == 0:
                    pe.wait_ge(G["loaded"][g], LOADS * (i + 1))
                if h >= 2:
                    pe.wait_ge(HD["power"][h - 2], i + 1)
                else:
                    pe.wait_ge(HD["power"][h + H - 2], i)
                for jk in range(NB):
                    at, n = KEYS_AT[jk], T - 128 * jk
                    k, q = ks[:, g, h % GH, jk * 128:(jk + 1) * 128], qs[:, g, h % GH, jk * 128:T]
                    if softmax:
                        pe.matmul(ps[:, h % 2, at:at + 128], K["cb"]("identb"), K["cb"]("neg_across"),
                                  start=True, stop=False)
                        last = pe.matmul(ps[:, h % 2, at:at + 128], k, q[:, 0:128], start=False, stop=True)
                        if n > 128:
                            last = pe.matmul(ps[:, h % 2, at + 128:at + n], k, q[:, 128:n], start=True, stop=True)
                    else:
                        last = pe.matmul(ps[:, h % 2, at:at + n], k, q, start=True, stop=True)
                last.then_inc(HD["score"][h], 1)

            def values(i, h0):
                g = h0 // GH
                if h0 % GH == 0:
                    if g >= 2:
                        pe.wait_ge(G["out"][g - 2], i + 1)
                    elif g == 0 and not softmax:
                        pe.wait_ge(S["vsum"], i)
                        pe.wait_ge(S["half"], 1)
                    else:
                        pe.wait_ge(G["out"][g + 2], i)
                    open_bank(pe, K, O[:, g % 2, :])
                pe.wait_ge(G["va"][g], i + 1)
                for jk in range(NB):
                    at, n = KEYS_AT[jk], T - 128 * jk
                    for h in (h0, h0 + 1):
                        if jk == 0:
                            pe.wait_ge(weights[h], i + 1)
                        last = pe.matmul(O[32 * (h % GH):32 * (h % GH) + 2 * DV, g % 2, jk * 128:T], va[:, jk, h, :],
                                         pw[:, h % BUF, at // T, at % T:at % T + n], start=False,
                                         stop=(h % GH == GH - 1 and jk == NB - 1), skip_group_check=True)
                        if jk == NB - 1:
                            last.then_inc(HD["av"][h], 1)

            def sums(i):
                pe.wait_ge(S["vc"], i + 1)
                pe.wait_ge(G["out"][GROUPS - 2], i + 1)
                for jk in range(NB):
                    last = pe.matmul(O[:, 0, jk * 128:T], vc[:, jk].rearrange("p h d -> p (h d)"),
                                     cst("halfwide")[:, 0:T - 128 * jk], start=(jk == 0), stop=(jk == NB - 1),
                                     skip_group_check=True)
                last.then_inc(S["sums"], 1)

            def turn(i, last):
                for h in range(0, H, 2):
                    for ahead in (h + 2, h + 3):
                        if ahead < H:
                            scores(i, ahead)
                        elif not last:
                            scores(i + 1, ahead - H)
                    if h == H - 2 and not softmax:
                        sums(i)
                    values(i, h)

            if not softmax:
                pe.matmul(O[:, 0, :], cst("ones")[0:1, :], cst("halfcount"), start=True, stop=True).then_inc(S["count"], 1)
            scores(0, 0)
            scores(0, 1)
            with pe.Fori(0, B - 1) as i:
                turn(i, False)
            turn(B - 1, True)

        @block.scalar
        def _(act):
            with act.Fori(0, B) as i:
                for h in range(H):
                    act.wait_ge(HD["score"][h], i + 1)
                    if h >= BUF:
                        act.wait_ge(HD["av"][h - BUF], i + 1)
                    else:
                        act.wait_ge(HD["av"][h + H - BUF], i)
                    act.activation(pw[:, h % BUF].rearrange("p g x -> p (g x)")[:, 0:SPAN], ps[:, h % 2, 0:SPAN],
                                   ACT.Exp if softmax else ACT.Square, scale=SC[0],
                                   bias=0.0 if softmax else cst("rhalf")).then_inc(HD["power"][h], 1)

        @block.gpsimd
        def _(gp):
            def fetch(i, g):
                gp.wait_ge(HD["av"][GH * g + GH - 1], i)
                gp.nop(nofuse=True)
                gp.tensor_copy(va[:, :, g * GH:(g + 1) * GH, 0:DV],
                               VA[:, bass.ds(i * NB, NB), g * GH:(g + 1) * GH, 0:DV]).then_inc(G["va"][g], 1)

            def place(i, g):
                gp.wait_ge(G["out"][g], i + 1)
                gp.wait_ge(S["y"], i)
                gp.nop(nofuse=True)
                for a in range(GH):
                    h = g * GH + a
                    gp.dma_start(den[h * DV:(h + 1) * DV, :],
                                 osb[32 * a + DV:32 * a + 2 * DV, g, :]).then_inc(G["den_placed"][g], 16)

            def turn(i, first):
                for g in range(GROUPS):
                    fetch(i, g)
                    if not first:
                        place(i - 1, g)
                if not softmax:
                    gp.wait_ge(S["sums"], i)
                    gp.nop(nofuse=True)
                    gp.tensor_copy(vc[:], VA[:, bass.ds(i * NB, NB), :, 0:DV]).then_inc(S["vc"], 1)

            gp.memset(va[:], 1.0).then_inc(S["ready"], 1)
            gp.wait_ge(S["ready"], 1)
            turn(0, True)
            with gp.Fori(1, B) as i:
                turn(i, False)
            for g in range(GROUPS):
                place(B - 1, g)

        @block.vector
        def _(v):
            if softmax:
                v.memset(ks[:], 1.0).then_inc(S["ones"], 1)
            else:
                v.wait_ge(S["count"], 1)
                v.tensor_copy(half[:], O[:, 0, :]).then_inc(S["half"], 1)
                v.wait_ge(S["half"], 1)

            def evacuate(i, g):
                v.wait_ge(HD["av"][GH * g + GH - 1], i + 1)
                v.wait_ge(G["num_placed"][g], 16 * GH * i)
                v.wait_ge(G["den_placed"][g], 16 * GH * i)
                v.tensor_copy(osb[:, g, :], O[:, g % 2, :]).then_inc(G["out"][g], 1)

            def finish(i):
                for g in range(GROUPS):
                    v.wait_ge(G["num_placed"][g], 16 * GH * (i + 1))
                    v.wait_ge(G["den_placed"][g], 16 * GH * (i + 1))
                if softmax:
                    v.reciprocal(rec[:], den[:]).then_inc(S["rec"], 1)
                else:
                    v.scalar_tensor_tensor(out=rec[:], in0=den[:], scalar=1e-12, in1=half[:],
                                           op0=ALU.add, op1=ALU.add).then_inc(S["den"], 1)
                    v.tensor_tensor(num[:], num[:], vsum[:], ALU.add).then_inc(S["num"], 1)
                    v.wait_ge(S["den"], i + 1)
                    v.reciprocal(rec[:], rec[:]).then_inc(S["rec"], 1)
                    v.wait_ge(S["num"], i + 1)
                v.wait_ge(S["rec"], i + 1)
                v.tensor_tensor(out[:, bass.ds(i * T, T)], num[:], rec[:], ALU.mult).then_inc(S["y"], 1)

            def turn(i, first):
                for h in range(H):
                    if not softmax:
                        v.wait_ge(HD["power"][h], i + 1)
                        v.tensor_tensor(pw[:, h % BUF, :, 0:128], pw[:, h % BUF, :, 0:128],
                                        cst("tri").unsqueeze(1).to_broadcast([128, 3, 128]), ALU.mult)
                        v.tensor_tensor(pw[:, h % BUF, 1, 384:512], pw[:, h % BUF, 1, 384:512], cst("tri"),
                                        ALU.mult).then_inc(HD["masked"][h], 1)
                    if h % GH == 1 and h > GH:
                        evacuate(i, h // GH - 1)
                    if h == GH + 2 and not first:
                        finish(i - 1)
                if not softmax:
                    v.wait_ge(S["sums"], i + 1)
                    v.tensor_copy(vsum[:], O[:, 0, :]).then_inc(S["vsum"], 1)
                evacuate(i, GROUPS - 1)
                if not softmax:
                    v.wait_ge(S["vsum"], i + 1)

            turn(0, True)
            with v.Fori(1, B) as i:
                turn(i, False)
            finish(B - 1)


def maxima_and_mlp_phase(nc, K):
    XN, GX, W = K["XN"], K["GX"], K["w2f"]
    F = 4
    STEPS = F + 4 * F + 2
    Pd, Md, cst, cb = K["Pd"], K["Md"], K["cst"], K["cb"]
    H, D = GROUPS * GH, 8
    R = len(TERMS) * D
    LOADS = 16 * 2 * len(TERMS)
    with ExitStack() as ctx:
        S = sems(nc, ctx, "mx", "tps hi mid stored")
        G = sems(nc, ctx, "mxg", "loaded", GROUPS)["loaded"]
        HD = sems(nc, ctx, "mxh", "far top", H)
        M = sems(nc, ctx, "gm", "ops out")
        L = [sems(nc, ctx, f"gm{n}", "ps sb", F) for n in range(4)]
        ps = ctx.enter_context(nc.psum_tensor("mx_ps", [128, 3 * T], F32))
        mps = ctx.enter_context(nc.psum_tensor("gm_ps", [128, F, T], F32))
        h0 = ctx.enter_context(nc.sbuf_tensor("gm_h0", [128, F, T], F32))
        h1 = ctx.enter_context(nc.sbuf_tensor("gm_h1", [128, F, T], F32))
        h2 = ctx.enter_context(nc.sbuf_tensor("gm_h2", [128, F, T], F32))
        tps = ctx.enter_context(nc.psum_tensor("mx_tps", [H, T], F32))
        qs = ctx.enter_context(nc.sbuf_tensor("mx_qs", [R, GROUPS, GH, T], BF16))
        ks = ctx.enter_context(nc.sbuf_tensor("mx_ks", [R, GROUPS, GH, T], BF16))
        mx = ctx.enter_context(nc.sbuf_tensor("mx_mx", [128, NB, H], F32))
        parts = ctx.enter_context(nc.sbuf_tensor("mx_parts", [H, 2, T], BF16))
        block = ctx.enter_context(nc.Block())

        @block.sync
        def _(sp):
            with sp.Fori(0, B) as i:
                for g in range(GROUPS):
                    sp.wait_ge(HD["far"][GH * g + GH - 1], i)
                    load_stacks(sp, Pd, i, g * GH, GH, qs[:, g], ks[:, g], G[g], D)

        @block.tensor
        def _(pe):
            def layers(i, step):
                if step < F:
                    f = step
                    x = XN[:, bass.ds(i * T, T)]
                    for n in range(2):
                        bank = 2 * f % F + n
                        if f >= 2:
                            pe.wait_ge(L[n]["sb"][f - 2], i + 1)
                        else:
                            pe.wait_ge(M["out"] if bank == 0 else L[3]["sb"][bank], i)
                        pe.matmul(mps[:, bank, :], W(("w1", "w2")[n])[:, f * 128:(f + 1) * 128], x,
                                  start=True, stop=True).then_inc(L[n]["ps"][f], 1)
                    return
                n, f, half = 2 + (step - F) // (2 * F), (step - F) // 2 % F, step % 2
                if n < 4:
                    src, ready = ((h0, L[1]["sb"]), (h1, L[2]["sb"]))[n - 2]
                    if half == 0:
                        pe.wait_ge(L[f % 2]["sb"][2 + f // 2] if n == 2 else L[2]["sb"][f], i + 1)
                    for j in (2 * half, 2 * half + 1):
                        pe.wait_ge(ready[j], i + 1)
                        last = pe.matmul(mps[:, f, :], W(("h1", "h2")[n - 2])[:, j * 512 + f * 128:j * 512 + (f + 1) * 128],
                                         src[:, j, :], start=(j == 0), stop=(j == F - 1))
                    if half:
                        last.then_inc(L[n]["ps"][f], 1)
                else:
                    for j in (2 * half, 2 * half + 1):
                        pe.wait_ge(L[3]["sb"][j], i + 1)
                        last = pe.matmul(mps[:, 0, :], W("w3")[:, j * C:(j + 1) * C], h2[:, j, :],
                                         start=(j == 0), stop=(j == F - 1))
                    if half:
                        last.then_inc(M["ops"], 1)

            with pe.Fori(0, B) as i:
                for h in range(H):
                    g = h // GH
                    if h % GH == 0:
                        pe.wait_ge(G[g], LOADS * (i + 1))
                    if h:
                        pe.wait_ge(HD["top"][h - 1], i + 1)
                    else:
                        pe.wait_ge(HD["top"][H - 1], i)
                    for jq in range(NB):
                        at, n = QUERIES_AT[jq], 128 * (jq + 1)
                        q, k = qs[:, g, h % GH, jq * 128:(jq + 1) * 128], ks[:, g, h % GH, :]
                        if jq:
                            pe.matmul(ps[:, at:at + n - 128], q, k[:, 0:n - 128], start=True, stop=True)
                        pe.matmul(ps[:, at + n - 128:at + n], cb("identb"), cb("neg_down"),
                                  start=True, stop=False)
                        last = pe.matmul(ps[:, at + n - 128:at + n], q, k[:, n - 128:n],
                                         start=False, stop=True)
                    last.then_inc(HD["far"][h], 1)
                    layers(i, h)
                layers(i, H)
                pe.wait_ge(HD["top"][H - 1], i + 1)
                pe.wait_ge(S["mid"], i)
                for j in range(NB):
                    last = pe.transpose(tps[:, j * 128:(j + 1) * 128], mx[:, j, :], cst("ident"))
                last.then_inc(S["tps"], 1)
                for step in range(H + 1, STEPS):
                    layers(i, step)

        @block.vector
        def _(v):
            with v.Fori(0, B) as i:
                v.wait_ge(S["tps"], i)
                for h in range(H):
                    v.wait_ge(HD["far"][h], i + 1)
                    for jq in range(NB):
                        at = QUERIES_AT[jq]
                        last = v.tensor_reduce(mx[:, jq, h:h + 1], ps[:, at:at + 128 * (jq + 1)], AX.X,
                                               ALU.max, negate=True)
                    last.then_inc(HD["top"][h], 1)
                    if h < F:
                        f = h
                        v.wait_ge(L[1]["ps"][f], i + 1)
                        v.wait_ge(L[0]["sb"][f], i + 1)
                        v.wait_ge(L[2]["ps"][F - 1], i)
                        v.scalar_tensor_tensor(out=h0[:, f, :], in0=mps[:, 2 * f % F + 1, :], scalar=W("s2")[:, f:f + 1],
                                               in1=h1[:, f, :], op0=ALU.mult, op1=ALU.mult).then_inc(L[1]["sb"][f], 1)
                v.wait_ge(S["tps"], i + 1)
                v.wait_ge(S["stored"], 16 * i)
                v.tensor_copy(parts[:, 0, :], tps[:]).then_inc(S["hi"], 1)
                v.wait_ge(S["hi"], i + 1)
                v.tensor_tensor(parts[:, 1, :], tps[:], parts[:, 0, :], ALU.subtract).then_inc(S["mid"], 1)
                v.wait_ge(M["ops"], i + 1)
                v.tensor_scalar(GX[:, bass.ds(i * T, T)], mps[:, 0, :], W("s3"), None, ALU.mult).then_inc(M["out"], 1)

        @block.scalar
        def _(act):
            with act.Fori(0, B) as i:
                for f in range(F):
                    act.wait_ge(L[0]["ps"][f], i + 1)
                    act.wait_ge(L[3]["ps"][F - 1], i)
                    act.activation(h1[:, f, :], mps[:, 2 * f % F, :], ACT.Silu,
                                   scale=W("s1")[:, f:f + 1]).then_inc(L[0]["sb"][f], 1)
                for n, dst, sc in ((2, h1, "sh1"), (3, h2, "sh2")):
                    for f in range(F):
                        act.wait_ge(L[n]["ps"][f], i + 1)
                        if n == 3:
                            act.wait_ge(M["ops"], i)
                        act.activation(dst[:, f, :], mps[:, f, :], ACT.Gelu,
                                       scale=W(sc)[:, f:f + 1]).then_inc(L[n]["sb"][f], 1)
                act.wait_ge(S["mid"], i + 1)
                act.dma_start(Md[i].rearrange("n h t -> h n t"), parts[:]).then_inc(S["stored"], 16)
            act.wait_ge(S["stored"], 16 * B)


def project_phase(nc, K, tag, name, w, bias=0.0):
    X = K[name]
    L = 4
    with ExitStack() as ctx:
        S = sems(nc, ctx, tag, "ps out", L)
        ps = ctx.enter_context(nc.psum_tensor(tag + "_ps", [128, L, T], F32))
        block = ctx.enter_context(nc.Block())

        @block.tensor
        def _(pe):
            with pe.Fori(0, B // L) as i:
                for a in range(L):
                    pe.wait_ge(S["out"][a], i)
                    pe.matmul(ps[:, a, :], w, X[:, bass.ds((i * L + a) * T, T)],
                              start=True, stop=True).then_inc(S["ps"][a], 1)

        @block.scalar
        def _(act):
            with act.Fori(0, B // L) as i:
                for a in range(L):
                    act.wait_ge(S["ps"][a], i + 1)
                    act.activation(X[:, bass.ds((i * L + a) * T, T)], ps[:, a, :], ACT.Identity,
                                   bias=bias).then_inc(S["out"][a], 1)


def column_attention_phase(nc, K):
    GX, VA, Pd, cst = K["GX"], K["VA"], K["Pd"], K["cst"]
    H, D = GROUPS * GH, 8
    R = len(TERMS) * D
    AHEAD = 5
    BUF = 8
    LOADS = 16 * 2 * len(TERMS)
    with ExitStack() as ctx:
        G = sems(nc, ctx, "cag", "loaded out placed", GROUPS)
        U = sems(nc, ctx, "cau", "score top exp", NB)
        V = sems(nc, ctx, "cav", "value", BUF * NB)
        HD = sems(nc, ctx, "cah", "rz vz", H)
        ps = ctx.enter_context(nc.psum_tensor("ca_ps", [128, NB, T], F32))
        O = ctx.enter_context(nc.psum_tensor("ca_o", [128, 2, T], F32))
        qs = ctx.enter_context(nc.sbuf_tensor("ca_qs", [R, 2, GH, T], BF16))
        ks = ctx.enter_context(nc.sbuf_tensor("ca_ks", [R, 2, GH, T], BF16))
        pw = ctx.enter_context(nc.sbuf_tensor("ca_pw", [128, BUF, NB, T], F32))
        mx = ctx.enter_context(nc.sbuf_tensor("ca_mx", [128, H, NB], F32))
        z = ctx.enter_context(nc.sbuf_tensor("ca_z", [128, H, NB], F32))
        vs = ctx.enter_context(nc.sbuf_tensor("ca_vs", [128, BUF, NB, D], F32))
        osb = ctx.enter_context(nc.sbuf_tensor("ca_osb", [128, GROUPS, T], F32))
        block = ctx.enter_context(nc.Block())

        @block.sync
        def _(sp):
            def turn(i, first):
                for g in range(GROUPS):
                    if g >= 2 or not first:
                        sp.wait_ge(U["score"][NB - 1], i * H + GH * (g - 1))
                    load_stacks(sp, Pd, i, g * GH, GH, qs[:, g % 2], ks[:, g % 2], G["loaded"][g], D)

            turn(0, True)
            with sp.Fori(1, B) as i:
                turn(i, False)

        @block.gpsimd
        def _(gp):
            with gp.Fori(0, B) as i:
                for g in range(GROUPS):
                    gp.wait_ge(G["out"][g], i + 1)
                    for a in range(GH):
                        h = g * GH + a
                        gp.dma_start(GX[h * D:(h + 1) * D, bass.ds(i * T, T)],
                                     osb[32 * a:32 * a + D, g, :]).then_inc(G["placed"][g], 16)
            for g in range(GROUPS):
                gp.wait_ge(G["placed"][g], 16 * GH * B)

        @block.tensor
        def _(pe):
            def score(i, h, jk):
                if h % GH == 0 and jk == 0:
                    pe.wait_ge(G["loaded"][h // GH], LOADS * (i + 1))
                pe.wait_ge(U["exp"][jk], i * H + h)
                pe.matmul(ps[:, jk, :], ks[:, h // GH % 2, h % GH, jk * 128:(jk + 1) * 128],
                          qs[:, h // GH % 2, h % GH, :], start=True, stop=True).then_inc(U["score"][jk], 1)

            def value(i, h, jk):
                g = h // GH
                if jk == 0:
                    if h % GH == 0:
                        if g >= 2:
                            pe.wait_ge(G["out"][g - 2], i + 1)
                        else:
                            pe.wait_ge(G["out"][g + 2], i)
                        open_bank(pe, K, O[:, g % 2, :])
                    pe.wait_ge(HD["vz"][h], i + 1)
                last = h % GH == GH - 1 and jk == NB - 1
                pe.matmul(O[32 * (h % GH):32 * (h % GH) + D, g % 2, :], vs[:, h % BUF, jk, :],
                          pw[:, h % BUF, jk, :], start=False, stop=last, skip_group_check=True
                          ).then_inc(V["value"][h % BUF * NB + jk], 1)

            def turn(i, last):
                for h in range(0, H, GH):
                    for p in range(GH * NB):
                        ahead, jk = h + AHEAD + p // NB, p % NB
                        if ahead < H:
                            score(i, ahead, jk)
                        elif not last:
                            score(i + 1, ahead - H, jk)
                        if p % GH == GH - 1:
                            for a in range(GH):
                                value(i, h + a, p // GH)

            for h in range(AHEAD):
                for jk in range(NB):
                    score(0, h, jk)
            with pe.Fori(0, B - 1) as i:
                turn(i, False)
            turn(B - 1, True)

        @block.scalar
        def _(act):
            with act.Fori(0, B) as i:
                for h in range(H):
                    for jk in range(NB):
                        act.wait_ge(V["value"][h % BUF * NB + jk], i * (H // BUF) + h // BUF)
                        act.wait_ge(U["top"][jk], i * H + h + 1)
                        act.activation(pw[:, h % BUF, jk, :], ps[:, jk, :], ACT.Exp,
                                       bias=mx[:, h, jk:jk + 1], accum_out=z[:, h, jk:jk + 1]).then_inc(U["exp"][jk], 1)

        @block.vector
        def _(v):
            def weigh(i, h):
                v.wait_ge(U["exp"][NB - 1], i * H + h + 1)
                v.reciprocal(z[:, h, :], z[:, h, :]).then_inc(HD["rz"][h], 1)
                v.wait_ge(HD["rz"][h], i + 1)
                v.wait_ge(V["value"][h % BUF * NB + NB - 1], i * (H // BUF) + h // BUF)
                v.tensor_tensor(vs[:, h % BUF], VA[:, bass.ds(i * NB, NB), h, 0:D],
                                z[:, h, :].unsqueeze(2).to_broadcast([128, NB, D]), ALU.mult).then_inc(HD["vz"][h], 1)

            def evacuate(i, g):
                h = GH * g + GH - 1
                v.wait_ge(V["value"][h % BUF * NB + NB - 1], i * (H // BUF) + h // BUF + 1)
                v.wait_ge(G["placed"][g], 16 * GH * i)
                v.tensor_copy(osb[:, g, :], O[:, g % 2, :]).then_inc(G["out"][g], 1)

            def turn(i, first):
                for h in range(H):
                    for jk in range(NB):
                        v.wait_ge(U["score"][jk], i * H + h + 1)
                        v.tensor_reduce(mx[:, h, jk:jk + 1], ps[:, jk, :], AX.X,
                                        ALU.max, negate=True).then_inc(U["top"][jk], 1)
                        if h and jk == 1:
                            weigh(i, h - 1)
                    g = (h - AHEAD - 1) // GH
                    if (h - AHEAD) % GH == 0 and (h > AHEAD or not first):
                        evacuate(i if g >= 0 else i - 1, g % GROUPS)
                weigh(i, H - 1)

            turn(0, True)
            with v.Fori(1, B) as i:
                turn(i, False)
            evacuate(B - 1, GROUPS - 2)
            evacuate(B - 1, GROUPS - 1)


def l2_gelu_phase(nc, K):
    GX, cst, W = K["GX"], K["cst"], K["w3"]
    L = 4
    IT = B // L
    with ExitStack() as ctx:
        S = sems(nc, ctx, "lg", "z z1 sq ss std rs n w w1 sq2 ss2 std2 rs2 n2 out", L)
        ps = ctx.enter_context(nc.psum_tensor("lg_ps", [128, L, 2, T], F32))
        z = ctx.enter_context(nc.sbuf_tensor("lg_z", [128, L, T], F32))
        sq = ctx.enter_context(nc.sbuf_tensor("lg_sq", [128, L, T], F32))
        block = ctx.enter_context(nc.Block())

        def row(i, a):
            return bass.ds((i * L + a) * T, T)

        @block.tensor
        def _(pe):
            with pe.Fori(0, IT) as i:
                for a in range(L):
                    pe.wait_ge(S["z1"][a], i)
                    pe.matmul(ps[:, a, 0, :], W("wo"), GX[:, row(i, a)], start=True, stop=True).then_inc(S["z"][a], 1)
                for a in range(L):
                    pe.wait_ge(S["sq"][a], i + 1)
                    pe.wait_ge(S["std"][a], i)
                    pe.matmul(ps[:, a, 1, :], cst("ones"), sq[:, a, :], start=True, stop=True).then_inc(S["ss"][a], 1)
                for a in range(L):
                    pe.wait_ge(S["n"][a], i + 1)
                    pe.wait_ge(S["w1"][a], i)
                    pe.matmul(ps[:, a, 0, :], W("wff"), z[:, a, :], start=True, stop=True).then_inc(S["w"][a], 1)
                for a in range(L):
                    pe.wait_ge(S["sq2"][a], i + 1)
                    pe.wait_ge(S["std2"][a], i)
                    pe.matmul(ps[:, a, 1, :], cst("ones"), sq[:, a, :], start=True, stop=True).then_inc(S["ss2"][a], 1)

        @block.scalar
        def _(act):
            with act.Fori(0, IT) as i:
                for tag, src in (("", "z1"), ("2", "w1")):
                    for a in range(L):
                        act.wait_ge(S[src][a], i + 1)
                        act.activation(sq[:, a, :], z[:, a, :], ACT.Square).then_inc(S["sq" + tag][a], 1)
                    for a in range(L):
                        act.wait_ge(S["ss" + tag][a], i + 1)
                        act.activation(sq[:, a, :], ps[:, a, 1, :], ACT.Ln,
                                       bias=cst("tiny")).then_inc(S["std" + tag][a], 1)
                    for a in range(L):
                        act.wait_ge(S["std" + tag][a], i + 1)
                        act.activation(sq[:, a, :], sq[:, a, :], ACT.Exp, scale=-0.5).then_inc(S["rs" + tag][a], 1)
                for a in range(L):
                    act.wait_ge(S["n2"][a], i + 1)
                    act.activation(GX[:, row(i, a)], z[:, a, :], ACT.Gelu).then_inc(S["out"][a], 1)

        @block.vector
        def _(v):
            with v.Fori(0, IT) as i:
                for tag, src, dst, nd in (("", "z", "z1", "n"), ("2", "w", "w1", "n2")):
                    for a in range(L):
                        v.wait_ge(S[src][a], i + 1)
                        if not tag:
                            v.wait_ge(S["out"][a], i)
                        v.tensor_copy(z[:, a, :], ps[:, a, 0, :]).then_inc(S[dst][a], 1)
                    for a in range(L):
                        v.wait_ge(S["rs" + tag][a], i + 1)
                        v.tensor_tensor(z[:, a, :], z[:, a, :], sq[:, a, :], ALU.mult).then_inc(S[nd][a], 1)


def ssm_rows_phase(nc, K):
    XN, cst, W, Rd, COL = K["XN"], K["cst"], K["w3a"], K["Rd"], K["COL"]
    HB = B * 4
    with ExitStack() as ctx:
        S = sems(nc, ctx, "sr", "ps z az ez lz sp a1 adt ell sub gam bd beta cps col stored sp2")
        ps = ctx.enter_context(nc.psum_tensor("sr_ps", [HB, 3, T], F32))
        cps = ctx.enter_context(nc.psum_tensor("sr_cps", [128, 3, NB, HB], F32))
        z = ctx.enter_context(nc.sbuf_tensor("sr_z", [HB, 2, T], F32))
        e = ctx.enter_context(nc.sbuf_tensor("sr_e", [HB, 2, T], F32))
        q = ctx.enter_context(nc.sbuf_tensor("sr_q", [HB, 6, T], F32))
        block = ctx.enter_context(nc.Block())

        @block.tensor
        def _(pe):
            for n in range(3):
                for b in range(B):
                    last = pe.matmul(ps[:, n, :], W("rows")[:, (n * B + b) * HB:(n * B + b + 1) * HB],
                                     XN[:, b * T:(b + 1) * T], start=(b == 0), stop=(b == B - 1))
            last.then_inc(S["ps"], 1)
            pe.wait_ge(S["ell"], 1)
            pe.wait_ge(S["gam"], 1)
            pe.wait_ge(S["bd"], 1)
            for n in range(3):
                for j in range(NB):
                    last = pe.transpose(cps[:, n, j, :], q[:, n, j * 128:(j + 1) * 128], cst("ident")[0:HB, 0:HB])
            last.then_inc(S["cps"], 1)

        @block.scalar
        def _(act):
            act.wait_ge(S["ps"], 1)
            act.activation(q[:, 5, :], ps[:, 2, :], ACT.Sigmoid).then_inc(S["beta"], 1)
            act.wait_ge(S["z"], 1)
            act.activation(e[:], z[:], ACT.Abs).then_inc(S["az"], 1)
            act.wait_ge(S["az"], 1)
            act.activation(e[:], e[:], ACT.Exp, scale=-1.0).then_inc(S["ez"], 1)
            act.wait_ge(S["ez"], 1)
            act.activation(e[:], e[:], ACT.Ln, bias=1.0).then_inc(S["lz"], 1)

        @block.vector
        def _(v):
            v.wait_ge(S["ps"], 1)
            v.wait_ge(S["beta"], 1)
            v.tensor_scalar(z[:, 0, :], ps[:, 0, :], W("dt_bias"), None, ALU.add)
            v.tensor_copy(z[:, 1, :], ps[:, 1, :]).then_inc(S["z"], 1)
            v.wait_ge(S["z"], 1)
            v.wait_ge(S["lz"], 1)
            v.scalar_tensor_tensor(out=q[:, 3:5, :], in0=z[:], scalar=0.0, in1=e[:],
                                   op0=ALU.max, op1=ALU.add).then_inc(S["sp"], 1)
            v.wait_ge(S["sp"], 1)
            v.tensor_scalar(q[:, 4, :], q[:, 4, :], -1.0, -1e-4, ALU.mult, ALU.min).then_inc(S["a1"], 1)
            v.wait_ge(S["a1"], 1)
            v.tensor_tensor(q[:, 4, :], q[:, 4, :], q[:, 3, :], ALU.mult).then_inc(S["adt"], 1)
            v.wait_ge(S["adt"], 1)
            v.tensor_tensor_scan(q[:, 0, :], cst("onerow")[0:HB], q[:, 4, :], 0.0, ALU.mult, ALU.add).then_inc(S["ell"], 1)
            v.tensor_tensor(q[:, 2, :], q[:, 5, :], q[:, 3, :], ALU.mult).then_inc(S["bd"], 1)
            v.tensor_tensor(e[:, 0, 0:T - 1], q[:, 5, 0:T - 1], q[:, 5, 1:T], ALU.subtract)
            v.tensor_copy(e[:, 0, T - 1:T], q[:, 5, T - 1:T]).then_inc(S["sub"], 1)
            v.wait_ge(S["sub"], 1)
            v.scalar_tensor_tensor(out=q[:, 1, :], in0=e[:, 0, :], scalar=1.0, in1=q[:, 3, :],
                                   op0=ALU.add, op1=ALU.mult).then_inc(S["gam"], 1)
            v.wait_ge(S["cps"], 1)
            v.tensor_copy(COL[:], cps[:]).then_inc(S["col"], 1)
            v.wait_ge(S["col"], 1)

        @block.sync
        def _(sp):
            sp.wait_ge(S["ell"], 1)
            sp.dma_start(Rd[0], q[:, 3, :]).then_inc(S["stored"], 16)
            sp.dma_start(Rd[1], q[:, 0, :]).then_inc(S["stored"], 16)
            sp.wait_ge(S["stored"], 32)


def ssm_phase(nc, K):
    XN, SX, cst, W, Rd, COL = K["XN"], K["SX"], K["cst"], K["w3a"], K["Rd"], K["COL"]
    H = 4
    TWO_PI_HI, TWO_PI_LO = 6.28125, float(2 * np.pi - 6.28125)
    MAGIC = 1.5 * 2.0 ** 23
    Q_, K_ = 0, 1
    with ExitStack() as ctx:
        S = sems(nc, ctx, "ss", "xs dx rows bcps ang angsb pj2 xt sq ms std rs norm at th n n1 c1 c2 clamp "
                 "sin abs cos cosm yz sps s z0 z0sb z1 z1sb")
        HD = sems(nc, ctx, "sh", "cps b0 t2 turned qk dd dec m1 m2 dm a y", H)
        ps = ctx.enter_context(nc.psum_tensor("ss_ps", [128, 8, T], F32))
        sb = lambda name, *n: ctx.enter_context(nc.sbuf_tensor("ss_" + name, [128, *n], F32))
        xs, zs, bc, rot, dx = sb("xs", T), sb("zs", 2, T), sb("bc", 2, T), sb("rot", 2, T), sb("dx", 256)
        sq, xt, ang, th = sb("sq", 2, T), sb("xt", NB, 256), sb("ang", T), sb("th", 3, T)
        dtb, ellb = sb("dtb", T), sb("ellb", H, T)
        tb, t2, t3 = sb("tb", 2, T), sb("t2", 2, T), sb("t3", 2, T)
        kq, dec, aw = sb("kq", 2, 2, T), sb("dec", 2, 3, T), sb("aw", 2, 3, T)
        mm, own = sb("mm", H, NB, 128), sb("own", NB, 128)
        y = sb("y", 2, T)
        block = ctx.enter_context(nc.Block())

        @block.sync
        def _(sp):
            with sp.Fori(0, B) as i:
                sp.wait_ge(S["at"], i)
                sp.wait_ge(HD["dd"][H - 1], i)
                for h in range(H):
                    sp.dma_start(dtb[32 * h:32 * h + 32, :], Rd[0, bass.ds(i * H + h, 1), :].to_broadcast([32, T])
                                 ).then_inc(S["rows"], 16)
                    sp.dma_start(ellb[:, h, :], Rd[1, bass.ds(i * H + h, 1), :].to_broadcast([128, T])
                                 ).then_inc(S["rows"], 16)

        @block.tensor
        def _(pe):
            def project(i, bank, w):
                return pe.matmul(ps[:, bank, :], w, XN[:, bass.ds(i * T, T)], start=True, stop=True)

            def out(i):
                pe.wait_ge(S["yz"], i + 1)
                for n in range(2):
                    last = pe.matmul(ps[:, 7, :], W("out")[:, n * C:(n + 1) * C], y[:, n, :],
                                     start=(n == 0), stop=(n == 1))
                last.then_inc(S["sps"], 1)

            def turn(i, first):
                pe.wait_ge(HD["a"][H - 1], i)
                pe.wait_ge(HD["t2"][H - 1], i)
                project(i, 0, W("in")[:, 512:640])
                project(i, 1, W("in")[:, 640:768]).then_inc(S["bcps"], 1)
                project(i, 2, W("in")[:, 768:896]).then_inc(S["ang"], 1)
                project(i, 3, W("in_turned")[:, 0:128])
                project(i, 4, W("in_turned")[:, 128:256])
                if not first:
                    out(i - 1)
                pe.wait_ge(S["sq"], i + 1)
                for n in range(2):
                    last = pe.matmul(ps[:, 5 + n, :], cst("mean"), sq[:, n, :], start=True, stop=True)
                last.then_inc(S["ms"], 1)
                pe.wait_ge(S["s"], i)
                project(i, 7, W("in")[:, 0:128]).then_inc(S["z0"], 1)
                pe.wait_ge(S["std"], i + 1)
                pe.wait_ge(S["xs"], i + 1)
                for j in range(NB):
                    last = pe.matmul(ps[:, 5 + j // 2, (j % 2) * 256:(j % 2) * 256 + 256], xs[:, j * 128:(j + 1) * 128],
                                     W("in")[:, 256:512], start=True, stop=True)
                last.then_inc(S["pj2"], 1)
                pe.wait_ge(S["norm"], i + 1)
                pe.wait_ge(S["cosm"], i + 1)
                pe.wait_ge(S["sin"], i + 1)

                def spread(h):
                    if h:
                        pe.wait_ge(HD["t2"][h - 1], i + 1)
                    for n in range(2):
                        last = pe.matmul(ps[:, 3 + n, :], cst(("spread", "spread_sin")[n])[:, h * 128:(h + 1) * 128],
                                         th[:, 1 + n, :],
                                         start=True, stop=True)
                    last.then_inc(HD["cps"][h], 1)

                def products(h):
                    pe.wait_ge(HD["turned"][h], i + 1)
                    if h:
                        pe.wait_ge(HD["a"][h - 1], i + 1)
                    for jk in range(NB):
                        at, n = KEYS_AT[jk], T - 128 * jk
                        last = pe.matmul(ps[:, at // T, at % T:at % T + n], kq[:, h % 2, K_, jk * 128:(jk + 1) * 128],
                                         kq[:, h % 2, Q_, jk * 128:T], start=True, stop=True)
                    last.then_inc(HD["qk"][h], 1)

                def outputs(h):
                    pe.wait_ge(HD["a"][h], i + 1)
                    r = slice(64 * (h % 2), 64 * (h % 2) + 64)
                    for jk in range(NB):
                        at, n = KEYS_AT[jk], T - 128 * jk
                        last = pe.matmul(ps[r, 5 + h // 2, jk * 128:T], xt[:, jk, h * 64:(h + 1) * 64],
                                         aw[:, h % 2, at // T, at % T:at % T + n], start=False, stop=(jk == NB - 1),
                                         skip_group_check=True)
                    last.then_inc(HD["y"][h], 1)

                spread(0)
                pe.wait_ge(S["xt"], i + 1)
                for n in range(2):
                    pe.matmul(ps[:, 5 + n, :], dx[:, n * 128:(n + 1) * 128], XN[:, bass.ds(i * T, T)],
                              start=True, stop=False, skip_group_check=True)
                pe.wait_ge(S["z0sb"], i + 1)
                project(i, 7, W("in")[:, 128:256]).then_inc(S["z1"], 1)
                spread(1)
                for h in range(H):
                    products(h)
                    if h:
                        outputs(h - 1)
                    if h + 2 < H:
                        spread(h + 2)
                outputs(H - 1)

            pe.wait_ge(S["dx"], 1)
            turn(0, True)
            with pe.Fori(1, B) as i:
                turn(i, False)
            out(B - 1)

        @block.scalar
        def _(act):
            def finish(i):
                act.wait_ge(S["sps"], i + 1)
                act.activation(SX[:, bass.ds(i * T, T)], ps[:, 7, :], ACT.Copy).then_inc(S["s"], 1)

            def gate(i, n):
                act.wait_ge(S[f"z{n}"], i + 1)
                act.activation(zs[:, n, :], ps[:, 7, :], ACT.Silu).then_inc(S[f"z{n}sb"], 1)

            def turn(i, first):
                act.wait_ge(S["bcps"], i + 1)
                act.wait_ge(S["norm"], i)
                act.activation(sq[:], ps[:, 0:2, :], ACT.Square).then_inc(S["sq"], 1)
                act.wait_ge(S["ang"], i + 1)
                act.wait_ge(S["th"], i)
                act.activation(ang[:], ps[:, 2, :], ACT.Copy).then_inc(S["angsb"], 1)
                if not first:
                    finish(i - 1)
                act.wait_ge(S["ms"], i + 1)
                act.activation(sq[:], ps[:, 5:7, :], ACT.Ln, bias=cst("eps")).then_inc(S["std"], 1)
                act.wait_ge(S["std"], i + 1)
                act.activation(sq[:], sq[:], ACT.Exp, scale=-0.5).then_inc(S["rs"], 1)
                act.wait_ge(S["clamp"], i + 1)
                act.activation(th[:, 2, :], th[:, 0, :], ACT.Sin).then_inc(S["sin"], 1)
                act.activation(th[:, 1, :], th[:, 0, :], ACT.Abs).then_inc(S["abs"], 1)
                act.wait_ge(S["abs"], i + 1)
                act.activation(th[:, 1, :], th[:, 1, :], ACT.Sin, scale=-1.0, bias=cst("halfpi")).then_inc(S["cos"], 1)
                act.wait_ge(S["pj2"], i + 1)
                act.wait_ge(HD["y"][H - 1], i)
                act.activation(xt[:].rearrange("p j f -> p (j f)"), ps[:, 5:7, :].rearrange("p n t -> p (n t)"),
                               ACT.Copy).then_inc(S["xt"], 1)

                def biased(h):
                    if h:
                        act.wait_ge(HD["t2"][h - 1], i + 1)
                    for n in range(2):
                        last = act.activation(tb[:, n, :], bc[:, n, :], ACT.Identity,
                                              bias=W("bc_b")[:, n * H + h:n * H + h + 1])
                    last.then_inc(HD["b0"][h], 1)

                act.wait_ge(S["norm"], i + 1)
                biased(0)
                gate(i, 0)
                gate(i, 1)
                for h in range(H):
                    if h + 1 < H:
                        biased(h + 1)
                    act.wait_ge(HD["dd"][h], i + 1)
                    for g, n in ((0, T), (1, T), (2, 256)):
                        last = act.activation(dec[:, h % 2, g, 0:n], dec[:, h % 2, g, 0:n], ACT.Exp)
                    last.then_inc(HD["dec"][h], 1)

            turn(0, True)
            with act.Fori(1, B) as i:
                turn(i, False)
            finish(B - 1)

        @block.gpsimd
        def _(g):
            with g.Fori(0, B) as i:
                def turned(h):
                    g.wait_ge(HD["t2"][h], i + 1)
                    if h >= 2:
                        g.wait_ge(HD["qk"][h - 2], i + 1)
                    for n in range(2):
                        last = g.tensor_tensor(kq[:, h % 2, K_ if n == 0 else Q_, :], t2[:, n, :], t3[:, n, :], ALU.add)
                    last.then_inc(HD["turned"][h], 1)

                g.wait_ge(HD["dm"][H - 1], i)
                for h in range(H):
                    for n, c, src in ((0, 1, "stri"), (1, 2, "ident")):
                        if n and h:
                            g.wait_ge(HD["m2"][h - 1], i + 1)
                        last = g.tensor_tensor(mm[:, h] if n == 0 else own[:],
                                               cst(src).unsqueeze(1).to_broadcast([128, NB, 128]),
                                               COL[:, c, :, bass.ds(i * H + h, 1)].to_broadcast([128, NB, 128]),
                                               ALU.mult)
                    last.then_inc(HD["m1"][h], 1)
                    g.wait_ge(HD["m1"][h], i + 1)
                    g.tensor_tensor(mm[:, h], mm[:, h], own[:], ALU.add).then_inc(HD["m2"][h], 1)
                g.wait_ge(HD["m2"][H - 1], i + 1)
                turned(0)
                for h in range(H):
                    g.wait_ge(HD["dec"][h], i + 1)
                    for jk in range(NB):
                        at = KEYS_AT[jk]
                        d = dec[:, h % 2, at // T, at % T:at % T + 128]
                        last = g.tensor_tensor(d, d, mm[:, h, jk, :], ALU.mult)
                    last.then_inc(HD["dm"][h], 1)
                    if h + 1 < H:
                        turned(h + 1)

        @block.vector
        def _(v):
            v.tensor_tensor(dx[:], W("in")[:, 256:512], W("d_row"), ALU.mult).then_inc(S["dx"], 1)
            with v.Fori(0, B) as i:
                v.wait_ge(S["pj2"], i)
                v.tensor_copy(xs[:], XN[:, bass.ds(i * T, T)]).then_inc(S["xs"], 1)
                v.wait_ge(S["angsb"], i + 1)
                v.wait_ge(S["rows"], 16 * 2 * H * (i + 1))
                v.tensor_tensor(ang[:], ang[:], dtb[:], ALU.mult).then_inc(S["at"], 1)
                v.wait_ge(S["at"], i + 1)
                v.tensor_tensor_scan(th[:, 0, :], cst("onerow"), ang[:], 0.0, ALU.mult, ALU.add).then_inc(S["th"], 1)
                v.wait_ge(S["th"], i + 1)
                v.wait_ge(HD["cps"][H - 1], i)
                v.tensor_scalar(th[:, 1, :], th[:, 0, :], float(1 / (2 * np.pi)), MAGIC, ALU.mult,
                                ALU.add).then_inc(S["n"], 1)
                v.wait_ge(S["n"], i + 1)
                v.tensor_scalar(th[:, 1, :], th[:, 1, :], MAGIC, None, ALU.subtract).then_inc(S["n1"], 1)
                v.wait_ge(S["n1"], i + 1)
                v.scalar_tensor_tensor(out=th[:, 0, :], in0=th[:, 1, :], scalar=-TWO_PI_HI, in1=th[:, 0, :],
                                       op0=ALU.mult, op1=ALU.add).then_inc(S["c1"], 1)
                v.wait_ge(S["c1"], i + 1)
                v.scalar_tensor_tensor(out=th[:, 0, :], in0=th[:, 1, :], scalar=-TWO_PI_LO, in1=th[:, 0, :],
                                       op0=ALU.mult, op1=ALU.add).then_inc(S["c2"], 1)
                v.wait_ge(S["c2"], i + 1)
                v.tensor_scalar(th[:, 0, :], th[:, 0, :], 3.1415925, -3.1415925, ALU.min,
                                ALU.max).then_inc(S["clamp"], 1)
                v.wait_ge(S["rs"], i + 1)
                v.wait_ge(HD["b0"][H - 1], i)
                for n in range(2):
                    v.scalar_tensor_tensor(out=bc[:, n, :], in0=ps[:, n, :], scalar=W("bc_w")[:, n:n + 1],
                                           in1=sq[:, n, :], op0=ALU.mult, op1=ALU.mult)
                    last = v.scalar_tensor_tensor(out=rot[:, n, :], in0=ps[:, 3 + n, :], scalar=W("bc_rw")[:, n:n + 1],
                                                  in1=sq[:, n, :], op0=ALU.mult, op1=ALU.mult)
                last.then_inc(S["norm"], 1)
                v.wait_ge(S["cos"], i + 1)
                v.tensor_scalar(th[:, 1, :], th[:, 1, :], 1.0, None, ALU.subtract).then_inc(S["cosm"], 1)
                v.wait_ge(S["norm"], i + 1)

                def prepare(h):
                    v.wait_ge(HD["cps"][h], i + 1)
                    if h:
                        v.wait_ge(HD["turned"][h - 1], i + 1)
                    v.wait_ge(HD["b0"][h], i + 1)
                    for n in range(2):
                        v.scalar_tensor_tensor(out=t2[:, n, :], in0=ps[:, 3, :], scalar=1.0, in1=tb[:, n, :],
                                               op0=ALU.add, op1=ALU.mult)
                        last = v.scalar_tensor_tensor(out=t3[:, n, :], in0=rot[:, n, :],
                                                      scalar=W("bc_rb")[:, n * H + h:n * H + h + 1], in1=ps[:, 4, :],
                                                      op0=ALU.add, op1=ALU.mult)
                    last.then_inc(HD["t2"][h], 1)
                    if h >= 2:
                        v.wait_ge(HD["a"][h - 2], i + 1)
                    for jk in range(NB):
                        at, n = KEYS_AT[jk], T - 128 * jk
                        last = v.tensor_scalar(dec[:, h % 2, at // T, at % T:at % T + n], ellb[:, h, jk * 128:T],
                                               COL[:, 0, jk, bass.ds(i * H + h, 1)], 0.0, ALU.subtract, ALU.min)
                    last.then_inc(HD["dd"][h], 1)

                def weigh(h):
                    v.wait_ge(HD["qk"][h], i + 1)
                    v.wait_ge(HD["dm"][h], i + 1)
                    if h >= 2:
                        v.wait_ge(HD["y"][h - 2], i + 1)
                    for jk in range(NB):
                        at, n = KEYS_AT[jk], T - 128 * jk
                        g, o = at // T, at % T
                        last = v.tensor_tensor(aw[:, h % 2, g, o:o + 128], ps[:, g, o:o + 128], dec[:, h % 2, g, o:o + 128],
                                               ALU.mult)
                        if n > 128:
                            last = v.scalar_tensor_tensor(
                                out=aw[:, h % 2, g, o + 128:o + n], in0=ps[:, g, o + 128:o + n],
                                scalar=COL[:, 1, jk, bass.ds(i * H + h, 1)], in1=dec[:, h % 2, g, o + 128:o + n],
                                op0=ALU.mult, op1=ALU.mult)
                    last.then_inc(HD["a"][h], 1)

                prepare(0)
                for h in range(H):
                    if h + 1 < H:
                        prepare(h + 1)
                    weigh(h)
                v.wait_ge(HD["y"][H - 1], i + 1)
                v.wait_ge(S["sps"], i)
                v.wait_ge(S["z1sb"], i + 1)
                v.tensor_tensor(y[:], ps[:, 5:7, :], zs[:], ALU.mult).then_inc(S["yz"], 1)


def rows_at(places, n):
    out = np.zeros((n, places[0][1].shape[1]), np.float32)
    for at, a in places:
        out[at:at + a.shape[0]] = a
    return out


def col(a):
    return np.reshape(a, (-1, 1))


def w0_parts(I):
    L = lambda n: I["L0_attn_" + n]
    return {
        "maa_x": col(L("time_maa_x")), "maa": L("time_maa").reshape(4, C).T,
        "maa_w1": L("time_maa_w1").T,
        "maa_w2": L("time_maa_w2").transpose(0, 2, 1).reshape(128, C),
        "receptance": L("receptance").T, "gate_w1": L("gate_w1").T, "gate_w2": L("gate_w2").T,
        "key_w": L("key_w").T, "value": L("value").T, "output": L("output").T,
        "kkk_mk_w1": rows_at([(0, L("time_kkk_w1")), (32, L("mk_w1"))], 64).T,
        "kkk_w2": rows_at([(0, L("time_kkk_w2").T)], 32),
        "mk_w2": rows_at([(32, L("mk_w2").T)], 64),
        "decay_aaa_ma_w1": rows_at([(0, L("time_decay_w1")), (64, L("time_aaa_w1")), (96, L("ma_w1"))], 128).T,
        "decay_w2": L("time_decay_w2").T,
        "aaa_w2": rows_at([(64, L("time_aaa_w2").T)], 96),
        "ma_w2": rows_at([(96, L("ma_w2").T)], 128),
        "decay": col(L("time_decay")), "aaaaa": col(L("time_aaaaa")), "misc_a": col(L("time_misc_a")),
        "misc_k": col(L("time_misc_k")), "ln_w": col(L("ln_w")), "ln_b": col(L("ln_b")),
        "faaaa": col(L("time_faaaa")), "router": I["L0_ffn_Wr"].T,
    }


def w1_parts(I):
    return {
        "q": I["L1_attn_Wq"].T, "k": I["L1_attn_Wk"].T,
        "v": I["L1_attn_Wv"].T, "o": I["L1_attn_Wo"].T, "gate": I["L1_ffn_Wg"],
        "ffb1": I["L1_ffn_b1"].reshape(-1, 128).T, "ffb2": I["L1_ffn_b2"].T,
    }


def w2_parts(I):
    L = lambda n: I["L2_attn_" + n]
    w, b = L("qkv_w"), L("qkv_b")
    return {
        "q": w[:, 0:C], "k": w[:, C:2 * C], "qk_b": b[0:2 * C].reshape(2, C).T,
        "v": w[:, 2 * C:], "v_b_row": np.broadcast_to(b[2 * C:], (128, C)),
        "o": L("out_w"), "o_b": col(L("out_b")), "g_attn": col(L("g_attn")), "b_attn": col(L("b_attn")),
        "g1": col(L("g1")), "b1": col(L("b1")), "g2": col(L("g2")), "b2": col(L("b2")),
        "w_ctx": L("w_ctx"), "w_x": L("w_x"), "b_inl": col(L("b_inl")),
        "ff_w1": L("ff_w1"), "ff_b1": L("ff_b1").reshape(4, 128).T,
        "ff_w2": L("ff_w2").reshape(4, 128, C).transpose(1, 0, 2).reshape(128, 4 * C), "ff_b2": col(L("ff_b2")),
    }


def w2f_parts(I):
    L = lambda n: I["L2_ffn_" + n]
    wide = lambda w: w.T.reshape(4, 128, -1).transpose(1, 0, 2).reshape(128, -1)
    cols = lambda b: b.reshape(4, 128).T
    return {
        "w1": L("w1_w").T, "w2": L("w2_w").T, "h1": wide(L("h1_w")), "h2": wide(L("h2_w")), "w3": wide(L("w3_w")),
        "s1": cols(L("w1_s")), "s2": cols(L("w2_s")), "sh1": cols(L("h1_s")), "sh2": cols(L("h2_s")),
        "s3": col(L("w3_s")),
    }


def w3f_parts(I):
    L = lambda n: I["L3_ffn_" + n]
    return {"q": L("Wq"), "k": L("Wk"), "v": L("Wv"), "wo": L("Wo"), "wff": L("Wff")}


def w3a_parts(I):
    L = lambda n: I["L3_attn_" + n]
    w = L("W_in")
    o = np.cumsum([0, 256, 256, 128, 128, 4, 4, 4, 32])
    z, x, bb, cc, dt, aa, trap, ang = [w[:, o[n]:o[n + 1]] for n in range(8)]
    rows = np.zeros((C, 3, B, B, 4), np.float32)
    for n, part in enumerate((dt, aa, trap)):
        for b in range(B):
            rows[:, n, b, b] = part

    def turned(a):
        return np.concatenate([a[..., 32:64], a[..., 0:32], np.zeros_like(a[..., 64:])], -1)

    return {
        "in": np.concatenate([z, x, bb, cc, ang, ang, ang, ang], 1), "rows": rows.reshape(C, -1),
        "out": L("W_out").reshape(2, 128, C).transpose(1, 0, 2).reshape(128, 2 * C),
        "dt_bias": col(np.broadcast_to(L("dt_bias"), (B, 4))), "bc_w": np.stack([L("B_norm_w"), L("C_norm_w")], 1),
        "bc_b": np.concatenate([L("B_bias"), L("C_bias")]).T,
        "bc_rb": turned(np.concatenate([L("B_bias"), L("C_bias")])).T,
        "bc_rw": turned(np.stack([L("B_norm_w"), L("C_norm_w")])).T,
        "in_turned": np.concatenate([turned(bb), turned(cc)], 1),
        "d_row": np.broadcast_to(np.repeat(L("D"), 64), (128, 256)),
    }


def constb_parts():
    i = np.arange(128)
    return {
        "identb": np.eye(128, dtype=np.float32),
        "neg_down": np.where(i[None] > i[:, None], -1e30, 0).astype(np.float32),
        "neg_across": np.where(i[:, None] > i[None], -1e30, 0).astype(np.float32),
    }


def closing(first, n):
    out = np.zeros((128, GROUPS, 128), np.float32)
    for g in range(GROUPS):
        for h in range(GH):
            for d in range(8):
                out[32 * h + first + (d if n > 1 else 0), g, 8 * (g * GH + h) + d] = 1
    return out.reshape(128, GROUPS * 128)


def const_parts():
    i = np.arange(128)
    return {
        "ident": np.eye(128, dtype=np.float32),
        "mean": np.full((128, 128), 1 / C, np.float32),
        "ones": np.ones((128, 128), np.float32),
        "headsum": (i[:, None] // 8 == i[None] // 8).astype(np.float32),
        "tri": (i[:, None] <= i[None]).astype(np.float32),
        "headmean": (i[:, None] // 8 == i[None] // 8).astype(np.float32) / 8,
        "exsum": (i[:, None] // 16 == i[None] // 16).astype(np.float32),
        "exbefore": ((i[:, None] // 16 == i[None] // 16) & (i[:, None] < i[None])).astype(np.float32),
        "onerow": np.ones((128, 512), np.float32),
        "stri": (i[:, None] < i[None]).astype(np.float32),
        "rot": ((i[:, None] < 64) & (i[None] < 64) & (i[:, None] == (i[None] + 32) % 64)).astype(np.float32),
        "spread": np.concatenate([((i[:, None] // 32 == h) & (i[None] < 64) & (i[:, None] % 32 == i[None] % 32))
                                  .astype(np.float32) for h in range(4)], 1),
        "spread_sin": np.concatenate([((i[:, None] // 32 == h) & (i[None] < 64) & (i[:, None] % 32 == i[None] % 32))
                                      * np.where(i[None] < 32, -1, 1).astype(np.float32) for h in range(4)], 1),
        "halfpi": np.full((128, 1), np.pi / 2, np.float32),
        "halfwide": np.concatenate([0.5 * (i[:, None] <= i[None]), np.full((128, T - 128), 0.5)], 1
                                   ).astype(np.float32),
        "halfcount": 0.5 * np.arange(1, T + 1, dtype=np.float32)[None],
        "close": closing(0, 8), "close_den": closing(8, 1),
        "flip": np.eye(128, dtype=np.float32)[::-1],
        "rhalf": np.full((128, 1), 0.5 ** 0.5, np.float32),
        "eps": np.full((128, 1), 1e-5, np.float32),
        "gn_eps": np.full((128, 1), 0.00064, np.float32),
        "mhalf": np.full((128, 1), -0.5, np.float32),
        "tiny": np.full((128, 1), 1e-24, np.float32),
    }


def pack(parts):
    at, place, cols = 0, {}, []
    for n, a in parts.items():
        full = np.zeros((128, a.shape[1]), np.float32)
        full[:a.shape[0]] = a
        place[n] = (at, a.shape[0], a.shape[1])
        at += a.shape[1]
        cols.append(full)
    return np.concatenate(cols, 1), place


def view(tile, place):
    def get(name):
        at, rows, n = place[name]
        return tile[0:rows, at:at + n]
    return get


def update_phase(nc, K, layer, out=None):
    X, SX, GX = K["X"], K["SX"], K["GX"]
    PARTS = 4
    N = NT // PARTS
    with ExitStack() as ctx:
        S = sems(nc, ctx, f"u{layer}", "gate prod added stored", 1)
        block = ctx.enter_context(nc.Block())

        @block.scalar
        def _(act):
            for n in range(PARTS):
                p = slice(n * N, (n + 1) * N)
                act.activation(GX[:, p], GX[:, p], ACT.Silu).then_inc(S["gate"], 1)

        @block.vector
        def _(v):
            for n in range(PARTS):
                p = slice(n * N, (n + 1) * N)
                v.wait_ge(S["gate"], n + 1)
                v.tensor_tensor(SX[:, p], SX[:, p], GX[:, p], ALU.mult).then_inc(S["prod"], 1)
                v.wait_ge(S["prod"], n + 1)
                v.tensor_tensor(X[:, p], X[:, p], SX[:, p], ALU.add).then_inc(S["added"], 1)

        if out is not None:
            @block.sync
            def _(sp):
                for n in range(PARTS):
                    p = slice(n * N, (n + 1) * N)
                    sp.wait_ge(S["added"], n + 1)
                    sp.dma_start(out[:, p], X[:, p]).then_inc(S["stored"], 16)
                sp.wait_ge(S["stored"], 16 * PARTS)


def load_phase(nc, tag, pairs):
    with ExitStack() as ctx:
        loaded = sems(nc, ctx, "ld" + tag, "loaded")["loaded"]
        block = ctx.enter_context(nc.Block())

        @block.sync
        def _(sp):
            for dst, src in pairs:
                sp.dma_start(dst, src).then_inc(loaded, 16)
            sp.wait_ge(loaded, 16 * len(pairs))


def zero_phase(nc, zero):
    with nc.Block() as block:
        @block.vector
        def _(v):
            v.memset(zero[:], 0.0)


def convert_phase(nc, dst, src):
    with nc.Block() as block:
        @block.vector
        def _(v):
            v.tensor_copy(dst, src)


def network(nc, A, out, places):
    with ExitStack() as ctx:
        K = {"A": A}
        for n in ("X", "XN", "SX", "GX"):
            K[n] = ctx.enter_context(nc.sbuf_tensor(n, [128, NT], F32))

        def weights(scope, name):
            n = places[name][1]
            tile = scope.enter_context(nc.sbuf_tensor("w_" + name, [128, n], F32))
            K[name] = view(tile, places[name][0])
            return tile[:], A[name]

        def scratch(name, shape, dtype):
            K[name] = nc.dram_tensor(name, shape, dtype, kind="Internal").ap()

        def tile(scope, name, shape, dtype, layer=""):
            K[name] = scope.enter_context(nc.sbuf_tensor(name + layer, shape, dtype))

        tile(ctx, "zero", [1, T], BF16)
        zero_phase(nc, K["zero"])
        first = [weights(ctx, "cst"), (K["X"][:], A["x"])]
        with ExitStack() as layer:
            load_phase(nc, "0", first + [weights(layer, "w0")])
            norm_phase(nc, K, "0")
            scratch("Qd", [8, B, 128, T], F32)
            scratch("Yd", [128, B, T], F32)
            scratch("Xt", [NT, C], F32)
            scratch("Acc", [NT, C], F32)
            tile(layer, "IDX", [128, E], U32)
            tile(layer, "WGT", [128, E], F32)
            with ExitStack() as choice:
                H = 64 + E
                tile(choice, "LOG", [H, NT // 2], F32)
                tile(choice, "BEST", [H, CAP], F32)
                tile(choice, "AT", [H, CAP], U32)
                tile(choice, "TOP", [H, 8], F32)
                tile(choice, "WHERE", [H, 8], U32)
                route_phase(nc, K)
                rwkv_pre_phase(nc, K)
                choice_phase(nc, K)
            scan_and_experts_phase(nc, K)
            rwkv_out_phase(nc, K)
            collect_phase(nc, K)
        update_phase(nc, K, "0")
        with ExitStack() as layer:
            load_phase(nc, "1", [weights(layer, "w1")])
            norm_phase(nc, K, "1")
            scratch("Pd1", [B, 2, 3, 2 * C, T], BF16)
            K["Pd"] = K["Pd1"]
            tile(layer, "VA", [128, NT // 128, 16, 9], F32, "1")
            split_phase(nc, K, "s1", "XN", K["w1"]("q"), K["w1"]("k"), K["w1"]("v"), 2, 16)
            causal_phase(nc, K, "ta", "SX", 16, False)
            project_phase(nc, K, "tp", "SX", K["w1"]("o"))
            scratch("Sd", [E1, NT], F32)
            scratch("Gd", [E1, NT], F32)
            choose_phase(nc, K)
            ffn1_phase(nc, K)
        update_phase(nc, K, "1")
        with ExitStack() as layer:
            n = places["cb_f32"][1]
            tile(layer, "VA", [128, NT // 128, 16, 9], F32, "2")
            tile(layer, "cb_tile", [128, n], BF16)
            K["cb"] = view(K["cb_tile"], places["cb_f32"][0])
            own = [weights(layer, "w2"), weights(layer, "cb_f32")]
            branch = layer.enter_context(ExitStack())
            load_phase(nc, "2", own + [weights(branch, "w2f")])
            norm_phase(nc, K, "2")
            at = {p: K["cb"](p) for p in places["cb_f32"][0]}
            for p in at:
                convert_phase(nc, at[p], K["cb_f32"](p))
            norm_phase(nc, K, "2a", "XN", "SX", K["w2"]("g_attn"), K["w2"]("b_attn"))
            scratch("Pd", [B, 2, 3, C, T], BF16)
            scratch("Md", [B, 2, 16, T], BF16)
            split_phase(nc, K, "s2", "SX", K["w2"]("q"), K["w2"]("k"), K["w2"]("v"), 1, 8, K["w2"]("qk_b"))
            maxima_and_mlp_phase(nc, K)
            branch.close()
            causal_phase(nc, K, "at", "SX", 8, True)
            project_phase(nc, K, "ap", "SX", K["w2"]("o"), K["w2"]("o_b"))
            inertia_phase(nc, K)
        update_phase(nc, K, "2")
        with ExitStack() as layer:
            load_phase(nc, "3", [weights(layer, "w3")])
            norm_phase(nc, K, "3")
            tile(layer, "VA", [128, NT // 128, 16, 9], F32, "3")
            split_phase(nc, K, "s3", "XN", K["w3"]("q"), K["w3"]("k"), K["w3"]("v"), 1, 8, qscale=float(1 / np.sqrt(C)))
            column_attention_phase(nc, K)
            l2_gelu_phase(nc, K)
        with ExitStack() as layer:
            load_phase(nc, "3a", [weights(layer, "w3a")])
            scratch("Rd", [2, B * 4, T], F32)
            tile(layer, "COL", [128, 3, NB, B * 4], F32)
            ssm_rows_phase(nc, K)
            ssm_phase(nc, K)
        update_phase(nc, K, "3", out)


def kernel(**inputs):
    import numpy as _np
    import concourse.bacc as _bacc
    from concourse import mybir as _mybir
    from concourse.bass_utils import run_bass_kernel_spmd as _run

    I = {n: _np.asarray(a) for n, a in inputs.items()}
    arrays, places = {}, {}
    for name, parts in (("cst", const_parts()), ("cb_f32", constb_parts()), ("w0", w0_parts(I)), ("w1", w1_parts(I)),
                        ("w2", w2_parts(I)), ("w2f", w2f_parts(I)), ("w3", w3f_parts(I)), ("w3a", w3a_parts(I))):
        a, place = pack(parts)
        arrays[name] = a
        places[name] = (place, a.shape[1])
    arrays["x"] = I["L0_attn_x"].reshape(NT, C).T
    arrays["e_w1"], arrays["e_w2"] = I["L0_ffn_W1"], I["L0_ffn_W2"]
    arrays["e_b1"] = I["L0_ffn_b1"].transpose(2, 0, 1).reshape(128, -1)
    arrays["e_b2"] = I["L0_ffn_b2"].reshape(1, -1)
    arrays["f1_w1"], arrays["f1_w2"] = I["L1_ffn_W1"], I["L1_ffn_W2"]
    arrays = {n: _np.ascontiguousarray(a) for n, a in arrays.items()}

    nc = _bacc.Bacc("TRN2", target_bir_lowering=False, num_devices=1)
    A = {n: nc.dram_tensor(n, a.shape, _mybir.dt.from_np(a.dtype), kind="ExternalInput").ap()
         for n, a in arrays.items()}
    out = nc.dram_tensor("out", (C, NT), F32, kind="ExternalOutput").ap()
    network(nc, A, out, places)
    r = _run(nc, [arrays], core_ids=[0])
    return _np.ascontiguousarray(r.results[0]["out"].T).reshape(B, T, C)
```
